# Optimizing a Trainium2 kernel written in Bass

```python
import numpy as np
import jax
import jax.numpy as jnp

def _softmax(x, axis=-1):
    return jax.nn.softmax(x, axis=axis)

def _gelu(x):
    return jax.nn.gelu(x, approximate=True)

def _silu(x):
    return jax.nn.silu(x)

def _sigmoid(x):
    return jax.nn.sigmoid(x)

def _layernorm(x, axis=-1, eps=1e-05):
    m = jnp.mean(x, axis=axis, keepdims=True)
    v = jnp.var(x, axis=axis, keepdims=True)
    return (x - m) / jnp.sqrt(v + eps)

def _scatter_add(tgt, idx, src, axis=0):
    return tgt.at[idx].add(src)

def _segment_sum(src, seg, n):
    return jax.ops.segment_sum(src, seg, n)
kernel_name = 'mk_hybrid_d4_jaxref_r8_c36e2b'

def setup_inputs(seed: int=0):
    np.random.seed(seed)
    _w = jnp.asarray

    def _L0_attn_a_setup():
        import jax, jax.numpy as jnp
        import numpy as np
        from jax import lax
        B, L, HS = (4, 512, 128)
        NH, DK, DV = (4, 32, 32)
        CONV, CHUNK, FIRS, FIRL = (4, 32, 5, 64)
        GIN, GH = (HS + 16, HS * 2 // 2)
        DECAY = 1.0 - 1.0 / 3000.0
        EPS_FLOOR = 0.08 * DECAY
        RMS_EPS = 1e-05

        def _l2norm(x):
            return x * lax.rsqrt(jnp.sum(x * x, -1, keepdims=True) + 1e-06)

        def _dwconv_causal(x, filt):
            K = filt.shape[-1]
            xf = jnp.transpose(x, (0, 2, 1))
            xf = jnp.pad(xf, ((0, 0), (0, 0), (K - 1, 0)))
            y = lax.conv_general_dilated(xf, filt[:, None, :], (1,), 'VALID', feature_group_count=filt.shape[0], dimension_numbers=('NCH', 'OIH', 'NCH'))
            return jnp.transpose(y, (0, 2, 1))

        def _delta_rule_chunkwise(q, k, v, beta, chunk=CHUNK):
            b, h, Lq, dk = q.shape
            dv = v.shape[-1]
            n = Lq // chunk
            q = _l2norm(q)
            k = _l2norm(k)
            v = v * beta[..., None]
            kb = k * beta[..., None]
            r = lambda x: x.reshape(b, h, n, chunk, -1)
            q, k, v, kb = (r(q), r(k), r(v), r(kb))
            strict_low = jnp.tril(jnp.ones((chunk, chunk), bool), -1)
            A = jnp.where(strict_low, -jnp.einsum('bhnid,bhnjd->bhnij', kb, k), 0.0)
            eye = jnp.eye(chunk, dtype=q.dtype)
            T = jax.scipy.linalg.solve_triangular(eye - A, jnp.broadcast_to(eye, A.shape), lower=True, unit_diagonal=True)
            u = T @ v
            w = T @ kb
            low = jnp.tril(jnp.ones((chunk, chunk), bool))

            def step(S, inp):
                qi, ki, ui, wi = inp
                attn = jnp.where(low, jnp.einsum('bhid,bhjd->bhij', qi, ki), 0.0)
                u_i = ui - wi @ S
                o_i = qi @ S + attn @ u_i
                S = S + jnp.einsum('bhcd,bhce->bhde', ki, u_i)
                return (S, o_i)
            mv = lambda x: jnp.moveaxis(x, 2, 0)
            S0 = jnp.zeros((b, h, dk, dv), q.dtype)
            S, o = lax.scan(step, S0, (mv(q), mv(k), mv(u), mv(w)))
            o = jnp.moveaxis(o, 0, 2).reshape(b, h, Lq, dv)
            return (o, S)

        def _stats(x):
            mean = jnp.mean(x, -1, keepdims=True)
            var = jnp.var(x, -1, keepdims=True)
            am = jnp.mean(jnp.abs(x), -1, keepdims=True)
            l2 = jnp.linalg.norm(x, axis=-1, keepdims=True)
            return jnp.concatenate([mean, var, am, l2], -1)
        key = jax.random.key(seed)
        ks = jax.random.split(key, 16)
        s = 0.02
        fs = jnp.zeros((NH, DV, FIRS)).at[..., -1].set(1.0) + 0.015 * jax.random.normal(ks[8], (NH, DV, FIRS))
        fl = jnp.zeros((NH, DV, FIRL)).at[..., -1].set(1.0) + 0.015 * jax.random.normal(ks[9], (NH, DV, FIRL))
        return {'hidden_states': jax.random.normal(ks[0], (B, L, HS), jnp.float32), 'Wq': s * jax.random.normal(ks[1], (NH * DK, HS)), 'Wk': s * jax.random.normal(ks[2], (NH * DK, HS)), 'Wv': s * jax.random.normal(ks[3], (NH * DV, HS)), 'Wb': s * jax.random.normal(ks[4], (NH, HS)), 'conv_q_w': s * jax.random.normal(ks[5], (NH * DK, CONV)), 'conv_k_w': s * jax.random.normal(ks[6], (NH * DK, CONV)), 'conv_v_w': s * jax.random.normal(ks[7], (NH * DV, CONV)), 'fir_short_filt': fs, 'fir_long_filt': fl, 'gate_W1': s * jax.random.normal(ks[10], (GH, GIN)), 'gate_b1': jnp.zeros((GH,)), 'gate_W2': s * jax.random.normal(ks[11], (4, GH)), 'gate_b2': jnp.zeros((4,)), 'gate_copy_bias': jnp.full((NH,), 4.0), 'gate_log_temp': jnp.log(jnp.full((NH,), 2.0)), 'o_norm_w': jnp.ones((DV,)), 'Wo': s * jax.random.normal(ks[12], (HS, NH * DV))}
    _L0_attn_a_in = _L0_attn_a_setup()

    def _L0_attn_b_setup():
        import jax, jax.numpy as jnp
        import numpy as np
        from jax import lax
        D_MODEL = 128
        EXPAND = 2
        D_INNER = EXPAND * D_MODEL
        D_STATE = 16
        D_CONV = 4
        DT_RANK = D_MODEL // 16
        B_SZ = 4
        SEQ = 256

        def _mamba_fwd(x, W_in, conv_w, conv_b, W_x, W_dt, b_dt, A_log, D, W_out):
            B, L, _ = x.shape
            xz = jnp.einsum('bld,ed->ble', x, W_in)
            u, z = jnp.split(xz, 2, axis=-1)
            u_nc = u.transpose(0, 2, 1)
            u_c = lax.conv_general_dilated(u_nc, conv_w[:, None, :], window_strides=(1,), padding=[(D_CONV - 1, 0)], feature_group_count=D_INNER, dimension_numbers=('NCH', 'OIH', 'NCH'))
            u_c = (u_c + conv_b[None, :, None]).transpose(0, 2, 1)
            u_c = jax.nn.silu(u_c)
            x_dbl = jnp.einsum('bld,ed->ble', u_c, W_x)
            dt_r, Bm, Cm = jnp.split(x_dbl, [DT_RANK, DT_RANK + D_STATE], axis=-1)
            dt = jax.nn.softplus(jnp.einsum('blr,dr->bld', dt_r, W_dt) + b_dt)
            A = -jnp.exp(A_log)

            def step(h, inp):
                dt_t, u_t, B_t, C_t = inp
                dA = jnp.exp(dt_t[..., None] * A)
                h = dA * h + (dt_t * u_t)[..., None] * B_t[:, None, :]
                y_t = jnp.einsum('bds,bs->bd', h, C_t)
                return (h, y_t)
            xs = (dt.transpose(1, 0, 2), u_c.transpose(1, 0, 2), Bm.transpose(1, 0, 2), Cm.transpose(1, 0, 2))
            h0 = jnp.zeros((B, D_INNER, D_STATE), dtype=x.dtype)
            _, ys = lax.scan(step, h0, xs)
            y = ys.transpose(1, 0, 2)
            y = y + u_c * D
            y = y * jax.nn.silu(z)
            out = jnp.einsum('bld,ed->ble', y, W_out)
            return out

        def _reference_tuple_inner(x, W_in, conv_w, conv_b, W_x, W_dt, b_dt, A_log, D, W_out):
            out = _mamba_fwd(x, W_in, conv_w, conv_b, W_x, W_dt, b_dt, A_log, D, W_out)
            return (out, None)
        key = jax.random.key(seed)
        ks = jax.random.split(key, 10)
        s = lambda k, shape, scale: jax.random.normal(k, shape, dtype=jnp.float32) * scale
        inp = {'x': s(ks[0], (B_SZ, SEQ, D_MODEL), 1.0), 'W_in': s(ks[1], (2 * D_INNER, D_MODEL), D_MODEL ** (-0.5)), 'conv_w': s(ks[2], (D_INNER, D_CONV), D_CONV ** (-0.5)), 'conv_b': s(ks[3], (D_INNER,), 0.02), 'W_x': s(ks[4], (DT_RANK + 2 * D_STATE, D_INNER), D_INNER ** (-0.5)), 'W_dt': s(ks[5], (D_INNER, DT_RANK), DT_RANK ** (-0.5)), 'b_dt': s(ks[6], (D_INNER,), 0.5), 'A_log': jnp.log(jnp.broadcast_to(jnp.arange(1, D_STATE + 1, dtype=jnp.float32), (D_INNER, D_STATE))), 'D': jnp.ones((D_INNER,), dtype=jnp.float32), 'W_out': s(ks[7], (D_MODEL, D_INNER), D_INNER ** (-0.5))}
        return inp
    _L0_attn_b_in = _L0_attn_b_setup()

    def _L0_ffn_setup():
        import jax, jax.numpy as jnp
        import numpy as np
        from jax.scipy.linalg import expm
        B, S, D, E, K, NROT = (2, 256, 128, 8, 2, 3)
        DF = 4 * D
        EPS = 1e-05
        key = jax.random.key(seed)
        ks = jax.random.split(key, 8)
        s = lambda d: 1.0 / np.sqrt(d)
        return {'x': jax.random.normal(ks[0], (B, S, D), jnp.float32), 'ln_g': jnp.ones((D,), jnp.float32), 'ln_b': jnp.zeros((D,), jnp.float32), 'abel_w': jax.random.normal(ks[1], (D, D), jnp.float32) * s(D), 'abel_b': jnp.zeros((D,), jnp.float32), 'gate_w_moe': jax.random.normal(ks[2], (D, E), jnp.float32) * s(D), 'gate_b_moe': jnp.zeros((E,), jnp.float32), 'w1': jax.random.normal(ks[3], (E, D, DF), jnp.float32) * s(D), 'b1': jnp.zeros((E, DF), jnp.float32), 'w2': jax.random.normal(ks[4], (E, DF, D), jnp.float32) * s(DF), 'b2': jnp.zeros((E, D), jnp.float32), 'gens': jax.random.normal(ks[5], (NROT, D, D), jnp.float32) * 0.02, 'mix_w': jax.random.normal(ks[6], (2 * D, 1), jnp.float32) * s(2 * D), 'mix_b': jnp.zeros((1,), jnp.float32)}
    _L0_ffn_in = _L0_ffn_setup()

    def _L1_attn_a_setup():
        import jax, jax.numpy as jnp
        import numpy as np
        D_MODEL = 128
        N_HEADS = 16
        HEAD_DIM = D_MODEL // N_HEADS

        def alibi_slopes(n_heads):
            base = 2.0 ** (-8.0 / n_heads)
            return jnp.asarray([base ** i for i in range(1, n_heads + 1)], dtype=jnp.float32)
        key = jax.random.key(seed)
        kx, kq, kk, kv, ko = jax.random.split(key, 5)
        B, T = (2, 256)
        scale = 0.02
        x = jax.random.normal(kx, (B, T, D_MODEL), dtype=jnp.float32)
        Wq = jax.random.normal(kq, (D_MODEL, D_MODEL), dtype=jnp.float32) * scale
        Wk = jax.random.normal(kk, (D_MODEL, D_MODEL), dtype=jnp.float32) * scale
        Wv = jax.random.normal(kv, (D_MODEL, D_MODEL), dtype=jnp.float32) * scale
        Wo = jax.random.normal(ko, (D_MODEL, D_MODEL), dtype=jnp.float32) * scale
        return {'x': x, 'Wq': Wq, 'Wk': Wk, 'Wv': Wv, 'Wo': Wo}
    _L1_attn_a_in = _L1_attn_a_setup()

    def _L1_attn_b_setup():
        import jax, jax.numpy as jnp
        import numpy as np
        EMB = 128
        HEADS = 8
        BUCKET = 64
        N_HASHES = 8

        def _lsh_attention(qk, v, rotations):
            B, t, d = qk.shape
            nh = N_HASHES
            bucket = BUCKET
            n_buckets = t // bucket
            n_bins = n_buckets
            rotated = jnp.einsum('btf,fhi->bhti', qk, rotations)
            rotated = jnp.concatenate([rotated, -rotated], axis=-1)
            buckets = jnp.argmax(rotated, axis=-1)
            offsets = (jnp.arange(nh) * n_buckets)[None, :, None]
            buckets = (buckets + offsets).reshape(B, nh * t)
            ticker = jnp.arange(nh * t)
            buckets_and_t = t * buckets + (ticker % t)[None, :]
            sticker = jnp.argsort(buckets_and_t, axis=-1, stable=True)
            undo_sort = jnp.argsort(sticker, axis=-1, stable=True)
            st = sticker % t
            sqk = jnp.take_along_axis(qk, st[:, :, None], axis=1)
            sv = jnp.take_along_axis(v, st[:, :, None], axis=1)
            bq_t = st.reshape(B, nh * n_bins, bucket)
            bqk = sqk.reshape(B, nh * n_bins, bucket, d)
            bv = sv.reshape(B, nh * n_bins, bucket, d)
            bq = bqk
            sq = jnp.maximum(jnp.sum(bqk * bqk, axis=-1, keepdims=True), 1e-12)
            bk = bqk * jax.lax.rsqrt(sq)

            def look_one_back(x):
                x1 = x.reshape((B, nh, n_bins) + x.shape[2:])
                x_extra = jnp.concatenate([x1[:, :, 1:2], x1[:, :, :-1]], axis=2)
                x_extra = x_extra.reshape(x.shape)
                return jnp.concatenate([x, x_extra], axis=2)
            bk = look_one_back(bk)
            bv = look_one_back(bv)
            bkv_t = look_one_back(bq_t)
            scale = d ** (-0.5)
            dots = jnp.einsum('bhie,bhje->bhij', bq * scale, bk)
            self_mask = (bq_t[:, :, :, None] == bkv_t[:, :, None, :]).astype(dots.dtype)
            dots = dots * (1.0 - self_mask) + self_mask * -100000.0
            dots_logsumexp = jax.scipy.special.logsumexp(dots, axis=-1, keepdims=True)
            probs = jnp.exp(dots - dots_logsumexp)
            bo = jnp.einsum('buij,buje->buie', probs, bv)
            so = bo.reshape(B, nh * t, d)
            slogits = dots_logsumexp.reshape(B, nh * t)
            o = jnp.take_along_axis(so, undo_sort[:, :, None], axis=1)
            logits = jnp.take_along_axis(slogits, undo_sort, axis=1)
            o = o.reshape(B, nh, t, d)
            logits = logits.reshape(B, nh, t, 1)
            w = jnp.exp(logits - jax.scipy.special.logsumexp(logits, axis=1, keepdims=True))
            return jnp.sum(o * w, axis=1)
        key = jax.random.key(seed)
        k0, k1, k2, k3, k4 = jax.random.split(key, 5)
        b, t, e = (2, 512, EMB)
        dh = e // HEADS
        n_buckets = t // BUCKET
        s = 1.0 / np.sqrt(e)
        return {'x': jax.random.normal(k0, (b, t, e), jnp.float32), 'w_qk': jax.random.normal(k1, (e, e), jnp.float32) * s, 'w_v': jax.random.normal(k2, (e, e), jnp.float32) * s, 'w_out': jax.random.normal(k3, (e, e), jnp.float32) * s, 'b_out': jnp.zeros((e,), jnp.float32), 'rotations': jax.random.normal(k4, (dh, N_HASHES, n_buckets // 2), jnp.float32)}
    _L1_attn_b_in = _L1_attn_b_setup()

    def _L1_ffn_setup():
        import jax, jax.numpy as jnp
        import numpy as np
        D_IN, D_HID = (128, 512)

        def _ternary(key, shape):
            return jax.random.randint(key, shape, -1, 2).astype(jnp.float32)

        def _tlin(x, w, s):
            return jnp.einsum('bsi,oi->bso', x, w) * s
        key = jax.random.key(seed)
        ks = jax.random.split(key, 12)
        inv = lambda fan: 1.0 / np.sqrt(fan).astype(np.float32)
        return {'x': jax.random.normal(ks[0], (4, 256, D_IN), dtype=jnp.float32), 'w1_w': _ternary(ks[1], (D_HID, D_IN)), 'w1_s': jax.random.uniform(ks[2], (D_HID,), dtype=jnp.float32) * inv(D_IN), 'w2_w': _ternary(ks[3], (D_HID, D_IN)), 'w2_s': jax.random.uniform(ks[4], (D_HID,), dtype=jnp.float32) * inv(D_IN), 'h1_w': _ternary(ks[5], (D_HID, D_HID)), 'h1_s': jax.random.uniform(ks[6], (D_HID,), dtype=jnp.float32) * inv(D_HID), 'h2_w': _ternary(ks[7], (D_HID, D_HID)), 'h2_s': jax.random.uniform(ks[8], (D_HID,), dtype=jnp.float32) * inv(D_HID), 'w3_w': _ternary(ks[9], (D_IN, D_HID)), 'w3_s': jax.random.uniform(ks[10], (D_IN,), dtype=jnp.float32) * inv(D_HID)}
    _L1_ffn_in = _L1_ffn_setup()

    def _L2_attn_a_setup():
        import jax, jax.numpy as jnp
        import numpy as np
        B, T, HID = (4, 256, 128)
        NH = 4
        KD, VD = (64, 128)
        DK, DV = (KD // NH, VD // NH)
        R = 32
        GLR = 64
        EPS = 1e-05

        def _rwkv6_scan(r, k, v, w, u):

            def step(S, xs):
                r_t, k_t, v_t, w_t = xs
                kv = k_t[..., :, None] * v_t[..., None, :]
                o_t = jnp.einsum('bhk,bhkv->bhv', r_t, S + u[None, :, :, None] * kv)
                S = jnp.exp(w_t)[..., None] * S + kv
                return (S, o_t)
            S0 = jnp.zeros(r.shape[:2] + (r.shape[-1], v.shape[-1]), r.dtype)
            mv = lambda x: jnp.moveaxis(x, 2, 0)
            _, o = jax.lax.scan(step, S0, (mv(r), mv(k), mv(v), mv(w)))
            return jnp.moveaxis(o, 0, 2)
        key = jax.random.key(seed)
        ks = jax.random.split(key, 20)
        g = lambda i, shape, s=0.02: jax.random.normal(ks[i], shape, dtype=jnp.float32) * s
        return {'hidden_states': jax.random.normal(ks[0], (B, T, HID), dtype=jnp.float32), 'mu0': g(1, (HID,), 0.1), 'W_x0': g(2, (5 * R, HID)), 'W_x2': g(3, (HID, 5 * R)), 'x_bias': g(4, (5, HID), 0.1), 'W_r': g(5, (KD, HID)), 'W_w1': g(6, (GLR, HID)), 'W_w2': g(7, (KD, GLR)), 'b_w2': g(8, (KD,), 0.1), 'W_k': g(9, (KD, HID)), 'W_v': g(10, (VD, HID)), 'W_g': g(11, (VD, HID)), 'bonus': g(12, (NH, DK), 0.1), 'gn_weight': jnp.ones((VD,), jnp.float32) + g(13, (VD,), 0.05), 'gn_bias': g(14, (VD,), 0.05), 'W_o': g(15, (HID, VD))}
    _L2_attn_a_in = _L2_attn_a_setup()

    def _L2_attn_b_setup():
        import jax, jax.numpy as jnp
        import numpy as np
        KEY_DIM = 128
        SCALE = KEY_DIM ** (-0.5)
        key = jax.random.key(seed)
        k1, k2, k3, k4 = jax.random.split(key, 4)
        B, S, E = (4, 256, 128)
        x = jax.random.normal(k1, (B, S, E), dtype=jnp.float32)
        WQ = jax.random.normal(k2, (KEY_DIM, E), dtype=jnp.float32) * E ** (-0.5)
        WK = jax.random.normal(k3, (KEY_DIM, E), dtype=jnp.float32) * E ** (-0.5)
        WV = jax.random.normal(k4, (KEY_DIM, E), dtype=jnp.float32) * E ** (-0.5)
        return {'x': x, 'WQ': WQ, 'WK': WK, 'WV': WV}
    _L2_attn_b_in = _L2_attn_b_setup()

    def _L2_ffn_setup():
        import jax, jax.numpy as jnp
        import numpy as np
        HIDDEN = 128
        N_ROUTED = 16
        N_SHARED = 2
        TOP_K = 2
        MID_R = HIDDEN // 4
        MID_S = HIDDEN // 2
        key = jax.random.key(seed)
        ks = jax.random.split(key, 8)
        s = 0.02
        return {'x': jax.random.normal(ks[0], (2, 128, HIDDEN), dtype=jnp.float32), 'router_w': jax.random.normal(ks[1], (HIDDEN, N_ROUTED), dtype=jnp.float32) * s, 'wg_r': jax.random.normal(ks[2], (N_ROUTED, HIDDEN, MID_R), dtype=jnp.float32) * s, 'wu_r': jax.random.normal(ks[3], (N_ROUTED, HIDDEN, MID_R), dtype=jnp.float32) * s, 'wd_r': jax.random.normal(ks[4], (N_ROUTED, MID_R, HIDDEN), dtype=jnp.float32) * s, 'wg_s': jax.random.normal(ks[5], (N_SHARED, HIDDEN, MID_S), dtype=jnp.float32) * s, 'wu_s': jax.random.normal(ks[6], (N_SHARED, HIDDEN, MID_S), dtype=jnp.float32) * s, 'wd_s': jax.random.normal(ks[7], (N_SHARED, MID_S, HIDDEN), dtype=jnp.float32) * s}
    _L2_ffn_in = _L2_ffn_setup()

    def _L3_attn_a_setup():
        import jax, jax.numpy as jnp
        import numpy as np
        N_HEADS = 16
        key = jax.random.key(seed)
        k1, k2 = jax.random.split(key)
        B, N, D = (2, 256, 128)
        hidden_states = jax.random.normal(k1, (B, N, D), dtype=jnp.float32)
        std = 0.02 / np.sqrt(2.0 * 24 * D)
        queries_weight = jax.random.normal(k2, (D, D), dtype=jnp.float32) * std
        return {'hidden_states': hidden_states, 'queries_weight': queries_weight}
    _L3_attn_a_in = _L3_attn_a_setup()

    def _L3_attn_b_setup():
        import jax, jax.numpy as jnp
        import numpy as np
        EMBED_DIM = 128
        NUM_HEADS = 16
        WINDOW = 128

        def _sliding_window_attention(x, Wq, bq, Wk, bk, Wv, bv, Wo, bo):
            B, S, D = x.shape
            H, w = (NUM_HEADS, WINDOW)
            hd = D // H
            bs = w
            nb = S // bs

            def proj(W, b):
                y = x @ W.T + b
                return y.reshape(B, S, H, hd).transpose(0, 2, 1, 3)
            q = proj(Wq, bq)
            k = proj(Wk, bk)
            v = proj(Wv, bv)
            qb = q.reshape(B, H, nb, bs, hd)
            pad = ((0, 0), (0, 0), (bs, bs), (0, 0))
            kp = jnp.pad(k, pad).reshape(B, H, nb + 2, bs, hd)
            vp = jnp.pad(v, pad).reshape(B, H, nb + 2, bs, hd)
            k_ctx = jnp.concatenate([kp[:, :, :-2], kp[:, :, 1:-1], kp[:, :, 2:]], axis=3)
            v_ctx = jnp.concatenate([vp[:, :, :-2], vp[:, :, 1:-1], vp[:, :, 2:]], axis=3)
            scale = 1.0 / np.sqrt(hd).astype(np.float32)
            scores = jnp.einsum('bhnqd,bhnkd->bhnqk', qb, k_ctx) * scale
            q_off = jnp.arange(bs)
            k_off = jnp.arange(3 * bs)
            rel = k_off[None, :] - bs - q_off[:, None]
            win_ok = jnp.abs(rel) <= w
            k_pos = (jnp.arange(nb)[:, None, None] - 1) * bs + k_off[None, None, :]
            valid = (k_pos >= 0) & (k_pos < S)
            mask = win_ok[None] & valid
            scores = jnp.where(mask[None, None], scores, jnp.float32(-jnp.inf))
            weights = jax.nn.softmax(scores, axis=-1)
            out = jnp.einsum('bhnqk,bhnkd->bhnqd', weights, v_ctx)
            out = out.reshape(B, H, S, hd).transpose(0, 2, 1, 3).reshape(B, S, D)
            return out @ Wo.T + bo
        key = jax.random.key(seed)
        ks = jax.random.split(key, 9)
        D = EMBED_DIM
        x = jax.random.normal(ks[0], (2, 1024, D), dtype=jnp.float32)
        s = 0.02
        Wq = jax.random.normal(ks[1], (D, D), dtype=jnp.float32) * s
        bq = jax.random.normal(ks[2], (D,), dtype=jnp.float32) * s
        Wk = jax.random.normal(ks[3], (D, D), dtype=jnp.float32) * s
        bk = jax.random.normal(ks[4], (D,), dtype=jnp.float32) * s
        Wv = jax.random.normal(ks[5], (D, D), dtype=jnp.float32) * s
        bv = jax.random.normal(ks[6], (D,), dtype=jnp.float32) * s
        Wo = jax.random.normal(ks[7], (D, D), dtype=jnp.float32) * s
        bo = jax.random.normal(ks[8], (D,), dtype=jnp.float32) * s
        return {'x': x, 'Wq': Wq, 'bq': bq, 'Wk': Wk, 'bk': bk, 'Wv': Wv, 'bv': bv, 'Wo': Wo, 'bo': bo}
    _L3_attn_b_in = _L3_attn_b_setup()

    def _L3_ffn_setup():
        import jax, jax.numpy as jnp
        import numpy as np
        E = 8
        TOP_K = 2
        B, S, D = (2, 512, 128)
        H = 512
        CAPACITY = 256

        def _moe(x, Wg, W1, b1, W2, b2):
            b, s, d = x.shape
            xf = x.reshape(b * s, d)
            logits = xf.astype(jnp.float32) @ Wg.astype(jnp.float32)
            probs = jax.nn.softmax(logits, axis=-1)
            vals, idx = jax.lax.top_k(probs, TOP_K)
            w = vals / (jnp.sum(vals, axis=-1, keepdims=True) + 1e-09)
            counts = jnp.zeros((E,), dtype=jnp.int32)
            combine = jnp.zeros((b * s, E), dtype=jnp.float32)
            for k in range(TOP_K):
                oh = jax.nn.one_hot(idx[:, k], E, dtype=jnp.int32)
                pos = jnp.cumsum(oh, axis=0) - 1 + counts[None, :]
                keep = (oh == 1) & (pos < CAPACITY)
                counts = counts + jnp.sum(keep.astype(jnp.int32), axis=0)
                combine = combine + w[:, k][:, None] * keep.astype(jnp.float32)
            out = jnp.zeros_like(xf)
            for e in range(E):
                h = jax.nn.gelu(xf @ W1[e] + b1[e])
                ye = h @ W2[e] + b2[e]
                out = out + combine[:, e][:, None].astype(xf.dtype) * ye
            return out.reshape(b, s, d)
        key = jax.random.key(seed)
        k0, k1, k2, k3 = jax.random.split(key, 4)
        return {'x': jax.random.normal(k0, (B, S, D), dtype=jnp.float32), 'Wg': jax.random.normal(k1, (D, E), dtype=jnp.float32) * 0.02, 'W1': jax.random.normal(k2, (E, D, H), dtype=jnp.float32) * 0.02, 'b1': jnp.zeros((E, H), dtype=jnp.float32), 'W2': jax.random.normal(k3, (E, H, D), dtype=jnp.float32) * 0.02, 'b2': jnp.zeros((E, D), dtype=jnp.float32)}
    _L3_ffn_in = _L3_ffn_setup()
    _d = {'L0_attn_a_hidden_states': _L0_attn_a_in['hidden_states'], 'L0_attn_a_Wq': _L0_attn_a_in['Wq'], 'L0_attn_a_Wk': _L0_attn_a_in['Wk'], 'L0_attn_a_Wv': _L0_attn_a_in['Wv'], 'L0_attn_a_Wb': _L0_attn_a_in['Wb'], 'L0_attn_a_conv_q_w': _L0_attn_a_in['conv_q_w'], 'L0_attn_a_conv_k_w': _L0_attn_a_in['conv_k_w'], 'L0_attn_a_conv_v_w': _L0_attn_a_in['conv_v_w'], 'L0_attn_a_fir_short_filt': _L0_attn_a_in['fir_short_filt'], 'L0_attn_a_fir_long_filt': _L0_attn_a_in['fir_long_filt'], 'L0_attn_a_gate_W1': _L0_attn_a_in['gate_W1'], 'L0_attn_a_gate_b1': _L0_attn_a_in['gate_b1'], 'L0_attn_a_gate_W2': _L0_attn_a_in['gate_W2'], 'L0_attn_a_gate_b2': _L0_attn_a_in['gate_b2'], 'L0_attn_a_gate_copy_bias': _L0_attn_a_in['gate_copy_bias'], 'L0_attn_a_gate_log_temp': _L0_attn_a_in['gate_log_temp'], 'L0_attn_a_o_norm_w': _L0_attn_a_in['o_norm_w'], 'L0_attn_a_Wo': _L0_attn_a_in['Wo'], 'L0_attn_b_W_in': _L0_attn_b_in['W_in'], 'L0_attn_b_conv_w': _L0_attn_b_in['conv_w'], 'L0_attn_b_conv_b': _L0_attn_b_in['conv_b'], 'L0_attn_b_W_x': _L0_attn_b_in['W_x'], 'L0_attn_b_W_dt': _L0_attn_b_in['W_dt'], 'L0_attn_b_b_dt': _L0_attn_b_in['b_dt'], 'L0_attn_b_A_log': _L0_attn_b_in['A_log'], 'L0_attn_b_D': _L0_attn_b_in['D'], 'L0_attn_b_W_out': _L0_attn_b_in['W_out'], 'L0_ffn_ln_g': _L0_ffn_in['ln_g'], 'L0_ffn_ln_b': _L0_ffn_in['ln_b'], 'L0_ffn_abel_w': _L0_ffn_in['abel_w'], 'L0_ffn_abel_b': _L0_ffn_in['abel_b'], 'L0_ffn_gate_w_moe': _L0_ffn_in['gate_w_moe'], 'L0_ffn_gate_b_moe': _L0_ffn_in['gate_b_moe'], 'L0_ffn_w1': _L0_ffn_in['w1'], 'L0_ffn_b1': _L0_ffn_in['b1'], 'L0_ffn_w2': _L0_ffn_in['w2'], 'L0_ffn_b2': _L0_ffn_in['b2'], 'L0_ffn_gens': _L0_ffn_in['gens'], 'L0_ffn_mix_w': _L0_ffn_in['mix_w'], 'L0_ffn_mix_b': _L0_ffn_in['mix_b'], 'L1_attn_a_Wq': _L1_attn_a_in['Wq'], 'L1_attn_a_Wk': _L1_attn_a_in['Wk'], 'L1_attn_a_Wv': _L1_attn_a_in['Wv'], 'L1_attn_a_Wo': _L1_attn_a_in['Wo'], 'L1_attn_b_w_qk': _L1_attn_b_in['w_qk'], 'L1_attn_b_w_v': _L1_attn_b_in['w_v'], 'L1_attn_b_w_out': _L1_attn_b_in['w_out'], 'L1_attn_b_b_out': _L1_attn_b_in['b_out'], 'L1_attn_b_rotations': _L1_attn_b_in['rotations'], 'L1_ffn_w1_w': _L1_ffn_in['w1_w'], 'L1_ffn_w1_s': _L1_ffn_in['w1_s'], 'L1_ffn_w2_w': _L1_ffn_in['w2_w'], 'L1_ffn_w2_s': _L1_ffn_in['w2_s'], 'L1_ffn_h1_w': _L1_ffn_in['h1_w'], 'L1_ffn_h1_s': _L1_ffn_in['h1_s'], 'L1_ffn_h2_w': _L1_ffn_in['h2_w'], 'L1_ffn_h2_s': _L1_ffn_in['h2_s'], 'L1_ffn_w3_w': _L1_ffn_in['w3_w'], 'L1_ffn_w3_s': _L1_ffn_in['w3_s'], 'L2_attn_a_mu0': _L2_attn_a_in['mu0'], 'L2_attn_a_W_x0': _L2_attn_a_in['W_x0'], 'L2_attn_a_W_x2': _L2_attn_a_in['W_x2'], 'L2_attn_a_x_bias': _L2_attn_a_in['x_bias'], 'L2_attn_a_W_r': _L2_attn_a_in['W_r'], 'L2_attn_a_W_w1': _L2_attn_a_in['W_w1'], 'L2_attn_a_W_w2': _L2_attn_a_in['W_w2'], 'L2_attn_a_b_w2': _L2_attn_a_in['b_w2'], 'L2_attn_a_W_k': _L2_attn_a_in['W_k'], 'L2_attn_a_W_v': _L2_attn_a_in['W_v'], 'L2_attn_a_W_g': _L2_attn_a_in['W_g'], 'L2_attn_a_bonus': _L2_attn_a_in['bonus'], 'L2_attn_a_gn_weight': _L2_attn_a_in['gn_weight'], 'L2_attn_a_gn_bias': _L2_attn_a_in['gn_bias'], 'L2_attn_a_W_o': _L2_attn_a_in['W_o'], 'L2_attn_b_WQ': _L2_attn_b_in['WQ'], 'L2_attn_b_WK': _L2_attn_b_in['WK'], 'L2_attn_b_WV': _L2_attn_b_in['WV'], 'L2_ffn_router_w': _L2_ffn_in['router_w'], 'L2_ffn_wg_r': _L2_ffn_in['wg_r'], 'L2_ffn_wu_r': _L2_ffn_in['wu_r'], 'L2_ffn_wd_r': _L2_ffn_in['wd_r'], 'L2_ffn_wg_s': _L2_ffn_in['wg_s'], 'L2_ffn_wu_s': _L2_ffn_in['wu_s'], 'L2_ffn_wd_s': _L2_ffn_in['wd_s'], 'L3_attn_a_queries_weight': _L3_attn_a_in['queries_weight'], 'L3_attn_b_Wq': _L3_attn_b_in['Wq'], 'L3_attn_b_bq': _L3_attn_b_in['bq'], 'L3_attn_b_Wk': _L3_attn_b_in['Wk'], 'L3_attn_b_bk': _L3_attn_b_in['bk'], 'L3_attn_b_Wv': _L3_attn_b_in['Wv'], 'L3_attn_b_bv': _L3_attn_b_in['bv'], 'L3_attn_b_Wo': _L3_attn_b_in['Wo'], 'L3_attn_b_bo': _L3_attn_b_in['bo'], 'L3_ffn_Wg': _L3_ffn_in['Wg'], 'L3_ffn_W1': _L3_ffn_in['W1'], 'L3_ffn_b1': _L3_ffn_in['b1'], 'L3_ffn_W2': _L3_ffn_in['W2'], 'L3_ffn_b2': _L3_ffn_in['b2']}
    _x0 = _d['L0_attn_a_hidden_states']
    _d['L0_attn_a_hidden_states'] = jax.random.normal(jax.random.fold_in(jax.random.key(seed), 1), (2, 1024, 128), dtype=_x0.dtype)
    del _x0
    return _d

def reference(L0_attn_a_hidden_states, L0_attn_a_Wq, L0_attn_a_Wk, L0_attn_a_Wv, L0_attn_a_Wb, L0_attn_a_conv_q_w, L0_attn_a_conv_k_w, L0_attn_a_conv_v_w, L0_attn_a_fir_short_filt, L0_attn_a_fir_long_filt, L0_attn_a_gate_W1, L0_attn_a_gate_b1, L0_attn_a_gate_W2, L0_attn_a_gate_b2, L0_attn_a_gate_copy_bias, L0_attn_a_gate_log_temp, L0_attn_a_o_norm_w, L0_attn_a_Wo, L0_attn_b_W_in, L0_attn_b_conv_w, L0_attn_b_conv_b, L0_attn_b_W_x, L0_attn_b_W_dt, L0_attn_b_b_dt, L0_attn_b_A_log, L0_attn_b_D, L0_attn_b_W_out, L0_ffn_ln_g, L0_ffn_ln_b, L0_ffn_abel_w, L0_ffn_abel_b, L0_ffn_gate_w_moe, L0_ffn_gate_b_moe, L0_ffn_w1, L0_ffn_b1, L0_ffn_w2, L0_ffn_b2, L0_ffn_gens, L0_ffn_mix_w, L0_ffn_mix_b, L1_attn_a_Wq, L1_attn_a_Wk, L1_attn_a_Wv, L1_attn_a_Wo, L1_attn_b_w_qk, L1_attn_b_w_v, L1_attn_b_w_out, L1_attn_b_b_out, L1_attn_b_rotations, L1_ffn_w1_w, L1_ffn_w1_s, L1_ffn_w2_w, L1_ffn_w2_s, L1_ffn_h1_w, L1_ffn_h1_s, L1_ffn_h2_w, L1_ffn_h2_s, L1_ffn_w3_w, L1_ffn_w3_s, L2_attn_a_mu0, L2_attn_a_W_x0, L2_attn_a_W_x2, L2_attn_a_x_bias, L2_attn_a_W_r, L2_attn_a_W_w1, L2_attn_a_W_w2, L2_attn_a_b_w2, L2_attn_a_W_k, L2_attn_a_W_v, L2_attn_a_W_g, L2_attn_a_bonus, L2_attn_a_gn_weight, L2_attn_a_gn_bias, L2_attn_a_W_o, L2_attn_b_WQ, L2_attn_b_WK, L2_attn_b_WV, L2_ffn_router_w, L2_ffn_wg_r, L2_ffn_wu_r, L2_ffn_wd_r, L2_ffn_wg_s, L2_ffn_wu_s, L2_ffn_wd_s, L3_attn_a_queries_weight, L3_attn_b_Wq, L3_attn_b_bq, L3_attn_b_Wk, L3_attn_b_bk, L3_attn_b_Wv, L3_attn_b_bv, L3_attn_b_Wo, L3_attn_b_bo, L3_ffn_Wg, L3_ffn_W1, L3_ffn_b1, L3_ffn_W2, L3_ffn_b2):

    def _L0_attn_a_ref(hidden_states, Wq, Wk, Wv, Wb, conv_q_w, conv_k_w, conv_v_w, fir_short_filt, fir_long_filt, gate_W1, gate_b1, gate_W2, gate_b2, gate_copy_bias, gate_log_temp, o_norm_w, Wo):
        import jax, jax.numpy as jnp
        import numpy as np
        from jax import lax
        B, L, HS = (4, 512, 128)
        NH, DK, DV = (4, 32, 32)
        CONV, CHUNK, FIRS, FIRL = (4, 32, 5, 64)
        GIN, GH = (HS + 16, HS * 2 // 2)
        DECAY = 1.0 - 1.0 / 3000.0
        EPS_FLOOR = 0.08 * DECAY
        RMS_EPS = 1e-05

        def _l2norm(x):
            return x * lax.rsqrt(jnp.sum(x * x, -1, keepdims=True) + 1e-06)

        def _dwconv_causal(x, filt):
            K = filt.shape[-1]
            xf = jnp.transpose(x, (0, 2, 1))
            xf = jnp.pad(xf, ((0, 0), (0, 0), (K - 1, 0)))
            y = lax.conv_general_dilated(xf, filt[:, None, :], (1,), 'VALID', feature_group_count=filt.shape[0], dimension_numbers=('NCH', 'OIH', 'NCH'))
            return jnp.transpose(y, (0, 2, 1))

        def _delta_rule_chunkwise(q, k, v, beta, chunk=CHUNK):
            b, h, Lq, dk = q.shape
            dv = v.shape[-1]
            n = Lq // chunk
            q = _l2norm(q)
            k = _l2norm(k)
            v = v * beta[..., None]
            kb = k * beta[..., None]
            r = lambda x: x.reshape(b, h, n, chunk, -1)
            q, k, v, kb = (r(q), r(k), r(v), r(kb))
            strict_low = jnp.tril(jnp.ones((chunk, chunk), bool), -1)
            A = jnp.where(strict_low, -jnp.einsum('bhnid,bhnjd->bhnij', kb, k), 0.0)
            eye = jnp.eye(chunk, dtype=q.dtype)
            T = jax.scipy.linalg.solve_triangular(eye - A, jnp.broadcast_to(eye, A.shape), lower=True, unit_diagonal=True)
            u = T @ v
            w = T @ kb
            low = jnp.tril(jnp.ones((chunk, chunk), bool))

            def step(S, inp):
                qi, ki, ui, wi = inp
                attn = jnp.where(low, jnp.einsum('bhid,bhjd->bhij', qi, ki), 0.0)
                u_i = ui - wi @ S
                o_i = qi @ S + attn @ u_i
                S = S + jnp.einsum('bhcd,bhce->bhde', ki, u_i)
                return (S, o_i)
            mv = lambda x: jnp.moveaxis(x, 2, 0)
            S0 = jnp.zeros((b, h, dk, dv), q.dtype)
            S, o = lax.scan(step, S0, (mv(q), mv(k), mv(u), mv(w)))
            o = jnp.moveaxis(o, 0, 2).reshape(b, h, Lq, dv)
            return (o, S)

        def _stats(x):
            mean = jnp.mean(x, -1, keepdims=True)
            var = jnp.var(x, -1, keepdims=True)
            am = jnp.mean(jnp.abs(x), -1, keepdims=True)
            l2 = jnp.linalg.norm(x, axis=-1, keepdims=True)
            return jnp.concatenate([mean, var, am, l2], -1)
        b, l, _ = hidden_states.shape
        silu = jax.nn.silu
        q = silu(_dwconv_causal(hidden_states @ Wq.T, conv_q_w))
        k = silu(_dwconv_causal(hidden_states @ Wk.T, conv_k_w))
        v = silu(_dwconv_causal(hidden_states @ Wv.T, conv_v_w))
        beta = jax.nn.sigmoid(hidden_states @ Wb.T)
        qh = q.reshape(b, l, NH, DK).transpose(0, 2, 1, 3)
        kh = k.reshape(b, l, NH, DK).transpose(0, 2, 1, 3)
        vh = v.reshape(b, l, NH, DV).transpose(0, 2, 1, 3)
        o_d, _S = _delta_rule_chunkwise(qh, kh, vh, beta.transpose(0, 2, 1))
        o_d = o_d.transpose(0, 2, 1, 3)
        v_direct = v.reshape(b, l, NH, DV)
        vc = v_direct.reshape(b, l, NH * DV)
        fir_s = _dwconv_causal(vc, fir_short_filt.reshape(NH * DV, FIRS)).reshape(b, l, NH, DV)
        fir_l = _dwconv_causal(vc, fir_long_filt.reshape(NH * DV, FIRL)).reshape(b, l, NH, DV)
        stats = jnp.concatenate([_stats(fir_s), _stats(fir_l), _stats(o_d), _stats(v_direct)], -1)
        gin = jnp.concatenate([jnp.broadcast_to(hidden_states[:, :, None, :], (b, l, NH, HS)), stats], -1)
        h1 = jax.nn.gelu(gin @ gate_W1.T + gate_b1)
        logits = h1 @ gate_W2.T + gate_b2
        bias_val = gate_copy_bias * DECAY
        logits = logits + bias_val[None, None, :, None] * jnp.array([0.0, 0.0, 0.0, 1.0], logits.dtype)
        temp = jnp.exp(gate_log_temp)
        wgt = jax.nn.softmax(logits / temp[None, None, :, None], -1)
        wgt = wgt * (1.0 - 4.0 * EPS_FLOOR) + EPS_FLOOR
        o = wgt[..., 0:1] * fir_s + wgt[..., 1:2] * fir_l + wgt[..., 2:3] * o_d + wgt[..., 3:4] * v_direct
        o = o * lax.rsqrt(jnp.mean(o * o, -1, keepdims=True) + RMS_EPS) * o_norm_w
        return o.reshape(b, l, NH * DV) @ Wo.T

    def _L0_attn_b_ref(x, W_in, conv_w, conv_b, W_x, W_dt, b_dt, A_log, D, W_out):
        import jax, jax.numpy as jnp
        import numpy as np
        from jax import lax
        D_MODEL = 128
        EXPAND = 2
        D_INNER = EXPAND * D_MODEL
        D_STATE = 16
        D_CONV = 4
        DT_RANK = D_MODEL // 16
        B_SZ = 4
        SEQ = 256

        def _mamba_fwd(x, W_in, conv_w, conv_b, W_x, W_dt, b_dt, A_log, D, W_out):
            B, L, _ = x.shape
            xz = jnp.einsum('bld,ed->ble', x, W_in)
            u, z = jnp.split(xz, 2, axis=-1)
            u_nc = u.transpose(0, 2, 1)
            u_c = lax.conv_general_dilated(u_nc, conv_w[:, None, :], window_strides=(1,), padding=[(D_CONV - 1, 0)], feature_group_count=D_INNER, dimension_numbers=('NCH', 'OIH', 'NCH'))
            u_c = (u_c + conv_b[None, :, None]).transpose(0, 2, 1)
            u_c = jax.nn.silu(u_c)
            x_dbl = jnp.einsum('bld,ed->ble', u_c, W_x)
            dt_r, Bm, Cm = jnp.split(x_dbl, [DT_RANK, DT_RANK + D_STATE], axis=-1)
            dt = jax.nn.softplus(jnp.einsum('blr,dr->bld', dt_r, W_dt) + b_dt)
            A = -jnp.exp(A_log)

            def step(h, inp):
                dt_t, u_t, B_t, C_t = inp
                dA = jnp.exp(dt_t[..., None] * A)
                h = dA * h + (dt_t * u_t)[..., None] * B_t[:, None, :]
                y_t = jnp.einsum('bds,bs->bd', h, C_t)
                return (h, y_t)
            xs = (dt.transpose(1, 0, 2), u_c.transpose(1, 0, 2), Bm.transpose(1, 0, 2), Cm.transpose(1, 0, 2))
            h0 = jnp.zeros((B, D_INNER, D_STATE), dtype=x.dtype)
            _, ys = lax.scan(step, h0, xs)
            y = ys.transpose(1, 0, 2)
            y = y + u_c * D
            y = y * jax.nn.silu(z)
            out = jnp.einsum('bld,ed->ble', y, W_out)
            return out

        def _reference_tuple_inner(x, W_in, conv_w, conv_b, W_x, W_dt, b_dt, A_log, D, W_out):
            out = _mamba_fwd(x, W_in, conv_w, conv_b, W_x, W_dt, b_dt, A_log, D, W_out)
            return (out, None)
        return _reference_tuple_inner(x, W_in, conv_w, conv_b, W_x, W_dt, b_dt, A_log, D, W_out)[0]

    def _L0_ffn_ref(x, ln_g, ln_b, abel_w, abel_b, gate_w_moe, gate_b_moe, w1, b1, w2, b2, gens, mix_w, mix_b):
        import jax, jax.numpy as jnp
        import numpy as np
        from jax.scipy.linalg import expm
        B, S, D, E, K, NROT = (2, 256, 128, 8, 2, 3)
        DF = 4 * D
        EPS = 1e-05
        residual = x
        mu = jnp.mean(x, axis=-1, keepdims=True)
        var = jnp.mean((x - mu) ** 2, axis=-1, keepdims=True)
        xn = (x - mu) * jax.lax.rsqrt(var + EPS) * ln_g + ln_b
        abel = jax.nn.gelu(xn @ abel_w + abel_b, approximate=False)
        logits = xn @ gate_w_moe + gate_b_moe
        tw, ti = jax.lax.top_k(logits, K)
        tw = jax.nn.softmax(tw, axis=-1)
        onehot = (ti[..., None] == jnp.arange(E)).astype(tw.dtype)
        wdense = jnp.sum(tw[..., None] * onehot, axis=2)
        h = jax.nn.gelu(jnp.einsum('bsd,edf->besf', xn, w1) + b1[None, :, None, :], approximate=False)
        eo = jnp.einsum('besf,efd->besd', h, w2) + b2[None, :, None, :]
        moe = jnp.einsum('besd,bse->bsd', eo, wdense)
        rot = expm(gens[0])
        for i in range(1, NROT):
            rot = rot @ expm(gens[i])
        nonabel = moe @ rot
        combined = jnp.concatenate([abel, nonabel], axis=-1)
        g = jax.nn.sigmoid(combined @ mix_w + mix_b)
        return residual + abel * (1.0 - g) + nonabel * g

    def _L1_attn_a_ref(x, Wq, Wk, Wv, Wo):
        import jax, jax.numpy as jnp
        import numpy as np
        D_MODEL = 128
        N_HEADS = 16
        HEAD_DIM = D_MODEL // N_HEADS

        def alibi_slopes(n_heads):
            base = 2.0 ** (-8.0 / n_heads)
            return jnp.asarray([base ** i for i in range(1, n_heads + 1)], dtype=jnp.float32)
        B, T, D = x.shape
        H, hd = (N_HEADS, HEAD_DIM)

        def proj(W):
            return (x @ W.T).reshape(B, T, H, hd).transpose(0, 2, 1, 3)
        q, k, v = (proj(Wq), proj(Wk), proj(Wv))
        scale = hd ** (-0.5)
        scores = jnp.einsum('bhqd,bhkd->bhqk', q, k) * scale
        pos = jnp.arange(T, dtype=jnp.float32)
        dist = jnp.abs(pos[:, None] - pos[None, :])
        causal = pos[:, None] >= pos[None, :]
        slopes = alibi_slopes(H)
        bias = -slopes[:, None, None] * jnp.where(causal, dist, 0.0)
        scores = scores + bias[None]
        scores = jnp.where(causal[None, None], scores, -jnp.inf)
        attn = jax.nn.softmax(scores, axis=-1)
        out = jnp.einsum('bhqk,bhkd->bhqd', attn, v)
        out = out.transpose(0, 2, 1, 3).reshape(B, T, D)
        return out @ Wo.T

    def _L1_attn_b_ref(x, w_qk, w_v, w_out, b_out, rotations):
        import jax, jax.numpy as jnp
        import numpy as np
        EMB = 128
        HEADS = 8
        BUCKET = 64
        N_HASHES = 8

        def _lsh_attention(qk, v, rotations):
            B, t, d = qk.shape
            nh = N_HASHES
            bucket = BUCKET
            n_buckets = t // bucket
            n_bins = n_buckets
            rotated = jnp.einsum('btf,fhi->bhti', qk, rotations)
            rotated = jnp.concatenate([rotated, -rotated], axis=-1)
            buckets = jnp.argmax(rotated, axis=-1)
            offsets = (jnp.arange(nh) * n_buckets)[None, :, None]
            buckets = (buckets + offsets).reshape(B, nh * t)
            ticker = jnp.arange(nh * t)
            buckets_and_t = t * buckets + (ticker % t)[None, :]
            sticker = jnp.argsort(buckets_and_t, axis=-1, stable=True)
            undo_sort = jnp.argsort(sticker, axis=-1, stable=True)
            st = sticker % t
            sqk = jnp.take_along_axis(qk, st[:, :, None], axis=1)
            sv = jnp.take_along_axis(v, st[:, :, None], axis=1)
            bq_t = st.reshape(B, nh * n_bins, bucket)
            bqk = sqk.reshape(B, nh * n_bins, bucket, d)
            bv = sv.reshape(B, nh * n_bins, bucket, d)
            bq = bqk
            sq = jnp.maximum(jnp.sum(bqk * bqk, axis=-1, keepdims=True), 1e-12)
            bk = bqk * jax.lax.rsqrt(sq)

            def look_one_back(x):
                x1 = x.reshape((B, nh, n_bins) + x.shape[2:])
                x_extra = jnp.concatenate([x1[:, :, 1:2], x1[:, :, :-1]], axis=2)
                x_extra = x_extra.reshape(x.shape)
                return jnp.concatenate([x, x_extra], axis=2)
            bk = look_one_back(bk)
            bv = look_one_back(bv)
            bkv_t = look_one_back(bq_t)
            scale = d ** (-0.5)
            dots = jnp.einsum('bhie,bhje->bhij', bq * scale, bk)
            self_mask = (bq_t[:, :, :, None] == bkv_t[:, :, None, :]).astype(dots.dtype)
            dots = dots * (1.0 - self_mask) + self_mask * -100000.0
            dots_logsumexp = jax.scipy.special.logsumexp(dots, axis=-1, keepdims=True)
            probs = jnp.exp(dots - dots_logsumexp)
            bo = jnp.einsum('buij,buje->buie', probs, bv)
            so = bo.reshape(B, nh * t, d)
            slogits = dots_logsumexp.reshape(B, nh * t)
            o = jnp.take_along_axis(so, undo_sort[:, :, None], axis=1)
            logits = jnp.take_along_axis(slogits, undo_sort, axis=1)
            o = o.reshape(B, nh, t, d)
            logits = logits.reshape(B, nh, t, 1)
            w = jnp.exp(logits - jax.scipy.special.logsumexp(logits, axis=1, keepdims=True))
            return jnp.sum(o * w, axis=1)
        b, t, e = x.shape
        h = HEADS
        dh = e // h
        qk = x @ w_qk
        v = x @ w_v

        def merge_heads(z):
            return z.reshape(b, t, h, dh).transpose(0, 2, 1, 3).reshape(b * h, t, dh)
        out = _lsh_attention(merge_heads(qk), merge_heads(v), rotations)
        out = out.reshape(b, h, t, dh).transpose(0, 2, 1, 3).reshape(b, t, e)
        return out @ w_out + b_out

    def _L1_ffn_ref(x, w1_w, w1_s, w2_w, w2_s, h1_w, h1_s, h2_w, h2_s, w3_w, w3_s):
        import jax, jax.numpy as jnp
        import numpy as np
        D_IN, D_HID = (128, 512)

        def _ternary(key, shape):
            return jax.random.randint(key, shape, -1, 2).astype(jnp.float32)

        def _tlin(x, w, s):
            return jnp.einsum('bsi,oi->bso', x, w) * s
        h = jax.nn.silu(_tlin(x, w1_w, w1_s)) * _tlin(x, w2_w, w2_s)
        h = jax.nn.gelu(_tlin(h, h1_w, h1_s), approximate=False)
        h = jax.nn.gelu(_tlin(h, h2_w, h2_s), approximate=False)
        return _tlin(h, w3_w, w3_s)

    def _L2_attn_a_ref(hidden_states, mu0, W_x0, W_x2, x_bias, W_r, W_w1, W_w2, b_w2, W_k, W_v, W_g, bonus, gn_weight, gn_bias, W_o):
        import jax, jax.numpy as jnp
        import numpy as np
        B, T, HID = (4, 256, 128)
        NH = 4
        KD, VD = (64, 128)
        DK, DV = (KD // NH, VD // NH)
        R = 32
        GLR = 64
        EPS = 1e-05

        def _rwkv6_scan(r, k, v, w, u):

            def step(S, xs):
                r_t, k_t, v_t, w_t = xs
                kv = k_t[..., :, None] * v_t[..., None, :]
                o_t = jnp.einsum('bhk,bhkv->bhv', r_t, S + u[None, :, :, None] * kv)
                S = jnp.exp(w_t)[..., None] * S + kv
                return (S, o_t)
            S0 = jnp.zeros(r.shape[:2] + (r.shape[-1], v.shape[-1]), r.dtype)
            mv = lambda x: jnp.moveaxis(x, 2, 0)
            _, o = jax.lax.scan(step, S0, (mv(r), mv(k), mv(v), mv(w)))
            return jnp.moveaxis(o, 0, 2)
        x = hidden_states
        shifted = jnp.pad(x, ((0, 0), (1, 0), (0, 0)))[:, :-1]
        delta = shifted - x
        xp = jnp.tanh((x + delta * mu0) @ W_x0.T)
        xp = xp.reshape(x.shape[0], x.shape[1], 5, R)
        mus = jnp.einsum('blnr,hnr->blnh', xp, W_x2.reshape(HID, 5, R)) + x_bias
        mu_r, mu_w, mu_k, mu_v, mu_g = (mus[:, :, i] for i in range(5))
        r = (x + delta * mu_r) @ W_r.T
        w = jnp.tanh((x + delta * mu_w) @ W_w1.T) @ W_w2.T + b_w2
        k = (x + delta * mu_k) @ W_k.T
        v = (x + delta * mu_v) @ W_v.T
        g = (x + delta * mu_g) @ W_g.T
        split = lambda t, d: t.reshape(t.shape[0], t.shape[1], NH, d).transpose(0, 2, 1, 3)
        r_, k_, w_ = (split(r, DK), split(k, DK), split(w, DK))
        v_ = split(v, DV)
        w_ = -jnp.exp(w_)
        o = _rwkv6_scan(r_, k_, v_, w_, bonus)
        o = o.transpose(0, 2, 1, 3)
        mean = o.mean(-1, keepdims=True)
        var = o.var(-1, keepdims=True)
        o = (o - mean) * jax.lax.rsqrt(var + EPS)
        o = o.reshape(x.shape[0], x.shape[1], VD) * gn_weight + gn_bias
        o = o * jax.nn.silu(g)
        return o @ W_o.T

    def _L2_attn_b_ref(x, WQ, WK, WV):
        import jax, jax.numpy as jnp
        import numpy as np
        KEY_DIM = 128
        SCALE = KEY_DIM ** (-0.5)
        q = jnp.einsum('bse,ke->bsk', x, WQ)
        k = jnp.einsum('bse,ke->bsk', x, WK)
        v = jnp.einsum('bse,ve->bsv', x, WV)
        scores = jnp.einsum('bsk,btk->bst', q, k) * SCALE
        masked = jnp.where(jnp.tril(scores) == 0, -jnp.inf, scores)
        attn = jax.nn.softmax(masked, axis=-1)
        return jnp.einsum('bst,btv->bsv', attn, v)

    def _L2_ffn_ref(x, router_w, wg_r, wu_r, wd_r, wg_s, wu_s, wd_s):
        import jax, jax.numpy as jnp
        import numpy as np
        HIDDEN = 128
        N_ROUTED = 16
        N_SHARED = 2
        TOP_K = 2
        MID_R = HIDDEN // 4
        MID_S = HIDDEN // 2
        orig_shape = x.shape
        flat = x.reshape(-1, orig_shape[-1])
        gs = jnp.einsum('td,ndm->tnm', flat, wg_s)
        us = jnp.einsum('td,ndm->tnm', flat, wu_s)
        out = jnp.einsum('tnm,nmd->td', jax.nn.silu(gs) * us, wd_s)
        logits = (flat @ router_w).astype(jnp.float32)
        probs = jax.nn.softmax(logits, axis=-1)
        weights, indices = jax.lax.top_k(probs, TOP_K)
        weights = weights / (weights.sum(axis=-1, keepdims=True) + 1e-09)
        weights = weights.astype(x.dtype)
        comb = jnp.sum(jax.nn.one_hot(indices, N_ROUTED, dtype=x.dtype) * weights[..., None], axis=1)
        g = jnp.einsum('td,edm->tem', flat, wg_r)
        u = jnp.einsum('td,edm->tem', flat, wu_r)
        h = jax.nn.silu(g) * u
        h = h * comb[:, :, None]
        out = out + jnp.einsum('tem,emd->td', h, wd_r)
        return out.reshape(orig_shape)

    def _L3_attn_a_ref(hidden_states, queries_weight):
        import jax, jax.numpy as jnp
        import numpy as np
        N_HEADS = 16
        B, N, D = hidden_states.shape
        H = N_HEADS
        hd = D // H
        q = (hidden_states @ queries_weight).reshape(B, N, H, hd).transpose(0, 2, 1, 3)
        xh = hidden_states.reshape(B, N, H, hd)
        k = xh.transpose(0, 2, 3, 1)
        v = xh.transpose(0, 2, 1, 3)
        pre_attn = jnp.tril(jnp.einsum('bhnd,bhdm->bhnm', q, k))
        attn = jnp.einsum('bhnm,bhmd->bhnd', pre_attn, v)
        return attn.transpose(0, 2, 1, 3).reshape(B, N, D)

    def _L3_attn_b_ref(x, Wq, bq, Wk, bk, Wv, bv, Wo, bo):
        import jax, jax.numpy as jnp
        import numpy as np
        EMBED_DIM = 128
        NUM_HEADS = 16
        WINDOW = 128

        def _sliding_window_attention(x, Wq, bq, Wk, bk, Wv, bv, Wo, bo):
            B, S, D = x.shape
            H, w = (NUM_HEADS, WINDOW)
            hd = D // H
            bs = w
            nb = S // bs

            def proj(W, b):
                y = x @ W.T + b
                return y.reshape(B, S, H, hd).transpose(0, 2, 1, 3)
            q = proj(Wq, bq)
            k = proj(Wk, bk)
            v = proj(Wv, bv)
            qb = q.reshape(B, H, nb, bs, hd)
            pad = ((0, 0), (0, 0), (bs, bs), (0, 0))
            kp = jnp.pad(k, pad).reshape(B, H, nb + 2, bs, hd)
            vp = jnp.pad(v, pad).reshape(B, H, nb + 2, bs, hd)
            k_ctx = jnp.concatenate([kp[:, :, :-2], kp[:, :, 1:-1], kp[:, :, 2:]], axis=3)
            v_ctx = jnp.concatenate([vp[:, :, :-2], vp[:, :, 1:-1], vp[:, :, 2:]], axis=3)
            scale = 1.0 / np.sqrt(hd).astype(np.float32)
            scores = jnp.einsum('bhnqd,bhnkd->bhnqk', qb, k_ctx) * scale
            q_off = jnp.arange(bs)
            k_off = jnp.arange(3 * bs)
            rel = k_off[None, :] - bs - q_off[:, None]
            win_ok = jnp.abs(rel) <= w
            k_pos = (jnp.arange(nb)[:, None, None] - 1) * bs + k_off[None, None, :]
            valid = (k_pos >= 0) & (k_pos < S)
            mask = win_ok[None] & valid
            scores = jnp.where(mask[None, None], scores, jnp.float32(-jnp.inf))
            weights = jax.nn.softmax(scores, axis=-1)
            out = jnp.einsum('bhnqk,bhnkd->bhnqd', weights, v_ctx)
            out = out.reshape(B, H, S, hd).transpose(0, 2, 1, 3).reshape(B, S, D)
            return out @ Wo.T + bo
        return _sliding_window_attention(x, Wq, bq, Wk, bk, Wv, bv, Wo, bo)

    def _L3_ffn_ref(x, Wg, W1, b1, W2, b2):
        import jax, jax.numpy as jnp
        import numpy as np
        E = 8
        TOP_K = 2
        B, S, D = (2, 512, 128)
        H = 512
        CAPACITY = 256

        def _moe(x, Wg, W1, b1, W2, b2):
            b, s, d = x.shape
            xf = x.reshape(b * s, d)
            logits = xf.astype(jnp.float32) @ Wg.astype(jnp.float32)
            probs = jax.nn.softmax(logits, axis=-1)
            vals, idx = jax.lax.top_k(probs, TOP_K)
            w = vals / (jnp.sum(vals, axis=-1, keepdims=True) + 1e-09)
            counts = jnp.zeros((E,), dtype=jnp.int32)
            combine = jnp.zeros((b * s, E), dtype=jnp.float32)
            for k in range(TOP_K):
                oh = jax.nn.one_hot(idx[:, k], E, dtype=jnp.int32)
                pos = jnp.cumsum(oh, axis=0) - 1 + counts[None, :]
                keep = (oh == 1) & (pos < CAPACITY)
                counts = counts + jnp.sum(keep.astype(jnp.int32), axis=0)
                combine = combine + w[:, k][:, None] * keep.astype(jnp.float32)
            out = jnp.zeros_like(xf)
            for e in range(E):
                h = jax.nn.gelu(xf @ W1[e] + b1[e])
                ye = h @ W2[e] + b2[e]
                out = out + combine[:, e][:, None].astype(xf.dtype) * ye
            return out.reshape(b, s, d)
        return _moe(x, Wg, W1, b1, W2, b2)
    x = L0_attn_a_hidden_states
    x = x + _L0_attn_a_ref(_layernorm(x, axis=-1), L0_attn_a_Wq, L0_attn_a_Wk, L0_attn_a_Wv, L0_attn_a_Wb, L0_attn_a_conv_q_w, L0_attn_a_conv_k_w, L0_attn_a_conv_v_w, L0_attn_a_fir_short_filt, L0_attn_a_fir_long_filt, L0_attn_a_gate_W1, L0_attn_a_gate_b1, L0_attn_a_gate_W2, L0_attn_a_gate_b2, L0_attn_a_gate_copy_bias, L0_attn_a_gate_log_temp, L0_attn_a_o_norm_w, L0_attn_a_Wo)
    x = x + _L0_ffn_ref(_layernorm(x, axis=-1), L0_ffn_ln_g, L0_ffn_ln_b, L0_ffn_abel_w, L0_ffn_abel_b, L0_ffn_gate_w_moe, L0_ffn_gate_b_moe, L0_ffn_w1, L0_ffn_b1, L0_ffn_w2, L0_ffn_b2, L0_ffn_gens, L0_ffn_mix_w, L0_ffn_mix_b)
    x = x + _L0_attn_b_ref(_layernorm(x, axis=-1), L0_attn_b_W_in, L0_attn_b_conv_w, L0_attn_b_conv_b, L0_attn_b_W_x, L0_attn_b_W_dt, L0_attn_b_b_dt, L0_attn_b_A_log, L0_attn_b_D, L0_attn_b_W_out)
    x = x + _L0_ffn_ref(_layernorm(x, axis=-1), L0_ffn_ln_g, L0_ffn_ln_b, L0_ffn_abel_w, L0_ffn_abel_b, L0_ffn_gate_w_moe, L0_ffn_gate_b_moe, L0_ffn_w1, L0_ffn_b1, L0_ffn_w2, L0_ffn_b2, L0_ffn_gens, L0_ffn_mix_w, L0_ffn_mix_b)
    x = x + _L1_attn_a_ref(_layernorm(x, axis=-1), L1_attn_a_Wq, L1_attn_a_Wk, L1_attn_a_Wv, L1_attn_a_Wo)
    x = x + _L1_ffn_ref(_layernorm(x, axis=-1), L1_ffn_w1_w, L1_ffn_w1_s, L1_ffn_w2_w, L1_ffn_w2_s, L1_ffn_h1_w, L1_ffn_h1_s, L1_ffn_h2_w, L1_ffn_h2_s, L1_ffn_w3_w, L1_ffn_w3_s)
    x = x + _L1_attn_b_ref(_layernorm(x, axis=-1), L1_attn_b_w_qk, L1_attn_b_w_v, L1_attn_b_w_out, L1_attn_b_b_out, L1_attn_b_rotations)
    x = x + _L1_ffn_ref(_layernorm(x, axis=-1), L1_ffn_w1_w, L1_ffn_w1_s, L1_ffn_w2_w, L1_ffn_w2_s, L1_ffn_h1_w, L1_ffn_h1_s, L1_ffn_h2_w, L1_ffn_h2_s, L1_ffn_w3_w, L1_ffn_w3_s)
    x = x + _L2_attn_a_ref(_layernorm(x, axis=-1), L2_attn_a_mu0, L2_attn_a_W_x0, L2_attn_a_W_x2, L2_attn_a_x_bias, L2_attn_a_W_r, L2_attn_a_W_w1, L2_attn_a_W_w2, L2_attn_a_b_w2, L2_attn_a_W_k, L2_attn_a_W_v, L2_attn_a_W_g, L2_attn_a_bonus, L2_attn_a_gn_weight, L2_attn_a_gn_bias, L2_attn_a_W_o)
    x = x + _L2_ffn_ref(_layernorm(x, axis=-1), L2_ffn_router_w, L2_ffn_wg_r, L2_ffn_wu_r, L2_ffn_wd_r, L2_ffn_wg_s, L2_ffn_wu_s, L2_ffn_wd_s)
    x = x + _L2_attn_b_ref(_layernorm(x, axis=-1), L2_attn_b_WQ, L2_attn_b_WK, L2_attn_b_WV)
    x = x + _L2_ffn_ref(_layernorm(x, axis=-1), L2_ffn_router_w, L2_ffn_wg_r, L2_ffn_wu_r, L2_ffn_wd_r, L2_ffn_wg_s, L2_ffn_wu_s, L2_ffn_wd_s)
    x = x + _L3_attn_a_ref(_layernorm(x, axis=-1), L3_attn_a_queries_weight)
    x = x + _L3_ffn_ref(_layernorm(x, axis=-1), L3_ffn_Wg, L3_ffn_W1, L3_ffn_b1, L3_ffn_W2, L3_ffn_b2)
    x = x + _L3_attn_b_ref(_layernorm(x, axis=-1), L3_attn_b_Wq, L3_attn_b_bq, L3_attn_b_Wk, L3_attn_b_bk, L3_attn_b_Wv, L3_attn_b_bv, L3_attn_b_Wo, L3_attn_b_bo)
    x = x + _L3_ffn_ref(_layernorm(x, axis=-1), L3_ffn_Wg, L3_ffn_W1, L3_ffn_b1, L3_ffn_W2, L3_ffn_b2)
    return x

_drawn_inputs = setup_inputs


def setup_inputs(seed=0):
    import zlib

    import numpy as np

    out = dict(_drawn_inputs(seed))
    spreads = {'L0_attn_a_gate_b1': (0.0, 0.1),
     'L0_attn_a_gate_b2': (0.0, 0.1),
     'L0_attn_a_gate_copy_bias': (4.0, 0.2),
     'L0_attn_a_gate_log_temp': (0.6931471824645996, 0.2),
     'L0_attn_a_o_norm_w': (1.0, 0.2),
     'L0_attn_b_D': (1.0, 0.2),
     'L0_ffn_ln_g': (1.0, 0.2),
     'L0_ffn_ln_b': (0.0, 0.1),
     'L0_ffn_abel_b': (0.0, 0.1),
     'L0_ffn_gate_b_moe': (0.0, 0.1),
     'L0_ffn_b1': (0.0, 0.1),
     'L0_ffn_b2': (0.0, 0.1),
     'L1_attn_b_b_out': (0.0, 0.1),
     'L3_ffn_b1': (0.0, 0.1),
     'L3_ffn_b2': (0.0, 0.1)}
    factors = {}
    for name, (base, spread) in spreads.items():
        noise = np.random.default_rng([zlib.crc32(name.encode()), seed]).standard_normal(out[name].shape)
        drawn = base * np.exp(spread * noise) if base else spread * noise
        out[name] = jnp.asarray(drawn.astype(out[name].dtype))
    for name, factor in factors.items():
        out[name] = (out[name] * factor).astype(out[name].dtype)
    return out
```

```python
from contextlib import ExitStack, contextmanager

import numpy as np
import concourse.bass as bass
from concourse import mybir

F32 = mybir.dt.float32
BF16 = mybir.dt.bfloat16
U32 = mybir.dt.uint32
ALU = mybir.AluOpType
ACT = mybir.ActivationFunctionType
AX = mybir.AxisListType

P = 128
D = 128
BATCH = 2
SEQ = 1024
NTOK = BATCH * SEQ
BLK = 512
NBLK = NTOK // BLK
NTILE = NTOK // P
EPS = 1e-5
STAGE_SEMS = 220


class Link:

    def __init__(self, eng, sem):
        self.eng, self.sem, self.n = eng, sem, 0

    def __call__(self, ins):
        self.n += 1
        ins.then_inc(self.sem, 1)
        self.eng.wait_ge(self.sem, self.n)


@contextmanager
def stage(nc, *names):
    with ExitStack() as st:
        sems = [st.enter_context(nc.semaphore(n, num=STAGE_SEMS + i)) for i, n in enumerate(names)]
        with nc.Block(no_gpsimd_drain=True) as block:
            yield (block, *sems)
        if sems:
            nc.all_engine_barrier(sems_to_clear=range(STAGE_SEMS, STAGE_SEMS + len(sems)))
        else:
            nc.all_engine_barrier()


def blk(i, n=BLK):
    return slice(i * n, (i + 1) * n)


class Core:

    def __init__(self, nc):
        self.nc, self.W, self.buffers = nc, {}, 0

    def sbuf(self, scope, name, shape, dt=F32):
        self.buffers += 1
        return scope.enter_context(self.nc.sbuf_tensor(f"{name}_{self.buffers}", shape, dt))


def turned_spread(nc, out, cols, ident):
    return nc.tensor.matmul(out, cols, ident, start=True, stop=True)


def layernorm(k, src, dst, gain=None, shift=None):
    nc, PS = k.nc, k.PS
    sq, rstd = k.lnA, k.rstd
    TB = BLK // P
    with stage(nc, "mean_ready", "centered", "squared", "var_ready", "std_ready", "rstd_ready", "spread_ready", "dve_own") as (block, mean_ready, centered, squared, var_ready, std_ready, rstd_ready, spread_ready, dve_own):
        @block.tensor
        def _(pe):
            for b in range(NBLK):
                nc.tensor.matmul(PS[:, b, :], k.mean_mat[:, :], src[:, blk(b)], start=True, stop=True).then_inc(mean_ready, 1)
            for b in range(NBLK):
                pe.wait_ge(squared, b + 1)
                for t in range(TB * b, TB * b + TB):
                    mm = nc.tensor.matmul(PS[:, 4, t:t + 1], sq[:, blk(t, P)], k.mean_mat[:, 0:1], start=True, stop=True)
            mm.then_inc(var_ready, 1)
            pe.wait_ge(rstd_ready, 1)
            pe.wait_ge(centered, 1)
            for b in range(NBLK):
                for t in range(TB * b, TB * b + TB):
                    mm = turned_spread(nc, PS[:, (5 + b) % 8, blk(t % TB, P)], rstd[:, t:t + 1].to_broadcast([P, P]), k.ident[:, :])
                mm.then_inc(spread_ready, 1)

        @block.scalar
        def _(act):
            for b in range(NBLK):
                act.wait_ge(centered, b + 1)
                nc.scalar.activation(sq[:, blk(b)], dst[:, blk(b)], ACT.Square).then_inc(squared, 1)
            act.wait_ge(var_ready, 1)
            nc.scalar.activation(rstd[:, :], PS[:, 4, 0:NTILE], ACT.Sqrt, bias=k.eps_col[:, 0:1]).then_inc(std_ready, 1)

        @block.vector
        def _(dve):
            own = Link(dve, dve_own)
            for b in range(NBLK):
                dve.wait_ge(mean_ready, b + 1)
                nc.vector.tensor_tensor(dst[:, blk(b)], src[:, blk(b)], PS[:, b, :], ALU.subtract).then_inc(centered, 1)
            dve.wait_ge(std_ready, 1)
            nc.vector.reciprocal(rstd[:, :], rstd[:, :]).then_inc(rstd_ready, 1)
            dve.wait_ge(centered, NBLK)
            for b in range(NBLK):
                dve.wait_ge(spread_ready, b + 1)
                own(nc.vector.tensor_tensor(dst[:, blk(b)], dst[:, blk(b)], PS[:, (5 + b) % 8, :], ALU.mult))
                if gain is not None:
                    own(nc.vector.tensor_scalar(dst[:, blk(b)], dst[:, blk(b)], gain, shift, ALU.mult, ALU.add))



def route_top2(k, E, router, bias_row, mode, gT):
    nc = k.nc
    CAP = 256
    with ExitStack() as st:
        def sb(n, shape, dt=F32):
            return k.sbuf(st, n, shape, dt)
        L = sb("rt_logits", [P, NTILE, E])
        EX = sb("rt_exp", [P, NTILE, E])
        V8 = sb("rt_v8", [P, NTILE, 8])
        I8 = sb("rt_i8", [P, NTILE, 8], U32)
        IF = sb("rt_if", [P, NTILE, 2])
        SC = sb("rt_sc", [P, 8, NTILE])
        OH = sb("rt_oh", [P, 4, NTILE, E])
        kinds = 4 if mode == "capacity" else 1
        T = sb("rt_T", [E, 3, NTOK]) if mode == "capacity" else None
        one = sb("rt_one", [P, 2])
        with stage(nc, "logits_ready", "shifted", "exp_done", "oh_done", "turned", "copied", "own_d") as (block, logits_ready, shifted, exp_done, oh_done, turned, copied, own_d):
            @block.tensor
            def _(pe):
                for t in range(NTILE):
                    mm = nc.tensor.matmul(k.PS[:, 0, t * E:(t + 1) * E], k.XN[:, blk(t, P)], router, start=True, stop=True)
                mm.then_inc(logits_ready, 1)
                pe.wait_ge(oh_done, 1)
                for q in range(kinds):
                    for b in range(NBLK):
                        if q:
                            pe.wait_ge(copied, (q - 1) * NBLK + b + 1)
                        for j in range(BLK // P):
                            mm = nc.tensor.transpose(k.PS[0:E, 1 + b, blk(j, P)], OH[:, q, 4 * b + j, :], k.ident[:, :])
                        mm.then_inc(turned, 1)

            @block.scalar
            def _(act):
                act.wait_ge(shifted, 1)
                if mode == "softmax2":
                    nc.scalar.activation(SC[:, 3, :], SC[:, 0, :], ACT.Sigmoid)
                    nc.scalar.activation(SC[:, 2, :], SC[:, 0, :], ACT.Sigmoid, scale=-1.0).then_inc(exp_done, 1)
                else:
                    nc.scalar.activation(SC[:, 1, :], SC[:, 0, :], ACT.Exp)
                    nc.scalar.activation(EX[:, :, :], EX[:, :, :], ACT.Exp).then_inc(exp_done, 1)

            @block.vector
            def _(dve):
                own = Link(dve, own_d)
                dve.wait_ge(logits_ready, 1)
                own(nc.vector.memset(one[:, :], 1.0))
                lp = k.PS[:, 0, 0:NTILE * E].rearrange("p (t e) -> p t e", e=E)
                if bias_row is not None:
                    own(nc.vector.tensor_tensor(L[:, :, :], lp, bias_row.unsqueeze(1).to_broadcast([P, NTILE, E]), ALU.add))
                else:
                    own(nc.vector.tensor_copy(L[:, :, :], lp))
                for t in range(NTILE):
                    m = nc.vector.max(V8[:, t, :], L[:, t, :])
                own(m)
                for t in range(NTILE):
                    m = nc.vector.max_index(I8[:, t, :], V8[:, t, :], L[:, t, :])
                own(m)
                if mode != "softmax2":
                    own(nc.vector.tensor_tensor(EX[:, :, :], L[:, :, :], V8[:, :, 0:1].to_broadcast([P, NTILE, E]), ALU.subtract))
                nc.vector.tensor_tensor(SC[:, 0, :], V8[:, :, 1], V8[:, :, 0], ALU.subtract).then_inc(shifted, 1)
                own(nc.vector.tensor_copy(IF[:, :, :], I8[:, :, 0:2]))
                io = k.iota_row[:, 0:E].unsqueeze(1).to_broadcast([P, NTILE, E])
                for q in range(2):
                    own(nc.vector.tensor_tensor(OH[:, q, :, :], io, IF[:, :, q:q + 1].to_broadcast([P, NTILE, E]), ALU.is_equal))
                dve.wait_ge(exp_done, 1)
                if mode != "softmax2":
                    own(nc.vector.tensor_reduce(SC[:, 4, :], EX[:, :, :], AX.X, ALU.add))
                    own(nc.vector.reciprocal(SC[:, 2, :], SC[:, 4, :]))
                    own(nc.vector.tensor_tensor(SC[:, 3, :], SC[:, 1, :], SC[:, 2, :], ALU.mult))
                    own(nc.vector.tensor_tensor(SC[:, 5, :], SC[:, 2, :], SC[:, 3, :], ALU.add))
                    own(nc.vector.tensor_scalar(SC[:, 5, :], SC[:, 5, :], 1e-9, None, ALU.add))
                    own(nc.vector.reciprocal(SC[:, 6, :], SC[:, 5, :]))
                    own(nc.vector.tensor_tensor(SC[:, 2, :], SC[:, 2, :], SC[:, 6, :], ALU.mult))
                    own(nc.vector.tensor_tensor(SC[:, 3, :], SC[:, 3, :], SC[:, 6, :], ALU.mult))
                for q in range(2):
                    own(nc.vector.tensor_tensor(OH[:, 2 + q, :, :], OH[:, q, :, :], SC[:, 2 + q, :].unsqueeze(2).to_broadcast([P, NTILE, E]), ALU.mult))
                if mode != "capacity":
                    own(nc.vector.tensor_tensor(OH[:, 0, :, :], OH[:, 2, :, :], OH[:, 3, :, :], ALU.add))
                nc.vector.memset(one[:, 0:1], 1.0).then_inc(oh_done, 1)
                for q in range(kinds):
                    for b in range(NBLK):
                        dve.wait_ge(turned, q * NBLK + b + 1)
                        dst = T[:, q, blk(b)] if q < kinds - 1 else gT[0:E, blk(b)]
                        nc.vector.tensor_copy(dst, k.PS[0:E, 1 + b, :]).then_inc(copied, 1)
                dve.wait_ge(copied, kinds * NBLK)
                if mode == "capacity":
                    seen = k.lnA[0:E, :]
                    cnt = SC[0:E, 7, 0:1]
                    ones = one[0:E, 0:1].to_broadcast([E, NTOK])
                    own(nc.vector.tensor_tensor_scan(seen, ones, T[:, 0, :], 0.0, ALU.mult, ALU.add))
                    own(nc.vector.tensor_scalar(cnt, seen[:, NTOK - 1:NTOK], float(CAP), None, ALU.min))
                    own(nc.vector.scalar_tensor_tensor(out=T[:, 2, :], in0=seen, scalar=float(CAP), in1=T[:, 2, :], op0=ALU.is_le, op1=ALU.mult))
                    own(nc.vector.tensor_tensor_scan(seen, ones, T[:, 1, :], cnt, ALU.mult, ALU.add))
                    own(nc.vector.scalar_tensor_tensor(out=gT[0:E, :], in0=seen, scalar=float(CAP), in1=gT[0:E, :], op0=ALU.is_le, op1=ALU.mult))
                    own(nc.vector.tensor_tensor(gT[0:E, :], gT[0:E, :], T[:, 2, :], ALU.add))


def experts(k, w1, b1, w2, b2, gT, func, acc, H, gb, tmp, tb):
    nc, PS = k.nc, k.PS
    E, C = 8, 4
    with stage(nc, "gate_spread", "gate_copied", "hid_ready", "hid_done", "out_ready", "out_used", "own_d") as (block, gate_spread, gate_copied, hid_ready, hid_done, out_ready, out_used, own_d):
        @block.tensor
        def _(pe):
            def hidden(e):
                if e >= 2:
                    pe.wait_ge(gate_copied, e - 1)
                nc.tensor.matmul(PS[:, 6 + e % 2, :], k.sel8[:, e, :], gT[0:E, bass.ds(tb, BLK)], start=True, stop=True).then_inc(gate_spread, 1)
                for c in range(C):
                    if e:
                        pe.wait_ge(hid_done, C * (e - 1) + c + 1)
                    nc.tensor.matmul(PS[:, c, :], w1[:, e, blk(c, P)], k.XN[:, bass.ds(tb, BLK)], start=True, stop=True).then_inc(hid_ready, 1)

            def out(e):
                if e >= 2:
                    pe.wait_ge(out_used, e - 1)
                for c in range(C):
                    pe.wait_ge(hid_done, C * e + c + 1)
                    mm = nc.tensor.matmul(PS[:, 4 + e % 2, :], w2[:, e, c, :], H[:, e % 2, c, :], start=(c == 0), stop=(c == C - 1))
                mm.then_inc(out_ready, 1)

            hidden(0)
            for e in range(1, E):
                hidden(e)
                out(e - 1)
            out(E - 1)

        @block.scalar
        def _(act):
            for e in range(E):
                act.wait_ge(gate_spread, e + 1)
                if e >= 2:
                    act.wait_ge(out_used, e - 1)
                nc.scalar.activation(gb[:, e % 2, :], PS[:, 6 + e % 2, :], ACT.Identity).then_inc(gate_copied, 1)
                if e >= 2:
                    act.wait_ge(out_ready, e - 1)
                for c in range(C):
                    act.wait_ge(hid_ready, C * e + c + 1)
                    nc.scalar.activation(H[:, e % 2, c, :], PS[:, c, :], func, bias=b1[:, e, c:c + 1]).then_inc(hid_done, 1)

        @block.vector
        def _(dve):
            own = Link(dve, own_d)
            for e in range(E):
                dve.wait_ge(out_ready, e + 1)
                dve.wait_ge(gate_copied, e + 1)
                dst = acc if e == 0 else tmp
                nc.vector.scalar_tensor_tensor(out=dst, in0=PS[:, 4 + e % 2, :], scalar=b2[:, e:e + 1], in1=gb[:, e % 2, :], op0=ALU.add, op1=ALU.mult).then_inc(out_used, 1)
                dve.wait_ge(out_used, e + 1)
                if e:
                    own(nc.vector.tensor_tensor(acc, acc, tmp, ALU.add))


def expert_buffers(k, st):
    def sb(n, shape):
        return k.sbuf(st, n, shape, F32)
    return sb("moe_H", [P, 2, 4, BLK]), sb("moe_gb", [P, 2, BLK]), sb("moe_tmp", [P, BLK]), sb("moe_acc", [P, BLK])


def l3_ffn(k):
    nc, W = k.nc, k.W
    layernorm(k, k.X, k.XN)
    route_top2(k, 8, W["L3_ffn_Wg"], None, "capacity", k.gT)
    with ExitStack() as st:
        H, gb, tmp, acc = expert_buffers(k, st)
        with nc.Fori(0, NTOK - BLK + 1, BLK) as tb:
            experts(k, W["L3_ffn_W1"], W["L3_ffn_b1"], W["L3_ffn_W2"], W["L3_ffn_b2"], k.gT, ACT.Gelu_apprx_tanh, acc[:, :], H, gb, tmp[:, :], tb)
            with stage(nc, "added") as (block, added):
                @block.vector
                def _(dve):
                    xb = k.X[:, bass.ds(tb, BLK)]
                    nc.vector.tensor_tensor(xb, xb, acc[:, :], ALU.add).then_inc(added, 1)
                    dve.wait_ge(added, 1)


def expm_product(k):
    nc, PS, g = k.nc, k.PS, k.W["L0_ffn_gens"]
    ORDER, SQ = 12, 4
    with ExitStack() as st:
        T = k.sbuf(st, "ex_T", [P, 2, 2, 3 * P], F32)
        with stage(nc, "prod", "next_done", "own_d") as (block, prod, next_done, own_d):
            @block.tensor
            def _(pe):
                for i in range(ORDER + SQ):
                    pe.wait_ge(next_done, 2 * i + 2)
                    for side in range(2):
                        for m in range(3):
                            cur = T[:, i % 2, side, blk(m, P)]
                            left = g[:, 1 - side, m, :] if i < ORDER else T[:, i % 2, 1 - side, blk(m, P)]
                            mm = nc.tensor.matmul(PS[:, 2 * (i % 2) + side, blk(m, P)], left, cur, start=True, stop=True)
                        mm.then_inc(prod, 1)
                pe.wait_ge(next_done, 2 * (ORDER + SQ) + 2)
                fin = T[:, (ORDER + SQ) % 2]
                nc.tensor.matmul(PS[:, 4, 0:P], fin[:, 0, blk(1, P)], fin[:, 1, blk(0, P)], start=True, stop=True).then_inc(prod, 1)
                pe.wait_ge(next_done, 2 * (ORDER + SQ) + 3)
                nc.tensor.matmul(PS[:, 5, 0:P], T[:, 1 - (ORDER + SQ) % 2, 0, 0:P], fin[:, 0, blk(2, P)], start=True, stop=True).then_inc(prod, 1)

            @block.vector
            def _(dve):
                eye3 = k.ident[:, :].unsqueeze(1).to_broadcast([P, 3, P])
                for side in range(2):
                    nc.vector.tensor_copy(T[:, 0, side, :].rearrange("p (m n) -> p m n", n=P), eye3).then_inc(next_done, 1)
                for i in range(ORDER + SQ):
                    for side in range(2):
                        dve.wait_ge(prod, 2 * i + side + 1)
                        src = PS[:, 2 * (i % 2) + side, 0:3 * P].rearrange("p (m n) -> p m n", n=P)
                        dst = T[:, (i + 1) % 2, side, :].rearrange("p (m n) -> p m n", n=P)
                        if i < ORDER:
                            nc.vector.scalar_tensor_tensor(out=dst, in0=src, scalar=1.0 / (2 ** SQ * (ORDER - i)), in1=eye3, op0=ALU.mult, op1=ALU.add).then_inc(next_done, 1)
                        else:
                            nc.vector.tensor_copy(dst, src).then_inc(next_done, 1)
                dve.wait_ge(prod, 2 * (ORDER + SQ) + 1)
                nc.vector.tensor_copy(T[:, 1 - (ORDER + SQ) % 2, 0, 0:P], PS[:, 4, 0:P]).then_inc(next_done, 1)
                dve.wait_ge(prod, 2 * (ORDER + SQ) + 2)
                nc.vector.tensor_copy(k.rot[:, :], PS[:, 5, 0:P]).then_inc(own_d, 1)
                for h in range(2):
                    nc.vector.tensor_copy(k.mixm[:, h, :], k.W["L0_ffn_mix_w"][:, h:h + 1].to_broadcast([P, P])).then_inc(own_d, 1)
                dve.wait_ge(own_d, 3)


def l0_ffn(k):
    nc, PS, W = k.nc, k.PS, k.W
    with ExitStack() as st:
        XL = k.sbuf(st, "l0f_xl", [P, NTOK], F32)
        layernorm(k, k.X, XL)
        layernorm(k, XL, k.XN, W["L0_ffn_ln_g"], W["L0_ffn_ln_b"])
        route_top2(k, 8, W["L0_ffn_gate_w_moe"], W["L0_ffn_gate_b_moe"], "softmax2", k.gT)
        H, gb, tmp, acc = expert_buffers(k, st)
        AB = k.sbuf(st, "l0f_ab", [P, 3, BLK], F32)
        with nc.Fori(0, NTOK - BLK + 1, BLK) as tb:
            experts(k, W["L0_ffn_w1"], W["L0_ffn_b1"], W["L0_ffn_w2"], W["L0_ffn_b2"], k.gT, ACT.Gelu, acc[:, :], H, gb, tmp[:, :], tb)
            with stage(nc, "mixed_ready", "ab", "na", "sig", "own_d") as (block, mixed_ready, ab, na, sig, own_d):
                abel, nonab, g = AB[:, 0, :], AB[:, 1, :], AB[:, 2, :]

                @block.tensor
                def _(pe):
                    nc.tensor.matmul(PS[:, 0, :], W["L0_ffn_abel_w"], k.XN[:, bass.ds(tb, BLK)], start=True, stop=True).then_inc(mixed_ready, 1)
                    nc.tensor.matmul(PS[:, 1, :], k.rot[:, :], acc[:, :], start=True, stop=True).then_inc(mixed_ready, 1)
                    pe.wait_ge(ab, 1)
                    pe.wait_ge(na, 1)
                    nc.tensor.matmul(PS[:, 2, :], k.mixm[:, 0, :], abel, start=True, stop=False)
                    nc.tensor.matmul(PS[:, 2, :], k.mixm[:, 1, :], nonab, start=False, stop=True).then_inc(mixed_ready, 1)

                @block.scalar
                def _(act):
                    act.wait_ge(mixed_ready, 1)
                    nc.scalar.activation(abel, PS[:, 0, :], ACT.Gelu, bias=W["L0_ffn_abel_b"]).then_inc(ab, 1)
                    act.wait_ge(mixed_ready, 3)
                    nc.scalar.activation(g, PS[:, 2, :], ACT.Sigmoid, bias=W["L0_ffn_mix_b"]).then_inc(sig, 1)

                @block.vector
                def _(dve):
                    own = Link(dve, own_d)
                    dve.wait_ge(mixed_ready, 2)
                    nc.vector.tensor_copy(nonab, PS[:, 1, :]).then_inc(na, 1)
                    xb = k.X[:, bass.ds(tb, BLK)]
                    own(nc.vector.tensor_tensor(xb, xb, XL[:, bass.ds(tb, BLK)], ALU.add))
                    dve.wait_ge(ab, 1)
                    dve.wait_ge(na, 1)
                    dve.wait_ge(sig, 1)
                    own(nc.vector.tensor_tensor(nonab, nonab, abel, ALU.subtract))
                    own(nc.vector.tensor_tensor(nonab, nonab, g, ALU.mult))
                    own(nc.vector.tensor_tensor(nonab, nonab, abel, ALU.add))
                    own(nc.vector.tensor_tensor(xb, xb, nonab, ALU.add))


def l1_ffn(k):
    nc, PS, W = k.nc, k.PS, k.W
    C = 4
    layernorm(k, k.X, k.XN)
    with ExitStack() as st:
        G = k.sbuf(st, "l1f_G", [P, C, BLK], F32)
        HA = k.sbuf(st, "l1f_HA", [P, C, BLK], F32)
        HB = k.sbuf(st, "l1f_HB", [P, C, BLK], F32)
        with nc.Fori(0, NTOK - BLK + 1, BLK) as tb:
            with stage(nc, "g_ready", "g_done", "a_done", "h1_ready", "h1_done", "h2_ready", "h2_done", "y_ready", "added") as (block, g_ready, g_done, a_done, h1_ready, h1_done, h2_ready, h2_done, y_ready, added):
                @block.tensor
                def _(pe):
                    xn = k.XN[:, bass.ds(tb, BLK)]
                    for c in range(C):
                        nc.tensor.matmul(PS[:, c, :], W["L1_ffn_w1"][:, blk(c, P)], xn, start=True, stop=True)
                        nc.tensor.matmul(PS[:, 4 + c, :], W["L1_ffn_w2"][:, blk(c, P)], xn, start=True, stop=True).then_inc(g_ready, 1)
                    for c in range(C):
                        pe.wait_ge(g_done, c + 1)
                        for q in range(C):
                            pe.wait_ge(a_done, q + 1)
                            mm = nc.tensor.matmul(PS[:, c, :], W["L1_ffn_h1"][:, q, blk(c, P)], HA[:, q, :], start=(q == 0), stop=(q == C - 1))
                        mm.then_inc(h1_ready, 1)
                    for c in range(C):
                        for q in range(C):
                            pe.wait_ge(h1_done, q + 1)
                            mm = nc.tensor.matmul(PS[:, 4 + c, :], W["L1_ffn_h2"][:, q, blk(c, P)], HB[:, q, :], start=(q == 0), stop=(q == C - 1))
                        mm.then_inc(h2_ready, 1)
                    for q in range(C):
                        pe.wait_ge(h2_done, q + 1)
                        mm = nc.tensor.matmul(PS[:, 0, :], W["L1_ffn_w3"][:, q, :], G[:, q, :], start=(q == 0), stop=(q == C - 1))
                    mm.then_inc(y_ready, 1)

                @block.scalar
                def _(act):
                    for c in range(C):
                        act.wait_ge(g_ready, c + 1)
                        nc.scalar.activation(G[:, c, :], PS[:, c, :], ACT.Silu, scale=W["L1_ffn_w1_s"][:, c:c + 1]).then_inc(g_done, 1)
                    for c in range(C):
                        act.wait_ge(h1_ready, c + 1)
                        nc.scalar.activation(HB[:, c, :], PS[:, c, :], ACT.Gelu, scale=W["L1_ffn_h1_s"][:, c:c + 1]).then_inc(h1_done, 1)
                    for c in range(C):
                        act.wait_ge(h2_ready, c + 1)
                        act.wait_ge(a_done, c + 1)
                        nc.scalar.activation(G[:, c, :], PS[:, 4 + c, :], ACT.Gelu, scale=W["L1_ffn_h2_s"][:, c:c + 1]).then_inc(h2_done, 1)

                @block.vector
                def _(dve):
                    for c in range(C):
                        dve.wait_ge(g_done, c + 1)
                        nc.vector.scalar_tensor_tensor(out=HA[:, c, :], in0=PS[:, 4 + c, :], scalar=W["L1_ffn_w2_s"][:, c:c + 1], in1=G[:, c, :], op0=ALU.mult, op1=ALU.mult).then_inc(a_done, 1)
                    dve.wait_ge(y_ready, 1)
                    xb = k.X[:, bass.ds(tb, BLK)]
                    nc.vector.scalar_tensor_tensor(out=xb, in0=PS[:, 0, :], scalar=W["L1_ffn_w3_s"], in1=xb, op0=ALU.mult, op1=ALU.add).then_inc(added, 1)
                    dve.wait_ge(added, 1)


def l2_ffn(k):
    nc, PS, W = k.nc, k.PS, k.W
    C = 4
    layernorm(k, k.X, k.XN)
    route_top2(k, 16, W["L2_ffn_router_w"], None, "renorm", k.gT)
    with ExitStack() as st:
        G = k.sbuf(st, "l2f_G", [P, C + 1, BLK], F32)
        H = k.sbuf(st, "l2f_H", [P, C + 1, BLK], F32)
        with nc.Fori(0, NTOK - BLK + 1, BLK) as tb:
            with stage(nc, "up_ready", "g_done", "u_used", "h_half", "h_done", "y_ready", "added") as (block, up_ready, g_done, u_used, h_half, h_done, y_ready, added):
                @block.tensor
                def _(pe):
                    xn = k.XN[:, bass.ds(tb, BLK)]
                    for c in range(C + 1):
                        wg = W["L2_ffn_wg_r"][:, blk(c, P)] if c < C else W["L2_ffn_wg_s"]
                        wu = W["L2_ffn_wu_r"][:, blk(c, P)] if c < C else W["L2_ffn_wu_s"]
                        if c >= 2:
                            pe.wait_ge(h_done, c - 1)
                        nc.tensor.matmul(PS[:, 3 * (c % 2), :], wg, xn, start=True, stop=True)
                        mm = nc.tensor.matmul(PS[:, 3 * (c % 2) + 1, :], wu, xn, start=True, stop=True)
                        if c < C:
                            mm = nc.tensor.matmul(PS[:, 3 * (c % 2) + 2, :], k.sel16[:, c, :], k.gT[0:16, bass.ds(tb, BLK)], start=True, stop=True)
                        mm.then_inc(up_ready, 1)
                    for c in range(C + 1):
                        pe.wait_ge(h_done, c + 1)
                        wd = W["L2_ffn_wd_r"][:, c, :] if c < C else W["L2_ffn_wd_s"]
                        mm = nc.tensor.matmul(PS[:, 6, :], wd, H[:, c, :], start=(c == 0), stop=(c == C))
                    mm.then_inc(y_ready, 1)

                @block.scalar
                def _(act):
                    for c in range(C + 1):
                        act.wait_ge(up_ready, c + 1)
                        nc.scalar.activation(G[:, c, :], PS[:, 3 * (c % 2), :], ACT.Silu).then_inc(g_done, 1)

                @block.vector
                def _(dve):
                    for c in range(C + 1):
                        dve.wait_ge(g_done, c + 1)
                        if c < C:
                            nc.vector.tensor_tensor(G[:, c, :], PS[:, 3 * (c % 2) + 1, :], G[:, c, :], ALU.mult).then_inc(h_half, 1)
                            dve.wait_ge(h_half, c + 1)
                            nc.vector.tensor_tensor(H[:, c, :], PS[:, 3 * (c % 2) + 2, :], G[:, c, :], ALU.mult).then_inc(h_done, 1)
                        else:
                            nc.vector.tensor_tensor(H[:, c, :], PS[:, 3 * (c % 2) + 1, :], G[:, c, :], ALU.mult).then_inc(h_done, 1)
                    dve.wait_ge(y_ready, 1)
                    xb = k.X[:, bass.ds(tb, BLK)]
                    nc.vector.tensor_tensor(xb, PS[:, 6, :], xb, ALU.add).then_inc(added, 1)
                    dve.wait_ge(added, 1)


NEG = -1e30
HG = 4
NT = SEQ // P


def zero_bank(nc, k, bank):
    return nc.tensor.matmul(k.PS[:, bank, :], k.zeros16[:, 0:P], k.zeros16[:, :], start=True, stop=False, skip_group_check=True)


MAXROW = 96
PAIRS = {8: [(a, c) for a in range(3) for c in range(3)],
         16: [(0, 0), (0, 1), (1, 0), (1, 1), (0, 2), (2, 0)]}


def expansion_constants(k, pool, own, SEL, dims, KX, QX):
    own(pool.memset(SEL[:, :, :, :, :], 0.0))
    for side in range(2):
        for g in range(HG):
            for n, pair in enumerate(PAIRS[dims]):
                v = SEL[:, side, g, pair[1 - side], n * dims:(n + 1) * dims]
                ins = pool.affine_select(out=v, in_=v, compare_op=ALU.not_equal, fill=1.0, base=-32 * g - 1, pattern=[[-1, dims]], channel_multiplier=1)
    own(ins)
    own(pool.memset(QX[MAXROW:P, :, :], 0.0))
    own(pool.memset(KX[MAXROW:P, :, :], 1.0))


def expand_heads(k, KS, QS, KX, QX, SEL, parts, rest):
    nc, PS = k.nc, k.PS
    SRC = [(0, 0), (0, 1), (1, 0), (1, 1)]
    with stage(nc, "high_done", "rest_done", "mid_done", "low_done", "ready", "act_took", "dve_took") as (block, high_done, rest_done, mid_done, low_done, ready, act_took, dve_took):
        @block.scalar
        def _(act):
            for n, (side, h) in enumerate(SRC):
                nc.scalar.activation(parts[:, side, 0, blk(h)], (KS, QS)[side][:, blk(h)], ACT.Identity).then_inc(high_done, 1)
            for n in range(5):
                if n < 4:
                    side, h = SRC[n]
                    act.wait_ge(rest_done, n + 1)
                    nc.scalar.activation(parts[:, side, 1, blk(h)], rest[:, n, :], ACT.Identity).then_inc(mid_done, 1)
                if n:
                    side, h = SRC[n - 1]
                    for g in (0, 2):
                        u = HG * (n - 1) + g
                        act.wait_ge(ready, u + 1)
                        nc.scalar.activation((KX, QX)[side][0:MAXROW, g, blk(h)], PS[0:MAXROW, u % 8, :], ACT.Identity).then_inc(act_took, 1)

        @block.vector
        def _(dve):
            def took(dve, n):
                side, h = SRC[n]
                for g in (1, 3):
                    u = HG * n + g
                    dve.wait_ge(ready, u + 1)
                    nc.vector.tensor_copy((KX, QX)[side][0:MAXROW, g, blk(h)], PS[0:MAXROW, u % 8, :]).then_inc(dve_took, 1)

            for n in range(5):
                if n < 4:
                    side, h = SRC[n]
                    dve.wait_ge(high_done, n + 1)
                    nc.vector.tensor_tensor(rest[:, n, :], (KS, QS)[side][:, blk(h)], parts[:, side, 0, blk(h)], ALU.subtract).then_inc(rest_done, 1)
                if n:
                    side, h = SRC[n - 1]
                    dve.wait_ge(mid_done, n)
                    nc.vector.tensor_tensor(parts[:, side, 2, blk(h)], rest[:, n - 1, :], parts[:, side, 1, blk(h)], ALU.subtract).then_inc(low_done, 1)
                if n > 1:
                    took(dve, n - 2)
            took(dve, 3)

        @block.tensor
        def _(pe):
            for n, (side, h) in enumerate(SRC):
                pe.wait_ge(low_done, n + 1)
                for g in range(HG):
                    u = HG * n + g
                    if u >= 8:
                        pe.wait_ge(dve_took if g % 2 else act_took, (u - 8) // 2 + 1)
                    for part in range(3):
                        mm = nc.tensor.matmul(PS[:, u % 8, :], SEL[:, side, g, part, :], parts[:, side, part, blk(h)], start=(part == 0), stop=(part == 2))
                    mm.then_inc(ready, 1)


def expand_maxima(k, M, NM, MB, QX):
    nc, PS = k.nc, k.PS
    with stage(nc, "m_ready", "turned", "taken", "own_d") as (block, m_ready, turned, taken, own_d):
        @block.vector
        def _(dve):
            own = Link(dve, own_d)
            own(nc.vector.tensor_scalar(NM[:, 0, :, :], M[:, :, :], -1.0, None, ALU.mult))
            own(nc.vector.tensor_copy(MB[:, :, :, 0], NM[:, 0, :, :]))
            own(nc.vector.tensor_tensor(NM[:, 1, :, :], NM[:, 0, :, :], MB[:, :, :, 0], ALU.subtract))
            own(nc.vector.tensor_copy(MB[:, :, :, 1], NM[:, 1, :, :]))
            nc.vector.tensor_tensor(MB[:, :, :, 2], NM[:, 1, :, :], MB[:, :, :, 1], ALU.subtract).then_inc(m_ready, 1)
            for g in (0, 2):
                dve.wait_ge(turned, g + 1)
                nc.vector.tensor_copy(QX[MAXROW:MAXROW + 3, g, :], PS[MAXROW:MAXROW + 3, 2 * g:2 * g + 2, :].rearrange("p a n -> p (a n)")).then_inc(taken, 1)
            dve.wait_ge(taken, HG)

        @block.scalar
        def _(act):
            for g in (1, 3):
                act.wait_ge(turned, g + 1)
                nc.scalar.activation(QX[MAXROW:MAXROW + 3, g, :], PS[MAXROW:MAXROW + 3, 2 * g:2 * g + 2, :].rearrange("p a n -> p (a n)"), ACT.Identity).then_inc(taken, 1)

        @block.tensor
        def _(pe):
            pe.wait_ge(m_ready, 1)
            for g in range(HG):
                for i in range(NT):
                    mm = nc.tensor.matmul(PS[MAXROW:MAXROW + 3, 2 * g + i // 4, blk(i % 4, P)], MB[:, g, i, :], k.identb[:, :], start=True, stop=True)
                mm.then_inc(turned, 1)


def head_attention(k, pre, causal):
    nc, PS, W = k.nc, k.PS, k.W
    biased = not causal
    if causal:
        klo = lambda i: 0
        khi = lambda i: i + 1
        qlo = lambda j: j
        qhi = lambda j: NT
    else:
        klo = lambda i: max(i - 1, 0)
        khi = lambda i: min(i + 2, NT)
        qlo, qhi = klo, khi
    pieces = []
    for j in range(NT):
        c = qlo(j) * P
        while c < qhi(j) * P:
            e = min((c // BLK + 1) * BLK, qhi(j) * P)
            pieces.append((j, c, e))
            c = e
    SLOTS = 3
    cuts = [(j, i) for j in range(NT) for i in range(qlo(j), qhi(j)) if (i == j if causal else i != j)]
    with ExitStack() as st:
        def sb(n, shape, dt=F32):
            return k.sbuf(st, n, shape, dt)
        XB, QS, KS = sb("at_x", [P, SEQ]), sb("at_q", [P, SEQ]), sb("at_k", [P, SEQ])
        V1 = sb("at_v", [P, NT, HG, 9])
        PT = sb("at_pt", [P, SLOTS, HG, BLK])
        M, NM, MB = sb("at_m", [P, HG, NT]), sb("at_nm", [P, 2, HG, NT]), sb("at_mb", [P, HG, NT, 3], BF16)
        SEL = sb("at_sel", [P, 2, HG, 3, P], BF16)
        KX, QX = sb("at_kx", [P, HG, SEQ], BF16), sb("at_qx", [P, HG, SEQ], BF16)
        parts, rest = sb("at_parts", [P, 2, 3, SEQ], BF16), k.lnA[:, :].rearrange("p (a n) -> p a n", a=4)
        MT = sb("at_mt", [P, HG, NT])
        OT, RQ = QS, sb("at_rq", [P, NT, HG])
        WS = sb("at_w", [P, 3, P])
        SPAN = SEQ if causal else 3 * P
        CM = sb("at_cm", [P, SPAN])
        TM = sb("at_tm", [P, 2, P])
        if causal:
            JR = sb("at_jr", [P, SEQ])
            AL = PT[:, 0:2, :, :].rearrange("p a g n -> p (a g n)").rearrange("p (g n) -> p g n", g=HG)
            SL, I128, JP, SJ = sb("at_sl", [P, 16]), sb("at_i128", [P, NT]), sb("at_jp", [P, NT]), sb("at_sj", [P, HG, NT])
        WqP, WkP, WoP, Wv = W[pre + "WqP"], W[pre + "WkP"], W[pre + "WoP"], W[pre + "Wv"]
        layernorm(k, k.X, k.XN)
        with stage(nc, "own_p") as (block, own_p):
            @block.gpsimd
            def _(pool):
                own = Link(pool, own_p)
                own(pool.memset(CM[:, :], 0.0))
                expansion_constants(k, pool, own, SEL, 8, KX, QX)
                own(pool.memset(TM[:, :, :], 0.0))
                for n in range(2):
                    sign = 1 - 2 * n
                    own(pool.affine_select(out=TM[:, n, :], in_=TM[:, n, :], compare_op=ALU.is_ge, fill=NEG, base=0, pattern=[[sign, P]], channel_multiplier=-sign))
                own(pool.memset(V1[:, :, :, :], 1.0))
                if causal:
                    own(pool.affine_select(out=CM[:, :], in_=CM[:, :], compare_op=ALU.is_ge, fill=NEG, base=SEQ - P, pattern=[[-1, SEQ]], channel_multiplier=1))
                    own(pool.iota(JR[:, :], [[1, SEQ]], base=P - SEQ, channel_multiplier=0, allow_small_or_imprecise_dtypes=True))
                    own(pool.iota(I128[:, :], [[P, NT]], base=0, channel_multiplier=0, allow_small_or_imprecise_dtypes=True))
                    own(pool.iota(JP[:, :], [[P, NT]], base=0, channel_multiplier=1, allow_small_or_imprecise_dtypes=True))
                    for h in range(16):
                        own(pool.memset(SL[:, h:h + 1], float(np.float32(2.0 ** (-0.5)) ** (h + 1))))
                else:
                    own(pool.affine_select(out=CM[:, :], in_=CM[:, :], compare_op=ALU.is_ge, fill=NEG, base=0, pattern=[[1, SPAN]], channel_multiplier=-1))
                    own(pool.affine_select(out=CM[:, :], in_=CM[:, :], compare_op=ALU.is_ge, fill=NEG, base=2 * P, pattern=[[-1, SPAN]], channel_multiplier=1))

        def body(b, r):
            tok = b * SEQ
            with stage(nc, "x_copied", "w_copied", "qk_ready", "v_ready", "own_d") as (block, x_copied, w_copied, qk_ready, v_ready, own_d):
                @block.scalar
                def _(act):
                    nc.scalar.activation(XB[:, :], k.XN[:, bass.ds(tok, SEQ)], ACT.Identity).then_inc(x_copied, 1)

                @block.vector
                def _(dve):
                    own = Link(dve, own_d)
                    for n, w in enumerate((WqP, WkP, WoP)):
                        nc.vector.tensor_copy(WS[:, n, :], w[:, bass.ds(r, 1), :].rearrange("p a n -> p (a n)")).then_inc(w_copied, 1)
                    if causal:
                        for g in range(HG):
                            slope = SL[:, bass.ds(r * HG + g, 1)]
                            nc.vector.scalar_tensor_tensor(out=AL[:, g, :], in0=JR[:, :], scalar=slope, in1=CM[:, :], op0=ALU.mult, op1=ALU.add)
                            own(nc.vector.tensor_scalar(SJ[:, g, :], JP[:, :], slope, None, ALU.mult))
                    for n in range(4):
                        dve.wait_ge(qk_ready, n + 1)
                        if n < 2:
                            if biased:
                                own(nc.vector.tensor_scalar(QS[:, blk(n)], PS[:, n, :], W[pre + "bqP"][:, bass.ds(r, 1)], 8.0 ** -0.5, ALU.add, ALU.mult))
                            else:
                                own(nc.vector.tensor_scalar(QS[:, blk(n)], PS[:, n, :], 8.0 ** -0.5, None, ALU.mult))
                        else:
                            bias = W[pre + "bkP"][:, bass.ds(r, 1)] if biased else 0.0
                            own(nc.vector.tensor_scalar(KS[:, blk(n - 2)], PS[:, n, :], bias, None, ALU.add))
                    dve.wait_ge(v_ready, 1)
                    src = PS[:, 4, 0:NT * 32].rearrange("p (t g d) -> p t g d", t=NT, g=HG)
                    for t in range(NT):
                        if biased:
                            bv = W[pre + "bv"][:, bass.ds(r * 32, 32)].rearrange("p (g d) -> p g d", g=HG)
                            ins = nc.vector.tensor_tensor(V1[:, t, :, 1:9], src[:, t], bv, ALU.add)
                        else:
                            ins = nc.vector.tensor_copy(V1[:, t, :, 1:9], src[:, t])
                    own(ins)

                @block.tensor
                def _(pe):
                    pe.wait_ge(x_copied, 1)
                    for n in range(4):
                        pe.wait_ge(w_copied, n // 2 + 1)
                        nc.tensor.matmul(PS[:, n, :], WS[:, n // 2, :], XB[:, blk(n % 2)], start=True, stop=True).then_inc(qk_ready, 1)
                    for t in range(NT):
                        mm = nc.tensor.matmul(PS[:, 4, blk(t, 32)], XB[:, blk(t, P)], Wv[:, bass.ds(r * 32, 32)], start=True, stop=True)
                    mm.then_inc(v_ready, 1)

            expand_heads(k, KS, QS, KX, QX, SEL, parts, rest)

            with stage(nc, "s_ready", "s_maxed", "own_d") as (block, s_ready, s_maxed, own_d):
                @block.tensor
                def _(pe):
                    for i in range(NT):
                        for g in range(HG):
                            n = HG * i + g
                            if n >= 4:
                                pe.wait_ge(s_maxed, n - 3)
                            c, e0 = klo(i) * P, khi(i) * P
                            o = c
                            while c < e0:
                                e = min(e0, o + ((c - o) // BLK + 1) * BLK)
                                q0 = 2 * (n % 4) * BLK + c - o
                                mm = nc.tensor.matmul(PS[:, :, :].rearrange("p a n -> p (a n)")[:, q0:q0 + e - c],
                                                      QX[0:MAXROW, g, blk(i, P)], KX[0:MAXROW, g, c:e], start=True, stop=True)
                                c = e
                            mm.then_inc(s_ready, 1)

                @block.vector
                def _(dve):
                    own = Link(dve, own_d)
                    for i in range(NT):
                        for g in range(HG):
                            n = HG * i + g
                            dve.wait_ge(s_ready, n + 1)
                            w = (khi(i) - klo(i)) * P
                            c0 = SEQ - w if causal else (klo(i) - i + 1) * P
                            mask = AL[:, g, c0:c0 + w] if causal else CM[:, c0:c0 + w]
                            q0 = 2 * (n % 4) * BLK
                            sc = PS[:, :, :].rearrange("p a n -> p (a n)")[:, q0:q0 + w]
                            nc.vector.tensor_tensor_reduce(sc, sc, mask, 1.0, -3e38, ALU.add, ALU.max, M[:, g, i:i + 1]).then_inc(s_maxed, 1)
                    dve.wait_ge(s_maxed, NT * HG)
                    if causal:
                        for g in range(HG):
                            own(nc.vector.scalar_tensor_tensor(out=MT[:, g, :], in0=I128[:, :], scalar=SL[:, bass.ds(r * HG + g, 1)], in1=M[:, g, :], op0=ALU.mult, op1=ALU.add))
            expand_maxima(k, MT if causal else M, NM, MB, QX)

            with stage(nc, "st_ready", "exp_done", "cut_done", "pv_done", "all_done") as (block, st_ready, exp_done, cut_done, pv_done, all_done):
                @block.tensor
                def _(pe):
                    zero_bank(nc, k, 6)
                    zero_bank(nc, k, 7)

                    def pv(x):
                        j, c, e = pieces[x]
                        pe.wait_ge(exp_done, HG * (x + 1))
                        for g in range(HG):
                            nc.tensor.matmul(PS[32 * g:32 * g + 9, 6 + c // BLK, c % BLK:(e - 1) % BLK + 1], V1[:, j, g, :], PT[:, x % SLOTS, g, 0:e - c],
                                             start=False, stop=(x == len(pieces) - 1), skip_group_check=True).then_inc(pv_done, 1)

                    for x, (j, c, e) in enumerate(pieces):
                        for g in range(HG):
                            n = HG * x + g
                            if n >= 6:
                                pe.wait_ge(exp_done, n - 5)
                            nc.tensor.matmul(PS[:, n % 6, 0:e - c], KX[0:MAXROW + 3, g, blk(j, P)], QX[0:MAXROW + 3, g, c:e], start=True, stop=True).then_inc(st_ready, 1)
                        if x:
                            pv(x - 1)
                    pv(len(pieces) - 1)

                def cut_tiles(x):
                    j, c, e = pieces[x]
                    return [i for jj, i in cuts if jj == j and c <= i * P < e]

                @block.scalar
                def _(act):
                    cut = 0
                    for x, (j, c, e) in enumerate(pieces):
                        if x >= SLOTS:
                            act.wait_ge(pv_done, HG * (x - SLOTS + 1))
                        for g in range(HG):
                            n = HG * x + g
                            act.wait_ge(st_ready, n + 1)
                            if cut_tiles(x):
                                cut += len(cut_tiles(x))
                                act.wait_ge(cut_done, cut)
                            bias = SJ[:, g, j:j + 1] if causal else 0.0
                            nc.scalar.activation(PT[:, x % SLOTS, g, 0:e - c], PS[:, n % 6, 0:e - c], ACT.Exp, bias=bias).then_inc(exp_done, 1)

                @block.vector
                def _(dve):
                    for x, (j, c, e) in enumerate(pieces):
                        for g in range(HG):
                            if cut_tiles(x):
                                dve.wait_ge(st_ready, HG * x + g + 1)
                            for i in cut_tiles(x):
                                o = i * P - c
                                tile = PS[:, (HG * x + g) % 6, o:o + P]
                                nc.vector.tensor_tensor(tile, tile, TM[:, 0 if i <= j else 1, :], ALU.add).then_inc(cut_done, 1)
                    dve.wait_ge(pv_done, HG * len(pieces))
                    nc.vector.tensor_copy(OT[:, 0:BLK], PS[:, 6, :]).then_inc(all_done, 1)
                    nc.vector.tensor_copy(OT[:, BLK:], PS[:, 7, :]).then_inc(all_done, 1)
                    dve.wait_ge(all_done, 2)

            with stage(nc, "den_ready", "rec_ready", "den_spread", "o_done", "y_ready", "own_d") as (block, den_ready, rec_ready, den_spread, o_done, y_ready, own_d):
                @block.tensor
                def _(pe):
                    for i in range(NT):
                        mm = nc.tensor.matmul(PS[:, 4, blk(i, HG)], OT[:, blk(i, P)], k.head_row[:, :], start=True, stop=True)
                    mm.then_inc(den_ready, 1)
                    pe.wait_ge(rec_ready, 1)
                    for i in range(NT):
                        for g in range(HG):
                            turned_spread(nc, PS[32 * g:32 * g + 32, i // 4, blk(i % 4, P)], RQ[:, i, g:g + 1].to_broadcast([P, 32]), k.ident[:, :]).then_inc(den_spread, 1)
                    for h in range(2):
                        pe.wait_ge(o_done, h + 1)
                        nc.tensor.matmul(PS[:, 2 + h, :], WS[:, 2, :], OT[:, blk(h)], start=True, stop=True).then_inc(y_ready, 1)

                @block.vector
                def _(dve):
                    own = Link(dve, own_d)
                    dve.wait_ge(den_ready, 1)
                    nc.vector.reciprocal(RQ[:, :, :], PS[:, 4, 0:NT * HG].rearrange("p (a b) -> p a b", b=HG)).then_inc(rec_ready, 1)
                    for h in range(2):
                        dve.wait_ge(den_spread, (h + 1) * HG * NT // 2)
                        nc.vector.tensor_tensor(OT[:, blk(h)], OT[:, blk(h)], PS[:, h, :], ALU.mult).then_inc(o_done, 1)
                    for h in range(2):
                        dve.wait_ge(y_ready, h + 1)
                        xb = k.X[:, bass.ds(tok + h * BLK, BLK)]
                        own(nc.vector.tensor_tensor(xb, xb, PS[:, 2 + h, :], ALU.add))

        with nc.Fori(0, BATCH) as b:
            with nc.Fori(0, 4) as r:
                body(b, r)
        if biased:
            with stage(nc, "bias_added") as (block, bias_added):
                @block.vector
                def _(dve):
                    nc.vector.tensor_scalar(k.X[:, :], k.X[:, :], W[pre + "bo"], None, ALU.add).then_inc(bias_added, 1)
                    dve.wait_ge(bias_added, 1)


def l1a(k):
    head_attention(k, "L1_attn_a_", True)


def l3b(k):
    head_attention(k, "L3_attn_b_", False)


def l2b(k):
    nc, PS, W = k.nc, k.PS, k.W
    layernorm(k, k.X, k.XN)
    with ExitStack() as st:
        def sb(n, shape, dt=F32):
            return k.sbuf(st, n, shape, dt)
        QT, KT, XB = sb("l2b_q", [P, SEQ]), sb("l2b_k", [P, SEQ]), sb("l2b_x", [P, SEQ])
        V = sb("l2b_v", [P, NT, P])
        CM = sb("l2b_cm", [P, SEQ])
        BIG = sb("l2b_big", [P, BLK])
        Z, E = sb("l2b_z", [P, SEQ]), sb("l2b_e", [P, SEQ])
        PT = sb("l2b_pt", [P, NT, P])
        small = sb("l2b_s", [P, 4])
        O, = sb("l2b_o", [P, P]),
        with stage(nc, "own_p") as (block, own_p):
            @block.gpsimd
            def _(pool):
                own = Link(pool, own_p)
                own(pool.memset(CM[:, :], 0.0))
                own(pool.affine_select(out=CM[:, :], in_=CM[:, :], compare_op=ALU.is_ge, fill=NEG, base=SEQ - P, pattern=[[-1, SEQ]], channel_multiplier=1))
                own(pool.memset(BIG[:, :], NEG))
        with nc.Fori(0, NTOK - SEQ + 1, SEQ) as tok:
            with stage(nc, "x_copied", "proj", "own_d", "own_a") as (block, x_copied, proj, own_d, own_a):
                @block.scalar
                def _(act):
                    nc.scalar.activation(XB[:, :], k.XN[:, bass.ds(tok, SEQ)], ACT.Identity).then_inc(x_copied, 1)
                    for n in range(2):
                        act.wait_ge(proj, 3 + n)
                        nc.scalar.activation(V[:, blk(n, 4), :], PS[:, 4 + n, :].rearrange("p (a b) -> p a b", b=P), ACT.Identity).then_inc(own_a, 1)

                @block.tensor
                def _(pe):
                    pe.wait_ge(x_copied, 1)
                    for n, w in enumerate(("L2_attn_b_WQ", "L2_attn_b_WK")):
                        for h in range(2):
                            mm = nc.tensor.matmul(PS[:, 2 * n + h, :], W[w], XB[:, blk(h)], start=True, stop=True)
                        mm.then_inc(proj, 1)
                    for n in range(2):
                        for t in range(4):
                            mm = nc.tensor.matmul(PS[:, 4 + n, blk(t, P)], XB[:, blk(4 * n + t, P)], W["L2_attn_b_WV"], start=True, stop=True)
                        mm.then_inc(proj, 1)

                @block.vector
                def _(dve):
                    own = Link(dve, own_d)
                    dve.wait_ge(proj, 1)
                    for h in range(2):
                        own(nc.vector.tensor_scalar(QT[:, blk(h)], PS[:, h, :], 128.0 ** -0.5, None, ALU.mult))
                    dve.wait_ge(proj, 2)
                    for h in range(2):
                        own(nc.vector.tensor_copy(KT[:, blk(h)], PS[:, 2 + h, :]))

            with stage(nc, "scores", "masked", "exp_done", "turned", "pt_done", "o_ready", "o_done", "o_turned", "used", "own_d") as (block, scores, masked, exp_done, turned, pt_done, o_ready, o_done, o_turned, used, own_d):
                @block.tensor
                def _(pe):
                    for i in range(NT):
                        w = (i + 1) * P
                        if i:
                            pe.wait_ge(masked, i)
                        for c in range(0, w, BLK):
                            mm = nc.tensor.matmul(PS[:, c // BLK, 0:min(BLK, w - c)], QT[:, blk(i, P)], KT[:, c:min(w, c + BLK)], start=True, stop=True)
                        mm.then_inc(scores, 1)
                        pe.wait_ge(exp_done, i + 1)
                        if i:
                            pe.wait_ge(pt_done, i)
                        for j in range(i + 1):
                            mm = nc.tensor.transpose(PS[:, 2 + j // 4, blk(j % 4, P)], E[:, blk(j, P)], k.ident[:, :])
                        mm.then_inc(turned, 1)
                        pe.wait_ge(pt_done, i + 1)
                        for j in range(i + 1):
                            mm = nc.tensor.matmul(PS[:, 4, 0:P], PT[:, j, :], V[:, j, :], start=(j == 0), stop=(j == i))
                        mm.then_inc(o_ready, 1)
                        pe.wait_ge(o_done, i + 1)
                        nc.tensor.transpose(PS[:, 5, 0:P], O[:, :], k.ident[:, :]).then_inc(o_turned, 1)

                @block.scalar
                def _(act):
                    for i in range(NT):
                        w = (i + 1) * P
                        act.wait_ge(masked, i + 1)
                        if i:
                            act.wait_ge(turned, i)
                        nc.scalar.activation(E[:, 0:w], Z[:, 0:w], ACT.Exp, bias=small[:, 1:2], accum_out=small[:, 2:3]).then_inc(exp_done, 1)

                @block.vector
                def _(dve):
                    own = Link(dve, own_d)
                    for i in range(NT):
                        w = (i + 1) * P
                        c0 = SEQ - w
                        dve.wait_ge(scores, i + 1)
                        for c in range(0, w, BLK):
                            n = min(BLK, w - c)
                            own(nc.vector.scalar_tensor_tensor(out=Z[:, c:c + n], in0=PS[:, c // BLK, 0:n], scalar=0.0, in1=BIG[:, 0:n], op0=ALU.is_equal, op1=ALU.mult))
                            own(nc.vector.tensor_tensor(Z[:, c:c + n], Z[:, c:c + n], PS[:, c // BLK, 0:n], ALU.add))
                        own(nc.vector.tensor_tensor(Z[:, 0:w], Z[:, 0:w], CM[:, c0:c0 + w], ALU.add))
                        own(nc.vector.tensor_reduce(small[:, 0:1], Z[:, 0:w], AX.X, ALU.max))
                        nc.vector.tensor_scalar(small[:, 1:2], small[:, 0:1], -1.0, None, ALU.mult).then_inc(masked, 1)
                        dve.wait_ge(turned, i + 1)
                        for h in range(i // 4 + 1):
                            m = min(4, i + 1 - 4 * h)
                            ins = nc.vector.tensor_copy(PT[:, 4 * h:4 * h + m, :], PS[:, 2 + h, 0:m * P].rearrange("p (a b) -> p a b", b=P))
                            if h == i // 4:
                                ins.then_inc(pt_done, 1)
                            else:
                                own(ins)
                        own(nc.vector.reciprocal(small[:, 3:4], small[:, 2:3]))
                        dve.wait_ge(o_ready, i + 1)
                        nc.vector.tensor_scalar(O[:, :], PS[:, 4, 0:P], small[:, 3:4], None, ALU.mult).then_inc(o_done, 1)
                        dve.wait_ge(o_turned, i + 1)
                        xb = k.X[:, bass.ds(tok + i * P, P)]
                        own(nc.vector.tensor_tensor(xb, xb, PS[:, 5, 0:P], ALU.add))


def l3a(k):
    nc, PS, W = k.nc, k.PS, k.W
    layernorm(k, k.X, k.XN)
    with ExitStack() as st:
        def sb(n, shape, dt=F32):
            return k.sbuf(st, n, shape, dt)
        XC, QC, XT = sb("l3a_x", [P, P]), sb("l3a_q", [P, P]), sb("l3a_xt", [P, 1 + P])
        QP, KP = sb("l3a_qp", [P, 4, P]), sb("l3a_kp", [P, 4, P])
        PT, OP = sb("l3a_pt", [P, 4, 4, P]), sb("l3a_op", [P, 4, P])
        S = sb("l3a_s", [P, P])
        TRI, HB, SEL, UNS = sb("l3a_tri", [P, P]), sb("l3a_hb", [P, P]), sb("l3a_sel", [P, 4, P]), sb("l3a_uns", [P, 4, P])
        with stage(nc, "own_p", "turned", "own_d") as (block, own_p, turned, own_d):
            @block.gpsimd
            def _(pool):
                own = Link(pool, own_p)
                own(pool.memset(XT[:, 0:1], 0.0))
                own(pool.memset(TRI[:, :], 1.0))
                own(pool.affine_select(out=TRI[:, :], in_=TRI[:, :], compare_op=ALU.is_ge, fill=0.0, base=0, pattern=[[1, P]], channel_multiplier=-1))
                own(pool.memset(HB[:, :], 1.0))
                hb = HB[:, :].rearrange("p (h d) -> p h d", d=8)
                own(pool.affine_select(out=hb, in_=hb, compare_op=ALU.is_ge, fill=0.0, base=0, pattern=[[-8, 16], [0, 8]], channel_multiplier=1))
                own(pool.affine_select(out=hb, in_=hb, compare_op=ALU.is_ge, fill=0.0, base=7, pattern=[[8, 16], [0, 8]], channel_multiplier=-1))
                own(pool.memset(SEL[:, :, :], 0.0))
                for r in range(4):
                    v = SEL[:, r, :].rearrange("p (g d) -> p g d", g=4)[:, :, 1:9]
                    own(pool.affine_select(out=v, in_=v, compare_op=ALU.not_equal, fill=1.0, base=-32 * r, pattern=[[-8, 4], [-1, 8]], channel_multiplier=1))

            @block.tensor
            def _(pe):
                pe.wait_ge(own_p, 11)
                for r in range(4):
                    mm = nc.tensor.transpose(PS[:, 0, blk(r, P)], SEL[:, r, :], k.ident[:, :])
                mm.then_inc(turned, 1)

            @block.vector
            def _(dve):
                dve.wait_ge(turned, 1)
                nc.vector.tensor_copy(UNS[:, :, :], PS[:, 0, :].rearrange("p (a b) -> p a b", b=P)).then_inc(own_d, 1)
                dve.wait_ge(own_d, 1)
        with nc.Fori(0, BATCH) as b:
            with stage(nc, "cleared") as (block, cleared):
                @block.vector
                def _(dve):
                    nc.vector.memset(S[:, :], 0.0).then_inc(cleared, 1)
                    dve.wait_ge(cleared, 1)
            with nc.Fori(0, NT) as c:
                tok = b * SEQ + c * P
                with stage(nc, "x_copied", "proj", "q_done", "p_done", "qp_done", "kp_done", "st_ready", "pt_done", "o_ready", "o_done", "y_ready", "own_d") as (block, x_copied, proj, q_done, p_done, qp_done, kp_done, st_ready, pt_done, o_ready, o_done, y_ready, own_d):
                    @block.tensor
                    def _(pe):
                        pe.wait_ge(x_copied, 1)
                        nc.tensor.matmul(PS[:, 0, 0:P], W["L3_attn_a_Wq"], XC[:, :], start=True, stop=True)
                        nc.tensor.transpose(PS[:, 0, P:2 * P], XC[:, :], k.ident[:, :]).then_inc(proj, 1)
                        for r in range(4):
                            mm = nc.tensor.matmul(PS[:, 1, blk(r, P)], SEL[:, r, :], XC[:, :], start=True, stop=True)
                        mm.then_inc(proj, 1)
                        pe.wait_ge(q_done, 1)
                        for r in range(4):
                            mm = nc.tensor.matmul(PS[:, 2, blk(r, P)], SEL[:, r, :], QC[:, :], start=True, stop=True)
                        mm.then_inc(proj, 1)
                        pe.wait_ge(qp_done, 1)
                        pe.wait_ge(kp_done, 1)
                        for g in range(4):
                            q = slice(32 * g, 32 * g + 9)
                            for r in range(4):
                                mm = nc.tensor.matmul(PS[:, 3 + g, blk(r, P)], KP[q, r, :], QP[q, r, :], start=True, stop=True)
                            mm.then_inc(st_ready, 1)
                        pe.wait_ge(p_done, 1)
                        zero_bank(nc, k, 7)
                        for r in range(4):
                            for g in range(4):
                                pe.wait_ge(pt_done, g + 1)
                                h = 4 * r + g
                                mm = nc.tensor.matmul(PS[32 * g:32 * g + 9, 7, blk(r, P)], XT[:, 8 * h:8 * h + 9], PT[:, g, r, :], start=False, stop=True, skip_group_check=True)
                        mm.then_inc(o_ready, 1)
                        pe.wait_ge(o_done, 1)
                        for r in range(4):
                            nc.tensor.matmul(PS[:, 1, 0:P], UNS[:, r, :], OP[:, r, :], start=(r == 0), stop=False)
                        nc.tensor.matmul(PS[:, 1, 0:P], S[:, :], QC[:, :], start=False, stop=True)
                        nc.tensor.matmul(PS[:, 2, 0:P], XT[:, 1:], XT[:, 1:], start=True, stop=True).then_inc(y_ready, 1)

                    @block.scalar
                    def _(act):
                        nc.scalar.activation(XC[:, :], k.XN[:, bass.ds(tok, P)], ACT.Identity).then_inc(x_copied, 1)
                        act.wait_ge(proj, 2)
                        nc.scalar.activation(KP[:, :, :], PS[:, 1, :].rearrange("p (a b) -> p a b", b=P), ACT.Identity).then_inc(kp_done, 1)

                    @block.vector
                    def _(dve):
                        own = Link(dve, own_d)
                        dve.wait_ge(proj, 1)
                        nc.vector.tensor_copy(QC[:, :], PS[:, 0, 0:P]).then_inc(q_done, 1)
                        nc.vector.tensor_copy(XT[:, 1:], PS[:, 0, P:2 * P]).then_inc(p_done, 1)
                        dve.wait_ge(proj, 3)
                        nc.vector.tensor_copy(QP[:, :, :], PS[:, 2, :].rearrange("p (a b) -> p a b", b=P)).then_inc(qp_done, 1)
                        for g in range(4):
                            dve.wait_ge(st_ready, g + 1)
                            nc.vector.tensor_tensor(PT[:, g, :, :], PS[:, 3 + g, :].rearrange("p (a b) -> p a b", b=P), TRI[:, :].unsqueeze(1).to_broadcast([P, 4, P]), ALU.mult).then_inc(pt_done, 1)
                        dve.wait_ge(o_ready, 1)
                        nc.vector.tensor_copy(OP[:, :, :], PS[:, 7, :].rearrange("p (a b) -> p a b", b=P)).then_inc(o_done, 1)
                        dve.wait_ge(y_ready, 1)
                        xb = k.X[:, bass.ds(tok, P)]
                        own(nc.vector.tensor_tensor(xb, xb, PS[:, 1, 0:P], ALU.add))
                        own(nc.vector.tensor_tensor(OP[:, 0, :], PS[:, 2, 0:P], HB[:, :], ALU.mult))
                        own(nc.vector.tensor_tensor(S[:, :], S[:, :], OP[:, 0, :], ALU.add))



def l0b(k):
    nc, PS, W = k.nc, k.PS, k.W
    NS, R = 16, 8
    layernorm(k, k.X, k.XN)
    with ExitStack() as st:
        def sb(n, shape, dt=F32):
            return k.sbuf(st, n, shape, dt)
        U, UC, Z = sb("mb_u", [P, 2, 3 + SEQ]), sb("mb_uc", [P, 2, SEQ]), sb("mb_z", [P, 2, SEQ])
        DT, DU = sb("mb_dt", [P, 2, SEQ]), sb("mb_du", [P, 2, SEQ])
        XD = sb("mb_xd", [40, SEQ])
        A = sb("mb_a", [P, 2, NS])
        DA, BU, HC = sb("mb_da", [P, 2, SEQ]), sb("mb_bu", [P, 2, SEQ]), sb("mb_hc", [P, 2, SEQ])
        HS, BS = sb("mb_h", [P, SEQ]), sb("mb_bs", [P, 2, SEQ])
        SELR = sb("mb_sel", [40, 2 * NS, P])
        with stage(nc, "own_p", "own_a", "own_d") as (block, own_p, own_a, own_d):
            @block.gpsimd
            def _(pool):
                own = Link(pool, own_p)
                own(pool.memset(U[:, :, 0:3], 0.0))
                own(pool.memset(SELR[:, :, :], 0.0))
                own(pool.affine_select(out=SELR[:, :, :], in_=SELR[:, :, :], compare_op=ALU.not_equal, fill=1.0, base=-R, pattern=[[-1, 2 * NS], [0, P]], channel_multiplier=1))

            @block.scalar
            def _(act):
                nc.scalar.activation(A[:, :, :], W["L0_attn_b_A_log"], ACT.Exp).then_inc(own_a, 1)

            @block.vector
            def _(dve):
                dve.wait_ge(own_a, 1)
                nc.vector.tensor_scalar(A[:, :, :], A[:, :, :], -1.0, None, ALU.mult).then_inc(own_d, 1)
                dve.wait_ge(own_d, 1)
        with nc.Fori(0, NTOK - SEQ + 1, SEQ) as tok:
            with stage(nc, "u_ready", "z_ready", "u_done", "z_done", "conv_done", "uc_done", "own_d") as (block, u_ready, z_ready, u_done, z_done, conv_done, uc_done, own_d):
                @block.tensor
                def _(pe):
                    for h in range(2):
                        for t in range(2):
                            nc.tensor.matmul(PS[:, 2 * h + t, :], W["L0_attn_b_W_in"][:, blk(h, P)], k.XN[:, bass.ds(tok + t * BLK, BLK)], start=True, stop=True).then_inc(u_ready, 1)
                    for h in range(2):
                        for t in range(2):
                            nc.tensor.matmul(PS[:, 4 + 2 * h + t, :], W["L0_attn_b_W_in"][:, blk(2 + h, P)], k.XN[:, bass.ds(tok + t * BLK, BLK)], start=True, stop=True).then_inc(z_ready, 1)

                @block.scalar
                def _(act):
                    for n in range(4):
                        act.wait_ge(u_ready, n + 1)
                        nc.scalar.activation(U[:, n // 2, 3 + (n % 2) * BLK:3 + (n % 2 + 1) * BLK], PS[:, n, :], ACT.Identity).then_inc(u_done, 1)
                    for n in range(4):
                        act.wait_ge(z_ready, n + 1)
                        nc.scalar.activation(Z[:, n // 2, blk(n % 2)], PS[:, 4 + n, :], ACT.Silu).then_inc(z_done, 1)
                    for h in range(2):
                        act.wait_ge(conv_done, h + 1)
                        nc.scalar.activation(UC[:, h, :], UC[:, h, :], ACT.Silu, bias=W["L0_attn_b_conv_b"][:, h:h + 1]).then_inc(uc_done, 1)

                @block.vector
                def _(dve):
                    own = Link(dve, own_d)
                    for h in range(2):
                        dve.wait_ge(u_done, 2 * h + 2)
                        w = W["L0_attn_b_conv_w"]
                        own(nc.vector.tensor_scalar(UC[:, h, :], U[:, h, 0:SEQ], w[:, h, 0:1], None, ALU.mult))
                        for j in range(1, 4):
                            ins = nc.vector.scalar_tensor_tensor(out=UC[:, h, :], in0=U[:, h, j:j + SEQ], scalar=w[:, h, j:j + 1], in1=UC[:, h, :], op0=ALU.mult, op1=ALU.add)
                            if j < 3:
                                own(ins)
                        ins.then_inc(conv_done, 1)

            with stage(nc, "xd_ready", "xd_done", "dt_ready", "v_done", "abs_done", "e_done", "ln_done", "own_d") as (block, xd_ready, xd_done, dt_ready, v_done, abs_done, e_done, ln_done, own_d):
                @block.tensor
                def _(pe):
                    for t in range(2):
                        for h in range(2):
                            mm = nc.tensor.matmul(PS[0:40, t, :], W["L0_attn_b_W_x"][:, h, :], UC[:, h, blk(t)], start=(h == 0), stop=(h == 1))
                        mm.then_inc(xd_ready, 1)
                    for t in range(2):
                        pe.wait_ge(xd_done, t + 1)
                        for h in range(2):
                            nc.tensor.matmul(PS[:, 2 + 2 * h + t, :], W["L0_attn_b_W_dt"][0:R, blk(h, P)], XD[0:R, blk(t)], start=True, stop=True).then_inc(dt_ready, 1)

                @block.vector
                def _(dve):
                    own = Link(dve, own_d)
                    for t in range(2):
                        dve.wait_ge(xd_ready, t + 1)
                        nc.vector.tensor_copy(XD[:, blk(t)], PS[0:40, t, :]).then_inc(xd_done, 1)
                    dve.wait_ge(dt_ready, 4)
                    for h in range(2):
                        v = PS[:, 2 + 2 * h:4 + 2 * h, :].rearrange("p a b -> p (a b)")
                        own(nc.vector.tensor_scalar(DU[:, h, :], v, W["L0_attn_b_b_dt"][:, h:h + 1], None, ALU.add))
                        nc.vector.tensor_scalar(DT[:, h, :], DU[:, h, :], 0.0, None, ALU.max).then_inc(v_done, 1)
                    dve.wait_ge(ln_done, 2)
                    dve.wait_ge(v_done, 2)
                    own(nc.vector.tensor_tensor(DT[:, :, :], DT[:, :, :], DU[:, :, :], ALU.add))
                    own(nc.vector.tensor_tensor(DU[:, :, :], DT[:, :, :], UC[:, :, :], ALU.mult))

                @block.scalar
                def _(act):
                    for h in range(2):
                        act.wait_ge(v_done, h + 1)
                        nc.scalar.activation(DU[:, h, :], DU[:, h, :], ACT.Abs).then_inc(abs_done, 1)
                    for h in range(2):
                        act.wait_ge(abs_done, h + 1)
                        nc.scalar.activation(DU[:, h, :], DU[:, h, :], ACT.Exp, scale=-1.0).then_inc(e_done, 1)
                    for h in range(2):
                        act.wait_ge(e_done, h + 1)
                        nc.scalar.activation(DU[:, h, :], DU[:, h, :], ACT.Ln, bias=1.0).then_inc(ln_done, 1)

            with stage(nc, "b_ready", "c_ready", "b_copied", "a_done", "bu_done", "scanned", "hc_done", "y_added", "y_done") as (block, b_ready, c_ready, b_copied, a_done, bu_done, scanned, hc_done, y_added, y_done):
                @block.tensor
                def _(pe):
                    def spread(n):
                        if n:
                            pe.wait_ge(b_copied, n)
                        for t in range(2):
                            mm = nc.tensor.matmul(PS[:, 4 + t, :], SELR[:, n, :], XD[:, blk(t)], start=True, stop=True)
                        mm.then_inc(b_ready, 1)
                        if n:
                            pe.wait_ge(hc_done, 2 * n)
                        for t in range(2):
                            mm = nc.tensor.matmul(PS[:, 6 + t, :], SELR[:, NS + n, :], XD[:, blk(t)], start=True, stop=True)
                        mm.then_inc(c_ready, 1)

                    for n in range(NS):
                        spread(n)
                        for h in range(2):
                            pe.wait_ge(hc_done, 2 * n + h + 1)
                            for t in range(2):
                                mm = nc.tensor.matmul(PS[:, 2 * h + t, :], k.ident[:, :], HC[:, h, blk(t)], start=(n == 0), stop=(n == NS - 1))
                            mm.then_inc(y_added, 1)

                @block.scalar
                def _(act):
                    for n in range(NS):
                        act.wait_ge(b_ready, n + 1)
                        if n >= 2:
                            act.wait_ge(bu_done, 2 * (n - 1))
                        nc.scalar.activation(BS[:, n % 2, :], PS[:, 4:6, :].rearrange("p a b -> p (a b)"), ACT.Identity).then_inc(b_copied, 1)
                        for h in range(2):
                            if n:
                                act.wait_ge(scanned, 2 * (n - 1) + h + 1)
                            nc.scalar.activation(DA[:, h, :], DT[:, h, :], ACT.Exp, scale=A[:, h, n:n + 1]).then_inc(a_done, 1)

                @block.gpsimd
                def _(pool):
                    for n in range(NS):
                        for h in range(2):
                            pool.wait_ge(b_copied, n + 1)
                            if n:
                                pool.wait_ge(scanned, 2 * (n - 1) + h + 1)
                            pool.tensor_tensor(BU[:, h, :], DU[:, h, :], BS[:, n % 2, :], ALU.mult).then_inc(bu_done, 1)

                @block.vector
                def _(dve):
                    for n in range(NS):
                        for h in range(2):
                            m = 2 * n + h
                            dve.wait_ge(a_done, m + 1)
                            dve.wait_ge(bu_done, m + 1)
                            if m:
                                dve.wait_ge(hc_done, m)
                            nc.vector.tensor_tensor_scan(HS[:, :], DA[:, h, :], BU[:, h, :], 0.0, ALU.mult, ALU.add).then_inc(scanned, 1)
                            dve.wait_ge(scanned, m + 1)
                            dve.wait_ge(c_ready, n + 1)
                            if n:
                                dve.wait_ge(y_added, 2 * (n - 1) + h + 1)
                            nc.vector.tensor_tensor(HC[:, h, :], HS[:, :], PS[:, 6:8, :].rearrange("p a b -> p (a b)"), ALU.mult).then_inc(hc_done, 1)
                    dve.wait_ge(y_added, 2 * NS)
                    for h in range(2):
                        y = PS[:, 2 * h:2 * h + 2, :].rearrange("p a b -> p (a b)")
                        nc.vector.scalar_tensor_tensor(out=UC[:, h, :], in0=UC[:, h, :], scalar=W["L0_attn_b_D"][:, h:h + 1], in1=y, op0=ALU.mult, op1=ALU.add).then_inc(y_done, 1)
                    for h in range(2):
                        dve.wait_ge(y_done, h + 1)
                        nc.vector.tensor_tensor(UC[:, h, :], UC[:, h, :], Z[:, h, :], ALU.mult).then_inc(y_done, 1)
                    dve.wait_ge(y_done, 4)

            with stage(nc, "out_ready", "added") as (block, out_ready, added):
                @block.tensor
                def _(pe):
                    for t in range(2):
                        for h in range(2):
                            mm = nc.tensor.matmul(PS[:, t, :], W["L0_attn_b_W_out"][:, h, :], UC[:, h, blk(t)], start=(h == 0), stop=(h == 1))
                        mm.then_inc(out_ready, 1)

                @block.vector
                def _(dve):
                    for t in range(2):
                        dve.wait_ge(out_ready, t + 1)
                        xb = k.X[:, bass.ds(tok + t * BLK, BLK)]
                        nc.vector.tensor_tensor(xb, xb, PS[:, t, :], ALU.add).then_inc(added, 1)
                    dve.wait_ge(added, 2)



def head_constants(k, pool, own, HB32, scale):
    own(pool.memset(HB32, scale))
    v = HB32.rearrange("p (h d) -> p h d", d=32)
    own(pool.affine_select(out=v, in_=v, compare_op=ALU.is_ge, fill=0.0, base=0, pattern=[[-32, 4], [0, 32]], channel_multiplier=1))
    own(pool.affine_select(out=v, in_=v, compare_op=ALU.is_ge, fill=0.0, base=31, pattern=[[32, 4], [0, 32]], channel_multiplier=-1))


def l2a(k):
    nc, PS, W = k.nc, k.PS, k.W
    DK = 16
    pre = "L2_attn_a_"
    layernorm(k, k.X, k.XN)
    with ExitStack() as st:
        def sb(n, shape, dt=F32):
            return k.sbuf(st, n, shape, dt)
        XS = sb("rw_x", [P, 1 + SEQ])
        DX, XX, XP, XP5 = sb("rw_dx", [P, SEQ]), sb("rw_xx", [P, 5, SEQ]), sb("rw_xp", [P, SEQ]), sb("rw_xp5", [32, SEQ])
        RKD = sb("rw_rkd", [64, 3, SEQ])
        T64 = sb("rw_t64", [64, SEQ])
        V, G = sb("rw_v", [P, SEQ]), sb("rw_g", [P, SEQ])
        KV, SS, SR = sb("rw_kv", [P, 2, SEQ]), sb("rw_ss", [P, 1 + SEQ]), sb("rw_sr", [P, 2, SEQ])
        SEL = sb("rw_sel", [64, DK, P])
        HO, BM = sb("rw_ho", [64, P]), sb("rw_bm", [P, P])
        with stage(nc, "own_p") as (block, own_p):
            @block.gpsimd
            def _(pool):
                own = Link(pool, own_p)
                own(pool.memset(XS[:, 0:1], 0.0))
                own(pool.memset(SS[:, 0:1], 0.0))
                head_constants(k, pool, own, BM[:, :], 1.0 / 32)
                own(pool.memset(SEL[:, :, :], 0.0))
                v = SEL[:, :, :].rearrange("q d (h v) -> q d h v", v=32)
                own(pool.affine_select(out=v, in_=v, compare_op=ALU.not_equal, fill=1.0, base=0, pattern=[[-1, DK], [-DK, 4], [0, 32]], channel_multiplier=1))
                own(pool.memset(HO[:, :], 1.0))
                v = HO[:, :].rearrange("q (h v) -> q h v", v=32)
                own(pool.affine_select(out=v, in_=v, compare_op=ALU.is_ge, fill=0.0, base=0, pattern=[[-DK, 4], [0, 32]], channel_multiplier=1))
                own(pool.affine_select(out=v, in_=v, compare_op=ALU.is_ge, fill=0.0, base=DK - 1, pattern=[[DK, 4], [0, 32]], channel_multiplier=-1))
        wide = lambda a: PS[:, a:a + 2, :].rearrange("p a b -> p (a b)")
        wide64 = lambda a: PS[0:64, a:a + 2, :].rearrange("p a b -> p (a b)")
        with nc.Fori(0, NTOK - SEQ + 1, SEQ) as tok:
            with stage(nc, "x_done", "xx_done", "xp_ready", "xp_done", "mu_ready", "mu_used", "own_d") as (block, x_done, xx_done, xp_ready, xp_done, mu_ready, mu_used, own_d):
                @block.scalar
                def _(act):
                    nc.scalar.activation(XS[:, 1:], k.XN[:, bass.ds(tok, SEQ)], ACT.Identity).then_inc(x_done, 1)
                    act.wait_ge(xp_ready, 2)
                    nc.scalar.activation(XP[:, :], wide(0), ACT.Tanh).then_inc(xp_done, 1)
                    nc.scalar.activation(XP5[:, :], PS[0:32, 2:4, :].rearrange("p a b -> p (a b)"), ACT.Tanh).then_inc(xp_done, 1)

                @block.vector
                def _(dve):
                    own = Link(dve, own_d)
                    dve.wait_ge(x_done, 1)
                    own(nc.vector.tensor_tensor(DX[:, :], XS[:, 0:SEQ], XS[:, 1:], ALU.subtract))
                    nc.vector.scalar_tensor_tensor(out=XX[:, 0, :], in0=DX[:, :], scalar=W[pre + "mu0"], in1=XS[:, 1:], op0=ALU.mult, op1=ALU.add).then_inc(xx_done, 1)
                    for i in range(5):
                        dve.wait_ge(mu_ready, i + 1)
                        if i == 0:
                            dve.wait_ge(xp_ready, 2)
                        nc.vector.scalar_tensor_tensor(out=XX[:, i, :], in0=wide(4 + 2 * (i % 2)), scalar=W[pre + "x_bias"][:, i:i + 1], in1=DX[:, :], op0=ALU.add, op1=ALU.mult).then_inc(mu_used, 1)
                        dve.wait_ge(mu_used, i + 1)
                        own(nc.vector.tensor_tensor(XX[:, i, :], XX[:, i, :], XS[:, 1:], ALU.add))

                @block.tensor
                def _(pe):
                    pe.wait_ge(xx_done, 1)
                    for t in range(2):
                        nc.tensor.matmul(PS[:, t, :], W[pre + "W_x0"][:, 0:P], XX[:, 0, blk(t)], start=True, stop=True)
                    for t in range(2):
                        nc.tensor.matmul(PS[0:32, 2 + t, :], W[pre + "W_x0"][:, P:160], XX[:, 0, blk(t)], start=True, stop=True).then_inc(xp_ready, 1)
                    pe.wait_ge(xp_done, 2)
                    for i in range(5):
                        if i >= 2:
                            pe.wait_ge(mu_used, i - 1)
                        q = slice(32 * i, 32 * i + 32) if i < 4 else slice(0, 32)
                        w = W[pre + "W_x2a"][q, :] if i < 4 else W[pre + "W_x2b"][q, :]
                        for t in range(2):
                            mm = nc.tensor.matmul(PS[:, 4 + 2 * (i % 2) + t, :], w, (XP if i < 4 else XP5)[q, blk(t)], start=True, stop=True)
                        mm.then_inc(mu_ready, 1)

            with stage(nc, "p_ready", "rkv_done", "w1_done", "w2_ready", "w_done", "g_done", "ruk_done", "own_a", "own_d") as (block, p_ready, rkv_done, w1_done, w2_ready, w_done, g_done, ruk_done, own_a, own_d):
                @block.tensor
                def _(pe):
                    for n, (w, i, m) in enumerate((("W_w1", 1, 64), ("W_r", 0, 64), ("W_k", 2, 64), ("W_v", 3, P))):
                        for t in range(2):
                            mm = nc.tensor.matmul(PS[0:m, 2 * n + t, :], W[pre + w], XX[:, i, blk(t)], start=True, stop=True)
                        mm.then_inc(p_ready, 1)
                    pe.wait_ge(w1_done, 1)
                    for t in range(2):
                        mm = nc.tensor.matmul(PS[0:64, t, :], W[pre + "W_w2"][0:64, :], T64[:, blk(t)], start=True, stop=True)
                    mm.then_inc(w2_ready, 1)
                    pe.wait_ge(rkv_done, 1)
                    for t in range(2):
                        mm = nc.tensor.matmul(PS[:, 2 + t, :], W[pre + "W_g"], XX[:, 4, blk(t)], start=True, stop=True)
                    mm.then_inc(p_ready, 1)
                    pe.wait_ge(ruk_done, 1)
                    for t in range(2):
                        mm = nc.tensor.matmul(PS[:, 4 + t, :], HO[:, :], T64[:, blk(t)], start=True, stop=True)
                    mm.then_inc(p_ready, 1)

                @block.scalar
                def _(act):
                    act.wait_ge(p_ready, 1)
                    nc.scalar.activation(T64[:, :], wide64(0), ACT.Tanh).then_inc(w1_done, 1)
                    act.wait_ge(w2_ready, 1)
                    nc.scalar.activation(RKD[:, 2, :], wide64(0), ACT.Exp, bias=W[pre + "b_w2"][0:64, :]).then_inc(own_a, 1)
                    act.wait_ge(own_a, 1)
                    nc.scalar.activation(RKD[:, 2, :], RKD[:, 2, :], ACT.Exp, scale=-1.0).then_inc(w_done, 1)
                    act.wait_ge(p_ready, 5)
                    nc.scalar.activation(G[:, :], wide(2), ACT.Silu).then_inc(g_done, 1)

                @block.vector
                def _(dve):
                    own = Link(dve, own_d)
                    for n in range(3):
                        dve.wait_ge(p_ready, n + 2)
                        dst = RKD[:, n, :] if n < 2 else V[:, :]
                        nc.vector.tensor_copy(dst, wide64(2 + 2 * n) if n < 2 else wide(6)).then_inc(rkv_done, 1)
                    dve.wait_ge(rkv_done, 3)
                    dve.wait_ge(w2_ready, 1)
                    own(nc.vector.tensor_scalar(T64[:, :], RKD[:, 0, :], W[pre + "bonus"][0:64, :], None, ALU.mult))
                    nc.vector.tensor_tensor(T64[:, :], T64[:, :], RKD[:, 1, :], ALU.mult).then_inc(ruk_done, 1)
                    dve.wait_ge(p_ready, 6)
                    own(nc.vector.tensor_tensor(DX[:, :], V[:, :], wide(4), ALU.mult))

            with stage(nc, "k_ready", "d_ready", "r_ready", "kv_done", "scanned", "sr_done", "o_added", "own_d") as (block, k_ready, d_ready, r_ready, kv_done, scanned, sr_done, o_added, own_d):
                @block.tensor
                def _(pe):
                    for n in range(DK):
                        if n:
                            pe.wait_ge(kv_done, n)
                        for t in range(2):
                            mm = nc.tensor.matmul(PS[:, t, :], SEL[:, n, :], RKD[:, 1, blk(t)], start=True, stop=True)
                        mm.then_inc(k_ready, 1)
                        if n:
                            pe.wait_ge(scanned, n)
                        for t in range(2):
                            mm = nc.tensor.matmul(PS[:, 2 + t, :], SEL[:, n, :], RKD[:, 2, blk(t)], start=True, stop=True)
                        mm.then_inc(d_ready, 1)
                        if n:
                            pe.wait_ge(sr_done, n)
                        for t in range(2):
                            mm = nc.tensor.matmul(PS[:, 4 + t, :], SEL[:, n, :], RKD[:, 0, blk(t)], start=True, stop=True)
                        mm.then_inc(r_ready, 1)
                        if n:
                            for t in range(2):
                                mm = nc.tensor.matmul(PS[:, 6 + t, :], k.ident[:, :], SR[:, (n - 1) % 2, blk(t)], start=(n == 1), stop=False)
                            mm.then_inc(o_added, 1)
                    pe.wait_ge(sr_done, DK)
                    for t in range(2):
                        mm = nc.tensor.matmul(PS[:, 6 + t, :], k.ident[:, :], SR[:, (DK - 1) % 2, blk(t)], start=False, stop=True)
                    mm.then_inc(o_added, 1)

                @block.vector
                def _(dve):
                    own = Link(dve, own_d)
                    for n in range(DK):
                        dve.wait_ge(k_ready, n + 1)
                        nc.vector.tensor_tensor(KV[:, 0, :], V[:, :], wide(0), ALU.mult).then_inc(kv_done, 1)
                        dve.wait_ge(kv_done, n + 1)
                        dve.wait_ge(d_ready, n + 1)
                        nc.vector.tensor_tensor_scan(SS[:, 1:], wide(2), KV[:, 0, :], 0.0, ALU.mult, ALU.add).then_inc(scanned, 1)
                        dve.wait_ge(scanned, n + 1)
                        dve.wait_ge(r_ready, n + 1)
                        if n >= 2:
                            dve.wait_ge(o_added, n - 1)
                        nc.vector.tensor_tensor(SR[:, n % 2, :], SS[:, 0:SEQ], wide(4), ALU.mult).then_inc(sr_done, 1)
                        dve.wait_ge(sr_done, n + 1)
                    dve.wait_ge(o_added, DK)
                    own(nc.vector.tensor_tensor(V[:, :], DX[:, :], wide(6), ALU.add))

            with stage(nc, "mean_ready", "centered", "squared", "var_ready", "std_done", "o_done", "y_ready", "own_d") as (block, mean_ready, centered, squared, var_ready, std_done, o_done, y_ready, own_d):
                @block.tensor
                def _(pe):
                    for t in range(2):
                        nc.tensor.matmul(PS[:, t, :], BM[:, :], V[:, blk(t)], start=True, stop=True).then_inc(mean_ready, 1)
                    for t in range(2):
                        pe.wait_ge(squared, 1)
                        nc.tensor.matmul(PS[:, 2 + t, :], BM[:, :], DX[:, blk(t)], start=True, stop=True).then_inc(var_ready, 1)
                    pe.wait_ge(o_done, 1)
                    for t in range(2):
                        nc.tensor.matmul(PS[:, 4 + t, :], W[pre + "W_o"], V[:, blk(t)], start=True, stop=True).then_inc(y_ready, 1)

                @block.scalar
                def _(act):
                    act.wait_ge(centered, 1)
                    nc.scalar.activation(DX[:, :], V[:, :], ACT.Square).then_inc(squared, 1)
                    act.wait_ge(var_ready, 2)
                    nc.scalar.activation(DX[:, :], wide(2), ACT.Sqrt, bias=k.eps_col[:, 0:1]).then_inc(std_done, 1)

                @block.vector
                def _(dve):
                    own = Link(dve, own_d)
                    dve.wait_ge(mean_ready, 2)
                    nc.vector.tensor_tensor(V[:, :], V[:, :], wide(0), ALU.subtract).then_inc(centered, 1)
                    dve.wait_ge(std_done, 1)
                    own(nc.vector.reciprocal(DX[:, :], DX[:, :]))
                    own(nc.vector.tensor_tensor(V[:, :], V[:, :], DX[:, :], ALU.mult))
                    own(nc.vector.tensor_scalar(V[:, :], V[:, :], W[pre + "gn_weight"], W[pre + "gn_bias"], ALU.mult, ALU.add))
                    nc.vector.tensor_tensor(V[:, :], V[:, :], G[:, :], ALU.mult).then_inc(o_done, 1)
                    for t in range(2):
                        dve.wait_ge(y_ready, t + 1)
                        xb = k.X[:, bass.ds(tok + t * BLK, BLK)]
                        own(nc.vector.tensor_tensor(xb, xb, PS[:, 4 + t, :], ALU.add))



def l0a(k):
    nc, PS, W = k.nc, k.PS, k.W
    pre = "L0_attn_a_"
    CH, NC = 32, SEQ // 32
    GC = 4
    DECAY = 1.0 - 1.0 / 3000.0
    FLOOR = 0.08 * DECAY
    layernorm(k, k.X, k.XN)
    with ExitStack() as st:
        def sb(n, shape, dt=F32):
            return k.sbuf(st, n, shape, dt)
        wide = lambda a: PS[:, a:a + 2, :].rearrange("p a b -> p (a b)")
        PADC, PADL = 3, 63
        HS_, HMASK = sb("dl_hs", [P, P]), sb("dl_hm", [P, 4])
        STL, STU, UPI = sb("dl_stl", [P, P]), sb("dl_stu", [P, P]), sb("dl_upi", [P, P])
        WBX = sb("dl_wb", [P, 4, 32])
        ZW = sb("dl_zw", [P, 4, 224])
        E3 = sb("dl_e3", [P, 4, 4, P])
        CB, TMP4 = sb("dl_cb", [P, 5]), sb("dl_t4", [P, 4])
        QI = [sb(f"dl_in{n}", [P, PADC + SEQ]) for n in range(3)]
        ARENA = sb("dl_arena", [P, 8, SEQ])
        Q, KK, KB, BETA, VC, KC, KBC = (ARENA[:, n, :] for n in range(7))
        VP = sb("dl_vp", [P, PADL + SEQ])
        V = VP[:, PADL:]
        OC = sb("dl_oc", [P, SEQ])
        FS, FL = k.lnA[:, 0:SEQ], k.lnA[:, SEQ:]
        OD = sb("dl_od", [P, SEQ])
        S = sb("dl_S", [P, 32])
        eps6 = sb("dl_eps6", [P, 1])
        with stage(nc, "own_p", "p_done", "exp_done", "own_d") as (block, own_p, p_done, exp_done, own_d):
            @block.gpsimd
            def _(pool):
                own = Link(pool, own_p)
                head_constants(k, pool, own, HS_[:, :], 1.0)
                own(pool.memset(HMASK[:, :], 1.0))
                own(pool.affine_select(out=HMASK[:, :], in_=HMASK[:, :], compare_op=ALU.is_ge, fill=0.0, base=0, pattern=[[-32, 4]], channel_multiplier=1))
                own(pool.affine_select(out=HMASK[:, :], in_=HMASK[:, :], compare_op=ALU.is_ge, fill=0.0, base=31, pattern=[[32, 4]], channel_multiplier=-1))
                own(pool.memset(STL[:, :], -1.0))
                own(pool.affine_select(out=STL[:, :], in_=STL[:, :], compare_op=ALU.is_gt, fill=0.0, base=0, pattern=[[-1, P]], channel_multiplier=1))
                own(pool.memset(STU[:, :], -1.0))
                own(pool.affine_select(out=STU[:, :], in_=STU[:, :], compare_op=ALU.is_gt, fill=0.0, base=0, pattern=[[1, P]], channel_multiplier=-1))
                own(pool.memset(UPI[:, :], 1.0))
                own(pool.affine_select(out=UPI[:, :], in_=UPI[:, :], compare_op=ALU.is_ge, fill=0.0, base=0, pattern=[[1, P]], channel_multiplier=-1))
                own(pool.memset(ZW[:, :, :], 0.0))
                own(pool.memset(E3[:, :, :, :], 0.0))
                own(pool.memset(eps6[:, :], 1e-6))
                for n in range(3):
                    own(pool.memset(QI[n][:, 0:PADC], 0.0))
                pool.memset(VP[:, 0:PADL], 0.0).then_inc(p_done, 1)
                pool.wait_ge(p_done, 1)

            @block.scalar
            def _(act):
                nc.scalar.activation(TMP4[:, :], W[pre + "log_temp"], ACT.Exp, scale=-1.0).then_inc(exp_done, 1)

            @block.vector
            def _(dve):
                own = Link(dve, own_d)
                dve.wait_ge(p_done, 1)
                dve.wait_ge(exp_done, 1)
                nc.vector.tensor_copy(WBX[:, :, :], W[pre + "Wb"].unsqueeze(2).to_broadcast([P, 4, 32]))
                nc.vector.tensor_copy(ZW[:, :, 96:128], W[pre + "W2"].unsqueeze(2).to_broadcast([P, 4, 32]))
                for q in range(4):
                    for kind, off in ((0, 0), (1, 32), (1, 96), (2, 64), (3, 32)):
                        v = E3[:, kind, q, off:off + 16].rearrange("p (h q) -> p h q", q=4)[:, :, q]
                        nc.vector.tensor_scalar(v, HMASK[:, :], 1.0 / 32, None, ALU.mult)
                own(nc.vector.tensor_tensor(TMP4[:, :], TMP4[:, :], HMASK[:, :], ALU.mult))
                own(nc.vector.tensor_reduce(CB[:, 4:5], TMP4[:, :], AX.X, ALU.add))
                own(nc.vector.tensor_tensor(TMP4[:, :], W[pre + "copy_bias"], HMASK[:, :], ALU.mult))
                own(nc.vector.tensor_reduce(CB[:, 3:4], TMP4[:, :], AX.X, ALU.add))
                own(nc.vector.tensor_copy(CB[:, 0:3], W[pre + "b2"][:, 0:3]))
                own(nc.vector.scalar_tensor_tensor(out=CB[:, 3:4], in0=CB[:, 3:4], scalar=DECAY, in1=W[pre + "b2"][:, 3:4], op0=ALU.mult, op1=ALU.add))

        @contextmanager
        def batches():
            with nc.Fori(0, NTOK - SEQ + 1, SEQ) as tok:
                yield tok

        with batches() as tok:
            with stage(nc, "p_ready", "in_done", "conv_done", "act_done", "beta_ready", "own_d") as (block, p_ready, in_done, conv_done, act_done, beta_ready, own_d):
                @block.tensor
                def _(pe):
                    for n, w in enumerate(("Wq", "Wk", "Wv")):
                        for t in range(2):
                            mm = nc.tensor.matmul(PS[:, 2 * n + t, :], W[pre + w], k.XN[:, bass.ds(tok + t * BLK, BLK)], start=True, stop=True)
                        mm.then_inc(p_ready, 1)
                    for t in range(2):
                        mm = nc.tensor.matmul(PS[:, 6 + t, :], WBX[:, :, :].rearrange("p a b -> p (a b)"), k.XN[:, bass.ds(tok + t * BLK, BLK)], start=True, stop=True)
                    mm.then_inc(beta_ready, 1)

                @block.scalar
                def _(act):
                    for n in range(3):
                        act.wait_ge(p_ready, n + 1)
                        nc.scalar.activation(QI[n][:, PADC:], wide(2 * n), ACT.Identity).then_inc(in_done, 1)
                    act.wait_ge(beta_ready, 1)
                    nc.scalar.activation(BETA[:, :], wide(6), ACT.Sigmoid).then_inc(act_done, 1)
                    for n, dst in enumerate((Q[:, :], KK[:, :], V)):
                        act.wait_ge(conv_done, n + 1)
                        nc.scalar.activation(dst, dst, ACT.Silu).then_inc(act_done, 1)

                @block.vector
                def _(dve):
                    own = Link(dve, own_d)
                    for n, dst in enumerate((Q[:, :], KK[:, :], V)):
                        dve.wait_ge(in_done, n + 1)
                        w = W[pre + "conv"]
                        own(nc.vector.tensor_scalar(dst, QI[n][:, 0:SEQ], w[:, n, 0:1], None, ALU.mult))
                        for j in range(1, 4):
                            ins = nc.vector.scalar_tensor_tensor(out=dst, in0=QI[n][:, j:j + SEQ], scalar=w[:, n, j:j + 1], in1=dst, op0=ALU.mult, op1=ALU.add)
                            if j < 3:
                                own(ins)
                        ins.then_inc(conv_done, 1)

            with stage(nc, "squared", "sum_ready", "root_done", "own_d") as (block, squared, sum_ready, root_done, own_d):
                @block.scalar
                def _(act):
                    for n, src in enumerate((Q, KK)):
                        nc.scalar.activation((FS, FL)[n][:, :], src[:, :], ACT.Square).then_inc(squared, 1)
                    for n in range(2):
                        act.wait_ge(sum_ready, n + 1)
                        nc.scalar.activation((FS, FL)[n][:, :], wide(2 * n), ACT.Sqrt, bias=eps6[:, 0:1]).then_inc(root_done, 1)

                @block.tensor
                def _(pe):
                    for n in range(2):
                        pe.wait_ge(squared, n + 1)
                        for t in range(2):
                            mm = nc.tensor.matmul(PS[:, 2 * n + t, :], HS_[:, :], (FS, FL)[n][:, blk(t)], start=True, stop=True)
                        mm.then_inc(sum_ready, 1)

                @block.vector
                def _(dve):
                    own = Link(dve, own_d)
                    own(nc.vector.tensor_tensor(OD[:, :], V, BETA[:, :], ALU.mult))
                    own(nc.vector.transpose(VC[:, :], OD[:, :]))
                    for n, dst in enumerate((Q, KK)):
                        dve.wait_ge(root_done, n + 1)
                        f = (FS, FL)[n]
                        own(nc.vector.reciprocal(f[:, :], f[:, :]))
                        own(nc.vector.tensor_tensor(dst[:, :], dst[:, :], f[:, :], ALU.mult))
                    own(nc.vector.tensor_tensor(KB[:, :], KK[:, :], BETA[:, :], ALU.mult))
                    nc.vector.transpose(KC[:, :], KK[:, :])
                    own(nc.vector.transpose(KBC[:, :], KB[:, :]))
                    for dst, n, w in ((FS, 5, W[pre + "fir_s"]), (FL, 64, W[pre + "fir_l"])):
                        off = PADL - (n - 1)
                        own(nc.vector.tensor_scalar(dst[:, :], VP[:, off:off + SEQ], w[:, 0:1], None, ALU.mult))
                        for j in range(1, n):
                            own(nc.vector.scalar_tensor_tensor(out=dst[:, :], in0=VP[:, off + j:off + j + SEQ], scalar=w[:, j:j + 1], in1=dst[:, :], op0=ALU.mult, op1=ALU.add))
                    own(nc.vector.memset(S[:, :], 0.0))

            with ExitStack() as st2:
                def sb2(n):
                    return k.sbuf(st2, n, [P, GC, P], F32)
                Kx, Kbx, Qx, Kcx, Kbcx, WT, AT = (sb2("dl_" + n) for n in ("kx", "kbx", "qx", "kcx", "kbcx", "wt", "at"))
                POW = [sb2("dl_p0"), sb2("dl_p1")]
                POT = [sb2("dl_q0"), sb2("dl_q1")]
                TT = sb2("dl_tt")
                UU = k.sbuf(st2, "dl_uu", [P, GC, 32], F32)
                UI = k.sbuf(st2, "dl_ui", [P, 32], F32)
                with nc.Fori(0, SEQ - GC * CH + 1, GC * CH) as at:
                    with stage(nc, "spread_done", "prod", "taken", "own_d") as (block, spread_done, prod, taken, own_d):
                        bank = lambda a: PS[:, a, :].rearrange("p (c n) -> p c n", n=P)

                        @block.vector
                        def _(dve):
                            own = Link(dve, own_d)
                            hm = HMASK[:, :].unsqueeze(1).unsqueeze(3).to_broadcast([P, GC, 4, 32])
                            for dst, src in ((Kx, KK), (Kbx, KB), (Qx, Q), (Kbcx, KBC), (Kcx, KC)):
                                v = src[:, bass.ds(at, GC * CH)].rearrange("p (c i) -> p c i", i=CH).unsqueeze(2).to_broadcast([P, GC, 4, 32])
                                nc.vector.tensor_tensor(dst[:, :, :].rearrange("p c (h i) -> p c h i", h=4), v, hm, ALU.mult).then_inc(spread_done, 1)

                            def m(x):
                                return x[:, :].unsqueeze(1).to_broadcast([P, GC, P])
                            dve.wait_ge(prod, 1)
                            nc.vector.tensor_tensor(POW[0][:, :, :], bank(0), m(STL), ALU.mult).then_inc(taken, 1)
                            dve.wait_ge(prod, 2)
                            nc.vector.tensor_tensor(POT[0][:, :, :], bank(1), m(STU), ALU.mult).then_inc(taken, 1)
                            dve.wait_ge(taken, 2)
                            nc.vector.tensor_tensor(TT[:, :, :], POT[0][:, :, :], m(k.ident), ALU.add).then_inc(taken, 1)
                            dve.wait_ge(prod, 3)
                            nc.vector.tensor_tensor(AT[:, :, :], bank(2), m(UPI), ALU.mult).then_inc(taken, 1)
                            for n in range(4):
                                dve.wait_ge(prod, 3 * n + 4)
                                nc.vector.tensor_copy(POW[(n + 1) % 2][:, :, :], bank(3)).then_inc(taken, 1)
                                dve.wait_ge(prod, 3 * n + 5)
                                nc.vector.tensor_copy(POT[(n + 1) % 2][:, :, :], bank(4)).then_inc(taken, 1)
                                dve.wait_ge(prod, 3 * n + 6)
                                nc.vector.tensor_tensor(TT[:, :, :], TT[:, :, :], bank(5), ALU.add).then_inc(taken, 1)
                                dve.wait_ge(taken, 3 * n + 7)
                            dve.wait_ge(prod, 16)
                            nc.vector.tensor_copy(WT[:, :, :], bank(6)).then_inc(taken, 1)
                            nc.vector.tensor_copy(UU[:, :, :], PS[:, 7, 0:GC * 32].rearrange("p (c n) -> p c n", n=32)).then_inc(taken, 1)
                            dve.wait_ge(taken, 18)

                        @block.tensor
                        def _(pe):
                            def each(a, left, right):
                                for c in range(GC):
                                    mm = nc.tensor.matmul(PS[:, a, blk(c, P)], left[:, c, :], right[:, c, :], start=True, stop=True)
                                mm.then_inc(prod, 1)
                            pe.wait_ge(spread_done, 2)
                            each(0, Kbx, Kx)
                            each(1, Kx, Kbx)
                            pe.wait_ge(spread_done, 3)
                            each(2, Kx, Qx)
                            for n in range(4):
                                pe.wait_ge(taken, 2 if n == 0 else 3 * n + 3)
                                a, b = POW[n % 2], POT[n % 2]
                                each(3, b, a)
                                each(4, a, b)
                                pe.wait_ge(taken, 3 * n + 5)
                                each(5, POW[(n + 1) % 2], TT)
                            pe.wait_ge(taken, 16)
                            pe.wait_ge(spread_done, 4)
                            for c in range(GC):
                                nc.tensor.matmul(PS[:, 6, blk(c, P)], Kbcx[:, c, :], TT[:, c, :], start=True, stop=True)
                            for c in range(GC):
                                mm = nc.tensor.matmul(PS[:, 7, blk(c, 32)], TT[:, c, :], VC[:, bass.ds(at + c * CH, CH)], start=True, stop=True)
                            mm.then_inc(prod, 1)

                    with stage(nc, "ws_ready", "u_done", "o_ready", "ks_ready", "s_done", "o_taken") as (block, ws_ready, u_done, o_ready, ks_ready, s_done, o_taken):
                        @block.tensor
                        def _(pe):
                            for c in range(GC):
                                if c:
                                    pe.wait_ge(s_done, c)
                                nc.tensor.matmul(PS[:, c % 2, 0:32], WT[:, c, :], S[:, :], start=True, stop=True).then_inc(ws_ready, 1)
                                if c >= 2:
                                    pe.wait_ge(o_taken, c - 1)
                                nc.tensor.matmul(PS[:, 2 + c % 2, 0:32], Qx[:, c, :], S[:, :], start=True, stop=False)
                                pe.wait_ge(u_done, c + 1)
                                nc.tensor.matmul(PS[:, 4 + c % 2, 0:32], Kcx[:, c, :], UI[:, :], start=True, stop=True).then_inc(ks_ready, 1)
                                nc.tensor.matmul(PS[:, 2 + c % 2, 0:32], AT[:, c, :], UI[:, :], start=False, stop=True).then_inc(o_ready, 1)

                        @block.vector
                        def _(dve):
                            for c in range(GC):
                                dve.wait_ge(ws_ready, c + 1)
                                if c:
                                    dve.wait_ge(o_ready, c)
                                nc.vector.tensor_tensor(UI[:, :], UU[:, c, :], PS[:, c % 2, 0:32], ALU.subtract).then_inc(u_done, 1)
                                dve.wait_ge(ks_ready, c + 1)
                                nc.vector.tensor_tensor(S[:, :], S[:, :], PS[:, 4 + c % 2, 0:32], ALU.add).then_inc(s_done, 1)
                                dve.wait_ge(s_done, c + 1)

                        @block.scalar
                        def _(act):
                            for c in range(GC):
                                act.wait_ge(o_ready, c + 1)
                                nc.scalar.activation(OC[:, bass.ds(at + c * CH, CH)], PS[:, 2 + c % 2, 0:32], ACT.Identity).then_inc(o_taken, 1)
                            act.wait_ge(o_taken, GC)

            with ExitStack() as st2:
                def sb2(n, shape):
                    return k.sbuf(st2, n, shape, F32)
                SRC, SQ, AB, LG = (ARENA[:, 2 * n:2 * n + 2, :].rearrange("p a (b c) -> p (a b) c", c=BLK) for n in range(4))
                STA, H1 = sb2("dl_sta", [P, BLK]), sb2("dl_h1", [P, 4, BLK])
                MX, O = sb2("dl_mx", [P, BLK]), sb2("dl_o", [P, BLK])
                with stage(nc, "own_d") as (block, own_d):
                    @block.vector
                    def _(dve):
                        nc.vector.transpose(OD[:, :], OC[:, :]).then_inc(own_d, 1)
                        dve.wait_ge(own_d, 1)
                with nc.Fori(0, SEQ - BLK + 1, BLK) as tb:
                    with stage(nc, "src_done", "sq_done", "st_ready", "st_done", "mean_sq", "h_ready", "h_done", "lg_ready", "own_d", "own_a") as (block, src_done, sq_done, st_ready, st_done, mean_sq, h_ready, h_done, lg_ready, own_d, own_a):
                        @block.vector
                        def _(dve):
                            own = Link(dve, own_d)
                            for n, a in enumerate((FS, FL, OD)):
                                nc.vector.tensor_copy(SRC[:, n, :], a[:, bass.ds(tb, BLK)]).then_inc(src_done, 1)
                            nc.vector.tensor_copy(SRC[:, 3, :], VP[:, bass.ds(tb + PADL, BLK)]).then_inc(src_done, 1)
                            dve.wait_ge(st_ready, 1)
                            own(nc.vector.tensor_copy(STA[:, :], PS[:, 0, :]))
                            own(nc.vector.tensor_copy(MX[32:64, :], PS[32:64, 1, :]))
                            own(nc.vector.tensor_tensor(MX[32:64, :], MX[32:64, :], MX[32:64, :], ALU.mult))
                            nc.vector.tensor_tensor(STA[32:64, :], STA[32:64, :], MX[32:64, :], ALU.subtract).then_inc(mean_sq, 1)

                        @block.scalar
                        def _(act):
                            for n in range(4):
                                act.wait_ge(src_done, n + 1)
                                nc.scalar.activation(SQ[:, n, :], SRC[:, n, :], ACT.Square)
                                nc.scalar.activation(AB[:, n, :], SRC[:, n, :], ACT.Abs).then_inc(sq_done, 1)
                            act.wait_ge(mean_sq, 1)
                            nc.scalar.activation(STA[96:128, :], STA[96:128, :], ACT.Sqrt, scale=32.0).then_inc(st_done, 1)
                            for h in range(4):
                                act.wait_ge(h_ready, h + 1)
                                nc.scalar.activation(H1[:, h, :], PS[:, 2 + h, :], ACT.Gelu_apprx_tanh, bias=W[pre + "b1"]).then_inc(h_done, 1)

                        @block.tensor
                        def _(pe):
                            for n in range(4):
                                pe.wait_ge(sq_done, n + 1)
                                nc.tensor.matmul(PS[:, 0, :], E3[:, 0, n, :], SRC[:, n, :], start=(n == 0), stop=False)
                                nc.tensor.matmul(PS[:, 0, :], E3[:, 1, n, :], SQ[:, n, :], start=False, stop=False)
                                nc.tensor.matmul(PS[:, 0, :], E3[:, 2, n, :], AB[:, n, :], start=False, stop=(n == 3))
                                mm = nc.tensor.matmul(PS[:, 1, :], E3[:, 3, n, :], SRC[:, n, :], start=(n == 0), stop=(n == 3))
                            mm.then_inc(st_ready, 1)
                            pe.wait_ge(st_done, 1)
                            for h in range(4):
                                nc.tensor.matmul(PS[:, 2 + h, :], W[pre + "W1x"], k.XN[:, bass.ds(tok + tb, BLK)], start=True, stop=False)
                                nc.tensor.matmul(PS[:, 2 + h, :], W[pre + "W1s"][:, h, :], STA[:, :], start=False, stop=True).then_inc(h_ready, 1)
                            for h in range(4):
                                pe.wait_ge(h_done, h + 1)
                            for j in range(4):
                                bank = (6, 7, 0, 1)[j]
                                for h in range(4):
                                    mm = nc.tensor.matmul(PS[:, bank, :], ZW[:, j, 96 - 32 * h:224 - 32 * h], H1[:, h, :], start=(h == 0), stop=(h == 3))
                            mm.then_inc(lg_ready, 1)

                    with stage(nc, "shifted", "exp_done", "mixed", "sq_done", "ms_ready", "rt_done", "o_done", "y_ready", "own_d") as (block, shifted, exp_done, mixed, sq_done, ms_ready, rt_done, o_done, y_ready, own_d):
                        @block.vector
                        def _(dve):
                            own = Link(dve, own_d)
                            for j in range(4):
                                own(nc.vector.tensor_scalar(LG[:, j, :], PS[:, (6, 7, 0, 1)[j], :], CB[:, j:j + 1], CB[:, 4:5], ALU.add, ALU.mult))
                            own(nc.vector.tensor_tensor(SQ[:, 0:2, :], LG[:, 0:2, :], LG[:, 2:4, :], ALU.max))
                            own(nc.vector.tensor_tensor(MX[:, :], SQ[:, 0, :], SQ[:, 1, :], ALU.max))
                            nc.vector.tensor_tensor(LG[:, :, :], LG[:, :, :], MX[:, :].unsqueeze(1).to_broadcast([P, 4, BLK]), ALU.subtract).then_inc(shifted, 1)
                            dve.wait_ge(exp_done, 1)
                            own(nc.vector.tensor_tensor(SQ[:, 0:2, :], LG[:, 0:2, :], LG[:, 2:4, :], ALU.add))
                            own(nc.vector.tensor_tensor(MX[:, :], SQ[:, 0, :], SQ[:, 1, :], ALU.add))
                            own(nc.vector.reciprocal(MX[:, :], MX[:, :]))
                            own(nc.vector.tensor_tensor(LG[:, :, :], LG[:, :, :], MX[:, :].unsqueeze(1).to_broadcast([P, 4, BLK]), ALU.mult))
                            own(nc.vector.tensor_scalar(LG[:, :, :], LG[:, :, :], 1.0 - 4.0 * FLOOR, FLOOR, ALU.mult, ALU.add))
                            own(nc.vector.tensor_tensor(LG[:, :, :], LG[:, :, :], SRC[:, :, :], ALU.mult))
                            own(nc.vector.tensor_tensor(SQ[:, 0:2, :], LG[:, 0:2, :], LG[:, 2:4, :], ALU.add))
                            nc.vector.tensor_tensor(O[:, :], SQ[:, 0, :], SQ[:, 1, :], ALU.add).then_inc(mixed, 1)
                            dve.wait_ge(rt_done, 1)
                            dve.wait_ge(mixed, 1)
                            own(nc.vector.reciprocal(MX[:, :], MX[:, :]))
                            own(nc.vector.tensor_tensor(O[:, :], O[:, :], MX[:, :], ALU.mult))
                            nc.vector.tensor_scalar(O[:, :], O[:, :], W[pre + "o_norm_w"], None, ALU.mult).then_inc(o_done, 1)
                            dve.wait_ge(y_ready, 1)
                            xb = k.X[:, bass.ds(tok + tb, BLK)]
                            own(nc.vector.tensor_tensor(xb, xb, PS[:, 3, :], ALU.add))

                        @block.scalar
                        def _(act):
                            act.wait_ge(shifted, 1)
                            nc.scalar.activation(LG[:, :, :], LG[:, :, :], ACT.Exp).then_inc(exp_done, 1)
                            act.wait_ge(mixed, 1)
                            nc.scalar.activation(AB[:, 0, :], O[:, :], ACT.Square).then_inc(sq_done, 1)
                            act.wait_ge(ms_ready, 1)
                            nc.scalar.activation(MX[:, :], PS[:, 2, :], ACT.Sqrt, scale=1.0 / 32, bias=k.eps_col[:, 0:1]).then_inc(rt_done, 1)

                        @block.tensor
                        def _(pe):
                            pe.wait_ge(sq_done, 1)
                            nc.tensor.matmul(PS[:, 2, :], HS_[:, :], AB[:, 0, :], start=True, stop=True).then_inc(ms_ready, 1)
                            pe.wait_ge(o_done, 1)
                            nc.tensor.matmul(PS[:, 3, :], W[pre + "Wo"], O[:, :], start=True, stop=True).then_inc(y_ready, 1)



def l1b(k):
    nc, PS, W = k.nc, k.PS, k.W
    pre = "L1_attn_b_"
    NHEAD, NHASH, NBIN = 8, 8, 16
    SELF = -1e5
    layernorm(k, k.X, k.XN)
    with ExitStack() as st:
        def sb(n, shape, dt=F32):
            return k.sbuf(st, n, shape, dt)
        OHT = sb("ls_oht", [P, 4, NTOK], BF16)
        V1 = sb("ls_v1", [P, NTILE, NHEAD, 17])
        RB = k.lnA[:, 0:NHEAD * NHASH * 8].rearrange("p (h n k) -> p h n k", h=NHEAD, n=NHASH)
        HM = sb("ls_hm", [P, NHEAD])
        W8 = sb("ls_w8", [P, 8])
        BASEM, SELP = sb("ls_basem", [P, P]), sb("ls_selp", [P, 2, P])
        HS32 = sb("ls_hs", [P, P])
        PC, BINC = sb("ls_pc", [P, 12]), sb("ls_binc", [P, 8])
        one = sb("ls_one", [P, 1])
        NI = sb("ls_ni", [P, P])
        SI = sb("ls_si", [P, P])
        with stage(nc, "own_p", "p_done", "own_d") as (block, own_p, p_done, own_d):
            @block.gpsimd
            def _(pool):
                own = Link(pool, own_p)
                own(pool.memset(V1[:, :, :, :], 1.0))
                own(pool.memset(one[:, :], 1.0))
                own(pool.memset(HM[:, :], 1.0))
                own(pool.affine_select(out=HM[:, :], in_=HM[:, :], compare_op=ALU.is_ge, fill=0.0, base=0, pattern=[[-16, 8]], channel_multiplier=1))
                own(pool.affine_select(out=HM[:, :], in_=HM[:, :], compare_op=ALU.is_ge, fill=0.0, base=15, pattern=[[16, 8]], channel_multiplier=-1))
                own(pool.iota(W8[:, :], [[-1, 8]], base=8, channel_multiplier=0, allow_small_or_imprecise_dtypes=True))
                own(pool.memset(BASEM[:, :], 1.0))
                own(pool.affine_select(out=BASEM[:, :], in_=BASEM[:, :], compare_op=ALU.is_gt, fill=0.0, base=0, pattern=[[1, P]], channel_multiplier=-1))
                v = BASEM[:, :].rearrange("p (a b) -> p a b", b=8)
                own(pool.affine_select(out=v, in_=v, compare_op=ALU.is_ge, fill=0.0, base=0, pattern=[[-8, 16], [0, 8]], channel_multiplier=1))
                own(pool.memset(SELP[:, :, :], 1.0))
                v = SELP[:, :, :].rearrange("p a (n b) -> p a n b", b=NBIN)
                own(pool.affine_select(out=v, in_=v, compare_op=ALU.is_ge, fill=0.0, base=0, pattern=[[-64, 2], [-8, 8], [0, NBIN]], channel_multiplier=1))
                own(pool.affine_select(out=v, in_=v, compare_op=ALU.is_ge, fill=0.0, base=7, pattern=[[64, 2], [8, 8], [0, NBIN]], channel_multiplier=-1))
                head_constants(k, pool, own, HS32[:, :], 1.0)
                own(pool.iota(PC[:, 0:7], [[16, 7]], base=16, channel_multiplier=0, allow_small_or_imprecise_dtypes=True))
                own(pool.iota(PC[:, 7:8], [[0, 1]], base=0, channel_multiplier=1, allow_small_or_imprecise_dtypes=True))
                own(pool.affine_select(out=NI[:, :], in_=one[:, 0:1].to_broadcast([P, P]), compare_op=ALU.not_equal, fill=0.0, base=0, pattern=[[-1, P]], channel_multiplier=1))
                pool.memset(PC[:, 8:9], 0.0).then_inc(p_done, 1)

            @block.vector
            def _(dve):
                own = Link(dve, own_d)
                dve.wait_ge(p_done, 1)
                own(nc.vector.tensor_scalar(SI[:, :], k.ident[:, :], SELF, None, ALU.mult))
                rot = W[pre + "rot"].rearrange("p (n k) -> p n k", k=4).unsqueeze(1).to_broadcast([P, NHEAD, NHASH, 4])
                hm = HM[:, :].unsqueeze(2).unsqueeze(3).to_broadcast([P, NHEAD, NHASH, 4])
                own(nc.vector.tensor_tensor(RB[:, :, :, 0:4], rot, hm, ALU.mult))
                own(nc.vector.tensor_scalar(RB[:, :, :, 4:8], RB[:, :, :, 0:4], -1.0, None, ALU.mult))
                own(nc.vector.tensor_scalar(PC[:, 0:7], PC[:, 0:7], PC[:, 7:8], None, ALU.is_le))
                own(nc.vector.tensor_reduce(PC[:, 8:9], PC[:, 0:7], AX.X, ALU.add))
                own(nc.vector.scalar_tensor_tensor(out=PC[:, 9:10], in0=PC[:, 8:9], scalar=-16.0, in1=PC[:, 7:8], op0=ALU.mult, op1=ALU.add))
                own(nc.vector.tensor_scalar(PC[:, 10:11], PC[:, 9:10], 1.0, 32.0, ALU.is_equal, ALU.mult))
                own(nc.vector.tensor_scalar(BINC[:, 0:1], PC[:, 9:10], -64.0, -31.5, ALU.mult, ALU.add))
                own(nc.vector.tensor_scalar(BINC[:, 1:2], PC[:, 9:10], -64.0, -63.5, ALU.mult, ALU.add))
                own(nc.vector.tensor_tensor(BINC[:, 1:2], BINC[:, 1:2], PC[:, 10:11], ALU.add))
                own(nc.vector.tensor_scalar(BINC[:, 2:3], PC[:, 10:11], 64.0, None, ALU.add))
                own(nc.vector.memset(BINC[:, 3:4], 69.0))

        with ExitStack() as st2:
            def sb2(n, shape):
                return k.sbuf(st2, n, shape, F32)
            XC, QC = sb2("ls_xc", [P, P]), sb2("ls_qc", [P, P])
            R, EQ, OH = sb2("ls_r", [P, 64, 8]), sb2("ls_eq", [P, 64, 8]), sb2("ls_oh", [P, 64, 8])
            MX, CD = sb2("ls_mx", [P, 64]), sb2("ls_cd", [P, 64])
            with nc.Fori(0, NTILE) as t:
                with stage(nc, "x_done", "q_ready", "q_done", "r_ready", "oh_done", "turned", "own_d", "own_a") as (block, x_done, q_ready, q_done, r_ready, oh_done, turned, own_d, own_a):
                    @block.scalar
                    def _(act):
                        nc.scalar.activation(XC[:, :], k.XN[:, bass.ds(t * P, P)], ACT.Identity).then_inc(x_done, 1)
                        act.wait_ge(q_ready, 1)
                        nc.scalar.activation(QC[:, :], PS[:, 0, 0:P], ACT.Identity).then_inc(q_done, 1)
                        act.wait_ge(q_ready, 2)
                        nc.scalar.activation(V1[:, bass.ds(t, 1), :, 1:17].rearrange("p a h f -> p (a h) f"), PS[:, 1, 0:P].rearrange("p (h f) -> p h f", f=16), ACT.Identity).then_inc(own_a, 1)
                        act.wait_ge(turned, 1)
                        nc.scalar.activation(OHT[:, :, bass.ds(t * P, P)], PS[:, 3, :].rearrange("p (a b) -> p a b", b=P), ACT.Identity).then_inc(own_a, 1)
                        act.wait_ge(own_a, 2)

                    @block.tensor
                    def _(pe):
                        pe.wait_ge(x_done, 1)
                        nc.tensor.matmul(PS[:, 0, 0:P], W[pre + "w_qk"], XC[:, :], start=True, stop=True).then_inc(q_ready, 1)
                        nc.tensor.matmul(PS[:, 1, 0:P], XC[:, :], W[pre + "w_v"], start=True, stop=True).then_inc(q_ready, 1)
                        pe.wait_ge(q_done, 1)
                        nc.tensor.matmul(PS[:, 2, :], QC[:, :], RB[:, :, :, :].rearrange("p h n k -> p (h n k)"), start=True, stop=True).then_inc(r_ready, 1)
                        pe.wait_ge(oh_done, 1)
                        for a in range(4):
                            mm = nc.tensor.transpose(PS[:, 3, blk(a, P)], OH[:, 16 * a:16 * a + 16, :].rearrange("p a b -> p (a b)"), k.ident[:, :])
                        mm.then_inc(turned, 1)

                    @block.vector
                    def _(dve):
                        own = Link(dve, own_d)
                        bc = lambda x: x.unsqueeze(2).to_broadcast([P, 64, 8])
                        w8 = W8[:, :].unsqueeze(1).to_broadcast([P, 64, 8])
                        dve.wait_ge(r_ready, 1)
                        own(nc.vector.tensor_copy(R[:, :, :], PS[:, 2, :].rearrange("p (a b) -> p a b", b=8)))
                        own(nc.vector.tensor_reduce(MX[:, :], R[:, :, :], AX.X, ALU.max))
                        own(nc.vector.tensor_tensor(EQ[:, :, :], R[:, :, :], bc(MX[:, :]), ALU.is_equal))
                        own(nc.vector.tensor_tensor(EQ[:, :, :], EQ[:, :, :], w8, ALU.mult))
                        own(nc.vector.tensor_reduce(CD[:, :], EQ[:, :, :], AX.X, ALU.max))
                        nc.vector.tensor_tensor(OH[:, :, :], w8, bc(CD[:, :]), ALU.is_equal).then_inc(oh_done, 1)

        KH, QH = sb("ls_kh", [P, HG, SEQ], BF16), sb("ls_qh", [P, HG, SEQ], BF16)
        QKS = sb("ls_qk", [P, 2, SEQ])
        QS, KS = QKS[:, 0, :], QKS[:, 1, :]
        V1S = sb("ls_v1s", [P, NT, HG, 17])
        WS = sb("ls_w", [P, 2, P])
        M2, M, MC = sb("ls_m2", [P, HG, NT, 2]), sb("ls_m", [P, HG, NT]), sb("ls_mc", [P, HG, NT])
        NM, MB = sb("ls_nm", [P, 2, HG, NT]), sb("ls_mb", [P, HG, NT, 3], BF16)
        A, D2 = sb("ls_a", [P, 3, BLK]), sb("ls_d", [P, 2, BLK])
        B = [QKS[:, n // 2, blk(n % 2)] for n in range(4)] + [k.lnA[:, blk(n)] for n in range(4)]
        SEL = sb("ls_sel", [P, 2, HG, 3, P], BF16)
        KX, QX = sb("ls_kx", [P, HG, SEQ], BF16), sb("ls_qx", [P, HG, SEQ], BF16)
        parts, rest = sb("ls_parts", [P, 2, 3, SEQ], BF16), k.lnA[:, :].rearrange("p (a n) -> p a n", a=4)
        CUM, VAL = k.lnA[:, 0:SEQ], k.lnA[:, SEQ:]
        OT, RD = CUM, VAL
        base = sb("ls_base", [P, 2])
        RQ = sb("ls_rq", [P, NT, HG])
        with stage(nc, "own_p") as (block, own_p):
            @block.gpsimd
            def _(pool):
                expansion_constants(k, pool, Link(pool, own_p), SEL, 16, KX, QX)

        def body(b, r):
            tok = b * SEQ
            wide = lambda a: PS[:, a:a + 2, :].rearrange("p a b -> p (a b)")
            for pp in range(2):
                with stage(nc, "scanned", "base_ready", "val_done", "pos_ready", "dist_done", "hot_done", "own_d") as (block, scanned, base_ready, val_done, pos_ready, dist_done, hot_done, own_d):
                    oh = OHT[:, bass.ds(2 * r + pp, 1), bass.ds(tok, SEQ)].rearrange("p a n -> p (a n)")

                    @block.vector
                    def _(dve):
                        own = Link(dve, own_d)
                        nc.vector.tensor_tensor_scan(CUM, one[:, 0:1].to_broadcast([P, SEQ]), oh, 0.0, ALU.mult, ALU.add).then_inc(scanned, 1)
                        dve.wait_ge(base_ready, 1)
                        dve.wait_ge(scanned, 1)
                        own(nc.vector.tensor_scalar(base[:, 0:1], PS[:, 0, 0:1], -1.0, None, ALU.add))
                        nc.vector.scalar_tensor_tensor(out=VAL, in0=CUM, scalar=base[:, 0:1], in1=oh, op0=ALU.add, op1=ALU.mult).then_inc(val_done, 1)
                        for hh in range(2):
                            g = 2 * pp + hh
                            for t in range(2):
                                for n, (dst, lim) in enumerate(((KH, 32.0), (QH, BINC[:, 2:3]))):
                                    u = 4 * hh + 2 * t + n
                                    dve.wait_ge(dist_done, u + 1)
                                    nc.vector.tensor_scalar(dst[:, g, blk(t)], (A, D2)[n][:, t, :], lim, None, ALU.is_le).then_inc(hot_done, 1)
                        dve.wait_ge(hot_done, 8)

                    @block.tensor
                    def _(pe):
                        pe.wait_ge(scanned, 1)
                        nc.tensor.matmul(PS[:, 0, 0:1], BASEM[:, :], CUM[:, SEQ - 1:SEQ], start=True, stop=True).then_inc(base_ready, 1)
                        pe.wait_ge(val_done, 1)
                        for hh in range(2):
                            for t in range(2):
                                nc.tensor.matmul(PS[:, 1 + 2 * hh + t, :], SELP[:, hh, :], VAL[:, blk(t)], start=True, stop=True).then_inc(pos_ready, 1)

                    @block.scalar
                    def _(act):
                        for hh in range(2):
                            for t in range(2):
                                act.wait_ge(pos_ready, 2 * hh + t + 1)
                                for n in range(2):
                                    if hh:
                                        act.wait_ge(hot_done, 2 * t + n + 1)
                                    nc.scalar.activation((A, D2)[n][:, t, :], PS[:, 1 + 2 * hh + t, :], ACT.Abs, bias=BINC[:, n:n + 1]).then_inc(dist_done, 1)

            with stage(nc, "w_copied", "q_ready", "q_done", "squared", "sum_ready", "clamped", "root_done", "own_d") as (block, w_copied, q_ready, q_done, squared, sum_ready, clamped, root_done, own_d):
                @block.tensor
                def _(pe):
                    pe.wait_ge(w_copied, 1)
                    for t in range(2):
                        mm = nc.tensor.matmul(PS[:, t, :], WS[:, 0, :], k.XN[:, bass.ds(tok + t * BLK, BLK)], start=True, stop=True)
                    mm.then_inc(q_ready, 1)
                    pe.wait_ge(squared, 1)
                    for t in range(2):
                        mm = nc.tensor.matmul(PS[:, 2 + t, :], HS32[:, :], OT[:, blk(t)], start=True, stop=True)
                    mm.then_inc(sum_ready, 1)

                @block.scalar
                def _(act):
                    act.wait_ge(q_done, 1)
                    nc.scalar.activation(OT, KS, ACT.Square).then_inc(squared, 1)
                    act.wait_ge(clamped, 1)
                    nc.scalar.activation(RD, RD, ACT.Sqrt).then_inc(root_done, 1)

                @block.vector
                def _(dve):
                    own = Link(dve, own_d)
                    nc.vector.tensor_copy(WS[:, 0, :], W[pre + "WqkP"][:, bass.ds(r, 1), :].rearrange("p a n -> p (a n)")).then_inc(w_copied, 1)
                    own(nc.vector.tensor_copy(WS[:, 1, :], W[pre + "WoP"][:, bass.ds(r, 1), :].rearrange("p a n -> p (a n)")))
                    own(nc.vector.tensor_copy(V1S[:, :, :, :], V1[:, bass.ds(b * NT, NT), bass.ds(r * HG, HG), :]))
                    dve.wait_ge(q_ready, 1)
                    nc.vector.tensor_copy(KS, wide(0)).then_inc(q_done, 1)
                    own(nc.vector.tensor_scalar(QS, wide(0), 0.25, None, ALU.mult))
                    dve.wait_ge(sum_ready, 1)
                    nc.vector.tensor_scalar(RD, wide(2), 1e-12, None, ALU.max).then_inc(clamped, 1)
                    dve.wait_ge(root_done, 1)
                    dve.wait_ge(q_done, 1)
                    own(nc.vector.reciprocal(RD, RD))
                    own(nc.vector.tensor_tensor(KS, KS, RD, ALU.mult))

            expand_heads(k, KS, QS, KX, QX, SEL, parts, rest)

            UNITS = [(g, i, t) for i in range(NT) for g in range(HG) for t in range(2)]
            with stage(nc, "sc_ready", "pen_done", "maxed", "own_d") as (block, sc_ready, pen_done, maxed, own_d):
                @block.tensor
                def _(pe):
                    for u, (g, i, t) in enumerate(UNITS):
                        if u >= 4:
                            pe.wait_ge(maxed, u - 3)
                        nc.tensor.matmul(PS[:, 4 + u % 4, :], QH[:, g, blk(i, P)], KH[:, g, blk(t)], start=True, stop=True)
                        nc.tensor.matmul(PS[:, u % 4, :], QX[0:MAXROW, g, blk(i, P)], KX[0:MAXROW, g, blk(t)], start=True, stop=True).then_inc(sc_ready, 1)

                @block.scalar
                def _(act):
                    for u, (g, i, t) in enumerate(UNITS):
                        act.wait_ge(sc_ready, u + 1)
                        if u >= 3:
                            act.wait_ge(maxed, u - 2)
                        nc.scalar.activation(A[:, u % 3, :], PS[:, 4 + u % 4, :], ACT.Exp, scale=-200.0, bias=BINC[:, 3:4]).then_inc(pen_done, 1)

                @block.vector
                def _(dve):
                    own = Link(dve, own_d)
                    for u, (g, i, t) in enumerate(UNITS):
                        dve.wait_ge(sc_ready, u + 1)
                        if t == i // 4:
                            tile = PS[:, u % 4, blk(i % 4, P)]
                            own(nc.vector.tensor_tensor(tile, tile, NI[:, :], ALU.mult))
                            own(nc.vector.tensor_tensor(tile, tile, SI[:, :], ALU.add))
                        dve.wait_ge(pen_done, u + 1)
                        sc = PS[:, u % 4, :]
                        nc.vector.tensor_tensor_reduce(sc, sc, A[:, u % 3, :], 1.0, -3e38, ALU.subtract, ALU.max, M2[:, g, i, t:t + 1]).then_inc(maxed, 1)
                    dve.wait_ge(maxed, len(UNITS))
                    own(nc.vector.tensor_reduce(M[:, :, :], M2[:, :, :, :], AX.X, ALU.max))
                    own(nc.vector.tensor_scalar(MC[:, :, :], M[:, :, :], -1.0, SELF, ALU.mult, ALU.add))
            expand_maxima(k, M, NM, MB, QX)

            UNITS = [(g, j, t) for j in range(NT) for t in range(2) for g in range(HG)]
            with stage(nc, "sc_ready", "diag_done", "exp_done", "p_done", "pv_done", "own_d", "copied") as (block, sc_ready, diag_done, exp_done, p_done, pv_done, own_d, copied):
                diags = [u for u, (g, j, t) in enumerate(UNITS) if t == j // 4]

                @block.tensor
                def _(pe):
                    zero_bank(nc, k, 6)
                    zero_bank(nc, k, 7)

                    def pv(x):
                        pe.wait_ge(p_done, HG * (x + 1))
                        for u in range(HG * x, HG * x + HG):
                            g, j, t = UNITS[u]
                            nc.tensor.matmul(PS[32 * g:32 * g + 17, 6 + t, :], V1S[:, j, g, :], B[u % (2 * HG)], start=False, stop=(x >= 2 * NT - 2), skip_group_check=True).then_inc(pv_done, 1)

                    for u, (g, j, t) in enumerate(UNITS):
                        if u >= 3:
                            pe.wait_ge(p_done, u - 2)
                        nc.tensor.matmul(PS[:, 3 + u % 3, :], KH[:, g, blk(j, P)], QH[:, g, blk(t)], start=True, stop=True)
                        nc.tensor.matmul(PS[:, u % 3, :], KX[0:MAXROW + 3, g, blk(j, P)], QX[0:MAXROW + 3, g, blk(t)], start=True, stop=True).then_inc(sc_ready, 1)
                        if u % HG == HG - 1 and u > HG:
                            pv(u // HG - 1)
                    pv(2 * NT - 1)

                @block.scalar
                def _(act):
                    for u, (g, j, t) in enumerate(UNITS):
                        act.wait_ge(sc_ready, u + 1)
                        if u in diags:
                            act.wait_ge(diag_done, diags.index(u) + 1)
                        if u >= 3:
                            act.wait_ge(p_done, u - 2)
                        nc.scalar.activation(A[:, u % 3, :], PS[:, u % 3, :], ACT.Exp).then_inc(exp_done, 1)

                @block.vector
                def _(dve):
                    own = Link(dve, own_d)

                    def diag(u):
                        g, j, t = UNITS[u]
                        if u in diags:
                            dve.wait_ge(sc_ready, u + 1)
                            tile = PS[:, u % 3, blk(j % 4, P)]
                            own(nc.vector.tensor_tensor(tile, tile, NI[:, :], ALU.mult))
                            nc.vector.scalar_tensor_tensor(out=tile, in0=k.ident[:, :], scalar=MC[:, g, j:j + 1], in1=tile, op0=ALU.mult, op1=ALU.add).then_inc(diag_done, 1)
                    diag(0)
                    for u, (g, j, t) in enumerate(UNITS):
                        if u + 1 < len(UNITS):
                            diag(u + 1)
                        dve.wait_ge(exp_done, u + 1)
                        if u >= 2 * HG:
                            dve.wait_ge(pv_done, u - 2 * HG + 1)
                        nc.vector.scalar_tensor_tensor(out=B[u % (2 * HG)], in0=A[:, u % 3, :], scalar=3e38, in1=PS[:, 3 + u % 3, :], op0=ALU.min, op1=ALU.mult).then_inc(p_done, 1)
                    dve.wait_ge(pv_done, len(UNITS))
                    nc.vector.tensor_copy(OT, wide(6)).then_inc(copied, 1)
                    dve.wait_ge(copied, 1)

            with stage(nc, "den_ready", "rec_ready", "den_spread", "o_done", "y_ready", "own_d") as (block, den_ready, rec_ready, den_spread, o_done, y_ready, own_d):
                @block.tensor
                def _(pe):
                    for i in range(NT):
                        mm = nc.tensor.matmul(PS[:, 4, blk(i, HG)], OT[:, blk(i, P)], k.head_row[:, :], start=True, stop=True)
                    mm.then_inc(den_ready, 1)
                    pe.wait_ge(rec_ready, 1)
                    for i in range(NT):
                        for g in range(HG):
                            turned_spread(nc, PS[32 * g:32 * g + 32, i // 4, blk(i % 4, P)], RQ[:, i, g:g + 1].to_broadcast([P, 32]), k.ident[:, :]).then_inc(den_spread, 1)
                    for h in range(2):
                        pe.wait_ge(o_done, h + 1)
                        nc.tensor.matmul(PS[:, 2 + h, :], WS[:, 1, :], OT[:, blk(h)], start=True, stop=True).then_inc(y_ready, 1)

                @block.vector
                def _(dve):
                    own = Link(dve, own_d)
                    dve.wait_ge(den_ready, 1)
                    nc.vector.reciprocal(RQ[:, :, :], PS[:, 4, 0:NT * HG].rearrange("p (a b) -> p a b", b=HG)).then_inc(rec_ready, 1)
                    for h in range(2):
                        dve.wait_ge(den_spread, (h + 1) * HG * NT // 2)
                        nc.vector.tensor_tensor(OT[:, blk(h)], OT[:, blk(h)], PS[:, h, :], ALU.mult).then_inc(o_done, 1)
                    for h in range(2):
                        dve.wait_ge(y_ready, h + 1)
                        xb = k.X[:, bass.ds(tok + h * BLK, BLK)]
                        own(nc.vector.tensor_tensor(xb, xb, PS[:, 2 + h, :], ALU.add))

        with nc.Fori(0, BATCH) as b:
            with nc.Fori(0, 2) as r:
                body(b, r)
        with stage(nc, "bias_added") as (block, bias_added):
            @block.vector
            def _(dve):
                nc.vector.tensor_scalar(k.X[:, :], k.X[:, :], W[pre + "b_out"], None, ALU.add).then_inc(bias_added, 1)
                dve.wait_ge(bias_added, 1)



SMALL_W = {
    "L0a": {
        "L0_attn_a_Wq": [P, P], "L0_attn_a_Wk": [P, P], "L0_attn_a_Wv": [P, P], "L0_attn_a_Wo": [P, P], "L0_attn_a_Wb": [P, 4],
        "L0_attn_a_conv": [P, 3, 4], "L0_attn_a_fir_s": [P, 5], "L0_attn_a_fir_l": [P, 64], "L0_attn_a_W1x": [P, P], "L0_attn_a_W1s": [P, 4, P],
        "L0_attn_a_b1": [P, 1], "L0_attn_a_W2": [P, 4], "L0_attn_a_b2": [P, 4], "L0_attn_a_copy_bias": [P, 4], "L0_attn_a_log_temp": [P, 4],
        "L0_attn_a_o_norm_w": [P, 1],
    },
    "L0": {
        "L0_ffn_ln_g": [P, 1], "L0_ffn_ln_b": [P, 1], "L0_ffn_abel_w": [P, P], "L0_ffn_abel_b": [P, 1], "L0_ffn_gate_w_moe": [P, 8],
        "L0_ffn_gate_b_moe": [P, 8], "L0_ffn_b1": [P, 8, 4], "L0_ffn_b2": [P, 8], "L0_ffn_mix_w": [P, 2], "L0_ffn_mix_b": [P, 1],
        "L0_ffn_gens": [P, 2, 3, P], "L0_attn_b_W_in": [P, 512], "L0_attn_b_conv_w": [P, 2, 4], "L0_attn_b_conv_b": [P, 2],
        "L0_attn_b_W_x": [P, 2, 40], "L0_attn_b_W_dt": [8, 256], "L0_attn_b_b_dt": [P, 2], "L0_attn_b_A_log": [P, 2, 16], "L0_attn_b_D": [P, 2],
        "L0_attn_b_W_out": [P, 2, P],
    },
    "L1": {
        "L1_ffn_w1_s": [P, 4], "L1_ffn_w2_s": [P, 4], "L1_ffn_h1_s": [P, 4], "L1_ffn_h2_s": [P, 4], "L1_ffn_w3_s": [P, 1], "L1_attn_a_WqP": [P, 4, P],
        "L1_attn_a_WkP": [P, 4, P], "L1_attn_a_WoP": [P, 4, P], "L1_attn_a_Wv": [P, P], "L1_attn_b_w_qk": [P, P], "L1_attn_b_w_v": [P, P],
        "L1_attn_b_rot": [P, 32], "L1_attn_b_WqkP": [P, 2, P], "L1_attn_b_WoP": [P, 2, P], "L1_attn_b_b_out": [P, 1],
    },
    "L2": {
        "L2_ffn_router_w": [P, 16], "L2_attn_b_WQ": [P, P], "L2_attn_b_WK": [P, P], "L2_attn_b_WV": [P, P], "L2_attn_a_mu0": [P, 1],
        "L2_attn_a_W_x0": [P, 160], "L2_attn_a_W_x2a": [P, P], "L2_attn_a_W_x2b": [32, P], "L2_attn_a_x_bias": [P, 5], "L2_attn_a_W_r": [P, 64],
        "L2_attn_a_W_w1": [P, 64], "L2_attn_a_W_w2": [64, 64], "L2_attn_a_b_w2": [64, 1], "L2_attn_a_W_k": [P, 64], "L2_attn_a_W_v": [P, P],
        "L2_attn_a_W_g": [P, P], "L2_attn_a_bonus": [64, 1], "L2_attn_a_gn_weight": [P, 1], "L2_attn_a_gn_bias": [P, 1], "L2_attn_a_W_o": [P, P],
    },
    "L3": {
        "L3_ffn_Wg": [P, 8], "L3_ffn_b1": [P, 8, 4], "L3_ffn_b2": [P, 8], "L3_attn_b_WqP": [P, 4, P], "L3_attn_b_WkP": [P, 4, P],
        "L3_attn_b_WoP": [P, 4, P], "L3_attn_b_Wv": [P, P], "L3_attn_b_bqP": [P, 4], "L3_attn_b_bkP": [P, 4], "L3_attn_b_bv": [P, P],
        "L3_attn_b_bo": [P, 1], "L3_attn_a_Wq": [P, P],
    },
}
FFN_W = {
    "L0": {"L0_ffn_w1": [P, 8, 512], "L0_ffn_w2": [P, 8, 4, P]},
    "L1": {"L1_ffn_w1": [P, 512], "L1_ffn_w2": [P, 512], "L1_ffn_h1": [P, 4, 512], "L1_ffn_h2": [P, 4, 512], "L1_ffn_w3": [P, 4, P]},
    "L2": {"L2_ffn_wg_r": [P, 512], "L2_ffn_wu_r": [P, 512], "L2_ffn_wd_r": [P, 4, P],
           "L2_ffn_wg_s": [P, P], "L2_ffn_wu_s": [P, P], "L2_ffn_wd_s": [P, P]},
    "L3": {"L3_ffn_W1": [P, 8, 512], "L3_ffn_W2": [P, 8, 4, P]},
}


def columns(shape):
    return int(np.prod(shape[1:]))


def pack_columns(group):
    return sum(columns(shape) for shape in group.values())


LOAD_PARTS = 4
FFN_COLS = max(pack_columns(group) for group in FFN_W.values())


def weight_views(k, place, group):
    at = 0
    for name, shape in group.items():
        ap = place[0:shape[0], at:at + columns(shape)]
        if len(shape) == 3:
            ap = ap.rearrange("p (a b) -> p a b", a=shape[1])
        if len(shape) == 4:
            ap = ap.rearrange("p (a b c) -> p a b c", a=shape[1], b=shape[2])
        k.W[name] = ap
        at += columns(shape)



def load_ffn(k, layer):
    nc, n = k.nc, pack_columns(FFN_W[layer])
    with stage(nc) as (block,):
        @block.sync
        def _(sp):
            for c in range(LOAD_PARTS):
                part = slice(c * n // LOAD_PARTS, (c + 1) * n // LOAD_PARTS)
                sp.dma_start(k.ffn_place[:, part], k.ins["ffn_" + layer][:, part]).then_inc(k.ffn_loaded, 16)
    k.ffn_count += 16 * LOAD_PARTS
    weight_views(k, k.ffn_place, FFN_W[layer])


def await_loads(k, sem, count):
    with stage(k.nc) as (block,):
        @block.sync
        def _(sp):
            sp.wait_ge(sem, count)


def constants(k, st):
    nc = k.nc

    def sb(n, shape, dt=F32):
        return k.sbuf(st, n, shape, dt)
    k.ident = sb("ident", [P, P])
    k.mean_mat = sb("mean_mat", [P, P])
    k.eps_col = sb("eps_col", [P, 1])
    k.rstd = sb("rstd", [P, NTILE])
    k.iota_row = sb("iota_row", [P, 16])
    k.sel8 = sb("sel8", [8, 8, P])
    k.sel16 = sb("sel16", [16, 4, P])
    k.rot = sb("rot", [P, P])
    k.mixm = sb("mixm", [P, 2, P])
    k.more = []
    k.zeros16 = sb("zeros16", [P, BLK], BF16)
    k.first_col = sb("first_col", [P, 1])
    k.head_row = sb("head_row", [P, 4])

    def attention_constants(pool, own):
        own(pool.memset(k.zeros16[:, :], 0.0))
        own(pool.memset(k.identb[:, :], 0.0))
        own(pool.affine_select(out=k.identb[:, :], in_=k.identb[:, :], compare_op=ALU.not_equal, fill=1.0, base=0, pattern=[[-1, P]], channel_multiplier=1))
        own(pool.memset(k.first_col[:, :], 0.0))
        own(pool.memset(k.head_row[:, :], 0.0))
        own(pool.affine_select(out=k.head_row[:, :], in_=k.head_row[:, :], compare_op=ALU.not_equal, fill=1.0, base=0, pattern=[[-32, 4]], channel_multiplier=1))
        for g in range(4):
            own(pool.affine_select(out=k.first_col[:, :], in_=k.first_col[:, :], compare_op=ALU.not_equal, fill=1.0, base=-32 * g, pattern=[[0, 1]], channel_multiplier=1))
    k.more.append(attention_constants)
    k.identb = sb("identb", [P, P], BF16)
    with stage(nc, "own_p") as (block, own_p):
        @block.gpsimd
        def _(pool):
            own = Link(pool, own_p)
            own(pool.memset(k.ident[:, :], 0.0))
            own(pool.affine_select(out=k.ident[:, :], in_=k.ident[:, :], compare_op=ALU.not_equal, fill=1.0, base=0, pattern=[[-1, P]], channel_multiplier=1))
            own(pool.memset(k.mean_mat[:, :], 1.0 / D))
            own(pool.memset(k.eps_col[:, :], EPS))
            own(pool.iota(k.iota_row[:, :], [[1, 16]], base=0, channel_multiplier=0, allow_small_or_imprecise_dtypes=True))
            own(pool.memset(k.sel8[:, :, :], 0.0))
            own(pool.affine_select(out=k.sel8[:, :, :], in_=k.sel8[:, :, :], compare_op=ALU.not_equal, fill=1.0, base=0, pattern=[[-1, 8], [0, P]], channel_multiplier=1))
            own(pool.memset(k.sel16[:, :, :], 0.0))
            own(pool.affine_select(out=k.sel16[:, :, :].rearrange("e c (q r) -> e c q r", r=32), in_=k.sel16[:, :, :].rearrange("e c (q r) -> e c q r", r=32),
                                   compare_op=ALU.not_equal, fill=1.0, base=0, pattern=[[-4, 4], [-1, 4], [0, 32]], channel_multiplier=1))
            for f in k.more:
                f(pool, own)


SUBLAYERS = ["l0a", "l0_ffn", "l0b", "l0_ffn", "l1a", "l1_ffn", "l1b", "l1_ffn",
             "l2a", "l2_ffn", "l2b", "l2_ffn", "l3a", "l3_ffn", "l3b", "l3_ffn"]


def program(nc, ins, out, first=0, last=16):
    k = Core(nc)
    k.ins, k.ffn_count = ins, 0
    run = {"l0a": l0a, "l0b": l0b, "l1a": l1a, "l1b": l1b, "l2a": l2a, "l2b": l2b, "l3a": l3a, "l3b": l3b,
           "l0_ffn": l0_ffn, "l1_ffn": l1_ffn, "l2_ffn": l2_ffn, "l3_ffn": l3_ffn}
    with ExitStack() as st:
        k.X = k.sbuf(st, "X", [P, NTOK])
        k.XN = k.sbuf(st, "XN", [P, NTOK])
        k.lnA = k.sbuf(st, "lnA", [P, NTOK])
        k.ffn_place = k.sbuf(st, "ffn_place", [P, FFN_COLS])
        k.PS = st.enter_context(nc.psum_tensor("PS", [P, 8, BLK], F32))
        k.ffn_loaded = st.enter_context(nc.semaphore("ffn_loaded"))
        small_loaded = st.enter_context(nc.semaphore("small_loaded"))
        places = {g: k.sbuf(st, "small_" + g, [P, pack_columns(group)]) for g, group in SMALL_W.items()}
        with stage(nc) as (block,):
            @block.sync
            def _(sp):
                for b in range(NBLK):
                    sp.dma_start(k.X[:, blk(b)], ins["x"][:, blk(b)]).then_inc(small_loaded, 16)
                for g in SMALL_W:
                    sp.dma_start(places[g][:, :], ins["small_" + g]).then_inc(small_loaded, 16)
        for g, group in SMALL_W.items():
            weight_views(k, places[g], group)
        load_ffn(k, SUBLAYERS[first | 1][0:2].upper())
        constants(k, st)
        await_loads(k, small_loaded, 16 * (NBLK + len(SMALL_W)))
        if first <= 3 and last > 1:
            expm_product(k)
        for i in range(first, last):
            name = SUBLAYERS[i]
            if name.endswith("ffn"):
                await_loads(k, k.ffn_loaded, k.ffn_count)
            with ExitStack() as layer:
                if name.endswith("ffn"):
                    k.gT = k.sbuf(layer, "gates", [16, NTOK])
                run[name](k)
            if name.endswith("ffn") and i + 2 < last and SUBLAYERS[i + 2] != name:
                load_ffn(k, SUBLAYERS[i + 2][0:2].upper())
        with stage(nc, "stored") as (block, stored):
            @block.sync
            def _(sp):
                for b in range(NBLK):
                    sp.dma_start(out[:, blk(b)], k.X[:, blk(b)]).then_inc(stored, 16)
                sp.wait_ge(stored, 16 * NBLK)


def layout(inputs):
    i = {n: np.asarray(a) for n, a in inputs.items()}

    def col(a, c=1):
        return a.reshape(c, P).T
    r = {"x": i["L0_attn_a_hidden_states"].reshape(NTOK, D).T}
    for n in ("L0_ffn_ln_g", "L0_ffn_ln_b", "L0_ffn_abel_b", "L1_ffn_w3_s"):
        r[n] = col(i[n])
    for n in ("L0_ffn_abel_w", "L0_ffn_gate_w_moe", "L3_ffn_Wg", "L2_ffn_router_w"):
        r[n] = i[n]
    r["L0_ffn_gate_b_moe"] = i["L0_ffn_gate_b_moe"].reshape(1, 8)
    r["L0_ffn_mix_b"] = i["L0_ffn_mix_b"].reshape(1, 1)
    r["L0_ffn_mix_w"] = i["L0_ffn_mix_w"].reshape(2, P).T
    g = i["L0_ffn_gens"]
    r["L0_ffn_gens"] = np.stack([g.transpose(1, 0, 2), g.transpose(2, 0, 1)], axis=1)
    for a, w1, w2 in (("L0_ffn_", "w1", "w2"), ("L3_ffn_", "W1", "W2")):
        r[a + w1] = i[a + w1].transpose(1, 0, 2).reshape(P, -1)
        r[a + w2] = i[a + w2].reshape(8, 4, P, D).transpose(2, 0, 1, 3).reshape(P, -1)
        r[a + "b1"] = i[a + "b1"].reshape(8, 4, P).transpose(2, 0, 1)
        r[a + "b2"] = i[a + "b2"].T
    for n in ("w1", "w2"):
        r["L1_ffn_" + n] = i[f"L1_ffn_{n}_w"].T
    for n in ("h1", "h2", "w3"):
        w = i[f"L1_ffn_{n}_w"]
        r["L1_ffn_" + n] = w.T.reshape(4, P, w.shape[0]).transpose(1, 0, 2).reshape(P, -1)
    for n in ("w1", "w2", "h1", "h2"):
        r[f"L1_ffn_{n}_s"] = col(i[f"L1_ffn_{n}_s"], 4)
    for n in ("wg_r", "wu_r", "wg_s", "wu_s"):
        r["L2_ffn_" + n] = i["L2_ffn_" + n].transpose(1, 0, 2).reshape(P, -1)
    r["L2_ffn_wd_r"] = i["L2_ffn_wd_r"].reshape(4, P, D).transpose(1, 0, 2).reshape(P, -1)
    r["L2_ffn_wd_s"] = i["L2_ffn_wd_s"].reshape(P, D)
    def padded(a):
        o = np.zeros(a.shape[:-1] + (4, 4, 32), a.dtype)
        o[..., 1:9] = a.reshape(a.shape[:-1] + (4, 4, 8))
        return o.reshape(a.shape[:-1] + (4, P))
    for a in ("L1_attn_a_", "L3_attn_b_"):
        r[a + "WqP"], r[a + "WkP"] = padded(i[a + "Wq"].T), padded(i[a + "Wk"].T)
        r[a + "WoP"] = padded(i[a + "Wo"]).transpose(2, 1, 0)
        r[a + "Wv"] = i[a + "Wv"].T
    r["L3_attn_b_bqP"], r["L3_attn_b_bkP"] = padded(i["L3_attn_b_bq"]).T, padded(i["L3_attn_b_bk"]).T
    r["L3_attn_b_bv"] = i["L3_attn_b_bv"].reshape(1, P)
    r["L3_attn_b_bo"] = col(i["L3_attn_b_bo"])
    for n in ("WQ", "WK", "WV"):
        r["L2_attn_b_" + n] = i["L2_attn_b_" + n].T
    r["L3_attn_a_Wq"] = i["L3_attn_a_queries_weight"]
    for n in ("conv_w", "A_log"):
        r["L0_attn_b_" + n] = i["L0_attn_b_" + n].reshape(2, P, -1).transpose(1, 0, 2)
    r["L0_attn_b_W_in"] = i["L0_attn_b_W_in"].T
    for n in ("conv_b", "b_dt", "D"):
        r["L0_attn_b_" + n] = col(i["L0_attn_b_" + n], 2)
    r["L0_attn_b_W_x"] = i["L0_attn_b_W_x"].T.reshape(2, P, 40).transpose(1, 0, 2)
    r["L0_attn_b_W_dt"] = i["L0_attn_b_W_dt"].T
    r["L0_attn_b_W_out"] = i["L0_attn_b_W_out"].T.reshape(2, P, P).transpose(1, 0, 2)
    for n in ("W_x0", "W_r", "W_w1", "W_w2", "W_k", "W_v", "W_g", "W_o", "x_bias"):
        r["L2_attn_a_" + n] = i["L2_attn_a_" + n].T
    r["L2_attn_a_W_x2a"], r["L2_attn_a_W_x2b"] = i["L2_attn_a_W_x2"].T[:P], i["L2_attn_a_W_x2"].T[P:]
    for n in ("mu0", "b_w2", "bonus", "gn_weight", "gn_bias"):
        r["L2_attn_a_" + n] = i["L2_attn_a_" + n].reshape(-1, 1)
    a = "L0_attn_a_"
    for n in ("Wq", "Wk", "Wv", "Wo", "Wb"):
        r[a + n] = i[a + n].T
    r[a + "conv"] = np.stack([i[a + f"conv_{n}_w"] for n in "qkv"], axis=1)
    r[a + "fir_s"], r[a + "fir_l"] = i[a + "fir_short_filt"].reshape(P, 5), i[a + "fir_long_filt"].reshape(P, 64)
    w1 = i[a + "gate_W1"].T
    r[a + "W1x"] = w1[:P]
    w1s = np.zeros((4, 32, 4, P), w1.dtype)
    for h in range(4):
        w1s[:, 4 * h:4 * h + 4, h] = w1[P:].reshape(4, 4, P).transpose(1, 0, 2)
    r[a + "W1s"] = w1s.reshape(P, 4, P)
    r[a + "b1"], r[a + "W2"] = i[a + "gate_b1"].reshape(P, 1), i[a + "gate_W2"].T
    r[a + "b2"] = i[a + "gate_b2"].reshape(1, 4)
    r[a + "copy_bias"], r[a + "log_temp"] = i[a + "gate_copy_bias"].reshape(1, 4), i[a + "gate_log_temp"].reshape(1, 4)
    r[a + "o_norm_w"] = np.broadcast_to(i[a + "o_norm_w"], (4, 32)).reshape(P, 1)
    def padded16(a):
        o = np.zeros(a.shape[:-1] + (2, 4, 32), a.dtype)
        o[..., 1:17] = a.reshape(a.shape[:-1] + (2, 4, 16))
        return o.reshape(a.shape[:-1] + (2, P))
    a = "L1_attn_b_"
    r[a + "w_qk"], r[a + "w_v"] = i[a + "w_qk"], i[a + "w_v"]
    r[a + "rot"] = np.broadcast_to(i[a + "rotations"].reshape(16, 32), (8, 16, 32)).reshape(P, 32)
    r[a + "WqkP"], r[a + "WoP"] = padded16(i[a + "w_qk"]), padded16(i[a + "w_out"].T).transpose(2, 1, 0)
    r[a + "b_out"] = col(i[a + "b_out"])
    def pack(group):
        o = np.zeros((P, pack_columns(group)), np.float32)
        at = 0
        for name, shape in group.items():
            a = np.asarray(r[name]).reshape(len(r[name]), columns(shape))
            o[0:shape[0], at:at + columns(shape)] = a
            at += columns(shape)
        return o
    packed = {"x": np.ascontiguousarray(r["x"])}
    packed.update({"small_" + g: pack(group) for g, group in SMALL_W.items()})
    packed.update({"ffn_" + g: pack(group) for g, group in FFN_W.items()})
    return packed


def kernel(**inputs):
    import concourse.bacc as bacc
    from concourse.bass_utils import run_bass_kernel_spmd

    arrays = layout(inputs)
    nc = bacc.Bacc("TRN2", target_bir_lowering=False, num_devices=1)
    ins = {n: nc.dram_tensor(f"in_{n}", a.shape, F32, kind="ExternalInput").ap() for n, a in arrays.items()}
    out = nc.dram_tensor("out_x", (D, NTOK), F32, kind="ExternalOutput").ap()
    program(nc, ins, out)
    r = run_bass_kernel_spmd(nc, [{f"in_{n}": a for n, a in arrays.items()}], core_ids=[0])
    return np.ascontiguousarray(r.results[0]["out_x"].T).reshape(BATCH, SEQ, D)
```

```python
from contextlib import ExitStack, contextmanager

import numpy as np
import concourse.bass as bass
from concourse import mybir

F32 = mybir.dt.float32
BF16 = mybir.dt.bfloat16
U32 = mybir.dt.uint32
ALU = mybir.AluOpType
ACT = mybir.ActivationFunctionType
AX = mybir.AxisListType

P = 128
D = 128
BATCH = 2
SEQ = 1024
NTOK = BATCH * SEQ
BLK = 512
NBLK = NTOK // BLK
NTILE = NTOK // P
EPS = 1e-5
STAGE_SEMS = 220


class Link:

    def __init__(self, eng, sem):
        self.eng, self.sem, self.n = eng, sem, 0

    def __call__(self, ins):
        self.n += 1
        ins.then_inc(self.sem, 1)
        self.eng.wait_ge(self.sem, self.n)


class Programs:

    def __init__(self, nc):
        self.nc = nc

    def tensor(self, program):
        program(self.nc.tensor)

    def vector(self, program):
        program(self.nc.vector)

    def scalar(self, program):
        program(self.nc.scalar)

    def gpsimd(self, program):
        program(self.nc.gpsimd)

    def sync(self, program):
        program(self.nc.sync)


@contextmanager
def stage(nc, *names):
    with ExitStack() as st:
        sems = [st.enter_context(nc.semaphore(n, num=STAGE_SEMS + i)) for i, n in enumerate(names)]
        yield (Programs(nc), *sems)
        if sems:
            nc.all_engine_barrier(sems_to_clear=range(STAGE_SEMS, STAGE_SEMS + len(sems)))
        else:
            nc.all_engine_barrier()


def blk(i, n=BLK):
    return slice(i * n, (i + 1) * n)


class Core:

    def __init__(self, nc):
        self.nc, self.W, self.buffers = nc, {}, 0

    def sbuf(self, scope, name, shape, dt=F32):
        self.buffers += 1
        return scope.enter_context(self.nc.sbuf_tensor(f"{name}_{self.buffers}", shape, dt))


def turned_spread(nc, out, cols, ident):
    return nc.tensor.matmul(out, cols, ident, start=True, stop=True)


def layernorm(k, src, dst, gain=None, shift=None, beside=None):
    nc, PS = k.nc, k.PS
    sq, rstd = k.lnA, k.rstd
    TB = BLK // P
    with stage(nc, "mean_ready", "centered", "squared", "var_ready", "std_ready", "rstd_ready", "spread_ready", "dve_own", "pool_own") as (block, mean_ready, centered, squared, var_ready, std_ready, rstd_ready, spread_ready, dve_own, pool_own):
        if beside is not None:
            @block.gpsimd
            def _(pool):
                beside(pool, Link(pool, pool_own))

        @block.tensor
        def _(pe):
            for b in range(NBLK):
                nc.tensor.matmul(PS[:, b, :], k.mean_mat[:, :], src[:, blk(b)], start=True, stop=True).then_inc(mean_ready, 1)
            for b in range(NBLK):
                pe.wait_ge(squared, b + 1)
                for t in range(TB * b, TB * b + TB):
                    mm = nc.tensor.matmul(PS[:, 4, t:t + 1], sq[:, blk(t, P)], k.mean_mat[:, 0:1], start=True, stop=True)
            mm.then_inc(var_ready, 1)
            pe.wait_ge(rstd_ready, 1)
            pe.wait_ge(centered, 1)
            for b in range(NBLK):
                for t in range(TB * b, TB * b + TB):
                    mm = turned_spread(nc, PS[:, (5 + b) % 8, blk(t % TB, P)], rstd[:, t:t + 1].to_broadcast([P, P]), k.ident[:, :])
                mm.then_inc(spread_ready, 1)

        @block.scalar
        def _(act):
            for b in range(NBLK):
                act.wait_ge(centered, b + 1)
                nc.scalar.activation(sq[:, blk(b)], dst[:, blk(b)], ACT.Square).then_inc(squared, 1)
            act.wait_ge(var_ready, 1)
            nc.scalar.activation(rstd[:, :], PS[:, 4, 0:NTILE], ACT.Sqrt, bias=k.eps_col[:, 0:1]).then_inc(std_ready, 1)

        @block.vector
        def _(dve):
            own = Link(dve, dve_own)
            for b in range(NBLK):
                dve.wait_ge(mean_ready, b + 1)
                nc.vector.tensor_tensor(dst[:, blk(b)], src[:, blk(b)], PS[:, b, :], ALU.subtract).then_inc(centered, 1)
            dve.wait_ge(std_ready, 1)
            nc.vector.reciprocal(rstd[:, :], rstd[:, :]).then_inc(rstd_ready, 1)
            dve.wait_ge(centered, NBLK)
            for b in range(NBLK):
                dve.wait_ge(spread_ready, b + 1)
                own(nc.vector.tensor_tensor(dst[:, blk(b)], dst[:, blk(b)], PS[:, (5 + b) % 8, :], ALU.mult))
                if gain is not None:
                    own(nc.vector.tensor_scalar(dst[:, blk(b)], dst[:, blk(b)], gain, shift, ALU.mult, ALU.add))



CAP = 256


def route_top2(k, E, router, bias_row, mode, gT, slots=None):
    nc = k.nc
    with ExitStack() as st:
        def sb(n, shape, dt=F32):
            return k.sbuf(st, n, shape, dt)
        L = sb("rt_logits", [P, NTILE, E])
        EX = sb("rt_exp", [P, NTILE, E])
        V8 = sb("rt_v8", [P, NTILE, 8])
        I8 = sb("rt_i8", [P, NTILE, 8], U32)
        IF = sb("rt_if", [P, NTILE, 2])
        SC = sb("rt_sc", [P, 8, NTILE])
        OH = sb("rt_oh", [P, 4, NTILE, E])
        kinds = 4 if mode == "capacity" else 1
        T = sb("rt_T", [E, 3, NTOK]) if mode == "capacity" else None
        one = sb("rt_one", [P, 2])
        with stage(nc, "logits_ready", "shifted", "exp_done", "oh_done", "turned", "copied", "own_d") as (block, logits_ready, shifted, exp_done, oh_done, turned, copied, own_d):
            @block.tensor
            def _(pe):
                for t in range(NTILE):
                    mm = nc.tensor.matmul(k.PS[:, 0, t * E:(t + 1) * E], k.XN[:, blk(t, P)], router, start=True, stop=True)
                mm.then_inc(logits_ready, 1)
                pe.wait_ge(oh_done, 1)
                for q in range(kinds):
                    for b in range(NBLK):
                        if q:
                            pe.wait_ge(copied, (q - 1) * NBLK + b + 1)
                        for j in range(BLK // P):
                            mm = nc.tensor.transpose(k.PS[0:E, 1 + b, blk(j, P)], OH[:, q, 4 * b + j, :], k.ident[:, :])
                        mm.then_inc(turned, 1)

            @block.scalar
            def _(act):
                act.wait_ge(shifted, 1)
                if mode == "softmax2":
                    nc.scalar.activation(SC[:, 3, :], SC[:, 0, :], ACT.Sigmoid)
                    nc.scalar.activation(SC[:, 2, :], SC[:, 0, :], ACT.Sigmoid, scale=-1.0).then_inc(exp_done, 1)
                else:
                    nc.scalar.activation(SC[:, 1, :], SC[:, 0, :], ACT.Exp)
                    nc.scalar.activation(EX[:, :, :], EX[:, :, :], ACT.Exp).then_inc(exp_done, 1)

            @block.vector
            def _(dve):
                own = Link(dve, own_d)
                dve.wait_ge(logits_ready, 1)
                own(nc.vector.memset(one[:, :], 1.0))
                lp = k.PS[:, 0, 0:NTILE * E].rearrange("p (t e) -> p t e", e=E)
                if bias_row is not None:
                    own(nc.vector.tensor_tensor(L[:, :, :], lp, bias_row.unsqueeze(1).to_broadcast([P, NTILE, E]), ALU.add))
                else:
                    own(nc.vector.tensor_copy(L[:, :, :], lp))
                for t in range(NTILE):
                    m = nc.vector.max(V8[:, t, :], L[:, t, :])
                own(m)
                for t in range(NTILE):
                    m = nc.vector.max_index(I8[:, t, :], V8[:, t, :], L[:, t, :])
                own(m)
                if mode != "softmax2":
                    own(nc.vector.tensor_tensor(EX[:, :, :], L[:, :, :], V8[:, :, 0:1].to_broadcast([P, NTILE, E]), ALU.subtract))
                nc.vector.tensor_tensor(SC[:, 0, :], V8[:, :, 1], V8[:, :, 0], ALU.subtract).then_inc(shifted, 1)
                own(nc.vector.tensor_copy(IF[:, :, :], I8[:, :, 0:2]))
                io = k.iota_row[:, 0:E].unsqueeze(1).to_broadcast([P, NTILE, E])
                for q in range(2):
                    own(nc.vector.tensor_tensor(OH[:, q, :, :], io, IF[:, :, q:q + 1].to_broadcast([P, NTILE, E]), ALU.is_equal))
                dve.wait_ge(exp_done, 1)
                if mode != "softmax2":
                    own(nc.vector.tensor_reduce(SC[:, 4, :], EX[:, :, :], AX.X, ALU.add))
                    own(nc.vector.reciprocal(SC[:, 2, :], SC[:, 4, :]))
                    own(nc.vector.tensor_tensor(SC[:, 3, :], SC[:, 1, :], SC[:, 2, :], ALU.mult))
                    own(nc.vector.tensor_tensor(SC[:, 5, :], SC[:, 2, :], SC[:, 3, :], ALU.add))
                    own(nc.vector.tensor_scalar(SC[:, 5, :], SC[:, 5, :], 1e-9, None, ALU.add))
                    own(nc.vector.reciprocal(SC[:, 6, :], SC[:, 5, :]))
                    own(nc.vector.tensor_tensor(SC[:, 2, :], SC[:, 2, :], SC[:, 6, :], ALU.mult))
                    own(nc.vector.tensor_tensor(SC[:, 3, :], SC[:, 3, :], SC[:, 6, :], ALU.mult))
                for q in range(2):
                    own(nc.vector.tensor_tensor(OH[:, 2 + q, :, :], OH[:, q, :, :], SC[:, 2 + q, :].unsqueeze(2).to_broadcast([P, NTILE, E]), ALU.mult))
                if mode != "capacity":
                    own(nc.vector.tensor_tensor(OH[:, 0, :, :], OH[:, 2, :, :], OH[:, 3, :, :], ALU.add))
                nc.vector.memset(one[:, 0:1], 1.0).then_inc(oh_done, 1)
                for q in range(kinds):
                    for b in range(NBLK):
                        dve.wait_ge(turned, q * NBLK + b + 1)
                        dst = T[:, q, blk(b)] if q < kinds - 1 else gT[0:E, blk(b)]
                        nc.vector.tensor_copy(dst, k.PS[0:E, 1 + b, :]).then_inc(copied, 1)
                dve.wait_ge(copied, kinds * NBLK)
                if mode == "capacity":
                    seen = k.lnA[0:E, :]
                    cnt = SC[0:E, 7, 0:1]
                    ones = one[0:E, 0:1].to_broadcast([E, NTOK])
                    own(nc.vector.tensor_tensor_scan(seen, ones, T[:, 0, :], 0.0, ALU.mult, ALU.add))
                    own(nc.vector.tensor_scalar(cnt, seen[:, NTOK - 1:NTOK], float(CAP), None, ALU.min))
                    own(nc.vector.scalar_tensor_tensor(out=T[:, 2, :], in0=seen, scalar=float(CAP), in1=T[:, 2, :], op0=ALU.is_le, op1=ALU.mult))
                    own(nc.vector.scalar_tensor_tensor(out=T[:, 0, :], in0=seen, scalar=float(CAP), in1=T[:, 0, :], op0=ALU.is_le, op1=ALU.mult))
                    own(nc.vector.tensor_tensor(slots, seen, T[:, 0, :], ALU.mult))
                    own(nc.vector.tensor_tensor_scan(seen, ones, T[:, 1, :], cnt, ALU.mult, ALU.add))
                    own(nc.vector.scalar_tensor_tensor(out=gT[0:E, :], in0=seen, scalar=float(CAP), in1=gT[0:E, :], op0=ALU.is_le, op1=ALU.mult))
                    own(nc.vector.scalar_tensor_tensor(out=T[:, 1, :], in0=seen, scalar=float(CAP), in1=T[:, 1, :], op0=ALU.is_le, op1=ALU.mult))
                    own(nc.vector.tensor_tensor(T[:, 1, :], seen, T[:, 1, :], ALU.mult))
                    own(nc.vector.tensor_tensor(slots, slots, T[:, 1, :], ALU.add))
                    own(nc.vector.tensor_tensor(gT[0:E, :], gT[0:E, :], T[:, 2, :], ALU.add))


def experts(k, w1, b1, w2, b2, gT, func, acc, H, gb, tmp, tb):
    nc, PS = k.nc, k.PS
    E, C = 8, 4
    with stage(nc, "gate_spread", "gate_copied", "hid_ready", "hid_done", "out_ready", "out_used", "own_d") as (block, gate_spread, gate_copied, hid_ready, hid_done, out_ready, out_used, own_d):
        @block.tensor
        def _(pe):
            def hidden(e):
                if e >= 2:
                    pe.wait_ge(gate_copied, e - 1)
                nc.tensor.matmul(PS[:, 6 + e % 2, :], k.sel8[:, e, :], gT[0:E, bass.ds(tb, BLK)], start=True, stop=True).then_inc(gate_spread, 1)
                for c in range(C):
                    if e:
                        pe.wait_ge(hid_done, C * (e - 1) + c + 1)
                    nc.tensor.matmul(PS[:, c, :], w1[:, e, blk(c, P)], k.XN[:, bass.ds(tb, BLK)], start=True, stop=True).then_inc(hid_ready, 1)

            def out(e):
                if e >= 2:
                    pe.wait_ge(out_used, e - 1)
                for c in range(C):
                    pe.wait_ge(hid_done, C * e + c + 1)
                    mm = nc.tensor.matmul(PS[:, 4 + e % 2, :], w2[:, e, c, :], H[:, e % 2, c, :], start=(c == 0), stop=(c == C - 1))
                mm.then_inc(out_ready, 1)

            hidden(0)
            for e in range(1, E):
                hidden(e)
                out(e - 1)
            out(E - 1)

        @block.scalar
        def _(act):
            for e in range(E):
                act.wait_ge(gate_spread, e + 1)
                if e >= 2:
                    act.wait_ge(out_used, e - 1)
                nc.scalar.activation(gb[:, e % 2, :], PS[:, 6 + e % 2, :], ACT.Identity).then_inc(gate_copied, 1)
                if e >= 2:
                    act.wait_ge(out_ready, e - 1)
                for c in range(C):
                    act.wait_ge(hid_ready, C * e + c + 1)
                    nc.scalar.activation(H[:, e % 2, c, :], PS[:, c, :], func, bias=b1[:, e, c:c + 1]).then_inc(hid_done, 1)

        @block.vector
        def _(dve):
            own = Link(dve, own_d)
            for e in range(E):
                dve.wait_ge(out_ready, e + 1)
                dve.wait_ge(gate_copied, e + 1)
                dst = acc if e == 0 else tmp
                nc.vector.scalar_tensor_tensor(out=dst, in0=PS[:, 4 + e % 2, :], scalar=b2[:, e:e + 1], in1=gb[:, e % 2, :], op0=ALU.add, op1=ALU.mult).then_inc(out_used, 1)
                dve.wait_ge(out_used, e + 1)
                if e:
                    own(nc.vector.tensor_tensor(acc, acc, tmp, ALU.add))


def expert_buffers(k, st):
    def sb(n, shape):
        return k.sbuf(st, n, shape, F32)
    return sb("moe_H", [P, 2, 4, BLK]), sb("moe_gb", [P, 2, BLK]), sb("moe_tmp", [P, BLK]), sb("moe_acc", [P, BLK])


def l3_ffn(k):
    nc, PS, W = k.nc, k.PS, k.W
    E, C, ST = 8, 4, CAP // P
    with ExitStack() as st:
        def sb(n, shape, dt=F32):
            return k.sbuf(st, n, shape, dt)
        slots, slots16 = sb("sp_slots", [E, NTOK]), sb("sp_slots16", [E, NTOK], BF16)
        XP = sb("sp_xp", [P, 3, NTILE, D], BF16)
        SLC, GC = sb("sp_slc", [P, NTILE, E]), sb("sp_gc", [P, NTILE, E])
        GP = sb("sp_gp", [P, NTILE, E, 3], BF16)
        SEL = sb("sp_sel", [E, E, P], BF16)
        PLACE_ROW, PLACE_COL = sb("sp_row", [P, CAP]), sb("sp_col", [P, ST])
        GATHER = sb("sp_gather", [P, 2, NTILE, CAP], BF16)
        SCATTER = sb("sp_scatter", [P, 2, ST, NTOK], BF16)
        XG, H = sb("sp_xg", [P, CAP]), sb("sp_h", [P, C, CAP])
        Y, YP, GS = sb("sp_y", [P, ST, D]), sb("sp_yp", [P, 3, ST, D], BF16), sb("sp_gs", [P, ST])
        rest = k.lnA

        def place_numbers(pool, own):
            own(pool.iota(PLACE_ROW[:, :], [[1, CAP]], base=1, channel_multiplier=0, allow_small_or_imprecise_dtypes=True))
            own(pool.iota(PLACE_COL[:, :], [[P, ST]], base=1, channel_multiplier=1, allow_small_or_imprecise_dtypes=True))

        layernorm(k, k.X, k.XN, beside=place_numbers)
        route_top2(k, E, W["L3_ffn_Wg"], None, "capacity", k.gT, slots[:, :])

        with stage(nc, "turned", "small_turned", "high_done", "rest_done", "mid_done", "low_done", "own_d") as (block, turned, small_turned, high_done, rest_done, mid_done, low_done, own_d):
            part = lambda n, b: XP[:, n, 4 * b:4 * b + 4, :].rearrange("p a b -> p (a b)")

            @block.tensor
            def _(pe):
                for b in range(NBLK):
                    for j in range(4):
                        mm = nc.tensor.transpose(PS[:, b, blk(j, P)], k.XN[:, blk(4 * b + j, P)], k.ident[:, :])
                    mm.then_inc(turned, 1)
                for n, rows in enumerate((slots, k.gT)):
                    for t in range(NTILE):
                        mm = nc.tensor.transpose(PS[:, 4 + n, blk(t, E)], rows[0:E, blk(t, P)], k.ident[0:E, 0:E])
                    mm.then_inc(small_turned, 1)

            @block.scalar
            def _(act):
                for b in range(NBLK):
                    act.wait_ge(turned, b + 1)
                    nc.scalar.activation(part(0, b), PS[:, b, :], ACT.Identity).then_inc(high_done, 1)
                for b in range(NBLK):
                    act.wait_ge(rest_done, b + 1)
                    nc.scalar.activation(part(1, b), rest[:, blk(b)], ACT.Identity).then_inc(mid_done, 1)

            @block.vector
            def _(dve):
                own = Link(dve, own_d)
                for b in range(NBLK):
                    dve.wait_ge(high_done, b + 1)
                    nc.vector.tensor_tensor(rest[:, blk(b)], PS[:, b, :], part(0, b), ALU.subtract).then_inc(rest_done, 1)
                nc.vector.tensor_copy(slots16[:, :], slots[:, :])
                nc.vector.tensor_copy(SEL[:, :, :], k.sel8[:, :, :])
                for b in range(NBLK):
                    dve.wait_ge(mid_done, b + 1)
                    nc.vector.tensor_tensor(part(2, b), rest[:, blk(b)], part(1, b), ALU.subtract).then_inc(low_done, 1)
                dve.wait_ge(small_turned, 2)
                nc.vector.tensor_copy(SLC[:, :, :], PS[:, 4, 0:NTILE * E].rearrange("p (a b) -> p a b", b=E))
                own(nc.vector.tensor_copy(GC[:, :, :], PS[:, 5, 0:NTILE * E].rearrange("p (a b) -> p a b", b=E)))
                own(nc.vector.tensor_copy(GP[:, :, :, 0], GC[:, :, :]))
                own(nc.vector.tensor_tensor(GC[:, :, :], GC[:, :, :], GP[:, :, :, 0], ALU.subtract))
                own(nc.vector.tensor_copy(GP[:, :, :, 1], GC[:, :, :]))
                own(nc.vector.tensor_tensor(GP[:, :, :, 2], GC[:, :, :], GP[:, :, :, 1], ALU.subtract))

        EARLY = NTILE // 2
        with stage(nc, "gather_made", "place_spread", "scatter_made", "x_ready", "x_copied", "gates_ready", "gates_done", "hid_ready", "hid_done",
                   "y_ready", "y_taken", "y_parts", "scattered", "own_d") as (block, gather_made, place_spread, scatter_made, x_ready, x_copied, gates_ready, gates_done,
                                                                             hid_ready, hid_done, y_ready, y_taken, y_parts, scattered, own_d):
            @block.tensor
            def _(pe):
                def gather(e, t):
                    pe.wait_ge(gather_made, NTILE * e + t + 1)
                    if t == 0 and e >= 2:
                        pe.wait_ge(y_taken, e - 1)
                    for part in range(3):
                        mm = nc.tensor.matmul(PS[:, 4, 0:CAP], XP[:, part, t, :], GATHER[:, e % 2, t, :], start=(t == 0 and part == 0), stop=(t == NTILE - 1 and part == 2))
                    if t == NTILE - 1:
                        mm.then_inc(x_ready, 1)

                def spread(e, b):
                    if NBLK * e + b:
                        pe.wait_ge(scatter_made, ST * (NBLK * e + b))
                    nc.tensor.matmul(PS[:, 7, :], SEL[:, e, :], slots16[:, blk(b)], start=True, stop=True).then_inc(place_spread, 1)

                def gates(e):
                    if e:
                        pe.wait_ge(hid_done, C * e)
                    for half in range(ST):
                        for t in range(NTILE):
                            mm = nc.tensor.matmul(PS[:, 6, 4 * half:4 * half + 3], GATHER[:, e % 2, t, blk(half, P)], GP[:, t, e, :], start=(t == 0), stop=(t == NTILE - 1))
                    mm.then_inc(gates_ready, 1)

                def hidden(e):
                    pe.wait_ge(x_copied, e + 1)
                    for c in range(C):
                        if c == 2:
                            pe.wait_ge(gates_done, e + 1)
                        mm = nc.tensor.matmul(PS[:, 5 + c // 2, blk(c % 2, CAP)], W["L3_ffn_W1"][:, e, blk(c, P)], XG[:, :], start=True, stop=True)
                        if c % 2:
                            mm.then_inc(hid_ready, 1)

                def output(e):
                    pe.wait_ge(hid_done, C * e + C)
                    if e + 1 < E:
                        pe.wait_ge(x_copied, e + 2)
                    for half in range(ST):
                        for c in range(C):
                            mm = nc.tensor.matmul(PS[:, 4, CAP + half * P:CAP + half * P + P], H[:, c, blk(half, P)], W["L3_ffn_W2"][:, e, c, :], start=(c == 0), stop=(c == C - 1))
                    mm.then_inc(y_ready, 1)

                def scatter(e):
                    pe.wait_ge(y_parts, e + 1)
                    pe.wait_ge(scatter_made, ST * NBLK * (e + 1))
                    for b in range(NBLK):
                        for half in range(ST):
                            for part in range(3):
                                first, last = half == 0 and part == 0, half == ST - 1 and part == 2
                                mm = nc.tensor.matmul(PS[:, b, :], YP[:, part, half, :], SCATTER[:, e % 2, half, blk(b)], start=(e == 0 and first), stop=(e == E - 1 and last))
                    mm.then_inc(scattered, 1)

                for t in range(NTILE):
                    gather(0, t)
                gates(0)
                for e in range(E):
                    hidden(e)
                    for b in range(NBLK):
                        spread(e, b)
                        if e + 1 < E:
                            for t in range(4 * b, 4 * b + 4):
                                gather(e + 1, t)
                    if e + 1 < E:
                        gates(e + 1)
                    output(e)
                    if e:
                        scatter(e - 1)
                scatter(E - 1)

            @block.scalar
            def _(act):
                for e in range(E):
                    act.wait_ge(x_ready, e + 1)
                    if e:
                        act.wait_ge(hid_ready, 2 * e)
                    nc.scalar.activation(XG[:, :], PS[:, 4, 0:CAP], ACT.Identity).then_inc(x_copied, 1)
                    if e:
                        act.wait_ge(y_ready, e)
                    for c in range(C):
                        act.wait_ge(hid_ready, 2 * e + c // 2 + 1)
                        nc.scalar.activation(H[:, c, :], PS[:, 5 + c // 2, blk(c % 2, CAP)], ACT.Gelu_apprx_tanh, bias=W["L3_ffn_b1"][:, e, c:c + 1]).then_inc(hid_done, 1)

            @block.vector
            def _(dve):
                own = Link(dve, own_d)

                def make_gather(e, t):
                    nc.vector.tensor_scalar(GATHER[:, e % 2, t, :], PLACE_ROW[:, :], SLC[:, t, e:e + 1], None, ALU.is_equal).then_inc(gather_made, 1)

                for e in range(2):
                    for t in range(NTILE if e == 0 else EARLY):
                        make_gather(e, t)
                for e in range(E):
                    dve.wait_ge(gates_ready, e + 1)
                    if e:
                        dve.wait_ge(y_parts, e)
                    g = PS[:, 6, 0:4 * ST].rearrange("p (a b) -> p a b", b=4)[:, :, 0:3]
                    nc.vector.tensor_reduce(GS[:, :], g, AX.X, ALU.add).then_inc(gates_done, 1)
                    for b in range(NBLK):
                        dve.wait_ge(place_spread, NBLK * e + b + 1)
                        if e >= 2:
                            dve.wait_ge(scattered, e - 1)
                        for half in range(ST):
                            nc.vector.tensor_scalar(SCATTER[:, e % 2, half, blk(b)], PS[:, 7, :], PLACE_COL[:, half:half + 1], None, ALU.is_equal).then_inc(scatter_made, 1)
                        if e + 1 < E:
                            late = (NTILE - EARLY) // NBLK
                            for t in range(EARLY + late * b, EARLY + late * (b + 1)):
                                make_gather(e + 1, t)
                    if e + 2 < E:
                        dve.wait_ge(x_ready, e + 1)
                        for t in range(EARLY):
                            make_gather(e + 2, t)
                    dve.wait_ge(y_ready, e + 1)
                    y = PS[:, 4, CAP:2 * CAP].rearrange("p (a b) -> p a b", b=D)
                    nc.vector.tensor_tensor(Y[:, :, :], y, W["L3_ffn_b2"][:, e, :].unsqueeze(1).to_broadcast([P, ST, D]), ALU.add).then_inc(y_taken, 1)
                    dve.wait_ge(y_taken, e + 1)
                    dve.wait_ge(gates_done, e + 1)
                    own(nc.vector.tensor_tensor(Y[:, :, :], Y[:, :, :], GS[:, :].unsqueeze(2).to_broadcast([P, ST, D]), ALU.mult))
                    if e:
                        dve.wait_ge(scattered, e)
                    own(nc.vector.tensor_copy(YP[:, 0, :, :], Y[:, :, :]))
                    own(nc.vector.tensor_tensor(Y[:, :, :], Y[:, :, :], YP[:, 0, :, :], ALU.subtract))
                    own(nc.vector.tensor_copy(YP[:, 1, :, :], Y[:, :, :]))
                    nc.vector.tensor_tensor(YP[:, 2, :, :], Y[:, :, :], YP[:, 1, :, :], ALU.subtract).then_inc(y_parts, 1)
                dve.wait_ge(scattered, E)
                for b in range(NBLK):
                    own(nc.vector.tensor_tensor(k.X[:, blk(b)], k.X[:, blk(b)], PS[:, b, :], ALU.add))


def expm_product(k):
    nc, PS, g = k.nc, k.PS, k.W["L0_ffn_gens"]
    ORDER, SQ = 12, 4
    with ExitStack() as st:
        T = k.sbuf(st, "ex_T", [P, 2, 2, 3 * P], F32)
        with stage(nc, "prod", "next_done", "own_d") as (block, prod, next_done, own_d):
            @block.tensor
            def _(pe):
                for i in range(ORDER + SQ):
                    pe.wait_ge(next_done, 2 * i + 2)
                    for side in range(2):
                        for m in range(3):
                            cur = T[:, i % 2, side, blk(m, P)]
                            left = g[:, 1 - side, m, :] if i < ORDER else T[:, i % 2, 1 - side, blk(m, P)]
                            mm = nc.tensor.matmul(PS[:, 2 * (i % 2) + side, blk(m, P)], left, cur, start=True, stop=True)
                        mm.then_inc(prod, 1)
                pe.wait_ge(next_done, 2 * (ORDER + SQ) + 2)
                fin = T[:, (ORDER + SQ) % 2]
                nc.tensor.matmul(PS[:, 4, 0:P], fin[:, 0, blk(1, P)], fin[:, 1, blk(0, P)], start=True, stop=True).then_inc(prod, 1)
                pe.wait_ge(next_done, 2 * (ORDER + SQ) + 3)
                nc.tensor.matmul(PS[:, 5, 0:P], T[:, 1 - (ORDER + SQ) % 2, 0, 0:P], fin[:, 0, blk(2, P)], start=True, stop=True).then_inc(prod, 1)

            @block.vector
            def _(dve):
                eye3 = k.ident[:, :].unsqueeze(1).to_broadcast([P, 3, P])
                for side in range(2):
                    nc.vector.tensor_copy(T[:, 0, side, :].rearrange("p (m n) -> p m n", n=P), eye3).then_inc(next_done, 1)
                for i in range(ORDER + SQ):
                    for side in range(2):
                        dve.wait_ge(prod, 2 * i + side + 1)
                        src = PS[:, 2 * (i % 2) + side, 0:3 * P].rearrange("p (m n) -> p m n", n=P)
                        dst = T[:, (i + 1) % 2, side, :].rearrange("p (m n) -> p m n", n=P)
                        if i < ORDER:
                            nc.vector.scalar_tensor_tensor(out=dst, in0=src, scalar=1.0 / (2 ** SQ * (ORDER - i)), in1=eye3, op0=ALU.mult, op1=ALU.add).then_inc(next_done, 1)
                        else:
                            nc.vector.tensor_copy(dst, src).then_inc(next_done, 1)
                dve.wait_ge(prod, 2 * (ORDER + SQ) + 1)
                nc.vector.tensor_copy(T[:, 1 - (ORDER + SQ) % 2, 0, 0:P], PS[:, 4, 0:P]).then_inc(next_done, 1)
                dve.wait_ge(prod, 2 * (ORDER + SQ) + 2)
                nc.vector.tensor_copy(k.rot[:, :], PS[:, 5, 0:P]).then_inc(own_d, 1)
                for h in range(2):
                    nc.vector.tensor_copy(k.mixm[:, h, :], k.W["L0_ffn_mix_w"][:, h:h + 1].to_broadcast([P, P])).then_inc(own_d, 1)
                dve.wait_ge(own_d, 3)


def l0_ffn(k):
    nc, PS, W = k.nc, k.PS, k.W
    with ExitStack() as st:
        XL = k.sbuf(st, "l0f_xl", [P, NTOK], F32)
        layernorm(k, k.X, XL)
        layernorm(k, XL, k.XN, W["L0_ffn_ln_g"], W["L0_ffn_ln_b"])
        route_top2(k, 8, W["L0_ffn_gate_w_moe"], W["L0_ffn_gate_b_moe"], "softmax2", k.gT)
        H, gb, tmp, acc = expert_buffers(k, st)
        AB = k.sbuf(st, "l0f_ab", [P, 3, BLK], F32)
        with nc.Fori(0, NTOK - BLK + 1, BLK) as tb:
            experts(k, W["L0_ffn_w1"], W["L0_ffn_b1"], W["L0_ffn_w2"], W["L0_ffn_b2"], k.gT, ACT.Gelu, acc[:, :], H, gb, tmp[:, :], tb)
            with stage(nc, "mixed_ready", "ab", "na", "sig", "own_d") as (block, mixed_ready, ab, na, sig, own_d):
                abel, nonab, g = AB[:, 0, :], AB[:, 1, :], AB[:, 2, :]

                @block.tensor
                def _(pe):
                    nc.tensor.matmul(PS[:, 0, :], W["L0_ffn_abel_w"], k.XN[:, bass.ds(tb, BLK)], start=True, stop=True).then_inc(mixed_ready, 1)
                    nc.tensor.matmul(PS[:, 1, :], k.rot[:, :], acc[:, :], start=True, stop=True).then_inc(mixed_ready, 1)
                    pe.wait_ge(ab, 1)
                    pe.wait_ge(na, 1)
                    nc.tensor.matmul(PS[:, 2, :], k.mixm[:, 0, :], abel, start=True, stop=False)
                    nc.tensor.matmul(PS[:, 2, :], k.mixm[:, 1, :], nonab, start=False, stop=True).then_inc(mixed_ready, 1)

                @block.scalar
                def _(act):
                    act.wait_ge(mixed_ready, 1)
                    nc.scalar.activation(abel, PS[:, 0, :], ACT.Gelu, bias=W["L0_ffn_abel_b"]).then_inc(ab, 1)
                    act.wait_ge(mixed_ready, 3)
                    nc.scalar.activation(g, PS[:, 2, :], ACT.Sigmoid, bias=W["L0_ffn_mix_b"]).then_inc(sig, 1)

                @block.vector
                def _(dve):
                    own = Link(dve, own_d)
                    dve.wait_ge(mixed_ready, 2)
                    nc.vector.tensor_copy(nonab, PS[:, 1, :]).then_inc(na, 1)
                    xb = k.X[:, bass.ds(tb, BLK)]
                    own(nc.vector.tensor_tensor(xb, xb, XL[:, bass.ds(tb, BLK)], ALU.add))
                    dve.wait_ge(ab, 1)
                    dve.wait_ge(na, 1)
                    dve.wait_ge(sig, 1)
                    own(nc.vector.tensor_tensor(nonab, nonab, abel, ALU.subtract))
                    own(nc.vector.tensor_tensor(nonab, nonab, g, ALU.mult))
                    own(nc.vector.tensor_tensor(nonab, nonab, abel, ALU.add))
                    own(nc.vector.tensor_tensor(xb, xb, nonab, ALU.add))


def l1_ffn(k):
    nc, PS, W = k.nc, k.PS, k.W
    C = 4
    layernorm(k, k.X, k.XN)
    with ExitStack() as st:
        G = k.sbuf(st, "l1f_G", [P, C, BLK], F32)
        HA = k.sbuf(st, "l1f_HA", [P, C, BLK], F32)
        HB = k.sbuf(st, "l1f_HB", [P, C, BLK], F32)
        with nc.Fori(0, NTOK - BLK + 1, BLK) as tb:
            with stage(nc, "g_ready", "g_done", "a_done", "h1_ready", "h1_done", "h2_ready", "h2_done", "y_ready", "added") as (block, g_ready, g_done, a_done, h1_ready, h1_done, h2_ready, h2_done, y_ready, added):
                @block.tensor
                def _(pe):
                    xn = k.XN[:, bass.ds(tb, BLK)]
                    for c in range(C):
                        nc.tensor.matmul(PS[:, c, :], W["L1_ffn_w1"][:, blk(c, P)], xn, start=True, stop=True)
                        nc.tensor.matmul(PS[:, 4 + c, :], W["L1_ffn_w2"][:, blk(c, P)], xn, start=True, stop=True).then_inc(g_ready, 1)
                    for c in range(C):
                        pe.wait_ge(g_done, c + 1)
                        for q in range(C):
                            pe.wait_ge(a_done, q + 1)
                            mm = nc.tensor.matmul(PS[:, c, :], W["L1_ffn_h1"][:, q, blk(c, P)], HA[:, q, :], start=(q == 0), stop=(q == C - 1))
                        mm.then_inc(h1_ready, 1)
                    for c in range(C):
                        for q in range(C):
                            pe.wait_ge(h1_done, q + 1)
                            mm = nc.tensor.matmul(PS[:, 4 + c, :], W["L1_ffn_h2"][:, q, blk(c, P)], HB[:, q, :], start=(q == 0), stop=(q == C - 1))
                        mm.then_inc(h2_ready, 1)
                    for q in range(C):
                        pe.wait_ge(h2_done, q + 1)
                        mm = nc.tensor.matmul(PS[:, 0, :], W["L1_ffn_w3"][:, q, :], G[:, q, :], start=(q == 0), stop=(q == C - 1))
                    mm.then_inc(y_ready, 1)

                @block.scalar
                def _(act):
                    for c in range(C):
                        act.wait_ge(g_ready, c + 1)
                        nc.scalar.activation(G[:, c, :], PS[:, c, :], ACT.Silu, scale=W["L1_ffn_w1_s"][:, c:c + 1]).then_inc(g_done, 1)
                    for c in range(C):
                        act.wait_ge(h1_ready, c + 1)
                        nc.scalar.activation(HB[:, c, :], PS[:, c, :], ACT.Gelu, scale=W["L1_ffn_h1_s"][:, c:c + 1]).then_inc(h1_done, 1)
                    for c in range(C):
                        act.wait_ge(h2_ready, c + 1)
                        act.wait_ge(a_done, c + 1)
                        nc.scalar.activation(G[:, c, :], PS[:, 4 + c, :], ACT.Gelu, scale=W["L1_ffn_h2_s"][:, c:c + 1]).then_inc(h2_done, 1)

                @block.vector
                def _(dve):
                    for c in range(C):
                        dve.wait_ge(g_done, c + 1)
                        nc.vector.scalar_tensor_tensor(out=HA[:, c, :], in0=PS[:, 4 + c, :], scalar=W["L1_ffn_w2_s"][:, c:c + 1], in1=G[:, c, :], op0=ALU.mult, op1=ALU.mult).then_inc(a_done, 1)
                    dve.wait_ge(y_ready, 1)
                    xb = k.X[:, bass.ds(tb, BLK)]
                    nc.vector.scalar_tensor_tensor(out=xb, in0=PS[:, 0, :], scalar=W["L1_ffn_w3_s"], in1=xb, op0=ALU.mult, op1=ALU.add).then_inc(added, 1)
                    dve.wait_ge(added, 1)


def l2_ffn(k):
    nc, PS, W = k.nc, k.PS, k.W
    C = 4
    layernorm(k, k.X, k.XN)
    route_top2(k, 16, W["L2_ffn_router_w"], None, "renorm", k.gT)
    with ExitStack() as st:
        G = k.sbuf(st, "l2f_G", [P, C + 1, BLK], F32)
        H = k.sbuf(st, "l2f_H", [P, C + 1, BLK], F32)
        with nc.Fori(0, NTOK - BLK + 1, BLK) as tb:
            with stage(nc, "up_ready", "g_done", "h_half", "h_done", "y_ready", "added") as (block, up_ready, g_done, h_half, h_done, y_ready, added):
                @block.tensor
                def _(pe):
                    xn = k.XN[:, bass.ds(tb, BLK)]
                    for c in range(C + 1):
                        wg = W["L2_ffn_wg_r"][:, blk(c, P)] if c < C else W["L2_ffn_wg_s"]
                        wu = W["L2_ffn_wu_r"][:, blk(c, P)] if c < C else W["L2_ffn_wu_s"]
                        if c >= 2:
                            pe.wait_ge(h_done, c - 1)
                        nc.tensor.matmul(PS[:, 3 * (c % 2), :], wg, xn, start=True, stop=True)
                        mm = nc.tensor.matmul(PS[:, 3 * (c % 2) + 1, :], wu, xn, start=True, stop=True)
                        if c < C:
                            mm = nc.tensor.matmul(PS[:, 3 * (c % 2) + 2, :], k.sel16[:, c, :], k.gT[0:16, bass.ds(tb, BLK)], start=True, stop=True)
                        mm.then_inc(up_ready, 1)
                    for c in range(C + 1):
                        pe.wait_ge(h_done, c + 1)
                        wd = W["L2_ffn_wd_r"][:, c, :] if c < C else W["L2_ffn_wd_s"]
                        mm = nc.tensor.matmul(PS[:, 6, :], wd, H[:, c, :], start=(c == 0), stop=(c == C))
                    mm.then_inc(y_ready, 1)

                @block.scalar
                def _(act):
                    for c in range(C + 1):
                        act.wait_ge(up_ready, c + 1)
                        nc.scalar.activation(G[:, c, :], PS[:, 3 * (c % 2), :], ACT.Silu).then_inc(g_done, 1)

                @block.vector
                def _(dve):
                    for c in range(C + 1):
                        dve.wait_ge(g_done, c + 1)
                        if c < C:
                            nc.vector.tensor_tensor(G[:, c, :], PS[:, 3 * (c % 2) + 1, :], G[:, c, :], ALU.mult).then_inc(h_half, 1)
                            dve.wait_ge(h_half, c + 1)
                            nc.vector.tensor_tensor(H[:, c, :], PS[:, 3 * (c % 2) + 2, :], G[:, c, :], ALU.mult).then_inc(h_done, 1)
                        else:
                            nc.vector.tensor_tensor(H[:, c, :], PS[:, 3 * (c % 2) + 1, :], G[:, c, :], ALU.mult).then_inc(h_done, 1)
                    dve.wait_ge(y_ready, 1)
                    xb = k.X[:, bass.ds(tb, BLK)]
                    nc.vector.tensor_tensor(xb, PS[:, 6, :], xb, ALU.add).then_inc(added, 1)
                    dve.wait_ge(added, 1)


NEG = -1e30
HG = 4
NT = SEQ // P


def zero_bank(nc, k, bank):
    return nc.tensor.matmul(k.PS[:, bank, :], k.zeros16[:, 0:P], k.zeros16[:, :], start=True, stop=False, skip_group_check=True)


MAXROW = 96
PAIRS = {8: [(a, c) for a in range(3) for c in range(3)],
         16: [(0, 0), (0, 1), (1, 0), (1, 1), (0, 2), (2, 0)]}


def expansion_constants(k, pool, own, SEL, dims, KX, QX):
    rows = HG * dims
    own(pool.memset(SEL[:, :, :, :, :], 0.0))
    for side in range(2):
        for g in range(HG):
            for n, pair in enumerate(PAIRS[dims]):
                part = pair[1 - side]
                product, place = (0, part) if rows == 32 or part < 2 else (1, 1)
                v = SEL[:, product, side, g, n * dims:(n + 1) * dims]
                ins = pool.affine_select(out=v, in_=v, compare_op=ALU.not_equal, fill=1.0, base=-rows * place - dims * g, pattern=[[-1, dims]], channel_multiplier=1)
    own(ins)
    own(pool.memset(QX[MAXROW:P, :, :], 0.0))
    own(pool.memset(KX[MAXROW:P, :, :], 1.0))


def expand_heads(k, KS, QS, KX, QX, SEL, PARTS, LOW, dims):
    nc, PS = k.nc, k.PS
    SRC = [(0, 0), (0, 1), (1, 0), (1, 1)]
    used = slice(0, 96) if dims == 8 else slice(0, P)
    mid = slice(32, 64) if dims == 8 else slice(64, P)
    low = slice(64, 96) if dims == 8 else slice(64, P)
    with stage(nc, "high_done", "rest_done", "mid_done", "low_rounded", "low_done", "ready", "act_took", "dve_took") as (block, high_done, rest_done, mid_done, low_rounded, low_done, ready, act_took, dve_took):
        @block.scalar
        def _(act):
            for side, h in SRC:
                nc.scalar.activation(PARTS[used, side, blk(h)], (KS, QS)[side][used, blk(h)], ACT.Identity).then_inc(high_done, 1)
            for n in range(5):
                if n < 4:
                    side, h = SRC[n]
                    act.wait_ge(rest_done, n + 1)
                    nc.scalar.activation(LOW[low, side, blk(h)], (KS, QS)[side][low, blk(h)], ACT.Identity).then_inc(low_rounded, 1)
                if n:
                    side, h = SRC[n - 1]
                    for g in (0, 2):
                        u = HG * (n - 1) + g
                        act.wait_ge(ready, u + 1)
                        nc.scalar.activation((KX, QX)[side][0:MAXROW, g, blk(h)], PS[0:MAXROW, u % 8, :], ACT.Identity).then_inc(act_took, 1)

        @block.gpsimd
        def _(pool):
            for n, (side, h) in enumerate(SRC):
                pool.wait_ge(rest_done, n + 1)
                nc.gpsimd.tensor_copy(PARTS[mid, side, blk(h)], (KS, QS)[side][mid, blk(h)]).then_inc(mid_done, 1)

        @block.vector
        def _(dve):
            def took(n):
                side, h = SRC[n]
                for g in (1, 3):
                    u = HG * n + g
                    dve.wait_ge(ready, u + 1)
                    nc.vector.tensor_copy((KX, QX)[side][0:MAXROW, g, blk(h)], PS[0:MAXROW, u % 8, :]).then_inc(dve_took, 1)

            for n in range(5):
                if n < 4:
                    side, h = SRC[n]
                    dve.wait_ge(high_done, n + 1)
                    x = (KS, QS)[side][used, blk(h)]
                    nc.vector.tensor_tensor(x, x, PARTS[used, side, blk(h)], ALU.subtract).then_inc(rest_done, 1)
                if n:
                    side, h = SRC[n - 1]
                    dve.wait_ge(low_rounded, n)
                    dst = PARTS if dims == 8 else LOW
                    nc.vector.tensor_tensor(dst[low, side, blk(h)], (KS, QS)[side][low, blk(h)], LOW[low, side, blk(h)], ALU.subtract).then_inc(low_done, 1)
                if n > 1:
                    took(n - 2)
            took(3)

        @block.tensor
        def _(pe):
            for n, (side, h) in enumerate(SRC):
                pe.wait_ge(low_done, n + 1)
                pe.wait_ge(mid_done, n + 1)
                for g in range(HG):
                    u = HG * n + g
                    if u >= 8:
                        pe.wait_ge(dve_took if g % 2 else act_took, (u - 8) // 2 + 1)
                    mm = nc.tensor.matmul(PS[:, u % 8, :], SEL[used, 0, side, g, :], PARTS[used, side, blk(h)], start=True, stop=(dims == 8))
                    if dims == 16:
                        mm = nc.tensor.matmul(PS[:, u % 8, :], SEL[low, 1, side, g, :], LOW[low, side, blk(h)], start=False, stop=True)
                    mm.then_inc(ready, 1)


def expand_maxima(k, M, NM, MB, QX):
    nc, PS = k.nc, k.PS
    with stage(nc, "m_ready", "turned", "taken", "own_d") as (block, m_ready, turned, taken, own_d):
        @block.vector
        def _(dve):
            own = Link(dve, own_d)
            own(nc.vector.tensor_scalar(NM[:, 0, :, :], M[:, :, :], -1.0, None, ALU.mult))
            own(nc.vector.tensor_copy(MB[:, :, :, 0], NM[:, 0, :, :]))
            own(nc.vector.tensor_tensor(NM[:, 1, :, :], NM[:, 0, :, :], MB[:, :, :, 0], ALU.subtract))
            own(nc.vector.tensor_copy(MB[:, :, :, 1], NM[:, 1, :, :]))
            nc.vector.tensor_tensor(MB[:, :, :, 2], NM[:, 1, :, :], MB[:, :, :, 1], ALU.subtract).then_inc(m_ready, 1)
            for g in (0, 2):
                dve.wait_ge(turned, g + 1)
                nc.vector.tensor_copy(QX[MAXROW:MAXROW + 3, g, :], PS[MAXROW:MAXROW + 3, 2 * g:2 * g + 2, :].rearrange("p a n -> p (a n)")).then_inc(taken, 1)
            dve.wait_ge(taken, HG)

        @block.scalar
        def _(act):
            for g in (1, 3):
                act.wait_ge(turned, g + 1)
                nc.scalar.activation(QX[MAXROW:MAXROW + 3, g, :], PS[MAXROW:MAXROW + 3, 2 * g:2 * g + 2, :].rearrange("p a n -> p (a n)"), ACT.Identity).then_inc(taken, 1)

        @block.tensor
        def _(pe):
            pe.wait_ge(m_ready, 1)
            for g in range(HG):
                for i in range(NT):
                    mm = nc.tensor.matmul(PS[MAXROW:MAXROW + 3, 2 * g + i // 4, blk(i % 4, P)], MB[:, g, i, :], k.identb[:, :], start=True, stop=True)
                mm.then_inc(turned, 1)


def head_attention(k, pre, causal):
    nc, PS, W = k.nc, k.PS, k.W
    biased = not causal
    if causal:
        klo = lambda i: 0
        khi = lambda i: i + 1
        qlo = lambda j: j
        qhi = lambda j: NT
    else:
        klo = lambda i: max(i - 1, 0)
        khi = lambda i: min(i + 2, NT)
        qlo, qhi = klo, khi
    pieces = []
    for j in range(NT):
        c = qlo(j) * P
        while c < qhi(j) * P:
            e = min((c // BLK + 1) * BLK, qhi(j) * P)
            pieces.append((j, c, e))
            c = e
    SLOTS = 3
    cuts = [(j, i) for j in range(NT) for i in range(qlo(j), qhi(j)) if (i == j if causal else i != j)]
    with ExitStack() as st:
        def sb(n, shape, dt=F32):
            return k.sbuf(st, n, shape, dt)
        QS, KS = sb("at_q", [P, SEQ]), sb("at_k", [P, SEQ])
        V1 = sb("at_v", [P, NT, HG, 9])
        PT = sb("at_pt", [P, SLOTS, HG, BLK])
        M, NM, MB = sb("at_m", [P, HG, NT]), sb("at_nm", [P, 2, HG, NT]), sb("at_mb", [P, HG, NT, 3], BF16)
        SEL = sb("at_sel", [P, 1, 2, HG, P], BF16)
        KX, QX = sb("at_kx", [P, HG, SEQ], BF16), sb("at_qx", [P, HG, SEQ], BF16)
        PARTS, LOW = sb("at_parts", [P, 2, SEQ], BF16), sb("at_low", [P, 2, SEQ], BF16)
        MT = sb("at_mt", [P, HG, NT])
        OT, RQ = sb("at_o", [P, SEQ]), sb("at_rq", [P, NT, HG])
        WS = sb("at_w", [P, 2, 32])
        WO = sb("at_wo", [P, P])
        SPAN = SEQ if causal else 3 * P
        CM = sb("at_cm", [P, SPAN])
        TM = sb("at_tm", [P, 2, P])
        if causal:
            JR = sb("at_jr", [P, SEQ])
            AL = sb("at_al", [P, HG, SEQ])
            SL, I128, JP, SJ = sb("at_sl", [P, 16]), sb("at_i128", [P, NT]), sb("at_jp", [P, NT]), sb("at_sj", [P, HG, NT])
        Wq, Wk, WoP, Wv = W[pre + "Wq"], W[pre + "Wk"], W[pre + "WoP"], W[pre + "Wv"]
        def layer_constants(pool, own):
            own(pool.memset(CM[:, :], 0.0))
            expansion_constants(k, pool, own, SEL, 8, KX, QX)
            own(pool.memset(TM[:, :, :], 0.0))
            for n in range(2):
                sign = 1 - 2 * n
                own(pool.affine_select(out=TM[:, n, :], in_=TM[:, n, :], compare_op=ALU.is_ge, fill=NEG, base=0, pattern=[[sign, P]], channel_multiplier=-sign))
            own(pool.memset(V1[:, :, :, :], 1.0))
            if causal:
                own(pool.affine_select(out=CM[:, :], in_=CM[:, :], compare_op=ALU.is_ge, fill=NEG, base=SEQ - P, pattern=[[-1, SEQ]], channel_multiplier=1))
                own(pool.iota(JR[:, :], [[1, SEQ]], base=P - SEQ, channel_multiplier=0, allow_small_or_imprecise_dtypes=True))
                own(pool.iota(I128[:, :], [[P, NT]], base=0, channel_multiplier=0, allow_small_or_imprecise_dtypes=True))
                own(pool.iota(JP[:, :], [[P, NT]], base=0, channel_multiplier=1, allow_small_or_imprecise_dtypes=True))
                for h in range(16):
                    own(pool.memset(SL[:, h:h + 1], float(np.float32(2.0 ** (-0.5)) ** (h + 1))))
            else:
                own(pool.affine_select(out=CM[:, :], in_=CM[:, :], compare_op=ALU.is_ge, fill=NEG, base=0, pattern=[[1, SPAN]], channel_multiplier=-1))
                own(pool.affine_select(out=CM[:, :], in_=CM[:, :], compare_op=ALU.is_ge, fill=NEG, base=2 * P, pattern=[[-1, SPAN]], channel_multiplier=1))

        layernorm(k, k.X, k.XN, beside=layer_constants)
        def output(block, tok, den_ready, rec_ready, den_spread, o_done, y_ready, added):
            @block.tensor
            def _(pe):
                for i in range(NT):
                    mm = nc.tensor.matmul(PS[:, 5, blk(i, HG)], OT[:, blk(i, P)], k.head_row[:, :], start=True, stop=True)
                mm.then_inc(den_ready, 1)
                pe.wait_ge(rec_ready, 1)
                for i in range(NT):
                    for g in range(HG):
                        turned_spread(nc, PS[32 * g:32 * g + 32, 6 + i // 4, blk(i % 4, P)], RQ[:, i, g:g + 1].to_broadcast([P, 32]), k.ident[:, :]).then_inc(den_spread, 1)
                for h in range(2):
                    pe.wait_ge(o_done, h + 1)
                    nc.tensor.matmul(PS[:, 6 + h, :], WO[:, :], OT[:, blk(h)], start=True, stop=True).then_inc(y_ready, 1)

            @block.vector
            def _(dve):
                dve.wait_ge(den_ready, 1)
                nc.vector.reciprocal(RQ[:, :, :], PS[:, 5, 0:NT * HG].rearrange("p (a b) -> p a b", b=HG)).then_inc(rec_ready, 1)
                for h in range(2):
                    dve.wait_ge(den_spread, (h + 1) * HG * NT // 2)
                    nc.vector.tensor_tensor(OT[:, blk(h)], OT[:, blk(h)], PS[:, 6 + h, :], ALU.mult).then_inc(o_done, 1)
                for h in range(2):
                    dve.wait_ge(y_ready, h + 1)
                    xb = k.X[:, tok + h * BLK:tok + (h + 1) * BLK]
                    nc.vector.tensor_tensor(xb, xb, PS[:, 6 + h, :], ALU.add).then_inc(added, 1)
                dve.wait_ge(added, 2)

        def body(b, r):
            tok = b * SEQ
            XB = k.XN[:, tok:tok + SEQ]
            with stage(nc, "w_copied", "qk_ready", "v_ready", "own_d", "den_ready", "rec_ready", "den_spread", "o_done", "y_ready", "added") as (block, w_copied, qk_ready, v_ready, own_d, den_ready, rec_ready, den_spread, o_done, y_ready, added):
                @block.vector
                def _(dve):
                    own = Link(dve, own_d)
                    if b == 0:
                        for n, w in enumerate((Wq, Wk)):
                            nc.vector.tensor_copy(WS[:, n, :], w[:, bass.ds(r * 32, 32)]).then_inc(w_copied, 1)
                        nc.vector.tensor_copy(WO[:, :], WoP[:, bass.ds(r, 1), :].rearrange("p a n -> p (a n)")).then_inc(w_copied, 1)
                        if causal:
                            for g in range(HG):
                                slope = SL[:, bass.ds(r * HG + g, 1)]
                                nc.vector.scalar_tensor_tensor(out=AL[:, g, :], in0=JR[:, :], scalar=slope, in1=CM[:, :], op0=ALU.mult, op1=ALU.add)
                                own(nc.vector.tensor_scalar(SJ[:, g, :], JP[:, :], slope, None, ALU.mult))
                    for n in range(4):
                        dve.wait_ge(qk_ready, 3 * (n + 1))
                        if n < 2:
                            if biased:
                                own(nc.vector.tensor_scalar(QS[0:96, blk(n)], PS[0:96, n, :], W[pre + "bq3"][0:96, bass.ds(r, 1)], 8.0 ** -0.5, ALU.add, ALU.mult))
                            else:
                                own(nc.vector.tensor_scalar(QS[0:96, blk(n)], PS[0:96, n, :], 8.0 ** -0.5, None, ALU.mult))
                        else:
                            bias = W[pre + "bk3"][0:96, bass.ds(r, 1)] if biased else 0.0
                            own(nc.vector.tensor_scalar(KS[0:96, blk(n - 2)], PS[0:96, n, :], bias, None, ALU.add))
                    dve.wait_ge(v_ready, 1)
                    src = PS[:, 4, 0:NT * 32].rearrange("p (t g d) -> p t g d", t=NT, g=HG)
                    for t in range(NT):
                        if biased:
                            bv = W[pre + "bv"][:, bass.ds(r * 32, 32)].rearrange("p (g d) -> p g d", g=HG)
                            ins = nc.vector.tensor_tensor(V1[:, t, :, 1:9], src[:, t], bv, ALU.add)
                        else:
                            ins = nc.vector.tensor_copy(V1[:, t, :, 1:9], src[:, t])
                    own(ins)

                @block.tensor
                def _(pe):
                    for n in range(4):
                        if b == 0:
                            pe.wait_ge(w_copied, n // 2 + 1)
                        for part in range(3):
                            nc.tensor.matmul(PS[blk(part, 32), n, :], WS[:, n // 2, :], XB[:, blk(n % 2)], start=True, stop=True).then_inc(qk_ready, 1)
                    for t in range(NT):
                        mm = nc.tensor.matmul(PS[:, 4, blk(t, 32)], XB[:, blk(t, P)], Wv[:, bass.ds(r * 32, 32)], start=True, stop=True)
                    mm.then_inc(v_ready, 1)

                if b:
                    output(block, 0, den_ready, rec_ready, den_spread, o_done, y_ready, added)

            expand_heads(k, KS, QS, KX, QX, SEL, PARTS, LOW, 8)

            with stage(nc, "s_ready", "s_maxed", "own_d") as (block, s_ready, s_maxed, own_d):
                @block.tensor
                def _(pe):
                    for i in range(NT):
                        for g in range(HG):
                            n = HG * i + g
                            if n >= 4:
                                pe.wait_ge(s_maxed, n - 3)
                            c, e0 = klo(i) * P, khi(i) * P
                            o = c
                            while c < e0:
                                e = min(e0, o + ((c - o) // BLK + 1) * BLK)
                                q0 = 2 * (n % 4) * BLK + c - o
                                mm = nc.tensor.matmul(PS[:, :, :].rearrange("p a n -> p (a n)")[:, q0:q0 + e - c],
                                                      QX[0:MAXROW, g, blk(i, P)], KX[0:MAXROW, g, c:e], start=True, stop=True)
                                c = e
                            mm.then_inc(s_ready, 1)

                @block.vector
                def _(dve):
                    own = Link(dve, own_d)
                    for i in range(NT):
                        for g in range(HG):
                            n = HG * i + g
                            dve.wait_ge(s_ready, n + 1)
                            w = (khi(i) - klo(i)) * P
                            c0 = SEQ - w if causal else (klo(i) - i + 1) * P
                            mask = AL[:, g, c0:c0 + w] if causal else CM[:, c0:c0 + w]
                            q0 = 2 * (n % 4) * BLK
                            sc = PS[:, :, :].rearrange("p a n -> p (a n)")[:, q0:q0 + w]
                            nc.vector.tensor_tensor_reduce(sc, sc, mask, 1.0, -3e38, ALU.add, ALU.max, M[:, g, i:i + 1]).then_inc(s_maxed, 1)
                    dve.wait_ge(s_maxed, NT * HG)
                    if causal:
                        for g in range(HG):
                            own(nc.vector.scalar_tensor_tensor(out=MT[:, g, :], in0=I128[:, :], scalar=SL[:, bass.ds(r * HG + g, 1)], in1=M[:, g, :], op0=ALU.mult, op1=ALU.add))
            expand_maxima(k, MT if causal else M, NM, MB, QX)

            with stage(nc, "st_ready", "exp_done", "cut_done", "pv_done", "all_done") as (block, st_ready, exp_done, cut_done, pv_done, all_done):
                @block.tensor
                def _(pe):
                    zero_bank(nc, k, 6)
                    zero_bank(nc, k, 7)

                    def pv(x):
                        j, c, e = pieces[x]
                        pe.wait_ge(exp_done, HG * (x + 1))
                        for g in range(HG):
                            nc.tensor.matmul(PS[32 * g:32 * g + 9, 6 + c // BLK, c % BLK:(e - 1) % BLK + 1], V1[:, j, g, :], PT[:, x % SLOTS, g, 0:e - c],
                                             start=False, stop=(x == len(pieces) - 1), skip_group_check=True).then_inc(pv_done, 1)

                    for x, (j, c, e) in enumerate(pieces):
                        for g in range(HG):
                            n = HG * x + g
                            if n >= 6:
                                pe.wait_ge(exp_done, n - 5)
                            nc.tensor.matmul(PS[:, n % 6, 0:e - c], KX[0:MAXROW + 3, g, blk(j, P)], QX[0:MAXROW + 3, g, c:e], start=True, stop=True).then_inc(st_ready, 1)
                        if x:
                            pv(x - 1)
                    pv(len(pieces) - 1)

                def cut_tiles(x):
                    j, c, e = pieces[x]
                    return [i for jj, i in cuts if jj == j and c <= i * P < e]

                @block.scalar
                def _(act):
                    cut = 0
                    for x, (j, c, e) in enumerate(pieces):
                        if x >= SLOTS:
                            act.wait_ge(pv_done, HG * (x - SLOTS + 1))
                        for g in range(HG):
                            n = HG * x + g
                            act.wait_ge(st_ready, n + 1)
                            if cut_tiles(x):
                                cut += len(cut_tiles(x))
                                act.wait_ge(cut_done, cut)
                            bias = SJ[:, g, j:j + 1] if causal else 0.0
                            nc.scalar.activation(PT[:, x % SLOTS, g, 0:e - c], PS[:, n % 6, 0:e - c], ACT.Exp, bias=bias).then_inc(exp_done, 1)

                @block.vector
                def _(dve):
                    for x, (j, c, e) in enumerate(pieces):
                        for g in range(HG):
                            if cut_tiles(x):
                                dve.wait_ge(st_ready, HG * x + g + 1)
                            for i in cut_tiles(x):
                                o = i * P - c
                                tile = PS[:, (HG * x + g) % 6, o:o + P]
                                nc.vector.tensor_tensor(tile, tile, TM[:, 0 if i <= j else 1, :], ALU.add).then_inc(cut_done, 1)
                    dve.wait_ge(pv_done, HG * len(pieces))
                    nc.vector.tensor_copy(OT[:, 0:BLK], PS[:, 6, :]).then_inc(all_done, 1)
                    nc.vector.tensor_copy(OT[:, BLK:], PS[:, 7, :]).then_inc(all_done, 1)
                    dve.wait_ge(all_done, 2)

        with nc.Fori(0, 4) as r:
            for b in range(BATCH):
                body(b, r)
            with stage(nc, "den_ready", "rec_ready", "den_spread", "o_done", "y_ready", "added") as (block, *signals):
                output(block, (BATCH - 1) * SEQ, *signals)
        if biased:
            with stage(nc, "bias_added") as (block, bias_added):
                @block.vector
                def _(dve):
                    nc.vector.tensor_scalar(k.X[:, :], k.X[:, :], W[pre + "bo"], None, ALU.add).then_inc(bias_added, 1)
                    dve.wait_ge(bias_added, 1)


def l1a(k):
    head_attention(k, "L1_attn_a_", True)


def l3b(k):
    head_attention(k, "L3_attn_b_", False)


def l2b(k):
    nc, PS, W = k.nc, k.PS, k.W
    with ExitStack() as st:
        def sb(n, shape, dt=F32):
            return k.sbuf(st, n, shape, dt)
        QT, KT, XB = sb("l2b_q", [P, SEQ]), sb("l2b_k", [P, SEQ]), sb("l2b_x", [P, SEQ])
        V = sb("l2b_v", [P, NT, P])
        CM = sb("l2b_cm", [P, SEQ])
        BIG = sb("l2b_big", [P, BLK])
        Z, E = sb("l2b_z", [P, 2, SEQ]), sb("l2b_e", [P, 2, SEQ])
        PT = sb("l2b_pt", [P, NT, P])
        small = sb("l2b_s", [P, 2, 4])
        O, = sb("l2b_o", [P, P]),
        def layer_constants(pool, own):
            own(pool.memset(CM[:, :], 0.0))
            own(pool.affine_select(out=CM[:, :], in_=CM[:, :], compare_op=ALU.is_ge, fill=NEG, base=SEQ - P, pattern=[[-1, SEQ]], channel_multiplier=1))
            own(pool.memset(BIG[:, :], NEG))

        layernorm(k, k.X, k.XN, beside=layer_constants)
        with nc.Fori(0, NTOK - SEQ + 1, SEQ) as tok:
            with stage(nc, "x_copied", "proj", "own_d", "own_a") as (block, x_copied, proj, own_d, own_a):
                @block.scalar
                def _(act):
                    nc.scalar.activation(XB[:, :], k.XN[:, bass.ds(tok, SEQ)], ACT.Identity).then_inc(x_copied, 1)
                    for n in range(2):
                        act.wait_ge(proj, 3 + n)
                        nc.scalar.activation(V[:, blk(n, 4), :], PS[:, 4 + n, :].rearrange("p (a b) -> p a b", b=P), ACT.Identity).then_inc(own_a, 1)

                @block.tensor
                def _(pe):
                    pe.wait_ge(x_copied, 1)
                    for n, w in enumerate(("L2_attn_b_WQ", "L2_attn_b_WK")):
                        for h in range(2):
                            mm = nc.tensor.matmul(PS[:, 2 * n + h, :], W[w], XB[:, blk(h)], start=True, stop=True)
                        mm.then_inc(proj, 1)
                    for n in range(2):
                        for t in range(4):
                            mm = nc.tensor.matmul(PS[:, 4 + n, blk(t, P)], XB[:, blk(4 * n + t, P)], W["L2_attn_b_WV"], start=True, stop=True)
                        mm.then_inc(proj, 1)

                @block.vector
                def _(dve):
                    own = Link(dve, own_d)
                    dve.wait_ge(proj, 1)
                    for h in range(2):
                        own(nc.vector.tensor_scalar(QT[:, blk(h)], PS[:, h, :], 128.0 ** -0.5, None, ALU.mult))
                    dve.wait_ge(proj, 2)
                    for h in range(2):
                        own(nc.vector.tensor_copy(KT[:, blk(h)], PS[:, 2 + h, :]))

            with stage(nc, "scores", "masked", "exp_done", "turned", "pt_done", "o_ready", "o_done", "o_turned", "added", "own_d") as (block, scores, masked, exp_done, turned, pt_done, o_ready, o_done, o_turned, added, own_d):
                score_bank = lambda i: 6 if i % 2 else 0

                @block.tensor
                def _(pe):
                    def score(i):
                        w = (i + 1) * P
                        if i >= 2:
                            pe.wait_ge(masked, i - 1)
                        for c in range(0, w, BLK):
                            mm = nc.tensor.matmul(PS[:, score_bank(i) + c // BLK, 0:min(BLK, w - c)], QT[:, blk(i, P)], KT[:, c:min(w, c + BLK)], start=True, stop=True)
                        mm.then_inc(scores, 1)

                    def turn_output(i):
                        pe.wait_ge(o_done, i + 1)
                        if i:
                            pe.wait_ge(added, i)
                        nc.tensor.transpose(PS[:, 5, 0:P], O[:, :], k.ident[:, :]).then_inc(o_turned, 1)

                    score(0)
                    for i in range(NT):
                        if i + 1 < NT:
                            score(i + 1)
                        pe.wait_ge(exp_done, i + 1)
                        if i:
                            pe.wait_ge(pt_done, i)
                        for j in range(i + 1):
                            mm = nc.tensor.transpose(PS[:, 2 + j // 4, blk(j % 4, P)], E[:, i % 2, blk(j, P)], k.ident[:, :])
                        mm.then_inc(turned, 1)
                        if i:
                            turn_output(i - 1)
                        pe.wait_ge(pt_done, i + 1)
                        for j in range(i + 1):
                            mm = nc.tensor.matmul(PS[:, 4, 0:P], PT[:, j, :], V[:, j, :], start=(j == 0), stop=(j == i))
                        mm.then_inc(o_ready, 1)
                    turn_output(NT - 1)

                @block.scalar
                def _(act):
                    for i in range(NT):
                        w = (i + 1) * P
                        act.wait_ge(masked, i + 1)
                        if i >= 2:
                            act.wait_ge(turned, i - 1)
                            act.wait_ge(o_done, i - 1)
                        nc.scalar.activation(E[:, i % 2, 0:w], Z[:, i % 2, 0:w], ACT.Exp, bias=small[:, i % 2, 1:2], accum_out=small[:, i % 2, 2:3]).then_inc(exp_done, 1)

                @block.vector
                def _(dve):
                    own = Link(dve, own_d)

                    def mask(i):
                        w = (i + 1) * P
                        c0 = SEQ - w
                        z = Z[:, i % 2, :]
                        dve.wait_ge(scores, i + 1)
                        if i >= 2:
                            dve.wait_ge(exp_done, i - 1)
                        for c in range(0, w, BLK):
                            n = min(BLK, w - c)
                            sc = PS[:, score_bank(i) + c // BLK, 0:n]
                            own(nc.vector.scalar_tensor_tensor(out=z[:, c:c + n], in0=sc, scalar=0.0, in1=BIG[:, 0:n], op0=ALU.is_equal, op1=ALU.mult))
                            own(nc.vector.tensor_tensor(z[:, c:c + n], z[:, c:c + n], sc, ALU.add))
                        own(nc.vector.tensor_tensor(z[:, 0:w], z[:, 0:w], CM[:, c0:c0 + w], ALU.add))
                        own(nc.vector.tensor_reduce(small[:, i % 2, 0:1], z[:, 0:w], AX.X, ALU.max))
                        nc.vector.tensor_scalar(small[:, i % 2, 1:2], small[:, i % 2, 0:1], -1.0, None, ALU.mult).then_inc(masked, 1)

                    def add(i):
                        dve.wait_ge(o_turned, i + 1)
                        xb = k.X[:, bass.ds(tok + i * P, P)]
                        nc.vector.tensor_tensor(xb, xb, PS[:, 5, 0:P], ALU.add).then_inc(added, 1)

                    mask(0)
                    for i in range(NT):
                        if i + 1 < NT:
                            mask(i + 1)
                        dve.wait_ge(turned, i + 1)
                        for h in range(i // 4 + 1):
                            m = min(4, i + 1 - 4 * h)
                            ins = nc.vector.tensor_copy(PT[:, 4 * h:4 * h + m, :], PS[:, 2 + h, 0:m * P].rearrange("p (a b) -> p a b", b=P))
                            if h == i // 4:
                                ins.then_inc(pt_done, 1)
                            else:
                                own(ins)
                        if i:
                            add(i - 1)
                        own(nc.vector.reciprocal(small[:, i % 2, 3:4], small[:, i % 2, 2:3]))
                        dve.wait_ge(o_ready, i + 1)
                        nc.vector.tensor_scalar(O[:, :], PS[:, 4, 0:P], small[:, i % 2, 3:4], None, ALU.mult).then_inc(o_done, 1)
                    add(NT - 1)
                    dve.wait_ge(added, NT)


def l3a(k):
    nc, PS, W = k.nc, k.PS, k.W
    layernorm(k, k.X, k.XN)
    with ExitStack() as st:
        def sb(n, shape, dt=F32):
            return k.sbuf(st, n, shape, dt)
        XC, QC, XT = sb("l3a_x", [P, P]), sb("l3a_q", [P, P]), sb("l3a_xt", [P, 1 + P])
        QP, KP = sb("l3a_qp", [P, 4, P]), sb("l3a_kp", [P, 4, P])
        PT, OP = sb("l3a_pt", [P, 4, 4, P]), sb("l3a_op", [P, 4, P])
        S = sb("l3a_s", [P, P])
        TRI, HB, SEL, UNS = sb("l3a_tri", [P, P]), sb("l3a_hb", [P, P]), sb("l3a_sel", [P, 4, P]), sb("l3a_uns", [P, 4, P])
        with stage(nc, "own_p", "turned", "own_d") as (block, own_p, turned, own_d):
            @block.gpsimd
            def _(pool):
                own = Link(pool, own_p)
                own(pool.memset(XT[:, 0:1], 0.0))
                own(pool.memset(TRI[:, :], 1.0))
                own(pool.affine_select(out=TRI[:, :], in_=TRI[:, :], compare_op=ALU.is_ge, fill=0.0, base=0, pattern=[[1, P]], channel_multiplier=-1))
                own(pool.memset(HB[:, :], 1.0))
                hb = HB[:, :].rearrange("p (h d) -> p h d", d=8)
                own(pool.affine_select(out=hb, in_=hb, compare_op=ALU.is_ge, fill=0.0, base=0, pattern=[[-8, 16], [0, 8]], channel_multiplier=1))
                own(pool.affine_select(out=hb, in_=hb, compare_op=ALU.is_ge, fill=0.0, base=7, pattern=[[8, 16], [0, 8]], channel_multiplier=-1))
                own(pool.memset(SEL[:, :, :], 0.0))
                for r in range(4):
                    v = SEL[:, r, :].rearrange("p (g d) -> p g d", g=4)[:, :, 1:9]
                    own(pool.affine_select(out=v, in_=v, compare_op=ALU.not_equal, fill=1.0, base=-32 * r, pattern=[[-8, 4], [-1, 8]], channel_multiplier=1))

            @block.tensor
            def _(pe):
                pe.wait_ge(own_p, 11)
                for r in range(4):
                    mm = nc.tensor.transpose(PS[:, 0, blk(r, P)], SEL[:, r, :], k.ident[:, :])
                mm.then_inc(turned, 1)

            @block.vector
            def _(dve):
                dve.wait_ge(turned, 1)
                nc.vector.tensor_copy(UNS[:, :, :], PS[:, 0, :].rearrange("p (a b) -> p a b", b=P)).then_inc(own_d, 1)
                dve.wait_ge(own_d, 1)
        with nc.Fori(0, BATCH) as b:
            with stage(nc, "cleared") as (block, cleared):
                @block.vector
                def _(dve):
                    nc.vector.memset(S[:, :], 0.0).then_inc(cleared, 1)
                    dve.wait_ge(cleared, 1)
            with nc.Fori(0, NT) as c:
                tok = b * SEQ + c * P
                with stage(nc, "x_copied", "proj", "q_done", "p_done", "qp_done", "kp_done", "st_ready", "pt_done", "o_ready", "o_done", "y_ready", "own_d") as (block, x_copied, proj, q_done, p_done, qp_done, kp_done, st_ready, pt_done, o_ready, o_done, y_ready, own_d):
                    @block.tensor
                    def _(pe):
                        pe.wait_ge(x_copied, 1)
                        nc.tensor.matmul(PS[:, 0, 0:P], W["L3_attn_a_Wq"], XC[:, :], start=True, stop=True)
                        nc.tensor.transpose(PS[:, 0, P:2 * P], XC[:, :], k.ident[:, :]).then_inc(proj, 1)
                        for r in range(4):
                            mm = nc.tensor.matmul(PS[:, 1, blk(r, P)], SEL[:, r, :], XC[:, :], start=True, stop=True)
                        mm.then_inc(proj, 1)
                        pe.wait_ge(q_done, 1)
                        for r in range(4):
                            mm = nc.tensor.matmul(PS[:, 2, blk(r, P)], SEL[:, r, :], QC[:, :], start=True, stop=True)
                        mm.then_inc(proj, 1)
                        pe.wait_ge(qp_done, 1)
                        pe.wait_ge(kp_done, 1)
                        for g in range(4):
                            q = slice(32 * g, 32 * g + 9)
                            for r in range(4):
                                mm = nc.tensor.matmul(PS[:, 3 + g, blk(r, P)], KP[q, r, :], QP[q, r, :], start=True, stop=True)
                            mm.then_inc(st_ready, 1)
                        pe.wait_ge(p_done, 1)
                        zero_bank(nc, k, 7)
                        for r in range(4):
                            for g in range(4):
                                pe.wait_ge(pt_done, g + 1)
                                h = 4 * r + g
                                mm = nc.tensor.matmul(PS[32 * g:32 * g + 9, 7, blk(r, P)], XT[:, 8 * h:8 * h + 9], PT[:, g, r, :], start=False, stop=True, skip_group_check=True)
                        mm.then_inc(o_ready, 1)
                        pe.wait_ge(o_done, 1)
                        for r in range(4):
                            nc.tensor.matmul(PS[:, 1, 0:P], UNS[:, r, :], OP[:, r, :], start=(r == 0), stop=False)
                        nc.tensor.matmul(PS[:, 1, 0:P], S[:, :], QC[:, :], start=False, stop=True)
                        nc.tensor.matmul(PS[:, 2, 0:P], XT[:, 1:], XT[:, 1:], start=True, stop=True).then_inc(y_ready, 1)

                    @block.scalar
                    def _(act):
                        nc.scalar.activation(XC[:, :], k.XN[:, bass.ds(tok, P)], ACT.Identity).then_inc(x_copied, 1)
                        act.wait_ge(proj, 2)
                        nc.scalar.activation(KP[:, :, :], PS[:, 1, :].rearrange("p (a b) -> p a b", b=P), ACT.Identity).then_inc(kp_done, 1)

                    @block.vector
                    def _(dve):
                        own = Link(dve, own_d)
                        dve.wait_ge(proj, 1)
                        nc.vector.tensor_copy(QC[:, :], PS[:, 0, 0:P]).then_inc(q_done, 1)
                        nc.vector.tensor_copy(XT[:, 1:], PS[:, 0, P:2 * P]).then_inc(p_done, 1)
                        dve.wait_ge(proj, 3)
                        nc.vector.tensor_copy(QP[:, :, :], PS[:, 2, :].rearrange("p (a b) -> p a b", b=P)).then_inc(qp_done, 1)
                        for g in range(4):
                            dve.wait_ge(st_ready, g + 1)
                            nc.vector.tensor_tensor(PT[:, g, :, :], PS[:, 3 + g, :].rearrange("p (a b) -> p a b", b=P), TRI[:, :].unsqueeze(1).to_broadcast([P, 4, P]), ALU.mult).then_inc(pt_done, 1)
                        dve.wait_ge(o_ready, 1)
                        nc.vector.tensor_copy(OP[:, :, :], PS[:, 7, :].rearrange("p (a b) -> p a b", b=P)).then_inc(o_done, 1)
                        dve.wait_ge(y_ready, 1)
                        xb = k.X[:, bass.ds(tok, P)]
                        own(nc.vector.tensor_tensor(xb, xb, PS[:, 1, 0:P], ALU.add))
                        own(nc.vector.tensor_tensor(OP[:, 0, :], PS[:, 2, 0:P], HB[:, :], ALU.mult))
                        own(nc.vector.tensor_tensor(S[:, :], S[:, :], OP[:, 0, :], ALU.add))



def l0b(k):
    nc, PS, W = k.nc, k.PS, k.W
    NS, R = 16, 8
    with ExitStack() as st:
        def sb(n, shape, dt=F32):
            return k.sbuf(st, n, shape, dt)
        U, UC, Z = sb("mb_u", [P, 2, 3 + SEQ]), sb("mb_uc", [P, 2, SEQ]), sb("mb_z", [P, 2, SEQ])
        DT, DU = sb("mb_dt", [P, 2, SEQ]), sb("mb_du", [P, 2, SEQ])
        XD = sb("mb_xd", [R, SEQ])
        BC, BCP, LOW = sb("mb_bc", [3 * 32, SEQ]), sb("mb_bcp", [3 * 32, SEQ], BF16), sb("mb_low", [3 * 32, SEQ], BF16)
        A = sb("mb_a", [P, 2, NS])
        HC = sb("mb_hc", [P, 2, 2, SEQ])
        DA, BU = (sb("mb_da0", [P, 2, SEQ]), sb("mb_da1", [P, 2, SEQ])), (sb("mb_bu0", [P, 2, SEQ]), U[:, :, 3:])
        HS, BS = sb("mb_h", [P, SEQ]), k.lnA[:, :].rearrange("p (a n) -> p a n", a=2)
        SELR = sb("mb_sel", [3 * 32, 2 * NS, P], BF16)
        def layer_constants(pool, own):
            own(pool.memset(U[:, :, 0:3], 0.0))
            own(pool.memset(SELR[:, :, :], 0.0))
            for part in range(3):
                own(pool.affine_select(out=SELR[:, :, :], in_=SELR[:, :, :], compare_op=ALU.not_equal, fill=1.0, base=-32 * part, pattern=[[-1, 2 * NS], [0, P]], channel_multiplier=1))

        layernorm(k, k.X, k.XN, beside=layer_constants)
        with stage(nc, "own_a", "own_d") as (block, own_a, own_d):
            @block.scalar
            def _(act):
                nc.scalar.activation(A[:, :, :], W["L0_attn_b_A_log"], ACT.Exp).then_inc(own_a, 1)

            @block.vector
            def _(dve):
                dve.wait_ge(own_a, 1)
                nc.vector.tensor_scalar(A[:, :, :], A[:, :, :], -1.0, None, ALU.mult).then_inc(own_d, 1)
                dve.wait_ge(own_d, 1)
        with nc.Fori(0, NTOK - SEQ + 1, SEQ) as tok:
            with stage(nc, "u_ready", "z_ready", "u_done", "z_done", "conv_done", "uc_done", "own_d") as (block, u_ready, z_ready, u_done, z_done, conv_done, uc_done, own_d):
                @block.tensor
                def _(pe):
                    for h in range(2):
                        for t in range(2):
                            nc.tensor.matmul(PS[:, 2 * h + t, :], W["L0_attn_b_W_in"][:, blk(h, P)], k.XN[:, bass.ds(tok + t * BLK, BLK)], start=True, stop=True).then_inc(u_ready, 1)
                    for h in range(2):
                        for t in range(2):
                            nc.tensor.matmul(PS[:, 4 + 2 * h + t, :], W["L0_attn_b_W_in"][:, blk(2 + h, P)], k.XN[:, bass.ds(tok + t * BLK, BLK)], start=True, stop=True).then_inc(z_ready, 1)

                @block.scalar
                def _(act):
                    for n in range(4):
                        act.wait_ge(u_ready, n + 1)
                        nc.scalar.activation(U[:, n // 2, 3 + (n % 2) * BLK:3 + (n % 2 + 1) * BLK], PS[:, n, :], ACT.Identity).then_inc(u_done, 1)
                    for n in range(4):
                        act.wait_ge(z_ready, n + 1)
                        nc.scalar.activation(Z[:, n // 2, blk(n % 2)], PS[:, 4 + n, :], ACT.Silu).then_inc(z_done, 1)
                    for h in range(2):
                        act.wait_ge(conv_done, h + 1)
                        nc.scalar.activation(UC[:, h, :], UC[:, h, :], ACT.Silu, bias=W["L0_attn_b_conv_b"][:, h:h + 1]).then_inc(uc_done, 1)

                @block.vector
                def _(dve):
                    own = Link(dve, own_d)
                    for h in range(2):
                        dve.wait_ge(u_done, 2 * h + 2)
                        w = W["L0_attn_b_conv_w"]
                        own(nc.vector.tensor_scalar(UC[:, h, :], U[:, h, 0:SEQ], w[:, h, 0:1], None, ALU.mult))
                        for j in range(1, 4):
                            ins = nc.vector.scalar_tensor_tensor(out=UC[:, h, :], in0=U[:, h, j:j + SEQ], scalar=w[:, h, j:j + 1], in1=UC[:, h, :], op0=ALU.mult, op1=ALU.add)
                            if j < 3:
                                own(ins)
                        ins.then_inc(conv_done, 1)

            with stage(nc, "xd_ready", "xd_done", "bc_ready", "dt_ready", "v_done", "abs_done", "e_done", "ln_done", "own_d") as (block, xd_ready, xd_done, bc_ready, dt_ready, v_done, abs_done, e_done, ln_done, own_d):
                @block.tensor
                def _(pe):
                    for t in range(2):
                        for h in range(2):
                            mm = nc.tensor.matmul(PS[0:R, t, :], W["L0_attn_b_W_x"][:, h, 0:R], UC[:, h, blk(t)], start=(h == 0), stop=(h == 1))
                        mm.then_inc(xd_ready, 1)
                    for t in range(2):
                        for h in range(2):
                            for part in range(3):
                                mm = nc.tensor.matmul(PS[blk(part, 32), 6 + t, :], W["L0_attn_b_W_x"][:, h, R:], UC[:, h, blk(t)], start=(h == 0), stop=(h == 1))
                                if h == 1:
                                    mm.then_inc(bc_ready, 1)
                    for t in range(2):
                        pe.wait_ge(xd_done, t + 1)
                        for h in range(2):
                            nc.tensor.matmul(PS[:, 2 + 2 * h + t, :], W["L0_attn_b_W_dt"][0:R, blk(h, P)], XD[0:R, blk(t)], start=True, stop=True).then_inc(dt_ready, 1)

                @block.vector
                def _(dve):
                    own = Link(dve, own_d)
                    for t in range(2):
                        dve.wait_ge(xd_ready, t + 1)
                        nc.vector.tensor_copy(XD[:, blk(t)], PS[0:R, t, :]).then_inc(xd_done, 1)
                    dve.wait_ge(bc_ready, 6)
                    own(nc.vector.tensor_copy(BC[:, :], PS[0:96, 6:8, :].rearrange("p a b -> p (a b)")))
                    own(nc.vector.tensor_copy(BCP[:, :], BC[:, :]))
                    own(nc.vector.tensor_tensor(BC[:, :], BC[:, :], BCP[:, :], ALU.subtract))
                    nc.vector.tensor_copy(BCP[32:64, :], BC[32:64, :])
                    own(nc.vector.tensor_copy(LOW[64:96, :], BC[64:96, :]))
                    own(nc.vector.tensor_tensor(BCP[64:96, :], BC[64:96, :], LOW[64:96, :], ALU.subtract))
                    dve.wait_ge(dt_ready, 4)
                    for h in range(2):
                        v = PS[:, 2 + 2 * h:4 + 2 * h, :].rearrange("p a b -> p (a b)")
                        own(nc.vector.tensor_scalar(DU[:, h, :], v, W["L0_attn_b_b_dt"][:, h:h + 1], None, ALU.add))
                        nc.vector.tensor_scalar(DT[:, h, :], DU[:, h, :], 0.0, None, ALU.max).then_inc(v_done, 1)
                    dve.wait_ge(ln_done, 2)
                    dve.wait_ge(v_done, 2)
                    own(nc.vector.tensor_tensor(DT[:, :, :], DT[:, :, :], DU[:, :, :], ALU.add))
                    own(nc.vector.tensor_tensor(DU[:, :, :], DT[:, :, :], UC[:, :, :], ALU.mult))

                @block.scalar
                def _(act):
                    for h in range(2):
                        act.wait_ge(v_done, h + 1)
                        nc.scalar.activation(DU[:, h, :], DU[:, h, :], ACT.Abs).then_inc(abs_done, 1)
                    for h in range(2):
                        act.wait_ge(abs_done, h + 1)
                        nc.scalar.activation(DU[:, h, :], DU[:, h, :], ACT.Exp, scale=-1.0).then_inc(e_done, 1)
                    for h in range(2):
                        act.wait_ge(e_done, h + 1)
                        nc.scalar.activation(DU[:, h, :], DU[:, h, :], ACT.Ln, bias=1.0).then_inc(ln_done, 1)

            with stage(nc, "b_ready", "c_ready", "b_copied", "a_done", "bu_done", "scanned", "hc_done", "y_added", "y_done") as (block, b_ready, c_ready, b_copied, a_done, bu_done, scanned, hc_done, y_added, y_done):
                @block.tensor
                def _(pe):
                    def spread(row, bank, ready):
                        for t in range(2):
                            mm = nc.tensor.matmul(PS[:, bank + t, :], SELR[:, row, :], BCP[:, blk(t)], start=True, stop=True)
                        mm.then_inc(ready, 1)

                    def add(n, h):
                        pe.wait_ge(hc_done, 2 * n + h + 1)
                        for t in range(2):
                            mm = nc.tensor.matmul(PS[:, 2 * h + t, :], k.ident[:, :], HC[:, n % 2, h, blk(t)], start=(n == 0), stop=(n == NS - 1))
                        mm.then_inc(y_added, 1)

                    spread(0, 4, b_ready)
                    spread(NS, 6, c_ready)
                    pe.wait_ge(b_copied, 1)
                    spread(1, 4, b_ready)
                    for n in range(NS):
                        if n < NS - 2:
                            pe.wait_ge(b_copied, n + 2)
                            spread(n + 2, 4, b_ready)
                        if n < NS - 1:
                            pe.wait_ge(hc_done, 2 * n + 2)
                            spread(NS + n + 1, 6, c_ready)
                        add(n, 0)
                        add(n, 1)

                @block.scalar
                def _(act):
                    for n in range(NS):
                        act.wait_ge(b_ready, n + 1)
                        if n >= 2:
                            act.wait_ge(bu_done, 2 * (n - 1))
                        nc.scalar.activation(BS[:, n % 2, :], PS[:, 4:6, :].rearrange("p a b -> p (a b)"), ACT.Identity).then_inc(b_copied, 1)
                        for h in range(2):
                            if n >= 2:
                                act.wait_ge(scanned, 2 * (n - 2) + h + 1)
                            nc.scalar.activation(DA[n % 2][:, h, :], DT[:, h, :], ACT.Exp, scale=A[:, h, n:n + 1]).then_inc(a_done, 1)

                @block.gpsimd
                def _(pool):
                    for n in range(NS):
                        for h in range(2):
                            pool.wait_ge(b_copied, n + 1)
                            if n >= 2:
                                pool.wait_ge(scanned, 2 * (n - 2) + h + 1)
                            pool.tensor_tensor(BU[n % 2][:, h, :], DU[:, h, :], BS[:, n % 2, :], ALU.mult).then_inc(bu_done, 1)

                @block.vector
                def _(dve):
                    for n in range(NS):
                        for h in range(2):
                            m = 2 * n + h
                            dve.wait_ge(a_done, m + 1)
                            dve.wait_ge(bu_done, m + 1)
                            if m:
                                dve.wait_ge(hc_done, m)
                            nc.vector.tensor_tensor_scan(HS[:, :], DA[n % 2][:, h, :], BU[n % 2][:, h, :], 0.0, ALU.mult, ALU.add).then_inc(scanned, 1)
                            dve.wait_ge(scanned, m + 1)
                            dve.wait_ge(c_ready, n + 1)
                            if n >= 2:
                                dve.wait_ge(y_added, 2 * (n - 2) + h + 1)
                            nc.vector.tensor_tensor(HC[:, n % 2, h, :], HS[:, :], PS[:, 6:8, :].rearrange("p a b -> p (a b)"), ALU.mult).then_inc(hc_done, 1)
                    dve.wait_ge(y_added, 2 * NS)
                    for h in range(2):
                        y = PS[:, 2 * h:2 * h + 2, :].rearrange("p a b -> p (a b)")
                        nc.vector.scalar_tensor_tensor(out=UC[:, h, :], in0=UC[:, h, :], scalar=W["L0_attn_b_D"][:, h:h + 1], in1=y, op0=ALU.mult, op1=ALU.add).then_inc(y_done, 1)
                    for h in range(2):
                        dve.wait_ge(y_done, h + 1)
                        nc.vector.tensor_tensor(UC[:, h, :], UC[:, h, :], Z[:, h, :], ALU.mult).then_inc(y_done, 1)
                    dve.wait_ge(y_done, 4)

            with stage(nc, "out_ready", "added") as (block, out_ready, added):
                @block.tensor
                def _(pe):
                    for t in range(2):
                        for h in range(2):
                            mm = nc.tensor.matmul(PS[:, t, :], W["L0_attn_b_W_out"][:, h, :], UC[:, h, blk(t)], start=(h == 0), stop=(h == 1))
                        mm.then_inc(out_ready, 1)

                @block.vector
                def _(dve):
                    for t in range(2):
                        dve.wait_ge(out_ready, t + 1)
                        xb = k.X[:, bass.ds(tok + t * BLK, BLK)]
                        nc.vector.tensor_tensor(xb, xb, PS[:, t, :], ALU.add).then_inc(added, 1)
                    dve.wait_ge(added, 2)



def head_constants(k, pool, own, out, scale, size=32):
    own(pool.memset(out, scale))
    v = out.rearrange("p (h d) -> p h d", d=size)
    own(pool.affine_select(out=v, in_=v, compare_op=ALU.is_ge, fill=0.0, base=0, pattern=[[-size, P // size], [0, size]], channel_multiplier=1))
    own(pool.affine_select(out=v, in_=v, compare_op=ALU.is_ge, fill=0.0, base=size - 1, pattern=[[size, P // size], [0, size]], channel_multiplier=-1))


def l2a(k):
    nc, PS, W = k.nc, k.PS, k.W
    DK = 16
    pre = "L2_attn_a_"
    with ExitStack() as st:
        def sb(n, shape, dt=F32):
            return k.sbuf(st, n, shape, dt)
        XS = sb("rw_x", [P, 1 + SEQ])
        DX, XX, XP, XP5 = sb("rw_dx", [P, SEQ]), sb("rw_xx", [P, 5, SEQ]), sb("rw_xp", [P, SEQ]), sb("rw_xp5", [32, SEQ])
        RKD = sb("rw_rkd", [P, 3, SEQ])
        HM, LOW = sb("rw_hm", [P, 3, SEQ], BF16), sb("rw_low", [P, 3, SEQ], BF16)
        T64 = sb("rw_t64", [64, SEQ])
        V, G = sb("rw_v", [P, SEQ]), sb("rw_g", [P, SEQ])
        KV, SS, SR = sb("rw_kv", [P, 2, SEQ]), sb("rw_ss", [P, 1 + SEQ]), sb("rw_sr", [P, 2, SEQ])
        SEL = sb("rw_sel", [P, DK, P], BF16)
        HO, BM = sb("rw_ho", [64, P]), sb("rw_bm", [P, P])
        def layer_constants(pool, own):
            own(pool.memset(XS[:, 0:1], 0.0))
            own(pool.memset(SS[:, 0:1], 0.0))
            head_constants(k, pool, own, BM[:, :], 1.0 / 32)
            own(pool.memset(SEL[:, :, :], 0.0))
            v = SEL[:, :, :].rearrange("q d (h v) -> q d h v", v=32)
            for part in range(2):
                own(pool.affine_select(out=v, in_=v, compare_op=ALU.not_equal, fill=1.0, base=-64 * part, pattern=[[-1, DK], [-DK, 4], [0, 32]], channel_multiplier=1))
            own(pool.memset(HO[:, :], 1.0))
            v = HO[:, :].rearrange("q (h v) -> q h v", v=32)
            own(pool.affine_select(out=v, in_=v, compare_op=ALU.is_ge, fill=0.0, base=0, pattern=[[-DK, 4], [0, 32]], channel_multiplier=1))
            own(pool.affine_select(out=v, in_=v, compare_op=ALU.is_ge, fill=0.0, base=DK - 1, pattern=[[DK, 4], [0, 32]], channel_multiplier=-1))

        layernorm(k, k.X, k.XN, beside=layer_constants)
        wide = lambda a: PS[:, a:a + 2, :].rearrange("p a b -> p (a b)")
        wide64 = lambda a: PS[0:64, a:a + 2, :].rearrange("p a b -> p (a b)")
        with nc.Fori(0, NTOK - SEQ + 1, SEQ) as tok:
            with stage(nc, "x_done", "xx_done", "xp_ready", "xp_done", "mu_ready", "mu_used", "own_d") as (block, x_done, xx_done, xp_ready, xp_done, mu_ready, mu_used, own_d):
                @block.scalar
                def _(act):
                    nc.scalar.activation(XS[:, 1:], k.XN[:, bass.ds(tok, SEQ)], ACT.Identity).then_inc(x_done, 1)
                    act.wait_ge(xp_ready, 2)
                    nc.scalar.activation(XP[:, :], wide(0), ACT.Tanh).then_inc(xp_done, 1)
                    nc.scalar.activation(XP5[:, :], PS[0:32, 2:4, :].rearrange("p a b -> p (a b)"), ACT.Tanh).then_inc(xp_done, 1)

                @block.vector
                def _(dve):
                    own = Link(dve, own_d)
                    dve.wait_ge(x_done, 1)
                    own(nc.vector.tensor_tensor(DX[:, :], XS[:, 0:SEQ], XS[:, 1:], ALU.subtract))
                    nc.vector.scalar_tensor_tensor(out=XX[:, 0, :], in0=DX[:, :], scalar=W[pre + "mu0"], in1=XS[:, 1:], op0=ALU.mult, op1=ALU.add).then_inc(xx_done, 1)
                    for i in range(5):
                        dve.wait_ge(mu_ready, i + 1)
                        if i == 0:
                            dve.wait_ge(xp_ready, 2)
                        nc.vector.scalar_tensor_tensor(out=XX[:, i, :], in0=wide(4 + 2 * (i % 2)), scalar=W[pre + "x_bias"][:, i:i + 1], in1=DX[:, :], op0=ALU.add, op1=ALU.mult).then_inc(mu_used, 1)
                        dve.wait_ge(mu_used, i + 1)
                        own(nc.vector.tensor_tensor(XX[:, i, :], XX[:, i, :], XS[:, 1:], ALU.add))

                @block.tensor
                def _(pe):
                    pe.wait_ge(xx_done, 1)
                    for t in range(2):
                        nc.tensor.matmul(PS[:, t, :], W[pre + "W_x0"][:, 0:P], XX[:, 0, blk(t)], start=True, stop=True)
                    for t in range(2):
                        nc.tensor.matmul(PS[0:32, 2 + t, :], W[pre + "W_x0"][:, P:160], XX[:, 0, blk(t)], start=True, stop=True).then_inc(xp_ready, 1)
                    pe.wait_ge(xp_done, 2)
                    for i in range(5):
                        if i >= 2:
                            pe.wait_ge(mu_used, i - 1)
                        q = slice(32 * i, 32 * i + 32) if i < 4 else slice(0, 32)
                        w = W[pre + "W_x2a"][q, :] if i < 4 else W[pre + "W_x2b"][q, :]
                        for t in range(2):
                            mm = nc.tensor.matmul(PS[:, 4 + 2 * (i % 2) + t, :], w, (XP if i < 4 else XP5)[q, blk(t)], start=True, stop=True)
                        mm.then_inc(mu_ready, 1)

            with stage(nc, "p_ready", "rkv_done", "w1_done", "w2_ready", "w_done", "g_done", "ruk_done", "own_a", "own_d") as (block, p_ready, rkv_done, w1_done, w2_ready, w_done, g_done, ruk_done, own_a, own_d):
                @block.tensor
                def _(pe):
                    for n, (w, i, m) in enumerate((("W_w1", 1, 64), ("W_r2", 0, P), ("W_k2", 2, P), ("W_v", 3, P))):
                        for t in range(2):
                            mm = nc.tensor.matmul(PS[0:m, 2 * n + t, :], W[pre + w], XX[:, i, blk(t)], start=True, stop=True)
                        mm.then_inc(p_ready, 1)
                    pe.wait_ge(w1_done, 1)
                    for t in range(2):
                        mm = nc.tensor.matmul(PS[:, t, :], W[pre + "W_w22"][0:64, :], T64[:, blk(t)], start=True, stop=True)
                    mm.then_inc(w2_ready, 1)
                    pe.wait_ge(rkv_done, 1)
                    for t in range(2):
                        mm = nc.tensor.matmul(PS[:, 2 + t, :], W[pre + "W_g"], XX[:, 4, blk(t)], start=True, stop=True)
                    mm.then_inc(p_ready, 1)
                    pe.wait_ge(ruk_done, 1)
                    for t in range(2):
                        mm = nc.tensor.matmul(PS[:, 4 + t, :], HO[:, :], T64[:, blk(t)], start=True, stop=True)
                    mm.then_inc(p_ready, 1)

                @block.scalar
                def _(act):
                    act.wait_ge(p_ready, 1)
                    nc.scalar.activation(T64[:, :], wide64(0), ACT.Tanh).then_inc(w1_done, 1)
                    act.wait_ge(w2_ready, 1)
                    nc.scalar.activation(RKD[:, 2, :], wide(0), ACT.Exp, bias=W[pre + "b_w22"]).then_inc(own_a, 1)
                    act.wait_ge(own_a, 1)
                    nc.scalar.activation(RKD[:, 2, :], RKD[:, 2, :], ACT.Exp, scale=-1.0).then_inc(w_done, 1)
                    act.wait_ge(p_ready, 5)
                    nc.scalar.activation(G[:, :], wide(2), ACT.Silu).then_inc(g_done, 1)

                @block.vector
                def _(dve):
                    own = Link(dve, own_d)
                    for n in range(3):
                        dve.wait_ge(p_ready, n + 2)
                        dst = RKD[:, n, :] if n < 2 else V[:, :]
                        nc.vector.tensor_copy(dst, wide(2 + 2 * n)).then_inc(rkv_done, 1)
                    dve.wait_ge(rkv_done, 3)
                    dve.wait_ge(w2_ready, 1)
                    own(nc.vector.tensor_scalar(T64[:, :], RKD[0:64, 0, :], W[pre + "bonus"][0:64, :], None, ALU.mult))
                    nc.vector.tensor_tensor(T64[:, :], T64[:, :], RKD[0:64, 1, :], ALU.mult).then_inc(ruk_done, 1)
                    dve.wait_ge(p_ready, 6)
                    own(nc.vector.tensor_tensor(DX[:, :], V[:, :], wide(4), ALU.mult))

            with stage(nc, "high_done", "rest_done", "mid_done", "low_done") as (block, high_done, rest_done, mid_done, low_done):
                @block.scalar
                def _(act):
                    for n in range(3):
                        nc.scalar.activation(HM[:, n, :], RKD[:, n, :], ACT.Identity).then_inc(high_done, 1)
                    for n in range(3):
                        act.wait_ge(rest_done, n + 1)
                        nc.scalar.activation(HM[64:P, n, :], RKD[64:P, n, :], ACT.Identity).then_inc(mid_done, 1)

                @block.vector
                def _(dve):
                    for n in range(3):
                        dve.wait_ge(high_done, n + 1)
                        nc.vector.tensor_tensor(RKD[64:P, n, :], RKD[64:P, n, :], HM[64:P, n, :], ALU.subtract).then_inc(rest_done, 1)
                    for n in range(3):
                        dve.wait_ge(mid_done, n + 1)
                        nc.vector.tensor_tensor(LOW[64:P, n, :], RKD[64:P, n, :], HM[64:P, n, :], ALU.subtract).then_inc(low_done, 1)
                    dve.wait_ge(low_done, 3)

            with stage(nc, "k_ready", "d_ready", "r_ready", "kv_done", "scanned", "sr_done", "o_added", "own_d") as (block, k_ready, d_ready, r_ready, kv_done, scanned, sr_done, o_added, own_d):
                @block.tensor
                def _(pe):
                    def spread(n, what, bank, ready):
                        for t in range(2):
                            nc.tensor.matmul(PS[:, bank + t, :], SEL[:, n, :], HM[:, what, blk(t)], start=True, stop=False)
                            mm = nc.tensor.matmul(PS[:, bank + t, :], SEL[64:P, n, :], LOW[64:P, what, blk(t)], start=False, stop=True)
                        mm.then_inc(ready, 1)

                    for n in range(DK):
                        if n:
                            pe.wait_ge(kv_done, n)
                        spread(n, 1, 0, k_ready)
                        if n:
                            pe.wait_ge(scanned, n)
                        spread(n, 2, 2, d_ready)
                        if n:
                            pe.wait_ge(sr_done, n)
                        spread(n, 0, 4, r_ready)
                        if n:
                            for t in range(2):
                                mm = nc.tensor.matmul(PS[:, 6 + t, :], k.ident[:, :], SR[:, (n - 1) % 2, blk(t)], start=(n == 1), stop=False)
                            mm.then_inc(o_added, 1)
                    pe.wait_ge(sr_done, DK)
                    for t in range(2):
                        mm = nc.tensor.matmul(PS[:, 6 + t, :], k.ident[:, :], SR[:, (DK - 1) % 2, blk(t)], start=False, stop=True)
                    mm.then_inc(o_added, 1)

                @block.vector
                def _(dve):
                    own = Link(dve, own_d)
                    for n in range(DK):
                        dve.wait_ge(k_ready, n + 1)
                        nc.vector.tensor_tensor(KV[:, 0, :], V[:, :], wide(0), ALU.mult).then_inc(kv_done, 1)
                        dve.wait_ge(kv_done, n + 1)
                        dve.wait_ge(d_ready, n + 1)
                        nc.vector.tensor_tensor_scan(SS[:, 1:], wide(2), KV[:, 0, :], 0.0, ALU.mult, ALU.add).then_inc(scanned, 1)
                        dve.wait_ge(scanned, n + 1)
                        dve.wait_ge(r_ready, n + 1)
                        if n >= 2:
                            dve.wait_ge(o_added, n - 1)
                        nc.vector.tensor_tensor(SR[:, n % 2, :], SS[:, 0:SEQ], wide(4), ALU.mult).then_inc(sr_done, 1)
                        dve.wait_ge(sr_done, n + 1)
                    dve.wait_ge(o_added, DK)
                    own(nc.vector.tensor_tensor(V[:, :], DX[:, :], wide(6), ALU.add))

            with stage(nc, "mean_ready", "centered", "squared", "var_ready", "std_done", "o_done", "y_ready", "own_d") as (block, mean_ready, centered, squared, var_ready, std_done, o_done, y_ready, own_d):
                @block.tensor
                def _(pe):
                    for t in range(2):
                        nc.tensor.matmul(PS[:, t, :], BM[:, :], V[:, blk(t)], start=True, stop=True).then_inc(mean_ready, 1)
                    for t in range(2):
                        pe.wait_ge(squared, 1)
                        nc.tensor.matmul(PS[:, 2 + t, :], BM[:, :], DX[:, blk(t)], start=True, stop=True).then_inc(var_ready, 1)
                    pe.wait_ge(o_done, 1)
                    for t in range(2):
                        nc.tensor.matmul(PS[:, 4 + t, :], W[pre + "W_o"], V[:, blk(t)], start=True, stop=True).then_inc(y_ready, 1)

                @block.scalar
                def _(act):
                    act.wait_ge(centered, 1)
                    nc.scalar.activation(DX[:, :], V[:, :], ACT.Square).then_inc(squared, 1)
                    act.wait_ge(var_ready, 2)
                    nc.scalar.activation(DX[:, :], wide(2), ACT.Sqrt, bias=k.eps_col[:, 0:1]).then_inc(std_done, 1)

                @block.vector
                def _(dve):
                    own = Link(dve, own_d)
                    dve.wait_ge(mean_ready, 2)
                    nc.vector.tensor_tensor(V[:, :], V[:, :], wide(0), ALU.subtract).then_inc(centered, 1)
                    dve.wait_ge(std_done, 1)
                    own(nc.vector.reciprocal(DX[:, :], DX[:, :]))
                    own(nc.vector.tensor_tensor(V[:, :], V[:, :], DX[:, :], ALU.mult))
                    own(nc.vector.tensor_scalar(V[:, :], V[:, :], W[pre + "gn_weight"], W[pre + "gn_bias"], ALU.mult, ALU.add))
                    nc.vector.tensor_tensor(V[:, :], V[:, :], G[:, :], ALU.mult).then_inc(o_done, 1)
                    for t in range(2):
                        dve.wait_ge(y_ready, t + 1)
                        xb = k.X[:, bass.ds(tok + t * BLK, BLK)]
                        own(nc.vector.tensor_tensor(xb, xb, PS[:, 4 + t, :], ALU.add))



def l0a(k):
    nc, PS, W = k.nc, k.PS, k.W
    pre = "L0_attn_a_"
    CH, NC = 32, SEQ // 32
    GC = 4
    DECAY = 1.0 - 1.0 / 3000.0
    FLOOR = 0.08 * DECAY
    with ExitStack() as st:
        def sb(n, shape, dt=F32):
            return k.sbuf(st, n, shape, dt)
        wide = lambda a: PS[:, a:a + 2, :].rearrange("p a b -> p (a b)")
        PADC, PADL = 3, 63
        HS_, HMASK = sb("dl_hs", [P, P]), sb("dl_hm", [P, 4])
        STL, STU, UPI = sb("dl_stl", [P, P]), sb("dl_stu", [P, P]), sb("dl_upi", [P, P])
        WBX = sb("dl_wb", [P, 4, 32])
        W2X = sb("dl_w2", [P, 4, 32])
        E3 = sb("dl_e3", [P, 4, 32])
        CB, TMP4 = sb("dl_cb", [P, 5]), sb("dl_t4", [P, 4])
        QI = [sb(f"dl_in{n}", [P, PADC + SEQ]) for n in range(3)]
        ARENA = sb("dl_arena", [P, 8, SEQ])
        Q, KK, KB, BETA, VC, KC, KBC = (ARENA[:, n, :] for n in range(7))
        VP = sb("dl_vp", [P, PADL + SEQ])
        V = VP[:, PADL:]
        OC = sb("dl_oc", [P, SEQ])
        FS, FL = k.lnA[:, 0:SEQ], k.lnA[:, SEQ:]
        OD = sb("dl_od", [P, SEQ])
        S = sb("dl_S", [P, 32])
        eps6 = sb("dl_eps6", [P, 1])
        def layer_constants(pool, own):
            head_constants(k, pool, own, HS_[:, :], 1.0)
            own(pool.memset(HMASK[:, :], 1.0))
            own(pool.affine_select(out=HMASK[:, :], in_=HMASK[:, :], compare_op=ALU.is_ge, fill=0.0, base=0, pattern=[[-32, 4]], channel_multiplier=1))
            own(pool.affine_select(out=HMASK[:, :], in_=HMASK[:, :], compare_op=ALU.is_ge, fill=0.0, base=31, pattern=[[32, 4]], channel_multiplier=-1))
            own(pool.memset(STL[:, :], -1.0))
            own(pool.affine_select(out=STL[:, :], in_=STL[:, :], compare_op=ALU.is_gt, fill=0.0, base=0, pattern=[[-1, P]], channel_multiplier=1))
            own(pool.memset(STU[:, :], -1.0))
            own(pool.affine_select(out=STU[:, :], in_=STU[:, :], compare_op=ALU.is_gt, fill=0.0, base=0, pattern=[[1, P]], channel_multiplier=-1))
            own(pool.memset(UPI[:, :], 1.0))
            own(pool.affine_select(out=UPI[:, :], in_=UPI[:, :], compare_op=ALU.is_ge, fill=0.0, base=0, pattern=[[1, P]], channel_multiplier=-1))
            own(pool.memset(E3[:, :, :], 0.0))
            own(pool.memset(eps6[:, :], 1e-6))
            for n in range(3):
                own(pool.memset(QI[n][:, 0:PADC], 0.0))
            own(pool.memset(VP[:, 0:PADL], 0.0))

        layernorm(k, k.X, k.XN, beside=layer_constants)
        with stage(nc, "exp_done", "own_d") as (block, exp_done, own_d):
            @block.scalar
            def _(act):
                nc.scalar.activation(TMP4[:, :], W[pre + "log_temp"], ACT.Exp, scale=-1.0).then_inc(exp_done, 1)

            @block.vector
            def _(dve):
                own = Link(dve, own_d)
                dve.wait_ge(exp_done, 1)
                nc.vector.tensor_copy(WBX[:, :, :], W[pre + "Wb"].unsqueeze(2).to_broadcast([P, 4, 32]))
                nc.vector.tensor_copy(W2X[:, :, :], W[pre + "W2"].unsqueeze(2).to_broadcast([P, 4, 32]))
                for q in range(4):
                    v = E3[:, q, 0:16].rearrange("p (h q) -> p h q", q=4)[:, :, q]
                    nc.vector.tensor_scalar(v, HMASK[:, :], 1.0 / 32, None, ALU.mult)
                own(nc.vector.tensor_tensor(TMP4[:, :], TMP4[:, :], HMASK[:, :], ALU.mult))
                own(nc.vector.tensor_reduce(CB[:, 4:5], TMP4[:, :], AX.X, ALU.add))
                own(nc.vector.tensor_tensor(TMP4[:, :], W[pre + "copy_bias"], HMASK[:, :], ALU.mult))
                own(nc.vector.tensor_reduce(CB[:, 3:4], TMP4[:, :], AX.X, ALU.add))
                own(nc.vector.tensor_copy(CB[:, 0:3], W[pre + "b2"][:, 0:3]))
                own(nc.vector.scalar_tensor_tensor(out=CB[:, 3:4], in0=CB[:, 3:4], scalar=DECAY, in1=W[pre + "b2"][:, 3:4], op0=ALU.mult, op1=ALU.add))

        @contextmanager
        def batches():
            with nc.Fori(0, NTOK - SEQ + 1, SEQ) as tok:
                yield tok

        with batches() as tok:
            with stage(nc, "p_ready", "in_done", "conv_done", "act_done", "beta_ready", "own_d") as (block, p_ready, in_done, conv_done, act_done, beta_ready, own_d):
                @block.tensor
                def _(pe):
                    for n, w in enumerate(("Wq", "Wk", "Wv")):
                        for t in range(2):
                            mm = nc.tensor.matmul(PS[:, 2 * n + t, :], W[pre + w], k.XN[:, bass.ds(tok + t * BLK, BLK)], start=True, stop=True)
                        mm.then_inc(p_ready, 1)
                    for t in range(2):
                        mm = nc.tensor.matmul(PS[:, 6 + t, :], WBX[:, :, :].rearrange("p a b -> p (a b)"), k.XN[:, bass.ds(tok + t * BLK, BLK)], start=True, stop=True)
                    mm.then_inc(beta_ready, 1)

                @block.scalar
                def _(act):
                    for n in range(3):
                        act.wait_ge(p_ready, n + 1)
                        nc.scalar.activation(QI[n][:, PADC:], wide(2 * n), ACT.Identity).then_inc(in_done, 1)
                    act.wait_ge(beta_ready, 1)
                    nc.scalar.activation(BETA[:, :], wide(6), ACT.Sigmoid).then_inc(act_done, 1)
                    for n, dst in enumerate((Q[:, :], KK[:, :], V)):
                        act.wait_ge(conv_done, n + 1)
                        nc.scalar.activation(dst, dst, ACT.Silu).then_inc(act_done, 1)

                @block.vector
                def _(dve):
                    own = Link(dve, own_d)
                    for n, dst in enumerate((Q[:, :], KK[:, :], V)):
                        dve.wait_ge(in_done, n + 1)
                        w = W[pre + "conv"]
                        own(nc.vector.tensor_scalar(dst, QI[n][:, 0:SEQ], w[:, n, 0:1], None, ALU.mult))
                        for j in range(1, 4):
                            ins = nc.vector.scalar_tensor_tensor(out=dst, in0=QI[n][:, j:j + SEQ], scalar=w[:, n, j:j + 1], in1=dst, op0=ALU.mult, op1=ALU.add)
                            if j < 3:
                                own(ins)
                        ins.then_inc(conv_done, 1)

            with stage(nc, "squared", "sum_ready", "root_done", "own_d") as (block, squared, sum_ready, root_done, own_d):
                @block.scalar
                def _(act):
                    for n, src in enumerate((Q, KK)):
                        nc.scalar.activation((FS, FL)[n][:, :], src[:, :], ACT.Square).then_inc(squared, 1)
                    for n in range(2):
                        act.wait_ge(sum_ready, n + 1)
                        nc.scalar.activation((FS, FL)[n][:, :], wide(2 * n), ACT.Sqrt, bias=eps6[:, 0:1]).then_inc(root_done, 1)

                @block.tensor
                def _(pe):
                    for n in range(2):
                        pe.wait_ge(squared, n + 1)
                        for t in range(2):
                            mm = nc.tensor.matmul(PS[:, 2 * n + t, :], HS_[:, :], (FS, FL)[n][:, blk(t)], start=True, stop=True)
                        mm.then_inc(sum_ready, 1)

                @block.vector
                def _(dve):
                    own = Link(dve, own_d)
                    own(nc.vector.tensor_tensor(OD[:, :], V, BETA[:, :], ALU.mult))
                    own(nc.vector.transpose(VC[:, :], OD[:, :]))
                    for n, dst in enumerate((Q, KK)):
                        dve.wait_ge(root_done, n + 1)
                        f = (FS, FL)[n]
                        own(nc.vector.reciprocal(f[:, :], f[:, :]))
                        own(nc.vector.tensor_tensor(dst[:, :], dst[:, :], f[:, :], ALU.mult))
                    own(nc.vector.tensor_tensor(KB[:, :], KK[:, :], BETA[:, :], ALU.mult))
                    nc.vector.transpose(KC[:, :], KK[:, :])
                    own(nc.vector.transpose(KBC[:, :], KB[:, :]))
                    own(nc.vector.memset(S[:, :], 0.0))

            with ExitStack() as st2:
                def sb2(n):
                    return k.sbuf(st2, n, [P, GC, P], F32)
                Qxs, Kcxs, WTs, ATs = ([sb2(f"dl_{n}{c}") for c in range(2)] for n in ("qx", "kcx", "wt", "at"))
                UUs = [k.sbuf(st2, f"dl_uu{c}", [P, GC, 32]) for c in range(2)]
                Kx, Kbx, Kbcx = (sb2("dl_" + n) for n in ("kx", "kbx", "kbcx"))
                POW = [sb2("dl_p0"), sb2("dl_p1")]
                POT = [sb2("dl_q0"), sb2("dl_q1")]
                TT = sb2("dl_tt")
                UI = k.sbuf(st2, "dl_ui", [P, 32], F32)
                STEP = GC * CH
                WIN, RINGS = k.sbuf(st2, "dl_win", [P, PADL + STEP]), 8
                YS, YL, YD = (k.sbuf(st2, "dl_y" + n, [P, STEP]) for n in "sld")
                RING = k.sbuf(st2, "dl_ring", [P, RINGS, STEP])
                ON_DVE = 24
                TAPS = [(YS, j, W[pre + "fir_s"][:, j:j + 1]) for j in range(5)] + [(YL, j, W[pre + "fir_l"][:, j:j + 1]) for j in range(64 - ON_DVE)]

                def chunk_pass(at, turn, matrices, state):
                    Qx, Kcx, WT, AT, UU = Qxs[turn], Kcxs[turn], WTs[turn], ATs[turn], UUs[turn]
                    Qo, Kco, WTo, ATo, UUo = (x[1 - turn] for x in (Qxs, Kcxs, WTs, ATs, UUs))
                    BW, BO = 6, 7
                    with stage(nc, "spread_done", "prod", "taken", "ws_ready", "u_done", "o_ready", "ks_ready", "s_done", "o_taken", "window_done", "scaled", "added", "fir_done", "dve_taps") as (block, spread_done, prod, taken, ws_ready, u_done, o_ready, ks_ready, s_done, o_taken, window_done, scaled, added, fir_done, dve_taps):
                        bank = lambda a: PS[:, a, :].rearrange("p (c n) -> p c n", n=P)

                        @block.gpsimd
                        def _(pool):
                            if not matrices:
                                return
                            for m, (y, tap, w) in enumerate(TAPS):
                                pool.wait_ge(scaled, m + 1)
                                if m:
                                    pool.wait_ge(added, m)
                                if tap:
                                    nc.gpsimd.tensor_tensor(y[:, :], y[:, :], RING[:, m % RINGS, :], ALU.add).then_inc(added, 1)
                                else:
                                    nc.gpsimd.tensor_copy(y[:, :], RING[:, m % RINGS, :]).then_inc(added, 1)

                        @block.vector
                        def _(dve):
                            def state_u(c):
                                dve.wait_ge(ws_ready, c + 1)
                                if c:
                                    dve.wait_ge(o_ready, c)
                                nc.vector.tensor_tensor(UI[:, :], UUo[:, c, :], PS[:, BW, 0:32], ALU.subtract).then_inc(u_done, 1)

                            def state_s(c):
                                dve.wait_ge(ks_ready, c + 1)
                                nc.vector.tensor_tensor(S[:, :], S[:, :], PS[:, BW, 32:64], ALU.add).then_inc(s_done, 1)
                                dve.wait_ge(s_done, c + 1)

                            own = Link(dve, dve_taps)

                            def taps(part):
                                for j in range(64 - ON_DVE + ON_DVE // 8 * part, 64 - ON_DVE + ON_DVE // 8 * (part + 1)):
                                    w = W[pre + "fir_l"][:, j:j + 1]
                                    if j == 64 - ON_DVE:
                                        dve.wait_ge(window_done, 1)
                                        own(nc.vector.tensor_scalar(YD[:, :], WIN[:, j:j + STEP], w, None, ALU.mult))
                                    else:
                                        own(nc.vector.scalar_tensor_tensor(out=YD[:, :], in0=WIN[:, j:j + STEP], scalar=w, in1=YD[:, :], op0=ALU.mult, op1=ALU.add))

                            def m(x):
                                return x[:, :].unsqueeze(1).to_broadcast([P, GC, P])
                            if matrices:
                                hm = HMASK[:, :].unsqueeze(1).unsqueeze(3).to_broadcast([P, GC, 4, 32])
                                for dst, src in ((Kx, KK), (Kbx, KB), (Qx, Q), (Kbcx, KBC), (Kcx, KC)):
                                    v = src[:, bass.ds(at, STEP)].rearrange("p (c i) -> p c i", i=CH).unsqueeze(2).to_broadcast([P, GC, 4, 32])
                                    nc.vector.tensor_tensor(dst[:, :, :].rearrange("p c (h i) -> p c h i", h=4), v, hm, ALU.mult).then_inc(spread_done, 1)
                                dve.wait_ge(prod, 1)
                                nc.vector.tensor_tensor(POW[0][:, :, :], bank(0), m(STL), ALU.mult).then_inc(taken, 1)
                                dve.wait_ge(prod, 2)
                                nc.vector.tensor_tensor(POT[0][:, :, :], bank(1), m(STU), ALU.mult).then_inc(taken, 1)
                                dve.wait_ge(taken, 2)
                                nc.vector.tensor_tensor(TT[:, :, :], POT[0][:, :, :], m(k.ident), ALU.add).then_inc(taken, 1)
                                dve.wait_ge(prod, 3)
                                nc.vector.tensor_tensor(AT[:, :, :], bank(2), m(UPI), ALU.mult).then_inc(taken, 1)
                            for n in range(4):
                                if state:
                                    state_u(n)
                                if matrices:
                                    dve.wait_ge(prod, 3 * n + 4)
                                    nc.vector.tensor_copy(POW[(n + 1) % 2][:, :, :], bank(3)).then_inc(taken, 1)
                                    dve.wait_ge(prod, 3 * n + 5)
                                    nc.vector.tensor_copy(POT[(n + 1) % 2][:, :, :], bank(4)).then_inc(taken, 1)
                                if state:
                                    state_s(n)
                                if matrices:
                                    taps(2 * n)
                                    dve.wait_ge(prod, 3 * n + 6)
                                    nc.vector.tensor_tensor(TT[:, :, :], TT[:, :, :], bank(5), ALU.add).then_inc(taken, 1)
                                    dve.wait_ge(taken, 3 * n + 7)
                                    taps(2 * n + 1)
                            if matrices:
                                dve.wait_ge(prod, 16)
                                nc.vector.tensor_copy(WT[:, :, :], bank(0)).then_inc(taken, 1)
                                nc.vector.tensor_copy(UU[:, :, :], PS[:, 1, 0:GC * 32].rearrange("p (c n) -> p c n", n=32)).then_inc(taken, 1)
                                dve.wait_ge(taken, 18)
                                dve.wait_ge(added, len(TAPS))
                                own(nc.vector.tensor_tensor(FL[:, bass.ds(at, STEP)], YL[:, :], YD[:, :], ALU.add))

                        @block.tensor
                        def _(pe):
                            def each(a, left, right):
                                for c in range(GC):
                                    mm = nc.tensor.matmul(PS[:, a, blk(c, P)], left[:, c, :], right[:, c, :], start=True, stop=True)
                                mm.then_inc(prod, 1)

                            def state_w(c):
                                if c:
                                    pe.wait_ge(s_done, c)
                                nc.tensor.matmul(PS[:, BW, 0:32], WTo[:, c, :], S[:, :], start=True, stop=True).then_inc(ws_ready, 1)

                            def state_k(c):
                                if c:
                                    pe.wait_ge(o_taken, c)
                                nc.tensor.matmul(PS[:, BO, 0:32], Qo[:, c, :], S[:, :], start=True, stop=False)
                                pe.wait_ge(u_done, c + 1)
                                nc.tensor.matmul(PS[:, BW, 32:64], Kco[:, c, :], UI[:, :], start=True, stop=True).then_inc(ks_ready, 1)
                                nc.tensor.matmul(PS[:, BO, 0:32], ATo[:, c, :], UI[:, :], start=False, stop=True).then_inc(o_ready, 1)

                            if matrices:
                                pe.wait_ge(spread_done, 2)
                                each(0, Kbx, Kx)
                                each(1, Kx, Kbx)
                                pe.wait_ge(spread_done, 3)
                                each(2, Kx, Qx)
                            for n in range(4):
                                if state:
                                    state_w(n)
                                if matrices:
                                    pe.wait_ge(taken, 2 if n == 0 else 3 * n + 3)
                                    a, b = POW[n % 2], POT[n % 2]
                                    each(3, b, a)
                                    each(4, a, b)
                                if state:
                                    state_k(n)
                                if matrices:
                                    pe.wait_ge(taken, 3 * n + 5)
                                    each(5, POW[(n + 1) % 2], TT)
                            if matrices:
                                pe.wait_ge(taken, 16)
                                pe.wait_ge(spread_done, 4)
                                for c in range(GC):
                                    nc.tensor.matmul(PS[:, 0, blk(c, P)], Kbcx[:, c, :], TT[:, c, :], start=True, stop=True)
                                for c in range(GC):
                                    mm = nc.tensor.matmul(PS[:, 1, blk(c, 32)], TT[:, c, :], VC[:, bass.ds(at + c * CH, CH)], start=True, stop=True)
                                mm.then_inc(prod, 1)

                        @block.scalar
                        def _(act):
                            if matrices:
                                nc.scalar.activation(WIN[:, :], VP[:, bass.ds(at, PADL + STEP)], ACT.Identity).then_inc(window_done, 1)
                            for c in range(GC):
                                if matrices:
                                    for m in range(len(TAPS) * c // GC, len(TAPS) * (c + 1) // GC):
                                        y, tap, w = TAPS[m]
                                        off = tap + (PADL - 4 if y is YS else 0)
                                        if m == 0:
                                            act.wait_ge(window_done, 1)
                                        if m >= RINGS:
                                            act.wait_ge(added, m - RINGS + 1)
                                        nc.scalar.activation(RING[:, m % RINGS, :], WIN[:, off:off + STEP], ACT.Identity, scale=w).then_inc(scaled, 1)
                                if state:
                                    act.wait_ge(o_ready, c + 1)
                                    nc.scalar.activation(OC[:, bass.ds(at - STEP + c * CH, CH)], PS[:, BO, 0:32], ACT.Identity).then_inc(o_taken, 1)
                            if state:
                                act.wait_ge(o_taken, GC)
                            if matrices:
                                act.wait_ge(added, 5)
                                nc.scalar.activation(FS[:, bass.ds(at, STEP)], YS[:, :], ACT.Identity).then_inc(fir_done, 1)
                                act.wait_ge(fir_done, 1)

                chunk_pass(0, 0, True, False)
                with nc.Fori(STEP, SEQ - 3 * STEP + 1, 2 * STEP) as at:
                    chunk_pass(at, 1, True, True)
                    chunk_pass(at + STEP, 0, True, True)
                chunk_pass(SEQ - STEP, 1, True, True)
                chunk_pass(SEQ, 0, False, True)

            with ExitStack() as st2:
                def sb2(n, shape):
                    return k.sbuf(st2, n, shape, F32)
                SRC, SQ, AB, LG = (ARENA[:, 2 * n:2 * n + 2, :].rearrange("p a (b c) -> p (a b) c", c=BLK) for n in range(4))
                STA, H1 = sb2("dl_sta", [P, BLK]), sb2("dl_h1", [P, 4, BLK])
                MX, O = sb2("dl_mx", [P, BLK]), sb2("dl_o", [P, BLK])
                with stage(nc, "own_d") as (block, own_d):
                    @block.vector
                    def _(dve):
                        nc.vector.transpose(OD[:, :], OC[:, :]).then_inc(own_d, 1)
                        dve.wait_ge(own_d, 1)
                with nc.Fori(0, SEQ - BLK + 1, BLK) as tb:
                    with stage(nc, "src_done", "sq_done", "st_ready", "st_done", "mean_sq", "h_ready", "h_done", "own_d") as (block, src_done, sq_done, st_ready, st_done, mean_sq, h_ready, h_done, own_d):
                        @block.vector
                        def _(dve):
                            own = Link(dve, own_d)
                            for n, a in enumerate((FS, FL, OD)):
                                nc.vector.tensor_copy(SRC[:, n, :], a[:, bass.ds(tb, BLK)]).then_inc(src_done, 1)
                            nc.vector.tensor_copy(SRC[:, 3, :], VP[:, bass.ds(tb + PADL, BLK)]).then_inc(src_done, 1)
                            dve.wait_ge(st_ready, 5)
                            own(nc.vector.tensor_copy(STA[:, :], PS[:, 0, :]))
                            own(nc.vector.tensor_copy(MX[32:64, :], PS[32:64, 1, :]))
                            own(nc.vector.tensor_tensor(MX[32:64, :], MX[32:64, :], MX[32:64, :], ALU.mult))
                            nc.vector.tensor_tensor(STA[32:64, :], STA[32:64, :], MX[32:64, :], ALU.subtract).then_inc(mean_sq, 1)

                        @block.scalar
                        def _(act):
                            for n in range(4):
                                act.wait_ge(src_done, n + 1)
                                nc.scalar.activation(SQ[:, n, :], SRC[:, n, :], ACT.Square)
                                nc.scalar.activation(AB[:, n, :], SRC[:, n, :], ACT.Abs).then_inc(sq_done, 1)
                            act.wait_ge(mean_sq, 1)
                            nc.scalar.activation(STA[96:128, :], STA[96:128, :], ACT.Sqrt, scale=32.0).then_inc(st_done, 1)
                            for h in range(4):
                                act.wait_ge(h_ready, h + 1)
                                nc.scalar.activation(H1[:, h, :], PS[:, 2 + h, :], ACT.Gelu_apprx_tanh, bias=W[pre + "b1"]).then_inc(h_done, 1)

                        @block.tensor
                        def _(pe):
                            for n in range(4):
                                pe.wait_ge(sq_done, n + 1)
                                for bank, quarter, x in ((0, 0, SRC), (0, 1, SQ), (0, 2, AB), (0, 3, SQ), (1, 1, SRC)):
                                    mm = nc.tensor.matmul(PS[blk(quarter, 32), bank, :], E3[:, n, :], x[:, n, :], start=(n == 0), stop=(n == 3))
                                    if n == 3:
                                        mm.then_inc(st_ready, 1)
                            pe.wait_ge(st_done, 1)
                            for h in range(4):
                                nc.tensor.matmul(PS[:, 2 + h, :], W[pre + "W1x"], k.XN[:, bass.ds(tok + tb, BLK)], start=True, stop=False)
                                nc.tensor.matmul(PS[:, 2 + h, :], W[pre + "W1s"][:, h, :], STA[:, :], start=False, stop=True).then_inc(h_ready, 1)
                            for h in range(4):
                                pe.wait_ge(h_done, h + 1)
                            for j in range(4):
                                bank = (6, 7, 0, 1)[j]
                                for h in range(4):
                                    mm = nc.tensor.matmul(PS[blk(h, 32), bank, :], W2X[:, j, :], H1[:, h, :], start=True, stop=True)

                    with stage(nc, "shifted", "exp_done", "mixed", "sq_done", "ms_ready", "rt_done", "o_done", "y_ready", "own_d") as (block, shifted, exp_done, mixed, sq_done, ms_ready, rt_done, o_done, y_ready, own_d):
                        @block.vector
                        def _(dve):
                            own = Link(dve, own_d)
                            for j in range(4):
                                own(nc.vector.tensor_scalar(LG[:, j, :], PS[:, (6, 7, 0, 1)[j], :], CB[:, j:j + 1], CB[:, 4:5], ALU.add, ALU.mult))
                            own(nc.vector.tensor_tensor(SQ[:, 0:2, :], LG[:, 0:2, :], LG[:, 2:4, :], ALU.max))
                            own(nc.vector.tensor_tensor(MX[:, :], SQ[:, 0, :], SQ[:, 1, :], ALU.max))
                            nc.vector.tensor_tensor(LG[:, :, :], LG[:, :, :], MX[:, :].unsqueeze(1).to_broadcast([P, 4, BLK]), ALU.subtract).then_inc(shifted, 1)
                            dve.wait_ge(exp_done, 1)
                            own(nc.vector.tensor_tensor(SQ[:, 0:2, :], LG[:, 0:2, :], LG[:, 2:4, :], ALU.add))
                            own(nc.vector.tensor_tensor(MX[:, :], SQ[:, 0, :], SQ[:, 1, :], ALU.add))
                            own(nc.vector.reciprocal(MX[:, :], MX[:, :]))
                            own(nc.vector.scalar_tensor_tensor(out=LG[:, :, :], in0=LG[:, :, :], scalar=1.0 - 4.0 * FLOOR, in1=MX[:, :].unsqueeze(1).to_broadcast([P, 4, BLK]), op0=ALU.mult, op1=ALU.mult))
                            own(nc.vector.scalar_tensor_tensor(out=LG[:, :, :], in0=LG[:, :, :], scalar=FLOOR, in1=SRC[:, :, :], op0=ALU.add, op1=ALU.mult))
                            own(nc.vector.tensor_tensor(SQ[:, 0:2, :], LG[:, 0:2, :], LG[:, 2:4, :], ALU.add))
                            nc.vector.tensor_tensor(O[:, :], SQ[:, 0, :], SQ[:, 1, :], ALU.add).then_inc(mixed, 1)
                            dve.wait_ge(rt_done, 1)
                            dve.wait_ge(mixed, 1)
                            own(nc.vector.reciprocal(MX[:, :], MX[:, :]))
                            nc.vector.scalar_tensor_tensor(out=O[:, :], in0=O[:, :], scalar=W[pre + "o_norm_w"], in1=MX[:, :], op0=ALU.mult, op1=ALU.mult).then_inc(o_done, 1)
                            dve.wait_ge(y_ready, 1)
                            xb = k.X[:, bass.ds(tok + tb, BLK)]
                            own(nc.vector.tensor_tensor(xb, xb, PS[:, 3, :], ALU.add))

                        @block.scalar
                        def _(act):
                            act.wait_ge(shifted, 1)
                            nc.scalar.activation(LG[:, :, :], LG[:, :, :], ACT.Exp).then_inc(exp_done, 1)
                            act.wait_ge(mixed, 1)
                            nc.scalar.activation(AB[:, 0, :], O[:, :], ACT.Square).then_inc(sq_done, 1)
                            act.wait_ge(ms_ready, 1)
                            nc.scalar.activation(MX[:, :], PS[:, 2, :], ACT.Sqrt, scale=1.0 / 32, bias=k.eps_col[:, 0:1]).then_inc(rt_done, 1)

                        @block.tensor
                        def _(pe):
                            pe.wait_ge(sq_done, 1)
                            nc.tensor.matmul(PS[:, 2, :], HS_[:, :], AB[:, 0, :], start=True, stop=True).then_inc(ms_ready, 1)
                            pe.wait_ge(o_done, 1)
                            nc.tensor.matmul(PS[:, 3, :], W[pre + "Wo"], O[:, :], start=True, stop=True).then_inc(y_ready, 1)



def l1b(k):
    nc, PS, W = k.nc, k.PS, k.W
    pre = "L1_attn_b_"
    NHEAD, NHASH, NBIN = 8, 8, 16
    SELF = -1e5
    with ExitStack() as st:
        def sb(n, shape, dt=F32):
            return k.sbuf(st, n, shape, dt)
        OHT = sb("ls_oht", [P, 4, NTOK], BF16)
        V1 = sb("ls_v1", [P, NTILE, NHEAD, 17])
        RB = k.lnA[:, 0:NHEAD * NHASH * 8].rearrange("p (h n k) -> p h n k", h=NHEAD, n=NHASH)
        HM = sb("ls_hm", [P, NHEAD])
        W8 = sb("ls_w8", [P, 8])
        BASEM, SELP = sb("ls_basem", [P, P]), sb("ls_selp", [P, 2, P])
        HS16 = sb("ls_hs", [P, P])
        PC, BINC = sb("ls_pc", [P, 12]), sb("ls_binc", [P, 8])
        one = sb("ls_one", [P, 1])
        NI = sb("ls_ni", [P, P])
        SI = sb("ls_si", [P, P])
        SEL = sb("ls_sel", [P, 2, 2, HG, P], BF16)
        KX, QX = sb("ls_kx", [P, HG, SEQ], BF16), sb("ls_qx", [P, HG, SEQ], BF16)

        def layer_constants(pool, own):
            expansion_constants(k, pool, own, SEL, 16, KX, QX)
            own(pool.memset(V1[:, :, :, :], 1.0))
            own(pool.memset(one[:, :], 1.0))
            own(pool.memset(HM[:, :], 1.0))
            own(pool.affine_select(out=HM[:, :], in_=HM[:, :], compare_op=ALU.is_ge, fill=0.0, base=0, pattern=[[-16, 8]], channel_multiplier=1))
            own(pool.affine_select(out=HM[:, :], in_=HM[:, :], compare_op=ALU.is_ge, fill=0.0, base=15, pattern=[[16, 8]], channel_multiplier=-1))
            own(pool.iota(W8[:, :], [[-1, 8]], base=8, channel_multiplier=0, allow_small_or_imprecise_dtypes=True))
            own(pool.memset(BASEM[:, :], 1.0))
            own(pool.affine_select(out=BASEM[:, :], in_=BASEM[:, :], compare_op=ALU.is_gt, fill=0.0, base=0, pattern=[[1, P]], channel_multiplier=-1))
            v = BASEM[:, :].rearrange("p (a b) -> p a b", b=8)
            own(pool.affine_select(out=v, in_=v, compare_op=ALU.is_ge, fill=0.0, base=0, pattern=[[-8, 16], [0, 8]], channel_multiplier=1))
            own(pool.memset(SELP[:, :, :], 1.0))
            v = SELP[:, :, :].rearrange("p a (n b) -> p a n b", b=NBIN)
            own(pool.affine_select(out=v, in_=v, compare_op=ALU.is_ge, fill=0.0, base=0, pattern=[[-64, 2], [-8, 8], [0, NBIN]], channel_multiplier=1))
            own(pool.affine_select(out=v, in_=v, compare_op=ALU.is_ge, fill=0.0, base=7, pattern=[[64, 2], [8, 8], [0, NBIN]], channel_multiplier=-1))
            head_constants(k, pool, own, HS16[:, :], 1.0, 16)
            own(pool.iota(PC[:, 0:7], [[16, 7]], base=16, channel_multiplier=0, allow_small_or_imprecise_dtypes=True))
            own(pool.iota(PC[:, 7:8], [[0, 1]], base=0, channel_multiplier=1, allow_small_or_imprecise_dtypes=True))
            own(pool.affine_select(out=NI[:, :], in_=one[:, 0:1].to_broadcast([P, P]), compare_op=ALU.not_equal, fill=0.0, base=0, pattern=[[-1, P]], channel_multiplier=1))

        layernorm(k, k.X, k.XN, beside=layer_constants)
        with stage(nc, "own_d") as (block, own_d):
            @block.vector
            def _(dve):
                own = Link(dve, own_d)
                own(nc.vector.tensor_scalar(SI[:, :], k.ident[:, :], SELF, None, ALU.mult))
                rot = W[pre + "rot"].rearrange("p (n k) -> p n k", k=4).unsqueeze(1).to_broadcast([P, NHEAD, NHASH, 4])
                hm = HM[:, :].unsqueeze(2).unsqueeze(3).to_broadcast([P, NHEAD, NHASH, 4])
                own(nc.vector.tensor_tensor(RB[:, :, :, 0:4], rot, hm, ALU.mult))
                own(nc.vector.tensor_scalar(RB[:, :, :, 4:8], RB[:, :, :, 0:4], -1.0, None, ALU.mult))
                own(nc.vector.tensor_scalar(PC[:, 0:7], PC[:, 0:7], PC[:, 7:8], None, ALU.is_le))
                own(nc.vector.tensor_reduce(PC[:, 8:9], PC[:, 0:7], AX.X, ALU.add))
                own(nc.vector.scalar_tensor_tensor(out=PC[:, 9:10], in0=PC[:, 8:9], scalar=-16.0, in1=PC[:, 7:8], op0=ALU.mult, op1=ALU.add))
                own(nc.vector.tensor_scalar(PC[:, 10:11], PC[:, 9:10], 1.0, 32.0, ALU.is_equal, ALU.mult))
                own(nc.vector.tensor_scalar(BINC[:, 0:1], PC[:, 9:10], -64.0, -31.5, ALU.mult, ALU.add))
                own(nc.vector.tensor_scalar(BINC[:, 1:2], PC[:, 9:10], -64.0, -63.5, ALU.mult, ALU.add))
                own(nc.vector.tensor_tensor(BINC[:, 1:2], BINC[:, 1:2], PC[:, 10:11], ALU.add))
                own(nc.vector.tensor_scalar(BINC[:, 2:3], PC[:, 10:11], 64.0, None, ALU.add))
                own(nc.vector.memset(BINC[:, 3:4], 69.0))

        with ExitStack() as st2:
            def sb2(n, shape):
                return k.sbuf(st2, n, shape, F32)
            TG = BLK // P
            XC, QC = sb2("ls_xc", [P, BLK]), sb2("ls_qc", [P, BLK])
            EQ, OH = sb2("ls_eq", [P, 64, 8]), sb2("ls_oh", [P, 2, 64, 8])
            MX, CD = sb2("ls_mx", [P, 64]), sb2("ls_cd", [P, 64])
            with nc.Fori(0, NTILE - TG + 1, TG) as t:
                with stage(nc, "x_done", "q_ready", "v_ready", "q_done", "r_ready", "oh_done", "turned", "own_d", "kept") as (block, x_done, q_ready, v_ready, q_done, r_ready, oh_done, turned, own_d, kept):
                    @block.scalar
                    def _(act):
                        nc.scalar.activation(XC[:, :], k.XN[:, bass.ds(t * P, BLK)], ACT.Identity).then_inc(x_done, 1)
                        act.wait_ge(q_ready, 1)
                        nc.scalar.activation(QC[:, :], PS[:, 0, :], ACT.Identity).then_inc(q_done, 1)
                        act.wait_ge(v_ready, 1)
                        nc.scalar.activation(V1[:, bass.ds(t, TG), :, 1:17].rearrange("p a h f -> p (a h) f"), PS[:, 1, :].rearrange("p (h f) -> p h f", f=16), ACT.Identity).then_inc(kept, 1)
                        for u in range(TG):
                            act.wait_ge(turned, u + 1)
                            nc.scalar.activation(OHT[:, :, bass.ds(t * P + u * P, P)], PS[:, 6 + u % 2, :].rearrange("p (a b) -> p a b", b=P), ACT.Identity).then_inc(kept, 1)
                        act.wait_ge(kept, TG + 1)

                    @block.tensor
                    def _(pe):
                        pe.wait_ge(x_done, 1)
                        nc.tensor.matmul(PS[:, 0, :], W[pre + "w_qk"], XC[:, :], start=True, stop=True).then_inc(q_ready, 1)
                        for u in range(TG):
                            mm = nc.tensor.matmul(PS[:, 1, blk(u, P)], XC[:, blk(u, P)], W[pre + "w_v"], start=True, stop=True)
                        mm.then_inc(v_ready, 1)
                        pe.wait_ge(q_done, 1)
                        for u in range(TG):
                            nc.tensor.matmul(PS[:, 2 + u, :], QC[:, blk(u, P)], RB[:, :, :, :].rearrange("p h n k -> p (h n k)"), start=True, stop=True).then_inc(r_ready, 1)
                        for u in range(TG):
                            pe.wait_ge(oh_done, u + 1)
                            if u >= 2:
                                pe.wait_ge(kept, u)
                            for a in range(4):
                                mm = nc.tensor.transpose(PS[:, 6 + u % 2, blk(a, P)], OH[:, u % 2, 16 * a:16 * a + 16, :].rearrange("p a b -> p (a b)"), k.ident[:, :])
                            mm.then_inc(turned, 1)

                    @block.vector
                    def _(dve):
                        own = Link(dve, own_d)
                        bc = lambda x: x.unsqueeze(2).to_broadcast([P, 64, 8])
                        w8 = W8[:, :].unsqueeze(1).to_broadcast([P, 64, 8])
                        for u in range(TG):
                            r = PS[:, 2 + u, :].rearrange("p (a b) -> p a b", b=8)
                            dve.wait_ge(r_ready, u + 1)
                            own(nc.vector.tensor_reduce(MX[:, :], r, AX.X, ALU.max))
                            own(nc.vector.tensor_tensor(EQ[:, :, :], r, bc(MX[:, :]), ALU.is_equal))
                            own(nc.vector.tensor_tensor(EQ[:, :, :], EQ[:, :, :], w8, ALU.mult))
                            own(nc.vector.tensor_reduce(CD[:, :], EQ[:, :, :], AX.X, ALU.max))
                            if u >= 2:
                                dve.wait_ge(turned, u - 1)
                            nc.vector.tensor_tensor(OH[:, u % 2, :, :], w8, bc(CD[:, :]), ALU.is_equal).then_inc(oh_done, 1)
                            dve.wait_ge(oh_done, u + 1)

        KH, QH = sb("ls_kh", [P, HG, SEQ], BF16), sb("ls_qh", [P, HG, SEQ], BF16)
        QKS = sb("ls_qk", [P, 2, SEQ])
        QS, KS = QKS[:, 0, :], QKS[:, 1, :]
        V1S = sb("ls_v1s", [P, NT, HG, 17])
        WS = sb("ls_w", [P, 2, P])
        M2, M, MC = sb("ls_m2", [P, HG, NT, 2]), sb("ls_m", [P, HG, NT]), sb("ls_mc", [P, HG, NT])
        NM, MB = sb("ls_nm", [P, 2, HG, NT]), sb("ls_mb", [P, HG, NT, 3], BF16)
        A, D2 = sb("ls_a", [P, 3, BLK]), sb("ls_d", [P, 2, BLK])
        B = [QKS[:, n // 2, blk(n % 2)] for n in range(4)] + [k.lnA[:, blk(n)] for n in range(4)]
        PARTS, LOW = sb("ls_parts", [P, 2, SEQ], BF16), sb("ls_low", [P, 2, SEQ], BF16)
        CUM, VAL = k.lnA[:, 0:SEQ], k.lnA[:, SEQ:]
        OT, RD = CUM, VAL
        base = sb("ls_base", [P, 2])
        RQ = sb("ls_rq", [P, NT, HG])

        def body(b, r):
            tok = b * SEQ
            wide = lambda a: PS[:, a:a + 2, :].rearrange("p a b -> p (a b)")
            for pp in range(2):
                with stage(nc, "scanned", "base_ready", "val_done", "pos_ready", "dist_done", "hot_done", "own_d") as (block, scanned, base_ready, val_done, pos_ready, dist_done, hot_done, own_d):
                    oh = OHT[:, bass.ds(2 * r + pp, 1), bass.ds(tok, SEQ)].rearrange("p a n -> p (a n)")

                    @block.vector
                    def _(dve):
                        own = Link(dve, own_d)
                        nc.vector.tensor_tensor_scan(CUM, one[:, 0:1].to_broadcast([P, SEQ]), oh, 0.0, ALU.mult, ALU.add).then_inc(scanned, 1)
                        dve.wait_ge(base_ready, 1)
                        dve.wait_ge(scanned, 1)
                        own(nc.vector.tensor_scalar(base[:, 0:1], PS[:, 0, 0:1], -1.0, None, ALU.add))
                        nc.vector.scalar_tensor_tensor(out=VAL, in0=CUM, scalar=base[:, 0:1], in1=oh, op0=ALU.add, op1=ALU.mult).then_inc(val_done, 1)
                        for hh in range(2):
                            g = 2 * pp + hh
                            for t in range(2):
                                for n, (dst, lim) in enumerate(((KH, 32.0), (QH, BINC[:, 2:3]))):
                                    u = 4 * hh + 2 * t + n
                                    dve.wait_ge(dist_done, u + 1)
                                    nc.vector.tensor_scalar(dst[:, g, blk(t)], (A, D2)[n][:, t, :], lim, None, ALU.is_le).then_inc(hot_done, 1)
                        dve.wait_ge(hot_done, 8)

                    @block.tensor
                    def _(pe):
                        pe.wait_ge(scanned, 1)
                        nc.tensor.matmul(PS[:, 0, 0:1], BASEM[:, :], CUM[:, SEQ - 1:SEQ], start=True, stop=True).then_inc(base_ready, 1)
                        pe.wait_ge(val_done, 1)
                        for hh in range(2):
                            for t in range(2):
                                nc.tensor.matmul(PS[:, 1 + 2 * hh + t, :], SELP[:, hh, :], VAL[:, blk(t)], start=True, stop=True).then_inc(pos_ready, 1)

                    @block.scalar
                    def _(act):
                        for hh in range(2):
                            for t in range(2):
                                act.wait_ge(pos_ready, 2 * hh + t + 1)
                                for n in range(2):
                                    if hh:
                                        act.wait_ge(hot_done, 2 * t + n + 1)
                                    nc.scalar.activation((A, D2)[n][:, t, :], PS[:, 1 + 2 * hh + t, :], ACT.Abs, bias=BINC[:, n:n + 1]).then_inc(dist_done, 1)

            with stage(nc, "w_copied", "q_ready", "q_done", "squared", "sum_ready", "clamped", "root_done", "own_d") as (block, w_copied, q_ready, q_done, squared, sum_ready, clamped, root_done, own_d):
                @block.tensor
                def _(pe):
                    pe.wait_ge(w_copied, 1)
                    for t in range(2):
                        mm = nc.tensor.matmul(PS[:, t, :], WS[:, 0, :], k.XN[:, bass.ds(tok + t * BLK, BLK)], start=True, stop=True)
                    mm.then_inc(q_ready, 1)
                    pe.wait_ge(squared, 1)
                    for t in range(2):
                        mm = nc.tensor.matmul(PS[:, 2 + t, :], HS16[:, :], OT[:, blk(t)], start=True, stop=True)
                    mm.then_inc(sum_ready, 1)

                @block.scalar
                def _(act):
                    act.wait_ge(q_done, 1)
                    nc.scalar.activation(OT, KS, ACT.Square).then_inc(squared, 1)
                    act.wait_ge(clamped, 1)
                    nc.scalar.activation(RD, RD, ACT.Sqrt).then_inc(root_done, 1)

                @block.vector
                def _(dve):
                    own = Link(dve, own_d)
                    nc.vector.tensor_copy(WS[:, 0, :], W[pre + "Wqk2"][:, bass.ds(r, 1), :].rearrange("p a n -> p (a n)")).then_inc(w_copied, 1)
                    own(nc.vector.tensor_copy(WS[:, 1, :], W[pre + "WoP"][:, bass.ds(r, 1), :].rearrange("p a n -> p (a n)")))
                    own(nc.vector.tensor_copy(V1S[:, :, :, :], V1[:, bass.ds(b * NT, NT), bass.ds(r * HG, HG), :]))
                    dve.wait_ge(q_ready, 1)
                    nc.vector.tensor_copy(KS, wide(0)).then_inc(q_done, 1)
                    own(nc.vector.tensor_scalar(QS, wide(0), 0.25, None, ALU.mult))
                    dve.wait_ge(sum_ready, 1)
                    nc.vector.tensor_scalar(RD, wide(2), 1e-12, None, ALU.max).then_inc(clamped, 1)
                    dve.wait_ge(root_done, 1)
                    dve.wait_ge(q_done, 1)
                    own(nc.vector.reciprocal(RD, RD))
                    own(nc.vector.tensor_tensor(KS, KS, RD, ALU.mult))

            expand_heads(k, KS, QS, KX, QX, SEL, PARTS, LOW, 16)

            UNITS = [(g, i, t) for i in range(NT) for g in range(HG) for t in range(2)]
            with stage(nc, "sc_ready", "pen_done", "maxed", "own_d") as (block, sc_ready, pen_done, maxed, own_d):
                @block.tensor
                def _(pe):
                    for u, (g, i, t) in enumerate(UNITS):
                        if u >= 4:
                            pe.wait_ge(maxed, u - 3)
                        nc.tensor.matmul(PS[:, 4 + u % 4, :], QH[:, g, blk(i, P)], KH[:, g, blk(t)], start=True, stop=True)
                        nc.tensor.matmul(PS[:, u % 4, :], QX[0:MAXROW, g, blk(i, P)], KX[0:MAXROW, g, blk(t)], start=True, stop=True).then_inc(sc_ready, 1)

                @block.scalar
                def _(act):
                    for u, (g, i, t) in enumerate(UNITS):
                        act.wait_ge(sc_ready, u + 1)
                        if u >= 3:
                            act.wait_ge(maxed, u - 2)
                        nc.scalar.activation(A[:, u % 3, :], PS[:, 4 + u % 4, :], ACT.Exp, scale=-200.0, bias=BINC[:, 3:4]).then_inc(pen_done, 1)

                @block.vector
                def _(dve):
                    own = Link(dve, own_d)
                    for u, (g, i, t) in enumerate(UNITS):
                        dve.wait_ge(sc_ready, u + 1)
                        if t == i // 4:
                            tile = PS[:, u % 4, blk(i % 4, P)]
                            own(nc.vector.tensor_tensor(tile, tile, NI[:, :], ALU.mult))
                            own(nc.vector.tensor_tensor(tile, tile, SI[:, :], ALU.add))
                        dve.wait_ge(pen_done, u + 1)
                        sc = PS[:, u % 4, :]
                        nc.vector.tensor_tensor_reduce(sc, sc, A[:, u % 3, :], 1.0, -3e38, ALU.subtract, ALU.max, M2[:, g, i, t:t + 1]).then_inc(maxed, 1)
                    dve.wait_ge(maxed, len(UNITS))
                    own(nc.vector.tensor_reduce(M[:, :, :], M2[:, :, :, :], AX.X, ALU.max))
                    own(nc.vector.tensor_scalar(MC[:, :, :], M[:, :, :], -1.0, SELF, ALU.mult, ALU.add))
            expand_maxima(k, M, NM, MB, QX)

            UNITS = [(g, j, t) for j in range(NT) for t in range(2) for g in range(HG)]
            with stage(nc, "sc_ready", "diag_done", "exp_done", "p_done", "pv_done", "own_d", "copied") as (block, sc_ready, diag_done, exp_done, p_done, pv_done, own_d, copied):
                diags = [u for u, (g, j, t) in enumerate(UNITS) if t == j // 4]

                @block.tensor
                def _(pe):
                    zero_bank(nc, k, 6)
                    zero_bank(nc, k, 7)

                    def pv(x):
                        pe.wait_ge(p_done, HG * (x + 1))
                        for u in range(HG * x, HG * x + HG):
                            g, j, t = UNITS[u]
                            nc.tensor.matmul(PS[32 * g:32 * g + 17, 6 + t, :], V1S[:, j, g, :], B[u % (2 * HG)], start=False, stop=(x >= 2 * NT - 2), skip_group_check=True).then_inc(pv_done, 1)

                    for u, (g, j, t) in enumerate(UNITS):
                        if u >= 3:
                            pe.wait_ge(p_done, u - 2)
                        nc.tensor.matmul(PS[:, 3 + u % 3, :], KH[:, g, blk(j, P)], QH[:, g, blk(t)], start=True, stop=True)
                        nc.tensor.matmul(PS[:, u % 3, :], KX[0:MAXROW + 3, g, blk(j, P)], QX[0:MAXROW + 3, g, blk(t)], start=True, stop=True).then_inc(sc_ready, 1)
                        if u % HG == HG - 1 and u > HG:
                            pv(u // HG - 1)
                    pv(2 * NT - 1)

                @block.scalar
                def _(act):
                    for u, (g, j, t) in enumerate(UNITS):
                        act.wait_ge(sc_ready, u + 1)
                        if u in diags:
                            act.wait_ge(diag_done, diags.index(u) + 1)
                        if u >= 3:
                            act.wait_ge(p_done, u - 2)
                        nc.scalar.activation(A[:, u % 3, :], PS[:, u % 3, :], ACT.Exp).then_inc(exp_done, 1)

                @block.vector
                def _(dve):
                    own = Link(dve, own_d)

                    def diag(u):
                        g, j, t = UNITS[u]
                        if u in diags:
                            dve.wait_ge(sc_ready, u + 1)
                            tile = PS[:, u % 3, blk(j % 4, P)]
                            own(nc.vector.tensor_tensor(tile, tile, NI[:, :], ALU.mult))
                            nc.vector.scalar_tensor_tensor(out=tile, in0=k.ident[:, :], scalar=MC[:, g, j:j + 1], in1=tile, op0=ALU.mult, op1=ALU.add).then_inc(diag_done, 1)
                    diag(0)
                    for u, (g, j, t) in enumerate(UNITS):
                        if u + 1 < len(UNITS):
                            diag(u + 1)
                        dve.wait_ge(exp_done, u + 1)
                        if u >= 2 * HG:
                            dve.wait_ge(pv_done, u - 2 * HG + 1)
                        nc.vector.scalar_tensor_tensor(out=B[u % (2 * HG)], in0=A[:, u % 3, :], scalar=3e38, in1=PS[:, 3 + u % 3, :], op0=ALU.min, op1=ALU.mult).then_inc(p_done, 1)
                    dve.wait_ge(pv_done, len(UNITS))
                    nc.vector.tensor_copy(OT, wide(6)).then_inc(copied, 1)
                    dve.wait_ge(copied, 1)

            with stage(nc, "den_ready", "rec_ready", "den_spread", "o_done", "y_ready", "own_d") as (block, den_ready, rec_ready, den_spread, o_done, y_ready, own_d):
                @block.tensor
                def _(pe):
                    for i in range(NT):
                        mm = nc.tensor.matmul(PS[:, 4, blk(i, HG)], OT[:, blk(i, P)], k.head_row[:, :], start=True, stop=True)
                    mm.then_inc(den_ready, 1)
                    pe.wait_ge(rec_ready, 1)
                    for i in range(NT):
                        for g in range(HG):
                            turned_spread(nc, PS[32 * g:32 * g + 32, i // 4, blk(i % 4, P)], RQ[:, i, g:g + 1].to_broadcast([P, 32]), k.ident[:, :]).then_inc(den_spread, 1)
                    for h in range(2):
                        pe.wait_ge(o_done, h + 1)
                        nc.tensor.matmul(PS[:, 2 + h, :], WS[:, 1, :], OT[:, blk(h)], start=True, stop=True).then_inc(y_ready, 1)

                @block.vector
                def _(dve):
                    own = Link(dve, own_d)
                    dve.wait_ge(den_ready, 1)
                    nc.vector.reciprocal(RQ[:, :, :], PS[:, 4, 0:NT * HG].rearrange("p (a b) -> p a b", b=HG)).then_inc(rec_ready, 1)
                    for h in range(2):
                        dve.wait_ge(den_spread, (h + 1) * HG * NT // 2)
                        nc.vector.tensor_tensor(OT[:, blk(h)], OT[:, blk(h)], PS[:, h, :], ALU.mult).then_inc(o_done, 1)
                    for h in range(2):
                        dve.wait_ge(y_ready, h + 1)
                        xb = k.X[:, bass.ds(tok + h * BLK, BLK)]
                        own(nc.vector.tensor_tensor(xb, xb, PS[:, 2 + h, :], ALU.add))

        with nc.Fori(0, BATCH) as b:
            with nc.Fori(0, 2) as r:
                body(b, r)
        with stage(nc, "bias_added") as (block, bias_added):
            @block.vector
            def _(dve):
                nc.vector.tensor_scalar(k.X[:, :], k.X[:, :], W[pre + "b_out"], None, ALU.add).then_inc(bias_added, 1)
                dve.wait_ge(bias_added, 1)



SMALL_W = {
    "L0a": {
        "L0_attn_a_Wq": [P, P], "L0_attn_a_Wk": [P, P], "L0_attn_a_Wv": [P, P], "L0_attn_a_Wo": [P, P], "L0_attn_a_Wb": [P, 4],
        "L0_attn_a_conv": [P, 3, 4], "L0_attn_a_fir_s": [P, 5], "L0_attn_a_fir_l": [P, 64], "L0_attn_a_W1x": [P, P], "L0_attn_a_W1s": [P, 4, P],
        "L0_attn_a_b1": [P, 1], "L0_attn_a_W2": [P, 4], "L0_attn_a_b2": [P, 4], "L0_attn_a_copy_bias": [P, 4], "L0_attn_a_log_temp": [P, 4],
        "L0_attn_a_o_norm_w": [P, 1],
    },
    "L0": {
        "L0_ffn_ln_g": [P, 1], "L0_ffn_ln_b": [P, 1], "L0_ffn_abel_w": [P, P], "L0_ffn_abel_b": [P, 1], "L0_ffn_gate_w_moe": [P, 8],
        "L0_ffn_gate_b_moe": [P, 8], "L0_ffn_b1": [P, 8, 4], "L0_ffn_b2": [P, 8], "L0_ffn_mix_w": [P, 2], "L0_ffn_mix_b": [P, 1],
        "L0_ffn_gens": [P, 2, 3, P], "L0_attn_b_W_in": [P, 512], "L0_attn_b_conv_w": [P, 2, 4], "L0_attn_b_conv_b": [P, 2],
        "L0_attn_b_W_x": [P, 2, 40], "L0_attn_b_W_dt": [8, 256], "L0_attn_b_b_dt": [P, 2], "L0_attn_b_A_log": [P, 2, 16], "L0_attn_b_D": [P, 2],
        "L0_attn_b_W_out": [P, 2, P],
    },
    "L1": {
        "L1_ffn_w1_s": [P, 4], "L1_ffn_w2_s": [P, 4], "L1_ffn_h1_s": [P, 4], "L1_ffn_h2_s": [P, 4], "L1_ffn_w3_s": [P, 1], "L1_attn_a_Wq": [P, P],
        "L1_attn_a_Wk": [P, P], "L1_attn_a_WoP": [P, 4, P], "L1_attn_a_Wv": [P, P], "L1_attn_b_w_qk": [P, P], "L1_attn_b_w_v": [P, P],
        "L1_attn_b_rot": [P, 32], "L1_attn_b_Wqk2": [P, 2, P], "L1_attn_b_WoP": [P, 2, P], "L1_attn_b_b_out": [P, 1],
    },
    "L2": {
        "L2_ffn_router_w": [P, 16], "L2_attn_b_WQ": [P, P], "L2_attn_b_WK": [P, P], "L2_attn_b_WV": [P, P], "L2_attn_a_mu0": [P, 1],
        "L2_attn_a_W_x0": [P, 160], "L2_attn_a_W_x2a": [P, P], "L2_attn_a_W_x2b": [32, P], "L2_attn_a_x_bias": [P, 5], "L2_attn_a_W_r2": [P, P],
        "L2_attn_a_W_w1": [P, 64], "L2_attn_a_W_w22": [64, P], "L2_attn_a_b_w22": [P, 1], "L2_attn_a_W_k2": [P, P], "L2_attn_a_W_v": [P, P],
        "L2_attn_a_W_g": [P, P], "L2_attn_a_bonus": [64, 1], "L2_attn_a_gn_weight": [P, 1], "L2_attn_a_gn_bias": [P, 1], "L2_attn_a_W_o": [P, P],
    },
    "L3": {
        "L3_ffn_Wg": [P, 8], "L3_ffn_b1": [P, 8, 4], "L3_ffn_b2": [P, 8, P], "L3_attn_b_Wq": [P, P], "L3_attn_b_Wk": [P, P],
        "L3_attn_b_WoP": [P, 4, P], "L3_attn_b_Wv": [P, P], "L3_attn_b_bq3": [P, 4], "L3_attn_b_bk3": [P, 4], "L3_attn_b_bv": [P, P],
        "L3_attn_b_bo": [P, 1], "L3_attn_a_Wq": [P, P],
    },
}
FFN_W = {
    "L0": {"L0_ffn_w1": [P, 8, 512], "L0_ffn_w2": [P, 8, 4, P]},
    "L1": {"L1_ffn_w1": [P, 512], "L1_ffn_w2": [P, 512], "L1_ffn_h1": [P, 4, 512], "L1_ffn_h2": [P, 4, 512], "L1_ffn_w3": [P, 4, P]},
    "L2": {"L2_ffn_wg_r": [P, 512], "L2_ffn_wu_r": [P, 512], "L2_ffn_wd_r": [P, 4, P],
           "L2_ffn_wg_s": [P, P], "L2_ffn_wu_s": [P, P], "L2_ffn_wd_s": [P, P]},
    "L3": {"L3_ffn_W1": [P, 8, 512], "L3_ffn_W2": [P, 8, 4, P]},
}


def columns(shape):
    return int(np.prod(shape[1:]))


def pack_columns(group):
    return sum(columns(shape) for shape in group.values())


LOAD_PARTS = 4
FFN_COLS = max(pack_columns(group) for group in FFN_W.values())


def weight_views(k, place, group):
    at = 0
    for name, shape in group.items():
        ap = place[0:shape[0], at:at + columns(shape)]
        if len(shape) == 3:
            ap = ap.rearrange("p (a b) -> p a b", a=shape[1])
        if len(shape) == 4:
            ap = ap.rearrange("p (a b c) -> p a b c", a=shape[1], b=shape[2])
        k.W[name] = ap
        at += columns(shape)



def load_ffn(k, layer):
    nc, n = k.nc, pack_columns(FFN_W[layer])
    with stage(nc) as (block,):
        @block.sync
        def _(sp):
            for c in range(LOAD_PARTS):
                part = slice(c * n // LOAD_PARTS, (c + 1) * n // LOAD_PARTS)
                sp.dma_start(k.ffn_place[:, part], k.ins["ffn_" + layer][:, part]).then_inc(k.ffn_loaded, 16)
    k.ffn_count += 16 * LOAD_PARTS
    weight_views(k, k.ffn_place, FFN_W[layer])


def await_loads(k, sem, count):
    with stage(k.nc) as (block,):
        @block.sync
        def _(sp):
            sp.wait_ge(sem, count)


def constants(k, st):
    nc = k.nc

    def sb(n, shape, dt=F32):
        return k.sbuf(st, n, shape, dt)
    k.ident = sb("ident", [P, P])
    k.mean_mat = sb("mean_mat", [P, P])
    k.eps_col = sb("eps_col", [P, 1])
    k.rstd = sb("rstd", [P, NTILE])
    k.iota_row = sb("iota_row", [P, 16])
    k.sel8 = sb("sel8", [8, 8, P])
    k.sel16 = sb("sel16", [16, 4, P])
    k.rot = sb("rot", [P, P])
    k.mixm = sb("mixm", [P, 2, P])
    k.more = []
    k.zeros16 = sb("zeros16", [P, BLK], BF16)
    k.head_row = sb("head_row", [P, 4])

    def attention_constants(pool, own):
        own(pool.memset(k.zeros16[:, :], 0.0))
        own(pool.memset(k.identb[:, :], 0.0))
        own(pool.affine_select(out=k.identb[:, :], in_=k.identb[:, :], compare_op=ALU.not_equal, fill=1.0, base=0, pattern=[[-1, P]], channel_multiplier=1))
        own(pool.memset(k.head_row[:, :], 0.0))
        own(pool.affine_select(out=k.head_row[:, :], in_=k.head_row[:, :], compare_op=ALU.not_equal, fill=1.0, base=0, pattern=[[-32, 4]], channel_multiplier=1))
    k.more.append(attention_constants)
    k.identb = sb("identb", [P, P], BF16)
    with stage(nc, "own_p") as (block, own_p):
        @block.gpsimd
        def _(pool):
            own = Link(pool, own_p)
            own(pool.memset(k.ident[:, :], 0.0))
            own(pool.affine_select(out=k.ident[:, :], in_=k.ident[:, :], compare_op=ALU.not_equal, fill=1.0, base=0, pattern=[[-1, P]], channel_multiplier=1))
            own(pool.memset(k.mean_mat[:, :], 1.0 / D))
            own(pool.memset(k.eps_col[:, :], EPS))
            own(pool.iota(k.iota_row[:, :], [[1, 16]], base=0, channel_multiplier=0, allow_small_or_imprecise_dtypes=True))
            own(pool.memset(k.sel8[:, :, :], 0.0))
            own(pool.affine_select(out=k.sel8[:, :, :], in_=k.sel8[:, :, :], compare_op=ALU.not_equal, fill=1.0, base=0, pattern=[[-1, 8], [0, P]], channel_multiplier=1))
            own(pool.memset(k.sel16[:, :, :], 0.0))
            own(pool.affine_select(out=k.sel16[:, :, :].rearrange("e c (q r) -> e c q r", r=32), in_=k.sel16[:, :, :].rearrange("e c (q r) -> e c q r", r=32),
                                   compare_op=ALU.not_equal, fill=1.0, base=0, pattern=[[-4, 4], [-1, 4], [0, 32]], channel_multiplier=1))
            for f in k.more:
                f(pool, own)


SUBLAYERS = ["l0a", "l0_ffn", "l0b", "l0_ffn", "l1a", "l1_ffn", "l1b", "l1_ffn",
             "l2a", "l2_ffn", "l2b", "l2_ffn", "l3a", "l3_ffn", "l3b", "l3_ffn"]


def program(nc, ins, out, first=0, last=16):
    k = Core(nc)
    k.ins, k.ffn_count = ins, 0
    run = {"l0a": l0a, "l0b": l0b, "l1a": l1a, "l1b": l1b, "l2a": l2a, "l2b": l2b, "l3a": l3a, "l3b": l3b,
           "l0_ffn": l0_ffn, "l1_ffn": l1_ffn, "l2_ffn": l2_ffn, "l3_ffn": l3_ffn}
    with ExitStack() as st:
        k.X = k.sbuf(st, "X", [P, NTOK])
        k.XN = k.sbuf(st, "XN", [P, NTOK])
        k.lnA = k.sbuf(st, "lnA", [P, NTOK])
        k.ffn_place = k.sbuf(st, "ffn_place", [P, FFN_COLS])
        k.PS = st.enter_context(nc.psum_tensor("PS", [P, 8, BLK], F32))
        k.ffn_loaded = st.enter_context(nc.semaphore("ffn_loaded"))
        small_loaded = st.enter_context(nc.semaphore("small_loaded"))
        places = {g: k.sbuf(st, "small_" + g, [P, pack_columns(group)]) for g, group in SMALL_W.items()}
        with stage(nc) as (block,):
            @block.sync
            def _(sp):
                for b in range(NBLK):
                    sp.dma_start(k.X[:, blk(b)], ins["x"][:, blk(b)]).then_inc(small_loaded, 16)
                for g in SMALL_W:
                    sp.dma_start(places[g][:, :], ins["small_" + g]).then_inc(small_loaded, 16)
        for g, group in SMALL_W.items():
            weight_views(k, places[g], group)
        load_ffn(k, SUBLAYERS[first | 1][0:2].upper())
        constants(k, st)
        await_loads(k, small_loaded, 16 * (NBLK + len(SMALL_W)))
        if first <= 3 and last > 1:
            expm_product(k)
        for i in range(first, last):
            name = SUBLAYERS[i]
            if name.endswith("ffn"):
                await_loads(k, k.ffn_loaded, k.ffn_count)
            with ExitStack() as layer:
                if name.endswith("ffn"):
                    k.gT = k.sbuf(layer, "gates", [16, NTOK])
                run[name](k)
            if name.endswith("ffn") and i + 2 < last and SUBLAYERS[i + 2] != name:
                load_ffn(k, SUBLAYERS[i + 2][0:2].upper())
        with stage(nc, "stored") as (block, stored):
            @block.sync
            def _(sp):
                for b in range(NBLK):
                    sp.dma_start(out[:, blk(b)], k.X[:, blk(b)]).then_inc(stored, 16)
                sp.wait_ge(stored, 16 * NBLK)


def layout(inputs):
    i = {n: np.asarray(a) for n, a in inputs.items()}

    def col(a, c=1):
        return a.reshape(c, P).T
    r = {"x": i["L0_attn_a_hidden_states"].reshape(NTOK, D).T}
    for n in ("L0_ffn_ln_g", "L0_ffn_ln_b", "L0_ffn_abel_b", "L1_ffn_w3_s"):
        r[n] = col(i[n])
    for n in ("L0_ffn_abel_w", "L0_ffn_gate_w_moe", "L3_ffn_Wg", "L2_ffn_router_w"):
        r[n] = i[n]
    r["L0_ffn_gate_b_moe"] = i["L0_ffn_gate_b_moe"].reshape(1, 8)
    r["L0_ffn_mix_b"] = i["L0_ffn_mix_b"].reshape(1, 1)
    r["L0_ffn_mix_w"] = i["L0_ffn_mix_w"].reshape(2, P).T
    g = i["L0_ffn_gens"]
    r["L0_ffn_gens"] = np.stack([g.transpose(1, 0, 2), g.transpose(2, 0, 1)], axis=1)
    for a, w1, w2 in (("L0_ffn_", "w1", "w2"), ("L3_ffn_", "W1", "W2")):
        r[a + w1] = i[a + w1].transpose(1, 0, 2).reshape(P, -1)
        r[a + w2] = i[a + w2].reshape(8, 4, P, D).transpose(2, 0, 1, 3).reshape(P, -1)
        r[a + "b1"] = i[a + "b1"].reshape(8, 4, P).transpose(2, 0, 1)
        r[a + "b2"] = i[a + "b2"].T
    r["L3_ffn_b2"] = np.broadcast_to(i["L3_ffn_b2"], (P, 8, D))
    for n in ("w1", "w2"):
        r["L1_ffn_" + n] = i[f"L1_ffn_{n}_w"].T
    for n in ("h1", "h2", "w3"):
        w = i[f"L1_ffn_{n}_w"]
        r["L1_ffn_" + n] = w.T.reshape(4, P, w.shape[0]).transpose(1, 0, 2).reshape(P, -1)
    for n in ("w1", "w2", "h1", "h2"):
        r[f"L1_ffn_{n}_s"] = col(i[f"L1_ffn_{n}_s"], 4)
    for n in ("wg_r", "wu_r", "wg_s", "wu_s"):
        r["L2_ffn_" + n] = i["L2_ffn_" + n].transpose(1, 0, 2).reshape(P, -1)
    r["L2_ffn_wd_r"] = i["L2_ffn_wd_r"].reshape(4, P, D).transpose(1, 0, 2).reshape(P, -1)
    r["L2_ffn_wd_s"] = i["L2_ffn_wd_s"].reshape(P, D)
    def padded(a):
        o = np.zeros(a.shape[:-1] + (4, 4, 32), a.dtype)
        o[..., 1:9] = a.reshape(a.shape[:-1] + (4, 4, 8))
        return o.reshape(a.shape[:-1] + (4, P))
    for a in ("L1_attn_a_", "L3_attn_b_"):
        r[a + "Wq"], r[a + "Wk"] = i[a + "Wq"].T, i[a + "Wk"].T
        r[a + "WoP"] = padded(i[a + "Wo"]).transpose(2, 1, 0)
        r[a + "Wv"] = i[a + "Wv"].T
    for n in ("bq", "bk"):
        r[f"L3_attn_b_{n}3"] = np.tile(i["L3_attn_b_" + n].reshape(4, 32).T, (4, 1))
    r["L3_attn_b_bv"] = i["L3_attn_b_bv"].reshape(1, P)
    r["L3_attn_b_bo"] = col(i["L3_attn_b_bo"])
    for n in ("WQ", "WK", "WV"):
        r["L2_attn_b_" + n] = i["L2_attn_b_" + n].T
    r["L3_attn_a_Wq"] = i["L3_attn_a_queries_weight"]
    for n in ("conv_w", "A_log"):
        r["L0_attn_b_" + n] = i["L0_attn_b_" + n].reshape(2, P, -1).transpose(1, 0, 2)
    r["L0_attn_b_W_in"] = i["L0_attn_b_W_in"].T
    for n in ("conv_b", "b_dt", "D"):
        r["L0_attn_b_" + n] = col(i["L0_attn_b_" + n], 2)
    r["L0_attn_b_W_x"] = i["L0_attn_b_W_x"].T.reshape(2, P, 40).transpose(1, 0, 2)
    r["L0_attn_b_W_dt"] = i["L0_attn_b_W_dt"].T
    r["L0_attn_b_W_out"] = i["L0_attn_b_W_out"].T.reshape(2, P, P).transpose(1, 0, 2)
    for n in ("W_x0", "W_r", "W_w1", "W_w2", "W_k", "W_v", "W_g", "W_o", "x_bias"):
        r["L2_attn_a_" + n] = i["L2_attn_a_" + n].T
    r["L2_attn_a_W_x2a"], r["L2_attn_a_W_x2b"] = i["L2_attn_a_W_x2"].T[:P], i["L2_attn_a_W_x2"].T[P:]
    for n in ("mu0", "b_w2", "bonus", "gn_weight", "gn_bias"):
        r["L2_attn_a_" + n] = i["L2_attn_a_" + n].reshape(-1, 1)
    for n in ("W_r", "W_k", "W_w2"):
        r[f"L2_attn_a_{n}2"] = np.concatenate([r["L2_attn_a_" + n]] * 2, axis=1)
    r["L2_attn_a_b_w22"] = np.concatenate([r["L2_attn_a_b_w2"]] * 2)
    a = "L0_attn_a_"
    for n in ("Wq", "Wk", "Wv", "Wo", "Wb"):
        r[a + n] = i[a + n].T
    r[a + "conv"] = np.stack([i[a + f"conv_{n}_w"] for n in "qkv"], axis=1)
    r[a + "fir_s"], r[a + "fir_l"] = i[a + "fir_short_filt"].reshape(P, 5), i[a + "fir_long_filt"].reshape(P, 64)
    w1 = i[a + "gate_W1"].T
    r[a + "W1x"] = w1[:P]
    w1s = np.zeros((4, 32, 4, P), w1.dtype)
    for h in range(4):
        w1s[:, 4 * h:4 * h + 4, h] = w1[P:].reshape(4, 4, P).transpose(1, 0, 2)
    r[a + "W1s"] = w1s.reshape(P, 4, P)
    r[a + "b1"], r[a + "W2"] = i[a + "gate_b1"].reshape(P, 1), i[a + "gate_W2"].T
    r[a + "b2"] = i[a + "gate_b2"].reshape(1, 4)
    r[a + "copy_bias"], r[a + "log_temp"] = i[a + "gate_copy_bias"].reshape(1, 4), i[a + "gate_log_temp"].reshape(1, 4)
    r[a + "o_norm_w"] = np.broadcast_to(i[a + "o_norm_w"], (4, 32)).reshape(P, 1)
    def padded16(a):
        o = np.zeros(a.shape[:-1] + (2, 4, 32), a.dtype)
        o[..., 1:17] = a.reshape(a.shape[:-1] + (2, 4, 16))
        return o.reshape(a.shape[:-1] + (2, P))
    a = "L1_attn_b_"
    r[a + "w_qk"], r[a + "w_v"] = i[a + "w_qk"], i[a + "w_v"]
    r[a + "rot"] = np.broadcast_to(i[a + "rotations"].reshape(16, 32), (8, 16, 32)).reshape(P, 32)
    r[a + "Wqk2"] = np.tile(i[a + "w_qk"].reshape(P, 2, 1, 64), (1, 1, 2, 1)).reshape(P, 2, P)
    r[a + "WoP"] = padded16(i[a + "w_out"].T).transpose(2, 1, 0)
    r[a + "b_out"] = col(i[a + "b_out"])
    def pack(group):
        o = np.zeros((P, pack_columns(group)), np.float32)
        at = 0
        for name, shape in group.items():
            a = np.asarray(r[name]).reshape(len(r[name]), columns(shape))
            o[0:shape[0], at:at + columns(shape)] = a
            at += columns(shape)
        return o
    packed = {"x": np.ascontiguousarray(r["x"])}
    packed.update({"small_" + g: pack(group) for g, group in SMALL_W.items()})
    packed.update({"ffn_" + g: pack(group) for g, group in FFN_W.items()})
    return packed


def kernel(**inputs):
    import concourse.bacc as bacc
    from concourse.bass_utils import run_bass_kernel_spmd

    arrays = layout(inputs)
    nc = bacc.Bacc("TRN2", target_bir_lowering=False, num_devices=1)
    ins = {n: nc.dram_tensor(f"in_{n}", a.shape, F32, kind="ExternalInput").ap() for n, a in arrays.items()}
    out = nc.dram_tensor("out_x", (D, NTOK), F32, kind="ExternalOutput").ap()
    program(nc, ins, out)
    r = run_bass_kernel_spmd(nc, [{f"in_{n}": a for n, a in arrays.items()}], core_ids=[0])
    return np.ascontiguousarray(r.results[0]["out_x"].T).reshape(BATCH, SEQ, D)
```
